# Optimizing a Trainium2 kernel written in Bass

```python
import numpy as np
import jax
import jax.numpy as jnp

def _softmax(x, axis=-1):
    return jax.nn.softmax(x, axis=axis)

def _gelu(x):
    return jax.nn.gelu(x, approximate=True)

def _silu(x):
    return jax.nn.silu(x)

def _sigmoid(x):
    return jax.nn.sigmoid(x)

def _layernorm(x, axis=-1, eps=1e-05):
    m = jnp.mean(x, axis=axis, keepdims=True)
    v = jnp.var(x, axis=axis, keepdims=True)
    return (x - m) / jnp.sqrt(v + eps)

def _scatter_add(tgt, idx, src, axis=0):
    return tgt.at[idx].add(src)

def _segment_sum(src, seg, n):
    return jax.ops.segment_sum(src, seg, n)
kernel_name = 'mk_adaln_d4_jaxref_r8_268b33'

def setup_inputs(seed: int=0):
    np.random.seed(seed)
    _w = jnp.asarray

    def _L0_attn_setup():
        import jax, jax.numpy as jnp
        import numpy as np
        from jax import lax
        D_MODEL, D_STATE, D_CONV, EXPAND = (128, 16, 4, 2)
        D_INNER = EXPAND * D_MODEL
        DT_RANK = (D_MODEL + 15) // 16
        B, T = (4, 256)

        def _causal_depthwise_conv(xb, conv_w, conv_b):
            inp = xb.transpose(0, 2, 1)
            ker = conv_w[:, None, :]
            dn = lax.conv_dimension_numbers(inp.shape, ker.shape, ('NCH', 'OIH', 'NCH'))
            out = lax.conv_general_dilated(inp, ker, window_strides=(1,), padding=[(D_CONV - 1, 0)], dimension_numbers=dn, feature_group_count=D_INNER)
            return (out + conv_b[None, :, None]).transpose(0, 2, 1)
        key = jax.random.key(seed)
        ks = jax.random.split(key, 10)
        s = lambda fan_in: 1.0 / np.sqrt(fan_in)
        return {'x': jax.random.normal(ks[0], (B, T, D_MODEL), dtype=jnp.float32), 'in_proj_w': jax.random.normal(ks[1], (D_MODEL, 2 * D_INNER), dtype=jnp.float32) * s(D_MODEL), 'conv_w': jax.random.normal(ks[2], (D_INNER, D_CONV), dtype=jnp.float32) * s(D_CONV), 'conv_b': jax.random.normal(ks[3], (D_INNER,), dtype=jnp.float32) * 0.1, 'x_proj_w': jax.random.normal(ks[4], (D_INNER, DT_RANK + 2 * D_STATE), dtype=jnp.float32) * s(D_INNER), 'dt_proj_w': jax.random.normal(ks[5], (DT_RANK, D_INNER), dtype=jnp.float32) * s(DT_RANK), 'dt_proj_b': jax.random.normal(ks[6], (D_INNER,), dtype=jnp.float32) * 0.1, 'A_log': jax.random.normal(ks[7], (D_INNER, D_STATE), dtype=jnp.float32) * 0.5, 'D_param': jnp.ones((D_INNER,), dtype=jnp.float32), 'out_proj_w': jax.random.normal(ks[8], (D_INNER, D_MODEL), dtype=jnp.float32) * s(D_INNER)}
    _L0_attn_in = _L0_attn_setup()

    def _L0_ffn_setup():
        import jax, jax.numpy as jnp
        import numpy as np
        DM, NE, ES, ESZ = (128, 16, 4, 64)
        BATCH, SEQ = (8, 256)
        key = jax.random.key(seed)
        k = jax.random.split(key, 5)
        scale = 0.02
        return {'x': jax.random.normal(k[0], (BATCH, SEQ, DM), dtype=jnp.float32), 'controller': jax.random.normal(k[1], (DM, NE, ES), dtype=jnp.float32) * scale, 'f1': jax.random.normal(k[2], (DM, NE, ES, ESZ), dtype=jnp.float32) * scale, 'f2': jax.random.normal(k[3], (NE, ES, ESZ, DM), dtype=jnp.float32) * scale, 'bias': jax.random.normal(k[4], (NE, ES, ESZ), dtype=jnp.float32) * scale}
    _L0_ffn_in = _L0_ffn_setup()
    _L0_c = _w((lambda *s: np.random.randn(*s).astype(np.float32) * 0.05)(4, 128))
    _L0_wmod = _w((lambda *s: np.random.randn(*s).astype(np.float32) * 0.05)(128, 6 * 128) * 128 ** (-0.5))

    def _L1_attn_setup():
        import jax, jax.numpy as jnp
        import numpy as np
        D_MODEL = 128
        N_HEADS = 16
        D_LATENT = 32
        HEAD_DIM = D_MODEL // N_HEADS

        def apply_rope(x):
            B, T, H, D = x.shape
            inv_freq = 1.0 / 10000.0 ** (jnp.arange(0, D, 2, dtype=jnp.float32) / D)
            t = jnp.arange(T, dtype=jnp.float32)
            freqs = t[:, None] * inv_freq[None, :]
            sin_f = jnp.sin(freqs)[None, :, None, :]
            cos_f = jnp.cos(freqs)[None, :, None, :]
            x1, x2 = jnp.split(x, 2, axis=-1)
            return jnp.concatenate([x1 * cos_f - x2 * sin_f, x1 * sin_f + x2 * cos_f], axis=-1)
        key = jax.random.key(seed)
        ks = jax.random.split(key, 10)
        B, T = (4, 512)
        s = lambda fan_in: 1.0 / np.sqrt(fan_in)
        return {'x': jax.random.normal(ks[0], (B, T, D_MODEL), dtype=jnp.float32), 'Wq': jax.random.normal(ks[1], (D_MODEL, D_MODEL), dtype=jnp.float32) * s(D_MODEL), 'bq': jnp.zeros((D_MODEL,), jnp.float32), 'Wdown': jax.random.normal(ks[2], (D_MODEL, D_LATENT), dtype=jnp.float32) * s(D_MODEL), 'bdown': jnp.zeros((D_LATENT,), jnp.float32), 'Wup': jax.random.normal(ks[3], (D_LATENT, 2 * D_MODEL), dtype=jnp.float32) * s(D_LATENT), 'bup': jnp.zeros((2 * D_MODEL,), jnp.float32), 'Wout': jax.random.normal(ks[4], (D_MODEL, D_MODEL), dtype=jnp.float32) * s(D_MODEL), 'bout': jnp.zeros((D_MODEL,), jnp.float32)}
    _L1_attn_in = _L1_attn_setup()

    def _L1_ffn_setup():
        import jax, jax.numpy as jnp
        import numpy as np
        B, S, H = (1, 128, 128)
        E = 128
        NEXP = 16
        TOPK = 2
        ALPHA = 1.702
        LIMIT = 7.0

        def _moe_forward(x, Wg, bg, Wgu, bgu, Wd, bd):
            b, s, h = x.shape
            xt = x.reshape(-1, h)
            logits = xt @ Wg.T + bg
            top_vals, top_idx = jax.lax.top_k(logits, TOPK)
            rw = jax.nn.softmax(top_vals.astype(jnp.float32), axis=-1).astype(xt.dtype)
            onehot = jax.nn.one_hot(top_idx, NEXP, dtype=xt.dtype)
            cw = jnp.einsum('tk,tke->te', rw, onehot)
            gu = jnp.einsum('th,ehf->tef', xt, Wgu) + bgu[None]
            gate = gu[..., ::2]
            up = gu[..., 1::2]
            gate = jnp.minimum(gate, LIMIT)
            up = jnp.clip(up, -LIMIT, LIMIT)
            glu = gate * jax.nn.sigmoid(gate * ALPHA)
            gated = (up + 1.0) * glu
            out_e = jnp.einsum('tef,efh->teh', gated, Wd) + bd[None]
            out = jnp.einsum('teh,te->th', out_e, cw)
            return out.reshape(b, s, h)
        key = jax.random.key(seed)
        ks = jax.random.split(key, 8)
        hidden_states = jax.random.normal(ks[0], (B, S, H), dtype=jnp.float32)
        Wg = jax.random.normal(ks[1], (NEXP, H), dtype=jnp.float32) / np.sqrt(H)
        bg = jax.random.normal(ks[2], (NEXP,), dtype=jnp.float32) * 0.01
        Wgu = jax.random.normal(ks[3], (NEXP, H, 2 * E), dtype=jnp.float32) / np.sqrt(H)
        bgu = jax.random.normal(ks[4], (NEXP, 2 * E), dtype=jnp.float32) * 0.01
        Wd = jax.random.normal(ks[5], (NEXP, E, H), dtype=jnp.float32) / np.sqrt(E)
        bd = jax.random.normal(ks[6], (NEXP, H), dtype=jnp.float32) * 0.01
        return {'hidden_states': hidden_states, 'Wg': Wg, 'bg': bg, 'Wgu': Wgu, 'bgu': bgu, 'Wd': Wd, 'bd': bd}
    _L1_ffn_in = _L1_ffn_setup()
    _L1_c = _w((lambda *s: np.random.randn(*s).astype(np.float32) * 0.05)(4, 128))
    _L1_wmod = _w((lambda *s: np.random.randn(*s).astype(np.float32) * 0.05)(128, 6 * 128) * 128 ** (-0.5))

    def _L2_attn_setup():
        import jax, jax.numpy as jnp
        import numpy as np
        B, N, E, H = (2, 256, 128, 8)
        HID = 128
        D = HID // H
        EPS = 1e-08

        def rms_norm(x, scale):
            rms = jnp.linalg.norm(x, axis=-1, keepdims=True) * x.shape[-1] ** (-0.5)
            return scale * (x / (rms + EPS))
        key = jax.random.key(seed)
        ks = jax.random.split(key, 12)
        s = 0.02
        return {'x': jax.random.normal(ks[0], (B, N, E), jnp.float32), 'Wq': jax.random.normal(ks[1], (HID, E), jnp.float32) * s, 'bq': jnp.zeros((HID,), jnp.float32), 'Wk': jax.random.normal(ks[2], (HID, E), jnp.float32) * s, 'bk': jnp.zeros((HID,), jnp.float32), 'Wv': jax.random.normal(ks[3], (HID, E), jnp.float32) * s, 'bv': jnp.zeros((HID,), jnp.float32), 'Wu': jax.random.normal(ks[4], (HID, E), jnp.float32) * s, 'bu': jnp.zeros((HID,), jnp.float32), 'Wo': jax.random.normal(ks[5], (E, HID), jnp.float32) * s, 'bo': jnp.zeros((E,), jnp.float32), 'scale': jnp.ones((HID,), jnp.float32)}
    _L2_attn_in = _L2_attn_setup()

    def _L2_ffn_setup():
        import jax, jax.numpy as jnp
        import numpy as np
        TOP_K = 2
        key = jax.random.key(seed)
        k0, k1, k2, k3 = jax.random.split(key, 4)
        B, T, C, E, F = (4, 256, 128, 8, 512)
        x = jax.random.normal(k0, (B, T, C), dtype=jnp.float32)
        gate_w = jax.random.normal(k1, (C, E), dtype=jnp.float32) * 0.02
        w1 = jax.random.normal(k2, (E, C, F), dtype=jnp.float32) * 0.02
        w2 = jax.random.normal(k3, (E, F, C), dtype=jnp.float32) * 0.02
        return {'x': x, 'gate_w': gate_w, 'w1': w1, 'w2': w2}
    _L2_ffn_in = _L2_ffn_setup()
    _L2_c = _w((lambda *s: np.random.randn(*s).astype(np.float32) * 0.05)(4, 128))
    _L2_wmod = _w((lambda *s: np.random.randn(*s).astype(np.float32) * 0.05)(128, 6 * 128) * 128 ** (-0.5))

    def _L3_attn_setup():
        import jax, jax.numpy as jnp
        import numpy as np
        DIM = 128
        HEADS = 16
        HEAD_DIM = DIM // HEADS
        WINDOW = 64
        NEG = -1000000000.0

        def _sliding_window_attn(x, Wq, bq, Wk, bk, Wv, bv, Wo, bo):
            B, S, D = x.shape
            H, hd, W = (HEADS, HEAD_DIM, WINDOW)
            nb = S // W

            def proj(Wp, bp):
                y = x @ Wp.T + bp
                return y.reshape(B, S, H, hd).transpose(0, 2, 1, 3)
            q = proj(Wq, bq)
            k = proj(Wk, bk)
            v = proj(Wv, bv)
            scale = hd ** (-0.5)
            qb = q.reshape(B, H, nb, W, hd)

            def window_kv(t):
                pad = jnp.concatenate([jnp.zeros((B, H, W, hd), t.dtype), t], axis=2)
                prev = pad[:, :, :S].reshape(B, H, nb, W, hd)
                cur = t.reshape(B, H, nb, W, hd)
                return jnp.concatenate([prev, cur], axis=3)
            kw = window_kv(k)
            vw = window_kv(v)
            scores = jnp.einsum('bhnqd,bhnkd->bhnqk', qb, kw) * scale
            t = jnp.arange(2 * W)
            s_ = jnp.arange(W)[:, None]
            n = jnp.arange(nb)[:, None, None]
            valid = (t <= s_ + W) & (t >= s_ + 1) & (n * W - W + t >= 0)
            scores = jnp.where(valid, scores, NEG)
            attn = jax.nn.softmax(scores, axis=-1)
            out = jnp.einsum('bhnqk,bhnkd->bhnqd', attn, vw)
            out = out.reshape(B, H, S, hd).transpose(0, 2, 1, 3).reshape(B, S, D)
            return out @ Wo.T + bo
        key = jax.random.key(seed)
        ks = jax.random.split(key, 9)
        s = 1.0 / np.sqrt(DIM)
        inp = {'x': jax.random.normal(ks[0], (2, 512, DIM), dtype=jnp.float32)}
        for i, name in enumerate(['q', 'k', 'v', 'o']):
            inp[f'W{name}'] = jax.random.uniform(ks[1 + 2 * i], (DIM, DIM), jnp.float32, -s, s)
            inp[f'b{name}'] = jax.random.uniform(ks[2 + 2 * i], (DIM,), jnp.float32, -s, s)
        return inp
    _L3_attn_in = _L3_attn_setup()

    def _L3_ffn_setup():
        import jax, jax.numpy as jnp
        import numpy as np
        import math
        D_MODEL = 128
        D_FF = 512
        NUM_EXPERTS = 8
        NUM_SHARED = 1
        E_ROUTED = NUM_EXPERTS - NUM_SHARED
        TOP_K = 2
        CAP_FACTOR = 1.25
        B, S = (4, 256)
        T = B * S
        CAPACITY = math.ceil(CAP_FACTOR * T * TOP_K / E_ROUTED)
        SHARED_SCALE = 1.0

        def _layernorm(x, g, b, eps=1e-05):
            mu = jnp.mean(x, axis=-1, keepdims=True)
            var = jnp.mean((x - mu) ** 2, axis=-1, keepdims=True)
            return (x - mu) * jax.lax.rsqrt(var + eps) * g + b
        key = jax.random.key(seed)
        ks = jax.random.split(key, 10)
        s = 0.02
        return {'x': jax.random.normal(ks[0], (B, S, D_MODEL), dtype=jnp.float32), 'ln_g': jnp.ones((D_MODEL,), jnp.float32), 'ln_b': jnp.zeros((D_MODEL,), jnp.float32), 'Wr': jax.random.normal(ks[1], (D_MODEL, E_ROUTED), jnp.float32) * s, 'W1': jax.random.normal(ks[2], (E_ROUTED, D_MODEL, D_FF), jnp.float32) * s, 'W3': jax.random.normal(ks[3], (E_ROUTED, D_MODEL, D_FF), jnp.float32) * s, 'W2': jax.random.normal(ks[4], (E_ROUTED, D_FF, D_MODEL), jnp.float32) * s, 'W1s': jax.random.normal(ks[5], (D_MODEL, D_FF), jnp.float32) * s, 'W3s': jax.random.normal(ks[6], (D_MODEL, D_FF), jnp.float32) * s, 'W2s': jax.random.normal(ks[7], (D_FF, D_MODEL), jnp.float32) * s}
    _L3_ffn_in = _L3_ffn_setup()
    _L3_c = _w((lambda *s: np.random.randn(*s).astype(np.float32) * 0.05)(4, 128))
    _L3_wmod = _w((lambda *s: np.random.randn(*s).astype(np.float32) * 0.05)(128, 6 * 128) * 128 ** (-0.5))
    _d = {'L0_attn_x': _L0_attn_in['x'], 'L0_attn_in_proj_w': _L0_attn_in['in_proj_w'], 'L0_attn_conv_w': _L0_attn_in['conv_w'], 'L0_attn_conv_b': _L0_attn_in['conv_b'], 'L0_attn_x_proj_w': _L0_attn_in['x_proj_w'], 'L0_attn_dt_proj_w': _L0_attn_in['dt_proj_w'], 'L0_attn_dt_proj_b': _L0_attn_in['dt_proj_b'], 'L0_attn_A_log': _L0_attn_in['A_log'], 'L0_attn_D_param': _L0_attn_in['D_param'], 'L0_attn_out_proj_w': _L0_attn_in['out_proj_w'], 'L0_ffn_controller': _L0_ffn_in['controller'], 'L0_ffn_f1': _L0_ffn_in['f1'], 'L0_ffn_f2': _L0_ffn_in['f2'], 'L0_ffn_bias': _L0_ffn_in['bias'], 'L0_c': _L0_c, 'L0_wmod': _L0_wmod, 'L1_attn_Wq': _L1_attn_in['Wq'], 'L1_attn_bq': _L1_attn_in['bq'], 'L1_attn_Wdown': _L1_attn_in['Wdown'], 'L1_attn_bdown': _L1_attn_in['bdown'], 'L1_attn_Wup': _L1_attn_in['Wup'], 'L1_attn_bup': _L1_attn_in['bup'], 'L1_attn_Wout': _L1_attn_in['Wout'], 'L1_attn_bout': _L1_attn_in['bout'], 'L1_ffn_Wg': _L1_ffn_in['Wg'], 'L1_ffn_bg': _L1_ffn_in['bg'], 'L1_ffn_Wgu': _L1_ffn_in['Wgu'], 'L1_ffn_bgu': _L1_ffn_in['bgu'], 'L1_ffn_Wd': _L1_ffn_in['Wd'], 'L1_ffn_bd': _L1_ffn_in['bd'], 'L1_c': _L1_c, 'L1_wmod': _L1_wmod, 'L2_attn_Wq': _L2_attn_in['Wq'], 'L2_attn_bq': _L2_attn_in['bq'], 'L2_attn_Wk': _L2_attn_in['Wk'], 'L2_attn_bk': _L2_attn_in['bk'], 'L2_attn_Wv': _L2_attn_in['Wv'], 'L2_attn_bv': _L2_attn_in['bv'], 'L2_attn_Wu': _L2_attn_in['Wu'], 'L2_attn_bu': _L2_attn_in['bu'], 'L2_attn_Wo': _L2_attn_in['Wo'], 'L2_attn_bo': _L2_attn_in['bo'], 'L2_attn_scale': _L2_attn_in['scale'], 'L2_ffn_gate_w': _L2_ffn_in['gate_w'], 'L2_ffn_w1': _L2_ffn_in['w1'], 'L2_ffn_w2': _L2_ffn_in['w2'], 'L2_c': _L2_c, 'L2_wmod': _L2_wmod, 'L3_attn_Wq': _L3_attn_in['Wq'], 'L3_attn_bq': _L3_attn_in['bq'], 'L3_attn_Wk': _L3_attn_in['Wk'], 'L3_attn_bk': _L3_attn_in['bk'], 'L3_attn_Wv': _L3_attn_in['Wv'], 'L3_attn_bv': _L3_attn_in['bv'], 'L3_attn_Wo': _L3_attn_in['Wo'], 'L3_attn_bo': _L3_attn_in['bo'], 'L3_ffn_ln_g': _L3_ffn_in['ln_g'], 'L3_ffn_ln_b': _L3_ffn_in['ln_b'], 'L3_ffn_Wr': _L3_ffn_in['Wr'], 'L3_ffn_W1': _L3_ffn_in['W1'], 'L3_ffn_W3': _L3_ffn_in['W3'], 'L3_ffn_W2': _L3_ffn_in['W2'], 'L3_ffn_W1s': _L3_ffn_in['W1s'], 'L3_ffn_W3s': _L3_ffn_in['W3s'], 'L3_ffn_W2s': _L3_ffn_in['W2s'], 'L3_c': _L3_c, 'L3_wmod': _L3_wmod}
    _x0 = _d['L0_attn_x']
    _d['L0_attn_x'] = jax.random.normal(jax.random.fold_in(jax.random.key(seed), 1), (4, 1024, 128), dtype=_x0.dtype)
    del _x0
    return _d

def reference(L0_attn_x, L0_attn_in_proj_w, L0_attn_conv_w, L0_attn_conv_b, L0_attn_x_proj_w, L0_attn_dt_proj_w, L0_attn_dt_proj_b, L0_attn_A_log, L0_attn_D_param, L0_attn_out_proj_w, L0_ffn_controller, L0_ffn_f1, L0_ffn_f2, L0_ffn_bias, L0_c, L0_wmod, L1_attn_Wq, L1_attn_bq, L1_attn_Wdown, L1_attn_bdown, L1_attn_Wup, L1_attn_bup, L1_attn_Wout, L1_attn_bout, L1_ffn_Wg, L1_ffn_bg, L1_ffn_Wgu, L1_ffn_bgu, L1_ffn_Wd, L1_ffn_bd, L1_c, L1_wmod, L2_attn_Wq, L2_attn_bq, L2_attn_Wk, L2_attn_bk, L2_attn_Wv, L2_attn_bv, L2_attn_Wu, L2_attn_bu, L2_attn_Wo, L2_attn_bo, L2_attn_scale, L2_ffn_gate_w, L2_ffn_w1, L2_ffn_w2, L2_c, L2_wmod, L3_attn_Wq, L3_attn_bq, L3_attn_Wk, L3_attn_bk, L3_attn_Wv, L3_attn_bv, L3_attn_Wo, L3_attn_bo, L3_ffn_ln_g, L3_ffn_ln_b, L3_ffn_Wr, L3_ffn_W1, L3_ffn_W3, L3_ffn_W2, L3_ffn_W1s, L3_ffn_W3s, L3_ffn_W2s, L3_c, L3_wmod):

    def _L0_attn_ref(x, in_proj_w, conv_w, conv_b, x_proj_w, dt_proj_w, dt_proj_b, A_log, D_param, out_proj_w):
        import jax, jax.numpy as jnp
        import numpy as np
        from jax import lax
        D_MODEL, D_STATE, D_CONV, EXPAND = (128, 16, 4, 2)
        D_INNER = EXPAND * D_MODEL
        DT_RANK = (D_MODEL + 15) // 16
        B, T = (4, 256)

        def _causal_depthwise_conv(xb, conv_w, conv_b):
            inp = xb.transpose(0, 2, 1)
            ker = conv_w[:, None, :]
            dn = lax.conv_dimension_numbers(inp.shape, ker.shape, ('NCH', 'OIH', 'NCH'))
            out = lax.conv_general_dilated(inp, ker, window_strides=(1,), padding=[(D_CONV - 1, 0)], dimension_numbers=dn, feature_group_count=D_INNER)
            return (out + conv_b[None, :, None]).transpose(0, 2, 1)
        xz = x @ in_proj_w
        xb, z = jnp.split(xz, 2, axis=-1)
        xb = jax.nn.silu(_causal_depthwise_conv(xb, conv_w, conv_b))
        proj = xb @ x_proj_w
        dt = jax.nn.softplus(proj[..., :DT_RANK] @ dt_proj_w + dt_proj_b)
        b = proj[..., DT_RANK:DT_RANK + D_STATE]
        c = proj[..., DT_RANK + D_STATE:]
        a = -jnp.exp(A_log)

        def step(state, ts):
            u_t, dt_t, b_t, c_t = ts
            da = jnp.exp(dt_t[:, :, None] * a)
            dbu = dt_t[:, :, None] * b_t[:, None, :] * u_t[:, :, None]
            state = da * state + dbu
            y_t = jnp.einsum('bds,bs->bd', state, c_t)
            return (state, y_t)
        state0 = jnp.zeros((x.shape[0], D_INNER, D_STATE), dtype=x.dtype)
        to_t = lambda v: jnp.swapaxes(v, 0, 1)
        _, ys = lax.scan(step, state0, (to_t(xb), to_t(dt), to_t(b), to_t(c)))
        y = jnp.swapaxes(ys, 0, 1)
        y = (y + D_param * xb) * jax.nn.silu(z)
        return y @ out_proj_w

    def _L0_ffn_ref(x, controller, f1, f2, bias):
        import jax, jax.numpy as jnp
        import numpy as np
        DM, NE, ES, ESZ = (128, 16, 4, 64)
        BATCH, SEQ = (8, 256)
        ne = controller.shape[1]
        d = x.shape[-1]
        grouped = x.reshape(x.shape[:-2] + (-1, ne, d))
        logits = jnp.einsum('...btd,des->...btes', grouped, controller)
        tie = jnp.linspace(0.0, 1e-06, ne, dtype=logits.dtype).reshape(ne, 1, 1)
        logits = logits + tie
        perm = (logits == jnp.max(logits, axis=-3, keepdims=True)).astype(x.dtype)
        sel = jnp.einsum('...btd,...btes->...besd', grouped, perm)
        inner = jax.nn.relu(jnp.einsum('...besd,desf->...besf', sel, f1) + bias)
        inter = jnp.einsum('...besf,esfd->...besd', inner, f2)
        out = jnp.einsum('...besd,...btes->...btd', inter, perm)
        return out.reshape(x.shape)

    def _L1_attn_ref(x, Wq, bq, Wdown, bdown, Wup, bup, Wout, bout):
        import jax, jax.numpy as jnp
        import numpy as np
        D_MODEL = 128
        N_HEADS = 16
        D_LATENT = 32
        HEAD_DIM = D_MODEL // N_HEADS

        def apply_rope(x):
            B, T, H, D = x.shape
            inv_freq = 1.0 / 10000.0 ** (jnp.arange(0, D, 2, dtype=jnp.float32) / D)
            t = jnp.arange(T, dtype=jnp.float32)
            freqs = t[:, None] * inv_freq[None, :]
            sin_f = jnp.sin(freqs)[None, :, None, :]
            cos_f = jnp.cos(freqs)[None, :, None, :]
            x1, x2 = jnp.split(x, 2, axis=-1)
            return jnp.concatenate([x1 * cos_f - x2 * sin_f, x1 * sin_f + x2 * cos_f], axis=-1)
        B, T, D = x.shape
        H, Dh = (N_HEADS, HEAD_DIM)
        q = x @ Wq + bq
        kv_latent = x @ Wdown + bdown
        kv = kv_latent @ Wup + bup
        q = q.reshape(B, T, H, Dh)
        kv = kv.reshape(B, T, H, 2 * Dh)
        k, v = jnp.split(kv, 2, axis=-1)
        q = apply_rope(q)
        k = apply_rope(k)
        att = jnp.einsum('bthd,btgd->bthg', q, k) / jnp.sqrt(jnp.float32(Dh))
        att = jax.nn.softmax(att, axis=-1)
        out = jnp.einsum('bthg,btgd->bthd', att, v)
        out = out.reshape(B, T, D)
        return out @ Wout + bout

    def _L1_ffn_ref(hidden_states, Wg, bg, Wgu, bgu, Wd, bd):
        import jax, jax.numpy as jnp
        import numpy as np
        B, S, H = (1, 128, 128)
        E = 128
        NEXP = 16
        TOPK = 2
        ALPHA = 1.702
        LIMIT = 7.0

        def _moe_forward(x, Wg, bg, Wgu, bgu, Wd, bd):
            b, s, h = x.shape
            xt = x.reshape(-1, h)
            logits = xt @ Wg.T + bg
            top_vals, top_idx = jax.lax.top_k(logits, TOPK)
            rw = jax.nn.softmax(top_vals.astype(jnp.float32), axis=-1).astype(xt.dtype)
            onehot = jax.nn.one_hot(top_idx, NEXP, dtype=xt.dtype)
            cw = jnp.einsum('tk,tke->te', rw, onehot)
            gu = jnp.einsum('th,ehf->tef', xt, Wgu) + bgu[None]
            gate = gu[..., ::2]
            up = gu[..., 1::2]
            gate = jnp.minimum(gate, LIMIT)
            up = jnp.clip(up, -LIMIT, LIMIT)
            glu = gate * jax.nn.sigmoid(gate * ALPHA)
            gated = (up + 1.0) * glu
            out_e = jnp.einsum('tef,efh->teh', gated, Wd) + bd[None]
            out = jnp.einsum('teh,te->th', out_e, cw)
            return out.reshape(b, s, h)
        return _moe_forward(hidden_states, Wg, bg, Wgu, bgu, Wd, bd)

    def _L2_attn_ref(x, Wq, bq, Wk, bk, Wv, bv, Wu, bu, Wo, bo, scale):
        import jax, jax.numpy as jnp
        import numpy as np
        B, N, E, H = (2, 256, 128, 8)
        HID = 128
        D = HID // H
        EPS = 1e-08

        def rms_norm(x, scale):
            rms = jnp.linalg.norm(x, axis=-1, keepdims=True) * x.shape[-1] ** (-0.5)
            return scale * (x / (rms + EPS))
        n = x.shape[-2]
        q = x @ Wq.T + bq
        u = x @ Wu.T + bu
        k = x @ Wk.T + bk
        v = x @ Wv.T + bv
        u = jax.nn.silu(u)
        v = jax.nn.silu(v)
        to_heads = lambda t: t.reshape(*t.shape[:-1], H, D).swapaxes(-3, -2)
        q, k, v = map(to_heads, (q, k, v))
        q = jax.nn.elu(q)
        k = jax.nn.elu(k)
        mask = jnp.tril(jnp.ones((n, n), q.dtype))
        energy = jnp.einsum('bhnd,bhmd->bhnm', q, k) * mask
        out = jnp.einsum('bhnm,bhmd->bhnd', energy, v)
        out = out.swapaxes(-3, -2).reshape(*x.shape[:-1], HID)
        out = rms_norm(out, scale)
        out = u * out
        return out @ Wo.T + bo

    def _L2_ffn_ref(x, gate_w, w1, w2):
        import jax, jax.numpy as jnp
        import numpy as np
        TOP_K = 2
        E = gate_w.shape[-1]
        probs = jax.nn.softmax(x @ gate_w, axis=-1)
        topw, topi = jax.lax.top_k(probs, TOP_K)
        topw = topw / topw.sum(axis=-1, keepdims=True)
        combine = (jax.nn.one_hot(topi, E, dtype=x.dtype) * topw[..., None]).sum(axis=-2)

        def body(acc, params):
            w1_i, w2_i, cw = params
            h = jax.nn.gelu(x @ w1_i, approximate=False)
            return (acc + cw[..., None] * (h @ w2_i), None)
        acc0 = jnp.zeros_like(x)
        out, _ = jax.lax.scan(body, acc0, (w1, w2, jnp.moveaxis(combine, -1, 0)))
        return out

    def _L3_attn_ref(x, Wq, bq, Wk, bk, Wv, bv, Wo, bo):
        import jax, jax.numpy as jnp
        import numpy as np
        DIM = 128
        HEADS = 16
        HEAD_DIM = DIM // HEADS
        WINDOW = 64
        NEG = -1000000000.0

        def _sliding_window_attn(x, Wq, bq, Wk, bk, Wv, bv, Wo, bo):
            B, S, D = x.shape
            H, hd, W = (HEADS, HEAD_DIM, WINDOW)
            nb = S // W

            def proj(Wp, bp):
                y = x @ Wp.T + bp
                return y.reshape(B, S, H, hd).transpose(0, 2, 1, 3)
            q = proj(Wq, bq)
            k = proj(Wk, bk)
            v = proj(Wv, bv)
            scale = hd ** (-0.5)
            qb = q.reshape(B, H, nb, W, hd)

            def window_kv(t):
                pad = jnp.concatenate([jnp.zeros((B, H, W, hd), t.dtype), t], axis=2)
                prev = pad[:, :, :S].reshape(B, H, nb, W, hd)
                cur = t.reshape(B, H, nb, W, hd)
                return jnp.concatenate([prev, cur], axis=3)
            kw = window_kv(k)
            vw = window_kv(v)
            scores = jnp.einsum('bhnqd,bhnkd->bhnqk', qb, kw) * scale
            t = jnp.arange(2 * W)
            s_ = jnp.arange(W)[:, None]
            n = jnp.arange(nb)[:, None, None]
            valid = (t <= s_ + W) & (t >= s_ + 1) & (n * W - W + t >= 0)
            scores = jnp.where(valid, scores, NEG)
            attn = jax.nn.softmax(scores, axis=-1)
            out = jnp.einsum('bhnqk,bhnkd->bhnqd', attn, vw)
            out = out.reshape(B, H, S, hd).transpose(0, 2, 1, 3).reshape(B, S, D)
            return out @ Wo.T + bo
        return _sliding_window_attn(x, Wq, bq, Wk, bk, Wv, bv, Wo, bo)

    def _L3_ffn_ref(x, ln_g, ln_b, Wr, W1, W3, W2, W1s, W3s, W2s):
        import jax, jax.numpy as jnp
        import numpy as np
        import math
        D_MODEL = 128
        D_FF = 512
        NUM_EXPERTS = 8
        NUM_SHARED = 1
        E_ROUTED = NUM_EXPERTS - NUM_SHARED
        TOP_K = 2
        CAP_FACTOR = 1.25
        B, S = (4, 256)
        T = B * S
        CAPACITY = math.ceil(CAP_FACTOR * T * TOP_K / E_ROUTED)
        SHARED_SCALE = 1.0

        def _layernorm(x, g, b, eps=1e-05):
            mu = jnp.mean(x, axis=-1, keepdims=True)
            var = jnp.mean((x - mu) ** 2, axis=-1, keepdims=True)
            return (x - mu) * jax.lax.rsqrt(var + eps) * g + b
        Bx, Sx, D = x.shape
        Tn = Bx * Sx
        h = _layernorm(x, ln_g, ln_b).reshape(Tn, D)
        logits = h @ Wr
        top_vals, top_idx = jax.lax.top_k(logits, TOP_K)
        gates = jax.nn.softmax(top_vals, axis=-1)
        idx = top_idx.T.reshape(-1)
        gat = gates.T.reshape(-1)
        tok = jnp.tile(jnp.arange(Tn), TOP_K)
        onehot = jax.nn.one_hot(idx, E_ROUTED, dtype=jnp.int32)
        pos = jnp.sum(jnp.cumsum(onehot, axis=0) * onehot, axis=-1) - 1
        keep = pos < CAPACITY
        pos_c = jnp.where(keep, pos, CAPACITY)
        xe = jnp.zeros((E_ROUTED, CAPACITY, D), h.dtype).at[idx, pos_c].set(h[tok], mode='drop')
        a = jnp.einsum('ecd,edf->ecf', xe, W1)
        b = jnp.einsum('ecd,edf->ecf', xe, W3)
        ye = jnp.einsum('ecf,efd->ecd', jax.nn.silu(a) * b, W2)
        out_slots = ye[jnp.clip(idx, 0, E_ROUTED - 1), jnp.clip(pos_c, 0, CAPACITY - 1)]
        out_slots = out_slots * (gat * keep.astype(gat.dtype))[:, None]
        routed = jnp.zeros((Tn, D), h.dtype).at[tok].add(out_slots)
        shared = jax.nn.silu(h @ W1s) * (h @ W3s) @ W2s
        out = routed + SHARED_SCALE * shared
        return out.reshape(Bx, Sx, D)
    x = L0_attn_x
    mod = (_silu(L0_c) @ L0_wmod).reshape(L0_c.shape[0], 6, 1, -1)
    sa, ca, ga, sb, cb, gb = (mod[:, 0], mod[:, 1], mod[:, 2], mod[:, 3], mod[:, 4], mod[:, 5])
    ga = (2 * (ga >= 0) - 1) * jnp.maximum(jnp.abs(ga), 0.25)
    gb = (2 * (gb >= 0) - 1) * jnp.maximum(jnp.abs(gb), 0.25)
    h = _layernorm(x, axis=-1) * (1 + ca) + sa
    x = x + ga * _L0_attn_ref(h, L0_attn_in_proj_w, L0_attn_conv_w, L0_attn_conv_b, L0_attn_x_proj_w, L0_attn_dt_proj_w, L0_attn_dt_proj_b, L0_attn_A_log, L0_attn_D_param, L0_attn_out_proj_w)
    h = _layernorm(x, axis=-1) * (1 + cb) + sb
    x = x + gb * _L0_ffn_ref(h, L0_ffn_controller, L0_ffn_f1, L0_ffn_f2, L0_ffn_bias)
    mod = (_silu(L1_c) @ L1_wmod).reshape(L1_c.shape[0], 6, 1, -1)
    sa, ca, ga, sb, cb, gb = (mod[:, 0], mod[:, 1], mod[:, 2], mod[:, 3], mod[:, 4], mod[:, 5])
    ga = (2 * (ga >= 0) - 1) * jnp.maximum(jnp.abs(ga), 0.25)
    gb = (2 * (gb >= 0) - 1) * jnp.maximum(jnp.abs(gb), 0.25)
    h = _layernorm(x, axis=-1) * (1 + ca) + sa
    x = x + ga * _L1_attn_ref(h, L1_attn_Wq, L1_attn_bq, L1_attn_Wdown, L1_attn_bdown, L1_attn_Wup, L1_attn_bup, L1_attn_Wout, L1_attn_bout)
    h = _layernorm(x, axis=-1) * (1 + cb) + sb
    x = x + gb * _L1_ffn_ref(h, L1_ffn_Wg, L1_ffn_bg, L1_ffn_Wgu, L1_ffn_bgu, L1_ffn_Wd, L1_ffn_bd)
    mod = (_silu(L2_c) @ L2_wmod).reshape(L2_c.shape[0], 6, 1, -1)
    sa, ca, ga, sb, cb, gb = (mod[:, 0], mod[:, 1], mod[:, 2], mod[:, 3], mod[:, 4], mod[:, 5])
    ga = (2 * (ga >= 0) - 1) * jnp.maximum(jnp.abs(ga), 0.25)
    gb = (2 * (gb >= 0) - 1) * jnp.maximum(jnp.abs(gb), 0.25)
    h = _layernorm(x, axis=-1) * (1 + ca) + sa
    x = x + ga * _L2_attn_ref(h, L2_attn_Wq, L2_attn_bq, L2_attn_Wk, L2_attn_bk, L2_attn_Wv, L2_attn_bv, L2_attn_Wu, L2_attn_bu, L2_attn_Wo, L2_attn_bo, L2_attn_scale)
    h = _layernorm(x, axis=-1) * (1 + cb) + sb
    x = x + gb * _L2_ffn_ref(h, L2_ffn_gate_w, L2_ffn_w1, L2_ffn_w2)
    mod = (_silu(L3_c) @ L3_wmod).reshape(L3_c.shape[0], 6, 1, -1)
    sa, ca, ga, sb, cb, gb = (mod[:, 0], mod[:, 1], mod[:, 2], mod[:, 3], mod[:, 4], mod[:, 5])
    ga = (2 * (ga >= 0) - 1) * jnp.maximum(jnp.abs(ga), 0.25)
    gb = (2 * (gb >= 0) - 1) * jnp.maximum(jnp.abs(gb), 0.25)
    h = _layernorm(x, axis=-1) * (1 + ca) + sa
    x = x + ga * _L3_attn_ref(h, L3_attn_Wq, L3_attn_bq, L3_attn_Wk, L3_attn_bk, L3_attn_Wv, L3_attn_bv, L3_attn_Wo, L3_attn_bo)
    h = _layernorm(x, axis=-1) * (1 + cb) + sb
    x = x + gb * _L3_ffn_ref(h, L3_ffn_ln_g, L3_ffn_ln_b, L3_ffn_Wr, L3_ffn_W1, L3_ffn_W3, L3_ffn_W2, L3_ffn_W1s, L3_ffn_W3s, L3_ffn_W2s)
    return x

_drawn_inputs = setup_inputs


def setup_inputs(seed=0):
    import zlib

    import numpy as np

    out = dict(_drawn_inputs(seed))
    spreads = {'L0_attn_D_param': (1.0, 0.2),
     'L1_attn_bq': (0.0, 0.497),
     'L1_attn_bdown': (0.0, 0.42),
     'L1_attn_bup': (0.0, 0.385),
     'L1_attn_bout': (0.0, 0.1),
     'L2_attn_bq': (0.0, 0.8),
     'L2_attn_bk': (0.0, 0.8),
     'L2_attn_bv': (0.0, 0.8),
     'L2_attn_bu': (0.0, 0.8),
     'L2_attn_bo': (0.0, 0.322),
     'L2_attn_scale': (1.0, 0.6),
     'L3_ffn_ln_g': (1.0, 0.6),
     'L3_ffn_ln_b': (0.0, 0.8)}
    factors = {'L0_attn_dt_proj_b': 3.597,
     'L0_ffn_controller': 3.12,
     'L0_ffn_f1': 3.274,
     'L0_ffn_f2': 2.876,
     'L0_ffn_bias': 8.0,
     'L1_ffn_bg': 4.671,
     'L1_ffn_bgu': 8.0,
     'L1_ffn_bd': 8.0,
     'L2_attn_Wq': 7.964,
     'L2_attn_Wk': 8.0,
     'L2_attn_Wv': 8.0,
     'L2_attn_Wu': 8.0,
     'L2_attn_Wo': 7.458,
     'L2_ffn_gate_w': 7.058,
     'L2_ffn_w1': 6.288,
     'L2_ffn_w2': 6.182,
     'L3_attn_Wq': 8.0,
     'L3_attn_bq': 8.0,
     'L3_attn_Wk': 8.0,
     'L3_attn_bk': 8.0,
     'L3_attn_Wv': 4.658,
     'L3_attn_bv': 7.629,
     'L3_attn_Wo': 3.911,
     'L3_attn_bo': 4.385,
     'L3_ffn_Wr': 8.0,
     'L3_ffn_W1': 8.0,
     'L3_ffn_W3': 8.0,
     'L3_ffn_W2': 8.0,
     'L3_ffn_W1s': 8.0,
     'L3_ffn_W3s': 8.0,
     'L3_ffn_W2s': 8.0,
     'L3_c': 3.035,
     'L3_wmod': 3.059}
    for name, (base, spread) in spreads.items():
        noise = np.random.default_rng([zlib.crc32(name.encode()), seed]).standard_normal(out[name].shape)
        drawn = base * np.exp(spread * noise) if base else spread * noise
        out[name] = jnp.asarray(drawn.astype(out[name].dtype))
    for name, factor in factors.items():
        out[name] = (out[name] * factor).astype(out[name].dtype)
    return out
```

```python
from contextlib import ExitStack

import concourse.bass as bass
from concourse import mybir
from concourse.alu_op_type import AluOpType as ALU
import numpy as np

F32 = mybir.dt.float32
BF16 = mybir.dt.bfloat16
U32 = mybir.dt.uint32
I32 = mybir.dt.int32
ACT = mybir.ActivationFunctionType
AX = mybir.AxisListType

P = 128
BATCH = 4
SEQ = 1024
TOK = BATCH * SEQ
TILE = 512
NT = TOK // TILE
TPB = SEQ // TILE
KT = TOK // P
LAYERS = 4
LN_EPS = 1e-5
LN_EXP_SET = "natural_log_exp_and_others"
SA, CA, GA, SB, CB, GB = range(6)


VECS = ([f"bg{e}" for e in range(16)] + [f"bu{e}" for e in range(16)]
        + [f"conv_w{k}{h}" for k in range(4) for h in range(2)]
        + [f"{n}{h}" for n in ("conv_b", "dt_b", "D") for h in range(2)]
        + [f"A_log{s}{h}" for s in range(16) for h in range(2)]
        + ["L1_bq", "L1_bq_rot", "L1_bk", "L1_bk_rot", "L1_bv", "L1_bout", "L1_bdown"]
        + ["L2_bq", "L2_bk", "L2_bv", "L2_bu", "L2_bo", "L2_scale"]
        + ["L3_bq", "L3_bk", "L3_bv", "L3_bo", "ln_g", "ln_b"])


class Core:

    def __init__(self, nc, ctx, ins):
        self.nc, self.ins = nc, ins
        self.ctx = ctx
        self.ln_calls = 0

        def sb(name, shape, dt=F32):
            return ctx.enter_context(nc.sbuf_tensor(name, shape, dt))

        self.x_t = sb("x_t", [P, TOK])
        self.h_t = sb("h_t", [P, TOK])
        self.mod = sb("mod", [P, LAYERS, 6, NT])
        self.mean_w = sb("mean_w", [P, P])
        self.ident = sb("ident", [P, P])
        self.ident_bf = sb("ident_bf", [P, P], BF16)
        self.vecs = sb("vecs", [P, len(VECS)])
        self.ln = {n: ctx.enter_context(nc.semaphore("ln_" + n))
                   for n in ("mean", "cent", "sq", "var", "logv", "rstd", "xn", "h")}


def vec(c, name):
    k = VECS.index(name)
    return c.vecs[:, k:k + 1]


def stage_setup(c):
    nc, ins = c.nc, c.ins
    with ExitStack() as s:
        wmod = s.enter_context(nc.sbuf_tensor("wmod", [P, LAYERS, 6 * P], F32))
        cond = s.enter_context(nc.sbuf_tensor("cond", [P, LAYERS, BATCH], F32))
        cond_silu = s.enter_context(nc.sbuf_tensor("cond_silu", [P, LAYERS, BATCH], F32))
        raw = s.enter_context(nc.sbuf_tensor("mod_raw", [P, LAYERS, 6, BATCH], F32))
        sign = s.enter_context(nc.sbuf_tensor("gate_sign", [P, LAYERS, 2, BATCH], F32))
        size = s.enter_context(nc.sbuf_tensor("gate_size", [P, LAYERS, 2, BATCH], F32))
        ps = s.enter_context(nc.psum_tensor("mod_ps", [P, LAYERS, 6, BATCH], F32))
        loaded = s.enter_context(nc.semaphore("setup_loaded"))
        silu_done = s.enter_context(nc.semaphore("setup_silu"))
        mod_done = s.enter_context(nc.semaphore("setup_mod"))
        step = s.enter_context(nc.semaphore("setup_step"))
        with nc.Block() as block:
            @block.sync
            def _(sp):
                sp.dma_start(c.x_t[:, :], ins["x_t"]).then_inc(loaded, 16)
                sp.dma_start(c.mean_w[:, :], ins["mean_w"]).then_inc(loaded, 16)
                sp.dma_start(c.ident[:, :], ins["ident"]).then_inc(loaded, 16)
                sp.dma_start(c.ident_bf[:, :], ins["ident_bf"]).then_inc(loaded, 16)
                sp.dma_start(c.vecs[:, :], ins["vecs"]).then_inc(loaded, 16)
                for l in range(LAYERS):
                    sp.dma_start(cond[:, l, :], ins[f"L{l}_c_t"]).then_inc(loaded, 16)
                    sp.dma_start(wmod[:, l, :], ins[f"L{l}_wmod"]).then_inc(loaded, 16)

            @block.scalar
            def _(act):
                act.wait_ge(loaded, 16 * (5 + 2 * LAYERS))
                nc.scalar.activation(cond_silu[:, :, :], cond[:, :, :], ACT.Silu).then_inc(silu_done, 1)

            @block.tensor
            def _(pe):
                pe.wait_ge(loaded, 16 * (5 + 2 * LAYERS))
                pe.wait_ge(silu_done, 1)
                for l in range(LAYERS):
                    for k in range(6):
                        mm = nc.tensor.matmul(ps[:, l, k, :], wmod[:, l, k * P:(k + 1) * P], cond_silu[:, l, :],
                                              start=True, stop=True)
                mm.then_inc(mod_done, 1)

            @block.vector
            def _(dve):
                dve.wait_ge(mod_done, 1)
                nc.vector.tensor_copy(raw[:, :, :, :], ps[:, :, :, :]).then_inc(step, 1)
                dve.wait_ge(step, 1)
                for n, k in enumerate((CA, CB)):
                    nc.vector.tensor_scalar(raw[:, :, k, :], raw[:, :, k, :], 1.0, None, ALU.add).then_inc(step, 1)
                for n, k in enumerate((GA, GB)):
                    nc.vector.tensor_scalar(sign[:, :, n, :], raw[:, :, k, :], 0.0, 2.0, ALU.is_ge,
                                            ALU.mult).then_inc(step, 1)
                dve.wait_ge(step, 5)
                for n, k in enumerate((GA, GB)):
                    nc.vector.scalar_tensor_tensor(size[:, :, n, :], sign[:, :, n, :], -1.0, raw[:, :, k, :],
                                                   ALU.add, ALU.mult).then_inc(step, 1)
                dve.wait_ge(step, 7)
                for n in range(2):
                    nc.vector.tensor_scalar(size[:, :, n, :], size[:, :, n, :], 0.25, None,
                                            ALU.max).then_inc(step, 1)
                dve.wait_ge(step, 9)
                for n, k in enumerate((GA, GB)):
                    nc.vector.scalar_tensor_tensor(raw[:, :, k, :], sign[:, :, n, :], -1.0, size[:, :, n, :],
                                                   ALU.add, ALU.mult).then_inc(step, 1)
                dve.wait_ge(step, 11)
                for l in range(LAYERS):
                    nc.vector.tensor_copy(
                        c.mod[:, l, :, :].rearrange("p k (b u) -> p k b u", u=TPB),
                        raw[:, l, :, :].unsqueeze(3).to_broadcast([P, 6, BATCH, TPB])).then_inc(step, 1)
                dve.wait_ge(step, 11 + LAYERS)


def stage_norm(c, src, dst, scale, shift):
    nc, base, call = c.nc, c.ln_calls * NT, c.ln_calls
    c.ln_calls += 1
    ln = c.ln
    with ExitStack() as s:
        xc = s.enter_context(nc.sbuf_tensor(f"ln_xc{call}", [P, 2, TILE], F32))
        sq = s.enter_context(nc.sbuf_tensor(f"ln_sq{call}", [P, 2, TILE], F32))
        lv = s.enter_context(nc.sbuf_tensor(f"ln_lv{call}", [P, 2, TILE], F32))
        eps = s.enter_context(nc.sbuf_tensor(f"ln_eps{call}", [P, 1], F32))
        mean_ps = s.enter_context(nc.psum_tensor(f"ln_mean_ps{call}", [P, 2, TILE], F32))
        var_ps = s.enter_context(nc.psum_tensor(f"ln_var_ps{call}", [P, 2, TILE], F32))
        eps_set = s.enter_context(nc.semaphore(f"ln_eps_set{call}"))
        with nc.Block() as block:
            @block.tensor
            def _(pe):
                with pe.Fori(0, NT // 2) as i:
                    for u in range(2):
                        nc.tensor.matmul(mean_ps[:, u, :], c.mean_w[:, :], src[:, bass.ts(i * 2 + u, TILE)],
                                         start=True, stop=True).then_inc(ln["mean"], 1)
                    for u in range(2):
                        pe.wait_ge(ln["sq"], i * 2 + (base + u + 1))
                        nc.tensor.matmul(var_ps[:, u, :], c.mean_w[:, :], sq[:, u, :],
                                         start=True, stop=True).then_inc(ln["var"], 1)

            @block.scalar
            def _(act):
                nc.scalar.preload_act_table_set(LN_EXP_SET)
                act.wait_ge(eps_set, 1)
                with act.Fori(0, NT // 2) as i:
                    for u in range(2):
                        act.wait_ge(ln["cent"], i * 2 + (base + u + 1))
                        nc.scalar.activation(sq[:, u, :], xc[:, u, :], ACT.Square).then_inc(ln["sq"], 1)
                    for u in range(2):
                        act.wait_ge(ln["var"], i * 2 + (base + u + 1))
                        nc.scalar.activation(lv[:, u, :], var_ps[:, u, :], ACT.Ln,
                                             bias=eps[:, 0:1]).then_inc(ln["logv"], 1)
                        act.wait_ge(ln["logv"], i * 2 + (base + u + 1))
                        nc.scalar.activation(lv[:, u, :], lv[:, u, :], ACT.Exp, scale=-0.5).then_inc(ln["rstd"], 1)

            @block.vector
            def _(dve):
                nc.vector.memset(eps[:, :], LN_EPS).then_inc(eps_set, 1)
                with dve.Fori(0, NT // 2) as i:
                    for u in range(2):
                        dve.wait_ge(ln["mean"], i * 2 + (base + u + 1))
                        nc.vector.tensor_tensor(xc[:, u, :], src[:, bass.ts(i * 2 + u, TILE)], mean_ps[:, u, :],
                                                ALU.subtract).then_inc(ln["cent"], 1)
                    for u in range(2):
                        dve.wait_ge(ln["rstd"], i * 2 + (base + u + 1))
                        nc.vector.tensor_tensor(xc[:, u, :], xc[:, u, :], lv[:, u, :],
                                                ALU.mult).then_inc(ln["xn"], 1)
                        dve.wait_ge(ln["xn"], i * 2 + (base + u + 1))
                        nc.vector.tensor_scalar(dst[:, bass.ts(i * 2 + u, TILE)], xc[:, u, :],
                                                scale(i * 2 + u), shift(i * 2 + u), ALU.mult,
                                                ALU.add).then_inc(ln["h"], 1)
                    dve.wait_ge(ln["h"], i * 2 + (base + 2))


def adaln(c, layer, k_shift, k_scale):
    stage_norm(c, c.x_t, c.h_t,
               lambda t: c.mod[:, layer, k_scale, bass.ds(t, 1)],
               lambda t: c.mod[:, layer, k_shift, bass.ds(t, 1)])


def recycle_semaphores(c):
    nc = c.nc
    given_back = sorted(nc.released_uncleared_semaphores)
    with nc.Block() as block:
        @block.gpsimd
        def _(pool):
            first = 0
            for k in range(1, len(given_back) + 1):
                if k == len(given_back) or given_back[k] != given_back[k - 1] + 1:
                    pool.sem_clear(range(given_back[first], given_back[k - 1] + 1))
                    first = k


def stage_store(c, out):
    nc = c.nc
    with ExitStack() as s:
        stored = s.enter_context(nc.semaphore("stored"))
        with nc.Block() as block:
            @block.sync
            def _(sp):
                sp.dma_start(out, c.x_t[:, :]).then_inc(stored, 16)
                sp.wait_ge(stored, 16)


LAG = 2
BUFS = LAG + 1


def stage_router(c, tag, experts, cw3, logits_bias=False, capacity=None):
    nc, ins = c.nc, c.ins
    E = experts
    small = [P, KT]
    full = [P, KT, E]
    with ExitStack() as s:
        def sb(name, shape, dt=F32):
            return s.enter_context(nc.sbuf_tensor(f"{tag}_{name}", shape, dt))

        def sem(name):
            return s.enter_context(nc.semaphore(f"{tag}_{name}"))

        wr = sb("wr", [P, E])
        rank = sb("rank", full)
        lb = sb("lb", full)
        lg = sb("lg", full)
        eq = sb("eq", full)
        hot = [sb("hot0", full), sb("hot1", full)]
        tmp = sb("tmp", full)
        tmp2 = sb("tmp2", full)
        mx = [sb("mx0", small), sb("mx1", small)]
        mr = sb("mr", small)
        gate = [sb("gate0", small), sb("gate1", small)]
        ex = sb("ex", small)
        cw = sb("cw", full)
        parts = sb("parts", [P, KT, 3, E], BF16)
        lg_ps = s.enter_context(nc.psum_tensor(f"{tag}_lg_ps", full, F32))
        tr_ps = s.enter_context(nc.psum_tensor(f"{tag}_tr_ps", [3 * E, KT, P], BF16))
        loaded, logits, step, ex_ready, ex_done, parts_done, turned = (
            sem(n) for n in ("loaded", "logits", "step", "ex_ready", "ex_done", "parts_done", "turned"))
        if capacity:
            hots = sb("hots", [P, 2, KT, E], BF16)
            upper = sb("upper", [P, P], BF16)
            ones = sb("ones", [P, P], BF16)
            tot = sb("tot", [P, 2 * KT, E])
            cum = sb("cum", [P, E, 2 * KT])
            pos = sb("pos", [P, 2, KT, E])
            zero = sb("zero", [P, 2 * KT])
            pre_ps = s.enter_context(nc.psum_tensor(f"{tag}_pre_ps", [P, 2, KT, E], F32))
            tot_ps = s.enter_context(nc.psum_tensor(f"{tag}_tot_ps", [P, 2 * KT, E], F32))
            hots_done, counted = sem("hots_done"), sem("counted")
        loads = 2 + bool(logits_bias) + 2 * bool(capacity)
        with nc.Block() as block:
            @block.sync
            def _(sp):
                sp.dma_start(wr[:, :], ins[f"{tag}_wr"]).then_inc(loaded, 16)
                sp.dma_start(rank[:, :, :].rearrange("p k e -> p (k e)"), ins[f"{tag}_rank"]).then_inc(loaded, 16)
                if logits_bias:
                    sp.dma_start(lb[:, :, :].rearrange("p k e -> p (k e)"), ins[f"{tag}_lb"]).then_inc(loaded, 16)
                if capacity:
                    sp.dma_start(upper[:, :], ins["upper_bf"]).then_inc(loaded, 16)
                    sp.dma_start(ones[:, :], ins["ones_bf"]).then_inc(loaded, 16)

            @block.tensor
            def _(pe):
                pe.wait_ge(loaded, 16 * loads)
                for k in range(KT):
                    mm = nc.tensor.matmul(lg_ps[:, k, :], c.h_t[:, k * P:(k + 1) * P], wr[:, :],
                                          start=True, stop=True)
                mm.then_inc(logits, 1)
                if capacity:
                    pe.wait_ge(hots_done, 2)
                    flat = hots[:, :, :, :].rearrange("p s k e -> p (s k e)")
                    nc.tensor.matmul(pre_ps[:, :, :, :].rearrange("p s k e -> p (s k e)"), upper[:, :], flat,
                                     start=True, stop=True).then_inc(counted, 1)
                    nc.tensor.matmul(tot_ps[:, :, :].rearrange("p k e -> p (k e)"), ones[:, :], flat,
                                     start=True, stop=True).then_inc(counted, 1)
                pe.wait_ge(parts_done, 3)
                for k in range(KT):
                    mm = nc.tensor.transpose(tr_ps[:, k, :], parts[:, k, :, :].rearrange("p a e -> p (a e)"),
                                             c.ident_bf[:, :])
                mm.then_inc(turned, 1)

            @block.scalar
            def _(act):
                act.wait_ge(ex_ready, 1)
                nc.scalar.activation(ex[:, :], ex[:, :], ACT.Exp).then_inc(ex_done, 1)
                act.wait_ge(turned, 1)
                half = KT // 2
                nc.scalar.copy(cw3[:, 0:half * P], tr_ps[:, 0:half, :].rearrange("p k t -> p (k t)"))

            @block.vector
            def _(dve):
                n = [0]

                def done(ins_):
                    n[0] += 1
                    ins_.then_inc(step, 1)
                    dve.wait_ge(step, n[0])

                def wide(a):
                    return a[:, :].unsqueeze(2).to_broadcast(full)

                tt, ts = nc.vector.tensor_tensor, nc.vector.tensor_scalar
                dve.wait_ge(loaded, 16 * loads)
                dve.wait_ge(logits, 1)
                if logits_bias:
                    done(tt(lg[:, :, :], lg_ps[:, :, :], lb[:, :, :], ALU.add))
                else:
                    done(nc.vector.tensor_copy(lg[:, :, :], lg_ps[:, :, :]))
                for k in range(2):
                    done(nc.vector.reduce_max(mx[k][:, :], lg[:, :, :], AX.X))
                    done(tt(eq[:, :, :], lg[:, :, :], wide(mx[k]), ALU.is_ge))
                    done(tt(eq[:, :, :], eq[:, :, :], rank[:, :, :], ALU.mult))
                    done(nc.vector.reduce_max(mr[:, :], eq[:, :, :], AX.X))
                    done(tt(hot[k][:, :, :], eq[:, :, :], wide(mr), ALU.is_equal))
                    if k == 0:
                        done(nc.vector.scalar_tensor_tensor(lg[:, :, :], hot[0][:, :, :], -3e38, lg[:, :, :],
                                                            ALU.mult, ALU.add))
                tt(ex[:, :], mx[1][:, :], mx[0][:, :], ALU.subtract).then_inc(ex_ready, 1)
                dve.wait_ge(ex_done, 1)
                done(ts(gate[1][:, :], ex[:, :], 1.0, None, ALU.add))
                done(nc.vector.reciprocal(gate[0][:, :], gate[1][:, :]))
                done(tt(gate[1][:, :], gate[0][:, :], ex[:, :], ALU.mult))
                if capacity:
                    for k in range(2):
                        nc.vector.tensor_copy(hots[:, k, :, :], hot[k][:, :, :]).then_inc(hots_done, 1)
                    done(nc.vector.memset(zero[:, :], 0.0))
                    dve.wait_ge(counted, 2)
                    done(nc.vector.tensor_copy(tot[:, :, :], tot_ps[:, :, :]))
                    for e in range(E):
                        done(nc.vector.tensor_tensor_scan(cum[:, e, :], tot[:, :, e], zero[:, :], 0.0,
                                                          ALU.add, ALU.add))
                    done(tt(tot[:, :, :], cum[:, :, :].rearrange("p e k -> p k e"), tot[:, :, :], ALU.subtract))
                    flat = pos[:, :, :, :].rearrange("p s k e -> p (s k) e")
                    done(tt(flat, pre_ps[:, :, :, :].rearrange("p s k e -> p (s k) e"), tot[:, :, :], ALU.add))
                    for k in range(2):
                        done(ts(tmp[:, :, :], pos[:, k, :, :], float(capacity), None, ALU.is_le))
                        done(tt(hot[k][:, :, :], hot[k][:, :, :], tmp[:, :, :], ALU.mult))
                done(tt(tmp[:, :, :], hot[0][:, :, :], wide(gate[0]), ALU.mult))
                done(tt(tmp2[:, :, :], hot[1][:, :, :], wide(gate[1]), ALU.mult))
                done(tt(cw[:, :, :], tmp[:, :, :], tmp2[:, :, :], ALU.add))
                rest = [cw, tmp, tmp2]
                for k in range(3):
                    nc.vector.tensor_copy(parts[:, :, k, :], rest[k][:, :, :]).then_inc(parts_done, 1)
                    if k < 2:
                        dve.wait_ge(parts_done, k + 1)
                        done(tt(rest[k + 1][:, :, :], rest[k][:, :, :], parts[:, :, k, :], ALU.subtract))
                dve.wait_ge(turned, 1)
                half = KT // 2
                nc.vector.tensor_copy(cw3[:, half * P:], tr_ps[:, half:, :].rearrange("p k t -> p (k t)"))


def stage_moe2(c):
    nc, ins, E, F = c.nc, c.ins, 8, 4
    S = E * F
    with ExitStack() as s:
        def sb(name, shape, dt=F32):
            return s.enter_context(nc.sbuf_tensor(f"m2_{name}", shape, dt))

        def sem(name):
            return s.enter_context(nc.semaphore(f"m2_{name}"))

        cw3 = sb("cw3", [3 * E, TOK], BF16)
        stage_router(c, "r2", E, cw3)
        w1 = sb("w1", [P, E, F, P])
        w2 = sb("w2", [P, E, F, P])
        pick = sb("pick", [3 * E, E, P], BF16)
        g = sb("g", [P, BUFS, TILE])
        gc = sb("gc", [P, BUFS, TILE])
        h_ps = s.enter_context(nc.psum_tensor("m2_h_ps", [P, BUFS, TILE], F32))
        cw_ps = s.enter_context(nc.psum_tensor("m2_cw_ps", [P, 2, TILE], F32))
        o_ps = s.enter_context(nc.psum_tensor("m2_o_ps", [P, 2, TILE], F32))
        loaded, h_ready, g_ready, gc_ready, cw_ready, o_ready, o_free = (
            sem(n) for n in ("loaded", "h_ready", "g_ready", "gc_ready", "cw_ready", "o_ready", "o_free"))
        with nc.Block() as block:
            @block.sync
            def _(sp):
                sp.dma_start(pick[:, :, :], ins["m2_pick"]).then_inc(loaded, 16)
                sp.dma_start(w1[:, :, :, :], ins["m2_w1"]).then_inc(loaded, 16)
                sp.dma_start(w2[:, :, :, :], ins["m2_w2"]).then_inc(loaded, 16)

            @block.tensor
            def _(pe):
                pe.wait_ge(loaded, 48)
                pe.sem_inc(o_free, 1)
                with pe.Fori(0, NT) as t:
                    tile = bass.ts(t, TILE)

                    def down(k):
                        pe.wait_ge(gc_ready, t * S + (k + 1))
                        return nc.tensor.matmul(o_ps[:, 0, :], w2[:, k // F, k % F, :], gc[:, k % BUFS, :],
                                                start=(k == 0), stop=(k == S - 1))
                    for k in range(S):
                        e, f = divmod(k, F)
                        if f == 0:
                            nc.tensor.matmul(cw_ps[:, e % 2, :], pick[:, e, :], cw3[:, tile], start=True,
                                             stop=True).then_inc(cw_ready, 1)
                        nc.tensor.matmul(h_ps[:, k % BUFS, :], w1[:, e, f, :], c.h_t[:, tile], start=True,
                                         stop=True).then_inc(h_ready, 1)
                        if k == LAG:
                            pe.wait_ge(o_free, t + 1)
                        if k >= LAG:
                            down(k - LAG)
                    for k in range(S - LAG, S):
                        mm = down(k)
                    mm.then_inc(o_ready, 1)

            @block.scalar
            def _(act):
                nc.scalar.preload_act_table(ACT.Gelu)
                with act.Fori(0, NT) as t:
                    for k in range(S):
                        act.wait_ge(h_ready, t * S + (k + 1))
                        nc.scalar.activation(g[:, k % BUFS, :], h_ps[:, k % BUFS, :], ACT.Gelu).then_inc(g_ready, 1)

            @block.vector
            def _(dve):
                with dve.Fori(0, NT) as t:
                    for k in range(S):
                        e, f = divmod(k, F)
                        if f == 0:
                            dve.wait_ge(cw_ready, t * E + (e + 1))
                        dve.wait_ge(g_ready, t * S + (k + 1))
                        m = nc.vector.tensor_tensor(gc[:, k % BUFS, :], g[:, k % BUFS, :], cw_ps[:, e % 2, :], ALU.mult)
                        m.then_inc(gc_ready, 1)
                    dve.wait_ge(o_ready, t + 1)
                    tile = bass.ts(t, TILE)
                    nc.vector.scalar_tensor_tensor(c.x_t[:, tile], o_ps[:, 0, :], c.mod[:, 2, GB, bass.ds(t, 1)],
                                                   c.x_t[:, tile], ALU.mult, ALU.add).then_inc(o_free, 1)


def layout_moe2(a, d, bf):
    d["r2_wr"] = a["L2_ffn_gate_w"]
    d["r2_rank"] = rank_const(8)
    d["m2_w1"] = a["L2_ffn_w1"].reshape(8, P, 4, P).transpose(1, 0, 2, 3)
    d["m2_w2"] = a["L2_ffn_w2"].reshape(8, 4, P, P).transpose(2, 0, 1, 3)
    d["m2_pick"] = pick_const(8, bf)


def rank_const(experts):
    return np.tile((experts - np.arange(experts, dtype=np.float32)), (P, KT)).astype(np.float32)


def pick_const(experts, bf):
    return np.tile(np.eye(experts)[:, :, None], (3, 1, P)).astype(bf)


LIMIT, ALPHA = 7.0, 1.702


def stage_moe1(c):
    nc, ins, S = c.nc, c.ins, 16
    with ExitStack() as s:
        def sb(name, shape, dt=F32):
            return s.enter_context(nc.sbuf_tensor(f"m1_{name}", shape, dt))

        def psum(name, bufs):
            return s.enter_context(nc.psum_tensor(f"m1_{name}", [P, bufs, TILE], F32))

        def sem(name):
            return s.enter_context(nc.semaphore(f"m1_{name}"))

        cw3 = sb("cw3", [3 * S, TOK], BF16)
        stage_router(c, "r1", S, cw3, logits_bias=True)
        wg, wu, wd = sb("wg", [P, S, P]), sb("wu", [P, S, P]), sb("wd", [P, S, P])
        bd3 = sb("bd3", [3 * S, P])
        cwf = sb("cwf", [3 * S, TILE])
        bu1 = sb("bu1", [P, S])
        pick = sb("pick", [3 * S, S, P], BF16)
        g, u, sg, gs, v, gc = (sb(n, [P, BUFS, TILE]) for n in ("g", "u", "sg", "gs", "v", "gc"))
        gate_ps, up_ps, cw_ps, o_ps = psum("gate_ps", 2), psum("up_ps", 2), psum("cw_ps", 2), psum("o_ps", 1)
        (loaded, bu1_set, gate_ready, up_ready, gu_free, cw_ready, g_ready, sg_ready, gs_ready, v_ready, gc_ready,
         cwf_ready, o_ready, o_free) = (
            sem(n) for n in ("loaded", "bu1_set", "gate_ready", "up_ready", "gu_free", "cw_ready", "g_ready",
                             "sg_ready", "gs_ready", "v_ready", "gc_ready", "cwf_ready", "o_ready", "o_free"))
        with nc.Block() as block:
            @block.sync
            def _(sp):
                for dst, name in ((wg, "m1_wg"), (wu, "m1_wu"), (wd, "m1_wd"), (pick, "m1_pick")):
                    sp.dma_start(dst[:, :, :], ins[name]).then_inc(loaded, 16)
                sp.dma_start(bd3[:, :], ins["m1_bd3"]).then_inc(loaded, 16)

            @block.tensor
            def _(pe):
                pe.wait_ge(loaded, 16 * 5)
                pe.sem_inc(gu_free, 2)
                pe.sem_inc(o_free, 1)
                with pe.Fori(0, NT) as t:
                    tile = bass.ts(t, TILE)

                    def down(k):
                        if k == 0:
                            pe.wait_ge(o_free, t + 1)
                            pe.wait_ge(cwf_ready, t + 1)
                            nc.tensor.matmul(o_ps[:, 0, :], bd3[:, :], cwf[:, :], start=True, stop=False)
                        pe.wait_ge(gc_ready, t * S + (k + 1))
                        return nc.tensor.matmul(o_ps[:, 0, :], wd[:, k, :], gc[:, k % BUFS, :], start=False,
                                                stop=(k == S - 1))
                    for k in range(S):
                        pe.wait_ge(gu_free, t * S + (k + 1))
                        nc.tensor.matmul(gate_ps[:, k % 2, :], wg[:, k, :], c.h_t[:, tile], start=True,
                                         stop=True).then_inc(gate_ready, 1)
                        nc.tensor.matmul(up_ps[:, k % 2, :], wu[:, k, :], c.h_t[:, tile], start=True,
                                         stop=True).then_inc(up_ready, 1)
                        if k >= LAG:
                            down(k - LAG)
                        nc.tensor.matmul(cw_ps[:, k % 2, :], pick[:, k, :], cw3[:, tile], start=True,
                                         stop=True).then_inc(cw_ready, 1)
                    for k in range(S - LAG, S):
                        mm = down(k)
                    mm.then_inc(o_ready, 1)

            @block.scalar
            def _(act):
                nc.scalar.preload_act_table(ACT.Sigmoid)
                with act.Fori(0, NT) as t:
                    for k in range(S):
                        act.wait_ge(g_ready, t * S + (k + 1))
                        nc.scalar.activation(sg[:, k % BUFS, :], g[:, k % BUFS, :], ACT.Sigmoid,
                                             scale=ALPHA).then_inc(sg_ready, 1)

            @block.gpsimd
            def _(pool):
                with pool.Fori(0, NT) as t:
                    nc.gpsimd.tensor_copy(cwf[:, :], cw3[:, bass.ts(t, TILE)]).then_inc(cwf_ready, 1)
                    for k in range(S):
                        b = k % BUFS
                        pool.wait_ge(sg_ready, t * S + (k + 1))
                        nc.gpsimd.tensor_tensor(gs[:, b, :], g[:, b, :], sg[:, b, :], ALU.mult).then_inc(gs_ready, 1)

            @block.vector
            def _(dve):
                first = VECS.index("bu0")
                nc.vector.tensor_scalar(bu1[:, :], c.vecs[:, first:first + S], 1.0, None, ALU.add).then_inc(bu1_set, 1)
                dve.wait_ge(bu1_set, 1)
                with dve.Fori(0, NT) as t:
                    tile = bass.ts(t, TILE)

                    def finish(k):
                        b = k % BUFS
                        dve.wait_ge(gs_ready, t * S + (k + 1))
                        dve.wait_ge(gu_free, t * S + (k + 3))
                        nc.vector.scalar_tensor_tensor(v[:, b, :], u[:, b, :], 1.0 - LIMIT, gs[:, b, :], ALU.max,
                                                       ALU.mult).then_inc(v_ready, 1)
                        dve.wait_ge(v_ready, t * S + (k + 1))
                        dve.wait_ge(cw_ready, t * S + (k + 1))
                        nc.vector.tensor_tensor(gc[:, b, :], v[:, b, :], cw_ps[:, k % 2, :],
                                                ALU.mult).then_inc(gc_ready, 1)
                    for k in range(S):
                        b = k % BUFS
                        dve.wait_ge(gate_ready, t * S + (k + 1))
                        nc.vector.tensor_scalar(g[:, b, :], gate_ps[:, k % 2, :], vec(c, f"bg{k}"), LIMIT, ALU.add,
                                                ALU.min).then_inc(g_ready, 1)
                        dve.wait_ge(up_ready, t * S + (k + 1))
                        nc.vector.tensor_scalar(u[:, b, :], up_ps[:, k % 2, :], bu1[:, k:k + 1], LIMIT + 1.0,
                                                ALU.add, ALU.min).then_inc(gu_free, 1)
                        if k >= 1:
                            finish(k - 1)
                    finish(S - 1)
                    dve.wait_ge(gc_ready, t * S + S)
                    dve.wait_ge(o_ready, t + 1)
                    nc.vector.scalar_tensor_tensor(c.x_t[:, tile], o_ps[:, 0, :], c.mod[:, 1, GB, bass.ds(t, 1)],
                                                   c.x_t[:, tile], ALU.mult, ALU.add).then_inc(o_free, 1)


def layout_moe1(a, d, bf):
    d["r1_wr"] = a["L1_ffn_Wg"].T
    d["r1_rank"] = rank_const(16)
    d["r1_lb"] = np.tile(a["L1_ffn_bg"], (P, KT))
    wgu = a["L1_ffn_Wgu"].transpose(1, 0, 2)
    d["m1_wg"], d["m1_wu"] = wgu[:, :, ::2], wgu[:, :, 1::2]
    d["m1_wd"] = a["L1_ffn_Wd"].transpose(1, 0, 2)
    d["m1_bd3"] = np.tile(a["L1_ffn_bd"], (3, 1))
    d["m1_pick"] = pick_const(16, bf)


def stage_moe3(c):
    nc, ins, E, F = c.nc, c.ins, 7, 4
    S = (E + 1) * F
    capacity = -(-5 * 1024 * 2 // (4 * E))
    stage_norm(c, c.h_t, c.h_t, lambda t: vec(c, "ln_g"), lambda t: vec(c, "ln_b"))
    with ExitStack() as s:
        def sb(name, shape, dt=F32):
            return s.enter_context(nc.sbuf_tensor(f"m3_{name}", shape, dt))

        def psum(name, bufs):
            return s.enter_context(nc.psum_tensor(f"m3_{name}", [P, bufs, TILE], F32))

        def sem(name):
            return s.enter_context(nc.semaphore(f"m3_{name}"))

        cw3 = sb("cw3", [3 * E, TOK], BF16)
        stage_router(c, "r3", E, cw3, capacity=capacity)
        w1, w3, w2 = (sb(n, [P, E + 1, F, P]) for n in ("w1", "w3", "w2"))
        pick = sb("pick", [3 * E, E, P], BF16)
        sa, v, gc = (sb(n, [P, BUFS, TILE]) for n in ("sa", "v", "gc"))
        a_ps, b_ps, cw_ps, o_ps = psum("a_ps", 2), psum("b_ps", 2), psum("cw_ps", 2), psum("o_ps", 1)
        loaded, a_ready, b_ready, ab_free, cw_ready, sa_ready, gc_ready, o_ready, o_free = (
            sem(n) for n in ("loaded", "a_ready", "b_ready", "ab_free", "cw_ready", "sa_ready", "gc_ready",
                             "o_ready", "o_free"))
        with nc.Block() as block:
            @block.sync
            def _(sp):
                sp.dma_start(pick[:, :, :], ins["m3_pick"]).then_inc(loaded, 16)
                for dst, name in ((w1, "m3_w1"), (w3, "m3_w3"), (w2, "m3_w2")):
                    sp.dma_start(dst[:, :, :, :], ins[name]).then_inc(loaded, 16)

            @block.tensor
            def _(pe):
                pe.wait_ge(loaded, 64)
                pe.sem_inc(ab_free, 2)
                pe.sem_inc(o_free, 1)
                with pe.Fori(0, NT) as t:
                    tile = bass.ts(t, TILE)

                    def down(k):
                        if k == 0:
                            pe.wait_ge(o_free, t + 1)
                        pe.wait_ge(gc_ready, t * S + (k + 1))
                        return nc.tensor.matmul(o_ps[:, 0, :], w2[:, k // F, k % F, :], gc[:, k % BUFS, :],
                                                start=(k == 0), stop=(k == S - 1))
                    for k in range(S):
                        e, f = divmod(k, F)
                        pe.wait_ge(ab_free, t * S + (k + 1))
                        nc.tensor.matmul(a_ps[:, k % 2, :], w1[:, e, f, :], c.h_t[:, tile], start=True,
                                         stop=True).then_inc(a_ready, 1)
                        nc.tensor.matmul(b_ps[:, k % 2, :], w3[:, e, f, :], c.h_t[:, tile], start=True,
                                         stop=True).then_inc(b_ready, 1)
                        if k >= LAG:
                            down(k - LAG)
                        if f == 0 and e < E:
                            nc.tensor.matmul(cw_ps[:, e % 2, :], pick[:, e, :], cw3[:, tile], start=True,
                                             stop=True).then_inc(cw_ready, 1)
                    for k in range(S - LAG, S):
                        mm = down(k)
                    mm.then_inc(o_ready, 1)

            @block.scalar
            def _(act):
                nc.scalar.preload_act_table(ACT.Silu)
                with act.Fori(0, NT) as t:
                    for k in range(S):
                        act.wait_ge(a_ready, t * S + (k + 1))
                        nc.scalar.activation(sa[:, k % BUFS, :], a_ps[:, k % 2, :], ACT.Silu).then_inc(sa_ready, 1)

            @block.vector
            def _(dve):
                with dve.Fori(0, NT) as t:
                    tile = bass.ts(t, TILE)
                    for k in range(S):
                        e, f = divmod(k, F)
                        b = k % BUFS
                        dve.wait_ge(sa_ready, t * S + (k + 1))
                        dve.wait_ge(b_ready, t * S + (k + 1))
                        nc.vector.tensor_tensor(v[:, b, :], sa[:, b, :], b_ps[:, k % 2, :],
                                                ALU.mult).then_inc(ab_free, 1)
                        dve.wait_ge(ab_free, t * S + (k + 3))
                        if e < E:
                            dve.wait_ge(cw_ready, t * E + (e + 1))
                            nc.vector.tensor_tensor(gc[:, b, :], v[:, b, :], cw_ps[:, e % 2, :],
                                                    ALU.mult).then_inc(gc_ready, 1)
                        else:
                            nc.vector.tensor_copy(gc[:, b, :], v[:, b, :]).then_inc(gc_ready, 1)
                    dve.wait_ge(gc_ready, t * S + S)
                    dve.wait_ge(o_ready, t + 1)
                    nc.vector.scalar_tensor_tensor(c.x_t[:, tile], o_ps[:, 0, :], c.mod[:, 3, GB, bass.ds(t, 1)],
                                                   c.x_t[:, tile], ALU.mult, ALU.add).then_inc(o_free, 1)


def layout_moe3(a, d, bf):
    d["r3_wr"] = a["L3_ffn_Wr"]
    d["r3_rank"] = rank_const(7)
    d["m3_pick"] = pick_const(7, bf)
    for n in ("w1", "w3"):
        w = np.concatenate([a[f"L3_ffn_{n.upper()}"], a[f"L3_ffn_{n.upper()}s"][None]])
        d[f"m3_{n}"] = w.reshape(8, P, 4, P).transpose(1, 0, 2, 3)
    w = np.concatenate([a["L3_ffn_W2"], a["L3_ffn_W2s"][None]])
    d["m3_w2"] = w.reshape(8, 4, P, P).transpose(2, 0, 1, 3)


HEADS, HD = 16, 8
SOFTMAX_SCALE = HD ** -0.5


class Chain:

    def __init__(self, eng, sem, per_turn=0, turn=0):
        self.eng, self.sem, self.base, self.n = eng, sem, turn * per_turn, 0
        self.per_turn = per_turn

    def __call__(self, ins):
        self.n += 1
        ins.then_inc(self.sem, 1)
        self.eng.wait_ge(self.sem, self.base + self.n)


def stage_head_attention(c):
    nc, ins = c.nc, c.ins
    SUB = SEQ // P
    POOL1, POOL2 = 13, 12
    with ExitStack() as s:
        def sb(name, shape, dt=F32):
            return s.enter_context(nc.sbuf_tensor(f"h1_{name}", shape, dt))

        def psum(name, shape):
            return s.enter_context(nc.psum_tensor(f"h1_{name}", shape, F32))

        def sem(name):
            return s.enter_context(nc.semaphore(f"h1_{name}"))

        wq = sb("wq", [P, 2, P])
        wkv = sb("wkv", [33, 3, P])
        bq = sb("bq", [1, 2, P])
        one = sb("one", [1, P])
        wdown, wo = sb("wdown", [P, 32]), sb("wo", [P, P])
        turn = sb("turn", [P, SUB, 2, HD])
        hb = sb("hb", [P, SEQ])
        lat = sb("lat", [33, SEQ])
        rc, rs = sb("rc", [P, 2, 2, P]), sb("rs", [P, 2, 2, P])
        qk, v = sb("qk", [P, 2, 2, P]), sb("v", [P, 2, P])
        pr1, pr2 = sb("pr1", [P, 2, HEADS, HEADS, HD]), sb("pr2", [P, 2, HEADS, HD, HEADS])
        sc, pe_ = sb("sc", [P, 2, HEADS, HEADS]), sb("e", [P, 2, HEADS, HEADS])
        mx, den, rden = sb("mx", [P, HEADS]), sb("den", [P, HEADS]), sb("rden", [P, HEADS])
        o, on = sb("o", [P, 2, P]), sb("on", [P, 2, P])
        y, z = sb("y", [P, 2, TILE]), sb("z", [P, 2, TILE])
        qk_ps = psum("qk_ps", [P, 2, 2, 2, P])
        v_ps = psum("v_ps", [P, 2, 4, P])
        lat_ps = psum("lat_ps", [32, TILE])
        y_ps, o_ps = psum("y_ps", [P, 2, TILE]), psum("o_ps", [P, TILE])
        names = ("loaded", "set", "h_copied", "lat_mm", "lat_ready", "qk_mm", "v_ready", "chain", "rope_ready", "p1",
                 "p1d", "s_ready", "e_ready", "p2", "p2d", "on_ready", "turned", "y_ready", "o_mm", "v_mm")
        (loaded, set_, h_copied, lat_mm, lat_ready, qk_mm, v_ready, chain, rope_ready, p1, p1d, s_ready, e_ready, p2,
         p2d, on_ready, turned, y_ready, o_mm, v_mm) = (sem(n) for n in names)
        CHAIN = 9 * SUB + 2 * TPB
        with nc.Block() as block:
            @block.sync
            def _(sp):
                for dst, name in ((wq[:, :, :], "h1_wq"), (wkv[:, :, :], "h1_wkv"), (bq[:, :, :], "h1_bq"),
                                  (wdown[:, :], "h1_wdown"), (wo[:, :], "h1_wo"), (turn[:, :, :, :], "h1_rope")):
                    sp.dma_start(dst, ins[name]).then_inc(loaded, 16)

            @block.tensor
            def _(pe):
                pe.wait_ge(loaded, 16 * 6)
                pe.wait_ge(set_, 2)
                with pe.Fori(0, BATCH) as b:
                    pe.wait_ge(h_copied, b + 1)
                    for u in range(TPB):
                        if u:
                            pe.wait_ge(lat_ready, b * 2 + u)
                        nc.tensor.matmul(lat_ps[:, :], wdown[:, :], hb[:, u * TILE:(u + 1) * TILE], start=True,
                                         stop=True).then_inc(lat_mm, 1)

                    def project(n):
                        if n >= 2:
                            pe.wait_ge(rope_ready, b * SUB + (n - 1))
                            pe.wait_ge(v_ready, b * SUB + (n - 1))
                        tok = slice(n * P, (n + 1) * P)
                        ps = qk_ps[:, n % 2, :, :, :]
                        nc.tensor.matmul(ps[:, :, 0, :], hb[:, tok], wq[:, :, :], start=True, stop=False,
                                         skip_group_check=True)
                        nc.tensor.matmul(ps[:, :, 0, :], one[:, :], bq[:, :, :], start=False, stop=True,
                                         skip_group_check=True)
                        nc.tensor.matmul(ps[:, :, 1, :], lat[:, tok], wkv[:, 0:2, :], start=False, stop=True,
                                         skip_group_check=True).then_inc(qk_mm, 1)
                        nc.tensor.matmul(v_ps[:, n % 2, 0, :], lat[:, tok], wkv[:, 2, :], start=True,
                                         stop=True).then_inc(v_mm, 1)

                    def turn_back(n):
                        pe.wait_ge(on_ready, b * SUB + (n + 1))
                        u, j = divmod(n, 4)
                        nc.tensor.transpose(y_ps[:, u, j * P:(j + 1) * P], on[:, n % 2, :],
                                            c.ident[:, :]).then_inc(turned, 1)

                    def out(u):
                        pe.wait_ge(y_ready, b * 2 + (u + 1))
                        nc.tensor.matmul(o_ps[:, :], wo[:, :], y[:, u, :], start=True, stop=True).then_inc(o_mm, 1)
                    pe.wait_ge(lat_ready, b * 2 + 2)
                    for n in range(SUB):
                        project(n)
                        if n >= 3:
                            turn_back(n - 3)
                    for n in range(SUB - 3, SUB):
                        turn_back(n)
                        if n == 5:
                            out(0)
                    out(1)

            @block.scalar
            def _(act):
                nc.scalar.preload_act_table(ACT.Exp)
                with act.Fori(0, BATCH) as b:
                    for u in range(TPB):
                        act.wait_ge(lat_mm, b * 2 + (u + 1))
                        nc.scalar.activation(lat[0:32, u * TILE:(u + 1) * TILE], lat_ps[:, :], ACT.Identity,
                                             bias=vec(c, "L1_bdown")[0:32, :]).then_inc(lat_ready, 1)
                    for n in range(SUB):
                        act.wait_ge(v_mm, b * SUB + (n + 1))
                        if n >= 2:
                            act.wait_ge(on_ready, b * SUB + (n - 1))
                        nc.scalar.copy(v[:, n % 2, :], v_ps[:, n % 2, 0, :]).then_inc(v_ready, 1)
                        if n >= 1:
                            act.wait_ge(s_ready, b * SUB + n)
                            nc.scalar.activation(pe_[:, (n - 1) % 2, :, :], sc[:, (n - 1) % 2, :, :], ACT.Exp,
                                                 scale=SOFTMAX_SCALE).then_inc(e_ready, 1)
                    act.wait_ge(s_ready, b * SUB + SUB)
                    nc.scalar.activation(pe_[:, (SUB - 1) % 2, :, :], sc[:, (SUB - 1) % 2, :, :], ACT.Exp,
                                         scale=SOFTMAX_SCALE).then_inc(e_ready, 1)

            def product1(eng, n, h0, h1):
                q = qk[:, n % 2, 0, h0 * HD:h1 * HD].rearrange("p (h d) -> p h d", d=HD)
                k = qk[:, n % 2, 1, :].rearrange("p (g d) -> p g d", d=HD)
                shape = [P, h1 - h0, HEADS, HD]
                return eng.tensor_tensor(pr1[:, n % 2, h0:h1, :, :], q.unsqueeze(2).to_broadcast(shape),
                                         k.unsqueeze(1).to_broadcast(shape), ALU.mult)

            def product2(eng, n, h0, h1):
                e = pe_[:, n % 2, h0:h1, :]
                w = v[:, n % 2, :].rearrange("p (g d) -> p d g", d=HD)
                shape = [P, h1 - h0, HD, HEADS]
                return eng.tensor_tensor(pr2[:, n % 2, h0:h1, :, :], e.unsqueeze(2).to_broadcast(shape),
                                         w.unsqueeze(1).to_broadcast(shape), ALU.mult)

            @block.gpsimd
            def _(pool):
                with pool.Fori(0, BATCH) as b:
                    def first(n):
                        pool.wait_ge(rope_ready, b * SUB + (n + 1))
                        if n >= 2:
                            pool.wait_ge(s_ready, b * SUB + (n - 1))
                        product1(nc.gpsimd, n, 0, POOL1).then_inc(p1, 1)

                    def second(n):
                        pool.wait_ge(e_ready, b * SUB + (n + 1))
                        pool.wait_ge(v_ready, b * SUB + (n + 1))
                        if n >= 2:
                            pool.wait_ge(on_ready, b * SUB + (n - 1))
                        product2(nc.gpsimd, n, 0, POOL2).then_inc(p2, 1)
                    first(0)
                    for n in range(SUB):
                        if n + 1 < SUB:
                            first(n + 1)
                        second(n)

            @block.vector
            def _(dve):
                nc.vector.memset(one[:, :], 1.0).then_inc(set_, 1)
                nc.vector.memset(lat[32:33, :], 1.0).then_inc(set_, 1)
                dve.wait_ge(loaded, 16 * 6)
                with dve.Fori(0, BATCH) as b:
                    done = Chain(dve, chain, CHAIN, b)
                    tt = nc.vector.tensor_tensor
                    nc.vector.tensor_copy(hb[:, :], c.h_t[:, bass.ts(b, SEQ)]).then_inc(h_copied, 1)

                    def rope(n):
                        dve.wait_ge(qk_mm, b * SUB + (n + 1))
                        if n >= 2:
                            dve.wait_ge(p1, b * SUB + (n - 1))
                        ps = qk_ps[:, n % 2, :, :, :]
                        for r, dst in ((0, rc), (1, rs)):
                            cs = turn[:, n, r, :].unsqueeze(1).to_broadcast([P, 2 * HEADS, HD])
                            done(tt(dst[:, n % 2, :, :].rearrange("p x (h d) -> p (x h) d", d=HD),
                                    ps[:, r, :, :].rearrange("p x (h d) -> p (x h) d", d=HD), cs, ALU.mult))
                        tt(qk[:, n % 2, :, :], rc[:, n % 2, :, :], rs[:, n % 2, :, :], ALU.add).then_inc(rope_ready, 1)

                    def scores(n):
                        dve.wait_ge(rope_ready, b * SUB + (n + 1))
                        done(product1(nc.vector, n, POOL1, HEADS))
                        dve.wait_ge(p1, b * SUB + (n + 1))
                        x = n % 2
                        done(nc.vector.reduce_sum(sc[:, x, :, :], pr1[:, x, :, :, :], AX.X))
                        done(nc.vector.reduce_max(mx[:, :], sc[:, x, :, :], AX.X))
                        tt(sc[:, x, :, :], sc[:, x, :, :], mx[:, :].unsqueeze(2).to_broadcast([P, HEADS, HEADS]),
                           ALU.subtract).then_inc(s_ready, 1)
                        dve.wait_ge(s_ready, b * SUB + (n + 1))

                    def weigh(n):
                        x = n % 2
                        dve.wait_ge(e_ready, b * SUB + (n + 1))
                        dve.wait_ge(v_ready, b * SUB + (n + 1))
                        done(product2(nc.vector, n, POOL2, HEADS))
                        done(nc.vector.reduce_sum(den[:, :], pe_[:, x, :, :], AX.X))
                        done(nc.vector.reciprocal(rden[:, :], den[:, :]))
                        dve.wait_ge(p2, b * SUB + (n + 1))
                        if n >= 2:
                            dve.wait_ge(turned, b * SUB + (n - 1))
                        done(nc.vector.reduce_sum(o[:, x, :].rearrange("p (h d) -> p h d", d=HD), pr2[:, x, :, :, :],
                                                  AX.X))
                        tt(on[:, x, :].rearrange("p (h d) -> p h d", d=HD),
                           o[:, x, :].rearrange("p (h d) -> p h d", d=HD),
                           rden[:, :].unsqueeze(2).to_broadcast([P, HEADS, HD]), ALU.mult).then_inc(on_ready, 1)
                        dve.wait_ge(on_ready, b * SUB + (n + 1))

                    def gather(u):
                        dve.wait_ge(turned, b * SUB + 4 * (u + 1))
                        nc.vector.tensor_copy(y[:, u, :], y_ps[:, u, :]).then_inc(y_ready, 1)

                    def add(u):
                        dve.wait_ge(o_mm, b * 2 + (u + 1))
                        t = b * 2 + u
                        done(nc.vector.tensor_scalar(z[:, u, :], o_ps[:, :], vec(c, "L1_bout"),
                                                     c.mod[:, 1, GA, bass.ds(t, 1)], ALU.add, ALU.mult))
                        done(tt(c.x_t[:, bass.ts(t, TILE)], c.x_t[:, bass.ts(t, TILE)], z[:, u, :], ALU.add))
                    rope(0)
                    rope(1)
                    for n in range(SUB):
                        scores(n)
                        if n + 2 < SUB:
                            rope(n + 2)
                        if n >= 1:
                            weigh(n - 1)
                    weigh(SUB - 1)
                    gather(0)
                    add(0)
                    gather(1)
                    add(1)
                    assert done.n == CHAIN


def layout_head_attention(a, d, bf):
    up = a["L1_attn_Wup"].reshape(32, HEADS, 2, HD)
    bup = a["L1_attn_bup"].reshape(HEADS, 2, HD)
    wk, wv = up[:, :, 0].reshape(32, P), up[:, :, 1].reshape(32, P)
    bk, bv = bup[:, 0].reshape(1, P), bup[:, 1].reshape(1, P)
    d["h1_wq"] = np.stack([a["L1_attn_Wq"], rope_swap(a["L1_attn_Wq"])], 1)
    d["h1_wkv"] = np.concatenate([np.stack([wk, rope_swap(wk), wv], 1), np.stack([bk, rope_swap(bk), bv], 1)])
    bq = a["L1_attn_bq"][None]
    d["h1_bq"] = np.stack([bq, rope_swap(bq)], 1)
    d["h1_wdown"], d["h1_wo"] = a["L1_attn_Wdown"], a["L1_attn_Wout"]
    inv = 1.0 / 10000.0 ** (np.arange(0, HD, 2, dtype=np.float32) / np.float32(HD))
    freqs = np.arange(SEQ, dtype=np.float32)[:, None] * inv[None, :].astype(np.float32)
    cos, sin = np.cos(freqs), np.sin(freqs)
    table = np.stack([np.concatenate([cos, cos], 1), np.concatenate([-sin, sin], 1)], 1)
    d["h1_rope"] = table.reshape(SEQ // P, P, 2, HD).transpose(1, 0, 2, 3).astype(np.float32)


def stage_linear_attention(c):
    nc, ins = c.nc, c.ins
    H = 8
    D = P // H
    CH = SEQ // P
    with ExitStack() as s:
        def sb(name, shape, dt=F32):
            return s.enter_context(nc.sbuf_tensor(f"a2_{name}", shape, dt))

        def psum(name, shape):
            return s.enter_context(nc.psum_tensor(f"a2_{name}", shape, F32))

        def sem(name):
            return s.enter_context(nc.semaphore(f"a2_{name}"))

        w = sb("w", [P, 4, P])
        wo = sb("wo", [P, P])
        tri = sb("tri", [P, P])
        hmask = sb("hmask", [P, H])
        bmask = sb("bmask", [P, P])
        vt, ut = sb("vt", [P, SEQ]), sb("ut", [P, SEQ])
        xb, neg, pos = (sb(n, [P, 2, TILE]) for n in ("xb", "neg", "pos"))
        qt, kt = sb("qt", [P, SEQ]), sb("kt", [P, SEQ])
        vn, kn = sb("vn", [P, CH, P]), sb("kn", [P, CH, P])
        qx = sb("qx", [P, 2, H, P])
        en = sb("en", [P, 2, H, P])
        kvm, kvs = sb("kvm", [P, P]), sb("kvs", [P, 2, P])
        o, on, sq = sb("o", [P, CH, P]), sb("on", [P, CH, P]), sb("sq", [P, P])
        ss, rr, tiny = sb("ss", [P, CH]), sb("rr", [P, CH]), sb("tiny", [P, 1])
        y, z = sb("y", [P, 2, TILE]), sb("z", [P, 2, TILE])
        ps = psum("ps", [P, 2, TILE])
        en_ps = psum("en_ps", [P, 2, TILE])
        tr_ps, out_ps, kv_ps, oo_ps = (psum(n, [P, TILE]) for n in ("tr_ps", "out_ps", "kv_ps", "oo_ps"))
        names = ("loaded", "set", "proj_mm", "proj_read", "silu_done", "exp_done", "neg_ready", "pos_ready",
                 "elu_ready", "turned", "tok_ready", "qx_ready", "en_mm", "en_ready", "kv_mm", "kvm_ready",
                 "kvs_ready", "out_mm", "out_read", "ss_ready", "ln_done", "rms_ready", "rms_chain", "on_ready",
                 "back", "y_ready", "o_mm", "z_ready", "x_ready")
        S = {n: sem(n) for n in names}
        with nc.Block() as block:
            @block.sync
            def _(sp):
                for dst, name in ((w[:, :, :], "a2_w"), (wo[:, :], "a2_wo"), (tri[:, :], "a2_tri"),
                                  (hmask[:, :], "a2_hmask"), (bmask[:, :], "a2_bmask")):
                    sp.dma_start(dst, ins[name]).then_inc(S["loaded"], 16)

            def energies(n):
                return en_ps if n % 2 == 0 else ps

            @block.tensor
            def _(pe):
                pe.wait_ge(S["loaded"], 16 * 5)
                with pe.Fori(0, BATCH) as b:
                    for i in range(8):
                        if i >= 2:
                            pe.wait_ge(S["proj_read"], b * 8 + (i - 1))
                        nc.tensor.matmul(ps[:, i % 2, :], w[:, i // 2, :], c.h_t[:, bass.ts(b * 2 + i % 2, TILE)],
                                         start=True, stop=True).then_inc(S["proj_mm"], 1)

                    def to_tokens(i, src, ready, value):
                        pe.wait_ge(S[ready], value)
                        if i:
                            pe.wait_ge(S["tok_ready"], b * 4 + i)
                        for j in range(4):
                            at = (i % 2) * 4 + j
                            mm = nc.tensor.transpose(tr_ps[:, j * P:(j + 1) * P], src[:, at * P:(at + 1) * P],
                                                     c.ident[:, :])
                        mm.then_inc(S["turned"], 1)
                    for i in range(2):
                        to_tokens(i, vt, "silu_done", b * 4 + (i + 1))
                    for i in range(2):
                        to_tokens(2 + i, kt, "elu_ready", b * 4 + (3 + i))

                    def energy(n):
                        pe.wait_ge(S["qx_ready"], b * CH + (n + 1))
                        if n >= 2:
                            pe.wait_ge(S["en_ready"], b * CH + (n - 1))
                        for j in range(2):
                            mm = nc.tensor.matmul(energies(n)[:, j, :], kt[:, n * P:(n + 1) * P],
                                                  qx[:, n % 2, 4 * j:4 * j + 4, :], start=True, stop=True)
                        mm.then_inc(S["en_mm"], 1)

                    def output(n):
                        pe.wait_ge(S["en_ready"], b * CH + (n + 1))
                        if n == 0:
                            pe.wait_ge(S["tok_ready"], b * 4 + 4)
                        else:
                            pe.wait_ge(S["kvs_ready"], b * CH + n)
                            pe.wait_ge(S["out_read"], b * CH + n)
                        if n:
                            nc.tensor.matmul(out_ps[:, 0:P], qt[:, n * P:(n + 1) * P], kvs[:, (n - 1) % 2, :],
                                             start=True, stop=False, skip_group_check=True)
                        for h in range(H):
                            mm = nc.tensor.matmul(out_ps[:, h * D:(h + 1) * D], en[:, n % 2, h, :],
                                                  vn[:, n, h * D:(h + 1) * D], start=(n == 0 and h == 0), stop=(h == H - 1),
                                                  skip_group_check=True)
                        mm.then_inc(S["out_mm"], 1)
                        if n:
                            pe.wait_ge(S["kvm_ready"], b * CH + n)
                        nc.tensor.matmul(kv_ps[:, 0:P], kn[:, n, :], vn[:, n, :], start=True,
                                         stop=True).then_inc(S["kv_mm"], 1)
                    energy(0)
                    for n in range(CH):
                        if n + 1 < CH:
                            energy(n + 1)
                        output(n)

                    def project(u):
                        pe.wait_ge(S["y_ready"], b * 2 + (u + 1))
                        if u:
                            pe.wait_ge(S["z_ready"], b * 2 + u)
                        nc.tensor.matmul(oo_ps[:, :], wo[:, :], y[:, u, :], start=True, stop=True).then_inc(S["o_mm"], 1)
                    pe.wait_ge(S["on_ready"], b + 1)
                    for u in range(2):
                        if u:
                            pe.wait_ge(S["y_ready"], b * 2 + u)
                        for j in range(4):
                            mm = nc.tensor.transpose(tr_ps[:, j * P:(j + 1) * P], on[:, u * 4 + j, :], c.ident[:, :])
                        mm.then_inc(S["back"], 1)
                        project(u)
                    pe.wait_ge(S["x_ready"], b * 2 + 2)

            @block.scalar
            def _(act):
                act.wait_ge(S["set"], 1)
                with act.Fori(0, BATCH) as b:
                    for i in range(4):
                        n, u = divmod(i, 2)
                        act.wait_ge(S["proj_mm"], b * 8 + (i + 1))
                        nc.scalar.activation((vt, ut)[n][:, u * TILE:(u + 1) * TILE], ps[:, u, :], ACT.Silu,
                                             bias=vec(c, ("L2_bv", "L2_bu")[n])).then_inc(S["silu_done"], 1)
                        act.wait_ge(S["silu_done"], b * 4 + (i + 1))
                        act.sem_inc(S["proj_read"], 1)
                    for i in range(4):
                        n, u = divmod(i, 2)
                        act.wait_ge(S["proj_mm"], b * 8 + (i + 5))
                        if i >= 2:
                            act.wait_ge(S["elu_ready"], b * 4 + (i - 1))
                        nc.scalar.activation(xb[:, u, :], ps[:, u, :], ACT.Identity,
                                             bias=vec(c, ("L2_bq", "L2_bk")[n])).then_inc(S["proj_read"], 1)
                        act.wait_ge(S["neg_ready"], b * 4 + (i + 1))
                        nc.scalar.activation(neg[:, u, :], neg[:, u, :], ACT.Exp).then_inc(S["exp_done"], 1)
                    for n in range(CH):
                        act.wait_ge(S["out_mm"], b * CH + (n + 1))
                        nc.scalar.copy(o[:, n, :], out_ps[:, 0:P]).then_inc(S["out_read"], 1)
                        act.wait_ge(S["out_read"], b * CH + (n + 1))
                        nc.scalar.activation(sq[:, :], o[:, n, :], ACT.Square, accum_out=ss[:, n:n + 1]).then_inc(S["ss_ready"], 1)
                        act.wait_ge(S["ss_ready"], b * CH + (n + 1))
                    nc.scalar.activation(rr[:, :], ss[:, :], ACT.Ln, bias=tiny[:, 0:1], scale=1.0 / P).then_inc(S["ln_done"], 1)
                    act.wait_ge(S["ln_done"], b + 1)
                    nc.scalar.activation(rr[:, :], rr[:, :], ACT.Exp, scale=0.5).then_inc(S["rms_ready"], 1)

            @block.gpsimd
            def _(pool):
                pool.wait_ge(S["loaded"], 16 * 5)
                with pool.Fori(0, BATCH) as b:
                    for n in range(CH):
                        pool.wait_ge(S["elu_ready"], b * 4 + (n // 4 + 1))
                        if n >= 2:
                            pool.wait_ge(S["en_mm"], b * CH + (n - 1))
                        shape = [P, H, P]
                        nc.gpsimd.tensor_tensor(qx[:, n % 2, :, :],
                                                qt[:, n * P:(n + 1) * P].unsqueeze(1).to_broadcast(shape),
                                                hmask[:, :].unsqueeze(2).to_broadcast(shape),
                                                ALU.mult).then_inc(S["qx_ready"], 1)

            @block.vector
            def _(dve):
                tt, ts = nc.vector.tensor_tensor, nc.vector.tensor_scalar
                nc.vector.memset(tiny[:, :], 1e-30).then_inc(S["set"], 1)
                dve.wait_ge(S["loaded"], 16 * 5)
                with dve.Fori(0, BATCH) as b:
                    def tokens(i):
                        dve.wait_ge(S["turned"], b * 4 + (i + 1))
                        dst = (vn, kn)[i // 2][:, (i % 2) * 4:(i % 2) * 4 + 4, :]
                        nc.vector.tensor_copy(dst, tr_ps[:, :].rearrange("p (j t) -> p j t", j=4)).then_inc(S["tok_ready"], 1)
                    for i in range(4):
                        n, u = divmod(i, 2)
                        dve.wait_ge(S["proj_read"], b * 8 + (i + 5))
                        ts(neg[:, u, :], xb[:, u, :], 0.0, None, ALU.min).then_inc(S["neg_ready"], 1)
                        ts(pos[:, u, :], xb[:, u, :], 0.0, None, ALU.max).then_inc(S["pos_ready"], 1)
                        dve.wait_ge(S["pos_ready"], b * 4 + (i + 1))
                        dve.wait_ge(S["exp_done"], b * 4 + (i + 1))
                        nc.vector.scalar_tensor_tensor((qt, kt)[n][:, u * TILE:(u + 1) * TILE], neg[:, u, :], -1.0,
                                                       pos[:, u, :], ALU.add, ALU.add).then_inc(S["elu_ready"], 1)
                    dve.wait_ge(S["elu_ready"], b * 4 + 4)
                    for i in range(4):
                        tokens(i)
                    for n in range(CH):
                        dve.wait_ge(S["en_mm"], b * CH + (n + 1))
                        if n >= 2:
                            dve.wait_ge(S["out_mm"], b * CH + (n - 1))
                        shape = [P, H, P]
                        tt(en[:, n % 2, :, :], energies(n)[:, :, :].rearrange("p j (h q) -> p (j h) q", q=P),
                           tri[:, :].unsqueeze(1).to_broadcast(shape), ALU.mult).then_inc(S["en_ready"], 1)
                        dve.wait_ge(S["kv_mm"], b * CH + (n + 1))
                        tt(kvm[:, :], kv_ps[:, 0:P], bmask[:, :], ALU.mult).then_inc(S["kvm_ready"], 1)
                        dve.wait_ge(S["kvm_ready"], b * CH + (n + 1))
                        if n == 0:
                            last = nc.vector.tensor_copy(kvs[:, 0, :], kvm[:, :])
                        else:
                            last = tt(kvs[:, n % 2, :], kvs[:, (n - 1) % 2, :], kvm[:, :], ALU.add)
                        last.then_inc(S["kvs_ready"], 1)
                        dve.wait_ge(S["kvs_ready"], b * CH + (n + 1))
                    dve.wait_ge(S["rms_ready"], b + 1)
                    chain = Chain(dve, S["rms_chain"], 2, b)
                    chain(ts(rr[:, :], rr[:, :], 1e-8, None, ALU.add))
                    chain(nc.vector.reciprocal(rr[:, :], rr[:, :]))
                    tt(on[:, :, :], o[:, :, :], rr[:, :].unsqueeze(2).to_broadcast([P, CH, P]),
                       ALU.mult).then_inc(S["on_ready"], 1)
                    for u in range(2):
                        t = b * 2 + u
                        dve.wait_ge(S["back"], b * 2 + (u + 1))
                        nc.vector.scalar_tensor_tensor(y[:, u, :], tr_ps[:, :], vec(c, "L2_scale"),
                                                       ut[:, u * TILE:(u + 1) * TILE], ALU.mult,
                                                       ALU.mult).then_inc(S["y_ready"], 1)
                        dve.wait_ge(S["o_mm"], b * 2 + (u + 1))
                        ts(z[:, u, :], oo_ps[:, :], vec(c, "L2_bo"), c.mod[:, 2, GA, bass.ds(t, 1)], ALU.add,
                           ALU.mult).then_inc(S["z_ready"], 1)
                        dve.wait_ge(S["z_ready"], b * 2 + (u + 1))
                        tt(c.x_t[:, bass.ts(t, TILE)], c.x_t[:, bass.ts(t, TILE)], z[:, u, :],
                           ALU.add).then_inc(S["x_ready"], 1)
                    dve.wait_ge(S["x_ready"], b * 2 + 2)


def layout_linear_attention(a, d, bf):
    d["a2_w"] = np.stack([a[f"L2_attn_W{n}"].T for n in "vuqk"], 1)
    d["a2_wo"] = a["L2_attn_Wo"].T
    d["a2_tri"] = np.triu(np.ones((P, P), np.float32))
    head = np.arange(P) // 16
    d["a2_hmask"] = (head[:, None] == np.arange(8)[None]).astype(np.float32)
    d["a2_bmask"] = (head[:, None] == head[None]).astype(np.float32)


HG = 4
GROUPS = BATCH * HEADS // HG
GCH = HG * HD
KP = 9 * HD
SOFTMAX_SCALE = HD ** -0.5


class Heads:

    def __init__(self, c, tag, stack):
        nc = c.nc
        self.parts = nc.dram_tensor(f"{tag}_parts", (2, 3, BATCH * P, SEQ), BF16, kind="Internal").ap()
        self.neg = nc.dram_tensor(f"{tag}_neg", (GROUPS * 2 * 3, HG * SEQ // 2), BF16, kind="Internal").ap()
        self.out = nc.dram_tensor(f"{tag}_out", (GROUPS * P, SEQ), F32, kind="Internal").ap()
        self.v_all = stack.enter_context(nc.sbuf_tensor(f"{tag}_v_all", [P, GROUPS, SEQ // P, GCH], F32))


def stage_project(c, tag, hd):
    nc, ins = c.nc, c.ins
    with ExitStack() as s:
        def sb(name, shape, dt=F32):
            return s.enter_context(nc.sbuf_tensor(f"{tag}p_{name}", shape, dt))

        def psum(name, shape):
            return s.enter_context(nc.psum_tensor(f"{tag}p_{name}", shape, F32))

        def sem(name):
            return s.enter_context(nc.semaphore(f"{tag}p_{name}"))

        wq, wk, wv = sb("wq", [P, P]), sb("wk", [P, P]), sb("wv", [P, P])
        hs = sb("hs", [P, 2, TILE])
        f = [sb(f"f{x}", [P, TILE]) for x in range(2)]
        r1 = [sb(f"r1{x}", [P, TILE]) for x in range(2)]
        r2 = [sb(f"r2{x}", [P, TILE]) for x in range(2)]
        pt = [sb(f"pt{x}", [P, 2, 3, TILE], BF16) for x in range(2)]
        qk_ps = [psum(f"qk_ps{x}", [P, TILE]) for x in range(2)]
        v_ps = psum("v_ps", [P, TILE // P, P])
        loaded, hs_ready, v_mm, v_free = (sem(n) for n in ("loaded", "hs_ready", "v_mm", "v_free"))
        mm, ps_free, f_ready, hi, r1_ready, mid, r2_ready, lo = (
            [sem(f"{n}{x}") for x in range(2)] for n in ("mm", "ps_free", "f_ready", "hi", "r1_ready", "mid",
                                                         "r2_ready", "lo"))
        stored = [[sem(f"stored{x}{u}") for u in range(2)] for x in range(2)]
        bias = [vec(c, f"{tag}_b{n}") for n in "qk"]
        with nc.Block() as block:
            @block.sync
            def _(sp):
                sp.dma_start(wq[:, :], ins[f"{tag}_wq"]).then_inc(loaded, 16)
                sp.dma_start(wk[:, :], ins[f"{tag}_wk"]).then_inc(loaded, 16)
                sp.dma_start(wv[:, :], ins[f"{tag}_wv"]).then_inc(loaded, 16)
                with sp.Fori(0, BATCH) as b:
                    for u in range(TPB):
                        for x in range(2):
                            sp.wait_ge(lo[x], b * 2 + (u + 2))
                            dst = hd.parts[x, :, bass.ts(b, P), u * TILE:(u + 1) * TILE]
                            sp.dma_start(dst.rearrange("r p t -> p r t"), pt[x][:, u, :, :]).then_inc(stored[x][u], 16)
                for x in range(2):
                    for u in range(2):
                        sp.wait_ge(stored[x][u], 16 * (BATCH + 1))

            @block.tensor
            def _(pe):
                pe.wait_ge(loaded, 16 * 3)
                for x in range(2):
                    pe.sem_inc(ps_free[x], 1)
                pe.sem_inc(v_free, 1)
                with pe.Fori(0, BATCH) as b:
                    for u in range(TPB):
                        n = b * 2 + (u + 1)
                        tile = bass.ts(b * 2 + u, TILE)
                        for x, w in enumerate((wq, wk)):
                            pe.wait_ge(ps_free[x], n)
                            nc.tensor.matmul(qk_ps[x][:, :], w[:, :], c.h_t[:, tile], start=True,
                                             stop=True).then_inc(mm[x], 1)
                        pe.wait_ge(hs_ready, n)
                        pe.wait_ge(v_free, n)
                        for j in range(TILE // P):
                            v = nc.tensor.matmul(v_ps[:, j, :], hs[:, u, j * P:(j + 1) * P], wv[:, :], start=True,
                                                 stop=True)
                        v.then_inc(v_mm, 1)

            @block.scalar
            def _(act):
                for x in range(2):
                    for u in range(2):
                        act.sem_inc(stored[x][u], 16)
                    act.sem_inc(lo[x], 1)
                with act.Fori(0, BATCH) as b:
                    for u in range(TPB):
                        n = b * 2 + (u + 1)
                        for x in range(2):
                            act.wait_ge(f_ready[x], n)
                            act.wait_ge(stored[x][u], b * 16 + 16)
                            nc.scalar.copy(pt[x][:, u, 0, :], f[x][:, :]).then_inc(hi[x], 1)
                        for x in range(2):
                            act.wait_ge(r1_ready[x], n)
                            nc.scalar.copy(pt[x][:, u, 1, :], r1[x][:, :]).then_inc(mid[x], 1)
                        for x in range(2):
                            act.wait_ge(r2_ready[x], n)
                            nc.scalar.copy(pt[x][:, u, 2, :], r2[x][:, :]).then_inc(lo[x], 1)

            @block.gpsimd
            def _(pool):
                with pool.Fori(0, BATCH) as b:
                    for u in range(TPB):
                        n = b * 2 + (u + 1)
                        for x in range(2):
                            pool.wait_ge(hi[x], n)
                            nc.gpsimd.tensor_tensor(r1[x][:, :], f[x][:, :], pt[x][:, u, 0, :],
                                                    ALU.subtract).then_inc(r1_ready[x], 1)
                        for x in range(2):
                            pool.wait_ge(mid[x], n)
                            nc.gpsimd.tensor_tensor(r2[x][:, :], r1[x][:, :], pt[x][:, u, 1, :],
                                                    ALU.subtract).then_inc(r2_ready[x], 1)

            @block.vector
            def _(dve):
                dve.wait_ge(loaded, 16 * 3)
                with dve.Fori(0, BATCH) as b:
                    for u in range(TPB):
                        n = b * 2 + (u + 1)
                        nc.vector.tensor_copy(hs[:, u, :], c.h_t[:, bass.ts(b * 2 + u, TILE)]).then_inc(hs_ready, 1)
                        for x in range(2):
                            dve.wait_ge(mm[x], n)
                            dve.wait_ge(lo[x], n)
                            nc.vector.tensor_scalar(f[x][:, :], qk_ps[x][:, :], bias[x], None,
                                                    ALU.add).then_inc(f_ready[x], 1)
                            dve.wait_ge(f_ready[x], n)
                            nc.vector.sem_inc(ps_free[x], 1)
                        dve.wait_ge(v_mm, n)
                        dst = hd.v_all[:, bass.ts(b, HG), u * 4:(u + 1) * 4, :]
                        nc.vector.tensor_copy(dst, v_ps[:, :, :].rearrange("p k (g c) -> p g k c", g=HG)).then_inc(v_free, 1)


def load_group(sp, hd, g, q9, k9, done):
    rows = [[hd.parts[x, part, bass.ts(g, GCH), :].rearrange("(d h) t -> d (h t)", h=HG) for part in range(3)]
            for x in range(2)]
    for a in range(3):
        at = slice(a * 3 * HD, (a + 1) * 3 * HD)
        sp.dma_start(q9[at, :, :].rearrange("p h t -> p (h t)"),
                     rows[0][a].unsqueeze(0).to_broadcast([3, HD, HG * SEQ])).then_inc(done, 16)
        sp.dma_start(k9[at, :, :].rearrange("p h t -> p (h t)"),
                     hd.parts[1, :, bass.ts(g, GCH), :].rearrange("r (d h) t -> r d (h t)", h=HG)).then_inc(done, 16)


LOADS = 6 * 16


def stage_window_attention(c):
    tag = "L3"
    nc, ins = c.nc, c.ins
    W = 64
    QT = SEQ // P
    with ExitStack() as s0:
        hd = Heads(c, tag, s0)
        stage_project(c, tag, hd)
        with ExitStack() as s:
            def sb(name, shape, dt=F32):
                return s.enter_context(nc.sbuf_tensor(f"{tag}a_{name}", shape, dt))

            def psum(name, shape):
                return s.enter_context(nc.psum_tensor(f"{tag}a_{name}", shape, F32))

            def sem(name):
                return s.enter_context(nc.semaphore(f"{tag}a_{name}"))

            q9 = [sb(f"q9_{i}", [KP + 3, HG, SEQ], BF16) for i in range(3)]
            k9 = [sb(f"k9_{i}", [KP + 3, HG, SEQ], BF16) for i in range(3)]
            va = [sb(f"va_{i}", [P, QT, HG, 32]) for i in range(3)]
            mask_q = sb("mask_q", [P, 2, W + P], BF16)
            mask_k = sb("mask_k", [P, HG, P], BF16)
            mask_w = sb("mask_w", [P, HG, W], BF16)
            p = sb("p", [P, 2, HG, P])
            pw = sb("pw", [P, 2, HG, W])
            neg = sb("neg", [P, 2, HG, 4])
            np_ = sb("neg_parts", [16, 2, 3, P], BF16)
            nr = sb("neg_rest", [16, 2, 2, P])
            o_sb = sb("o_sb", [P, 2, TILE])
            mx_ps, st_ps, sw_ps = psum("mx_ps", [P, 2, TILE]), psum("st_ps", [P, 2, HG, P]), psum("sw_ps", [P, 2, TILE])
            acc, tr_ps = psum("acc", [P, 4, P]), psum("tr_ps", [P, TILE])
            names = ("set", "masks", "va_ready", "mx_mm", "mx_done", "neg_turned", "neg_chain", "neg_parts",
                     "neg_out", "st_ready", "exp_done", "pv_done", "acc_out")
            (set_, masks, va_ready, mx_mm, mx_done, neg_turned, neg_chain, neg_parts, neg_out, st_ready,
             exp_done, pv_done, acc_out) = (sem(n) for n in names)
            loaded = [sem(f"loaded{i}") for i in range(3)]
            neg_in = [sem(f"neg_in{i}") for i in range(2)]
            stored = [sem(f"stored{i}") for i in range(2)]
            SLOTS = 2 * QT

            with nc.Block() as block:
                @block.sync
                def _(sp):
                    for dst, name in ((mask_q, "L3_mask_q"), (mask_k, "L3_mask_k"), (mask_w, "L3_mask_w")):
                        sp.dma_start(dst[:, :, :], ins[name]).then_inc(masks, 16)
                    sp.wait_ge(set_, 9)
                    for g in range(3):
                        load_group(sp, hd, g, q9[g], k9[g], loaded[g])

                    def maxima(g, u, half):
                        rows = hd.neg[bass.ds(g * 6 + half * 3, 3), :]
                        sp.wait_ge(neg_parts, g * 2 + (half + 1))
                        sp.dma_start(rows.rearrange("r (q t) -> q r t", t=P), np_[:, half, :, :]).then_inc(neg_out, 16)
                        sp.wait_ge(neg_out, g * 32 + 16 * (half + 1))
                        sp.dma_start(q9[u][KP:KP + 3, :, half * TILE:(half + 1) * TILE],
                                     rows.rearrange("r (h t) -> r h t", h=HG)).then_inc(neg_in[half], 16)

                    def store(g, half):
                        sp.wait_ge(acc_out, g * 2 + (half + 2))
                        sp.dma_start(hd.out[bass.ts(g, P), half * TILE:(half + 1) * TILE],
                                     o_sb[:, half, :]).then_inc(stored[half], 16)

                    def group(g, u, last=False, load=True):
                        for half in range(2):
                            if not last:
                                maxima(g + 1, (u + 1) % 3, half)
                            store(g, half)
                        if load:
                            load_group(sp, hd, g + 3, q9[u], k9[u], loaded[u])
                    for half in range(2):
                        sp.sem_inc(stored[half], 16)
                        maxima(0, 0, half)
                    loop = (GROUPS - 3) // 3
                    with sp.Fori(0, loop) as i:
                        for u in range(3):
                            group(i * 3 + u, u)
                    for g in range(3 * loop, GROUPS):
                        group(g, g % 3, last=(g == GROUPS - 1), load=(g + 3 < GROUPS))
                    for half in range(2):
                        sp.wait_ge(stored[half], (GROUPS + 1) * 16)

                @block.gpsimd
                def _(pool):
                    for i in range(3):
                        nc.gpsimd.memset(k9[i][64:, :, :], 1.0).then_inc(set_, 1)
                        pool.wait_ge(set_, 3 * i + 1)
                        nc.gpsimd.memset(va[i][:, :, :, HD:2 * HD], 1.0).then_inc(set_, 1)
                        pool.wait_ge(set_, 3 * i + 2)
                        nc.gpsimd.memset(va[i][:, :, :, 2 * HD:], 0.0).then_inc(set_, 1)
                        pool.wait_ge(set_, 3 * i + 3)

                    def values(g, u):
                        nc.gpsimd.tensor_copy(va[u][:, :, :, 0:HD],
                                              hd.v_all[:, bass.ds(g, 1), :, :].rearrange(
                                                  "p g k (h d) -> p (g k) h d", h=HG)).then_inc(va_ready, 1)
                    for g in range(3):
                        values(g, g)

                    def next_values(g, u):
                        pool.wait_ge(pv_done, g * QT - (2 * QT - 2))
                        values(g, u)
                    with pool.Fori(1, GROUPS // 3) as i:
                        for u in range(3):
                            next_values(i * 3 + u, u)
                    next_values(GROUPS - 1, 0)

                @block.tensor
                def _(pe):
                    pe.sem_inc(exp_done, 2)
                    pe.sem_inc(pv_done, 2)
                    pe.sem_inc(acc_out, 1)

                    def scores(g, u, n):
                        q, x = divmod(n, 2)
                        back = W if q else 0
                        free = g * SLOTS + (n - 1)
                        if not (isinstance(g, int) and free <= 0):
                            pe.wait_ge(mx_done, free)
                        out = mx_ps[:, x, 0:2 * (W + P)].rearrange("p (h k) -> p h k", h=2)[:, :, W - back:]
                        nc.tensor.matmul(out, c.ident_bf[:, :], mask_q[:, :, W - back:], start=True, stop=False,
                                         skip_group_check=True)
                        for h in range(2):
                            mm = nc.tensor.matmul(out[:, h, :], q9[u][0:KP, 2 * x + h, q * P:(q + 1) * P],
                                                  k9[u][0:KP, 2 * x + h, q * P - back:(q + 1) * P], start=False,
                                                  stop=True, skip_group_check=True)
                        mm.then_inc(mx_mm, 1)

                    def turn(g, half):
                        pe.wait_ge(mx_done, g * SLOTS + 8 * (half + 1))
                        if not (isinstance(g, int) and g + half == 0):
                            pe.wait_ge(neg_parts, g * 2 + half)
                        nc.tensor.transpose(tr_ps[0:16, 0:P], neg[:, half, :, :].rearrange("p h q -> p (h q)"),
                                            c.ident[:, :]).then_inc(neg_turned, 1)

                    def score(g, u, m):
                        pe.wait_ge(exp_done, g * QT + (m + 1))
                        q = slice(m * P, (m + 1) * P)
                        if m:
                            nc.tensor.matmul(sw_ps[W:, m % 2, 0:HG * W], c.ident_bf[:, W:], mask_w[:, :, :], start=True,
                                             stop=False, skip_group_check=True)
                            for h in range(HG):
                                nc.tensor.matmul(sw_ps[W:, m % 2, h * W:(h + 1) * W], k9[u][:, h, m * P - W:m * P],
                                                 q9[u][:, h, m * P:m * P + W], start=False, stop=True,
                                                 skip_group_check=True)
                        nc.tensor.matmul(st_ps[:, m % 2, :, :], c.ident_bf[:, :], mask_k[:, :, :], start=True, stop=False,
                                         skip_group_check=True)
                        for h in range(HG):
                            mm = nc.tensor.matmul(st_ps[:, m % 2, h, :], k9[u][:, h, q], q9[u][:, h, q], start=False,
                                                  stop=True, skip_group_check=True)
                        mm.then_inc(st_ready, 1)

                    def weigh(g, u, m):
                        half, j = divmod(m, 4)
                        if j == 0:
                            pe.wait_ge(acc_out, g * 2 + (half + 1))
                        pe.wait_ge(exp_done, g * QT + (m + 3))
                        for h in range(HG):
                            mm = nc.tensor.matmul(acc[32 * h:32 * h + 32, j, :], va[u][:, m, h, :], p[:, m % 2, h, :],
                                                  start=True, stop=(m == 0), skip_group_check=True)
                        if m:
                            for h in range(HG):
                                mm = nc.tensor.matmul(acc[32 * h:32 * h + 32, j, 0:W], va[u][W:, m - 1, h, :],
                                                      pw[W:, m % 2, h, :], start=False, stop=True, skip_group_check=True)
                        mm.then_inc(pv_done, 1)

                    def group(g, u, turn_, ahead):
                        pe.wait_ge(va_ready, g + 1)
                        if ahead:
                            pe.wait_ge(loaded[(u + 1) % 3], (turn_ + (u + 1) // 3) * LOADS + LOADS)
                        for n in range(SLOTS):
                            if ahead:
                                scores(g + 1, (u + 1) % 3, n)
                                if n == 9:
                                    turn(g + 1, 0)
                            m = n // 2
                            if n % 8 == 0:
                                pe.wait_ge(neg_in[n // 8], g * 16 + 16)
                            if n % 2 == 0:
                                score(g, u, m)
                            elif m:
                                weigh(g, u, m - 1)
                        if ahead:
                            turn(g + 1, 1)
                        weigh(g, u, QT - 1)
                    pe.wait_ge(masks, 48)
                    pe.wait_ge(loaded[0], LOADS)
                    for n in range(SLOTS):
                        scores(0, 0, n)
                        if n == 9:
                            turn(0, 0)
                    turn(0, 1)
                    with pe.Fori(0, GROUPS // 3) as i:
                        for u in range(3):
                            group(i * 3 + u, u, i, True)
                    group(GROUPS - 1, 0, GROUPS // 3, False)

                @block.scalar
                def _(act):
                    nc.scalar.preload_act_table(ACT.Exp)
                    with act.Fori(0, GROUPS) as g:
                        for m in range(QT):
                            act.wait_ge(st_ready, g * QT + (m + 1))
                            act.wait_ge(pv_done, g * QT + (m + 1))
                            if m:
                                nc.scalar.activation(pw[W:, m % 2, :, :],
                                                     sw_ps[W:, m % 2, 0:HG * W].rearrange("p (h q) -> p h q", h=HG),
                                                     ACT.Exp, scale=SOFTMAX_SCALE)
                            nc.scalar.activation(p[:, m % 2, :, :], st_ps[:, m % 2, :, :], ACT.Exp,
                                                 scale=SOFTMAX_SCALE).then_inc(exp_done, 1)

                @block.vector
                def _(dve):
                    def maximum(g, n):
                        q, x = divmod(n, 2)
                        dve.wait_ge(mx_mm, g * SLOTS + (n + 1))
                        keys = mx_ps[:, x, 0:2 * (W + P)].rearrange("p (h k) -> p h k", h=2)[:, :, 0 if q else W:]
                        nc.vector.tensor_reduce(neg[:, q // 4, 2 * x:2 * x + 2, q % 4:q % 4 + 1], keys, AX.X, ALU.max,
                                                negate=True).then_inc(mx_done, 1)

                    def split(g, half):
                        dve.wait_ge(neg_turned, g * 2 + (half + 1))
                        if not isinstance(g, int):
                            dve.wait_ge(neg_out, g * 32 + 16 * (half - 1))
                        src, k = tr_ps[0:16, 0:P], g * 8 + half * 4
                        for r in range(3):
                            out = np_[:, half, r, :]
                            if r == 2:
                                nc.vector.tensor_copy(out, src).then_inc(neg_parts, 1)
                                break
                            nc.vector.tensor_copy(out, src).then_inc(neg_chain, 1)
                            dve.wait_ge(neg_chain, k + (2 * r + 1))
                            nc.vector.tensor_tensor(nr[:, half, r, :], src, out, ALU.subtract).then_inc(neg_chain, 1)
                            dve.wait_ge(neg_chain, k + (2 * r + 2))
                            src = nr[:, half, r, :]

                    def evacuate(g, half):
                        dve.wait_ge(pv_done, g * QT + (4 * half + 6))
                        dve.wait_ge(stored[half], g * 16 + 16)
                        nc.vector.tensor_copy(o_sb[:, half, :], acc[:, :, :].rearrange("p j t -> p (j t)")).then_inc(acc_out, 1)

                    def maxima(g, own):
                        for n in range(SLOTS):
                            maximum(g, n)
                            if n == 10:
                                split(g, 0)
                            if n == 11 and own is not None:
                                evacuate(own, 0)
                        split(g, 1)
                    maxima(0, None)
                    with dve.Fori(0, GROUPS - 1) as g:
                        maxima(g + 1, g)
                        evacuate(g, 1)
                    evacuate(GROUPS - 1, 0)
                    evacuate(GROUPS - 1, 1)
        stage_attention_out(c, tag, 3, hd)


def stage_attention_out(c, tag, layer, hd):
    nc, ins = c.nc, c.ins
    with ExitStack() as s:
        def sb(name, shape, dt=F32):
            return s.enter_context(nc.sbuf_tensor(f"{tag}o_{name}", shape, dt))

        def sem(name):
            return s.enter_context(nc.semaphore(f"{tag}o_{name}"))

        wo = sb("wo", [P, P])
        od, r, y, z = (sb(n, [P, 2] + ([2] if n == "od" else []) + [TILE]) for n in ("od", "r", "y", "z"))
        o_ps = s.enter_context(nc.psum_tensor(f"{tag}o_ps", [P, 2, TILE], F32))
        loaded = [sem(f"loaded{u}") for u in range(2)]
        w_loaded, rec, scaled, ready, mm, gated, added = (
            sem(n) for n in ("w_loaded", "rec", "scaled", "ready", "mm", "gated", "added"))
        with nc.Block() as block:
            @block.sync
            def _(sp):
                sp.dma_start(wo[:, :], ins[f"{tag}_wo"]).then_inc(w_loaded, 16)
                sp.sem_inc(ready, 2)
                with sp.Fori(0, BATCH) as b:
                    for u in range(TPB):
                        sp.wait_ge(ready, b * 2 + (u + 1))
                        rows = hd.out[bass.ts(b, HG * P), u * TILE:(u + 1) * TILE].rearrange("(h r) t -> h r t", r=32)
                        for k in range(2):
                            sp.dma_start(od[:, u, k, :], rows[:, k * HD:(k + 1) * HD, :]).then_inc(loaded[u], 16)

            @block.tensor
            def _(pe):
                pe.wait_ge(w_loaded, 16)
                with pe.Fori(0, BATCH) as b:
                    for u in range(TPB):
                        pe.wait_ge(ready, b * 2 + (u + 3))
                        nc.tensor.matmul(o_ps[:, u, :], wo[:, :], y[:, u, :], start=True, stop=True).then_inc(mm, 1)

            @block.vector
            def _(dve):
                with dve.Fori(0, BATCH) as b:
                    for u in range(TPB):
                        n = b * 2 + (u + 1)
                        dve.wait_ge(loaded[u], b * 32 + 32)
                        nc.vector.reciprocal(r[:, u, :], od[:, u, 1, :]).then_inc(rec, 1)
                        dve.wait_ge(rec, n)
                        nc.vector.tensor_tensor(r[:, u, :], od[:, u, 0, :], r[:, u, :], ALU.mult).then_inc(scaled, 1)
                        dve.wait_ge(scaled, n)
                        nc.vector.tensor_scalar(y[:, u, :], r[:, u, :], vec(c, f"{tag}_bv"), None,
                                                ALU.add).then_inc(ready, 1)
                    for u in range(TPB):
                        n = b * 2 + (u + 1)
                        tile = bass.ts(b * 2 + u, TILE)
                        dve.wait_ge(mm, n)
                        nc.vector.tensor_scalar(z[:, u, :], o_ps[:, u, :], vec(c, f"{tag}_bo"),
                                                c.mod[:, layer, GA, bass.ds(b * 2 + u, 1)], ALU.add,
                                                ALU.mult).then_inc(gated, 1)
                        dve.wait_ge(gated, n)
                        nc.vector.tensor_tensor(c.x_t[:, tile], c.x_t[:, tile], z[:, u, :], ALU.add).then_inc(added, 1)
                    dve.wait_ge(added, b * 2 + 2)


def layout_window_attention(a, d, bf):
    order = np.arange(P).reshape(4, HG, HD).transpose(0, 2, 1).reshape(P)
    d["L3_wq"], d["L3_wk"] = a["L3_attn_Wq"].T[:, order], a["L3_attn_Wk"].T[:, order]
    d["L3_wv"], d["L3_wo"] = a["L3_attn_Wv"].T, a["L3_attn_Wo"].T
    W, never = 64, -1e9
    q = np.arange(P)[:, None]
    k = np.arange(-W, P)[None]
    mask = np.where((k <= q) & (k > q - W), 0.0, never)
    d["L3_mask_q"] = np.tile(mask[:, None, :], (1, 2, 1)).astype(bf)
    d["L3_mask_k"] = np.tile(mask[:, W:].T[:, None, :], (1, HG, 1)).astype(bf)
    earlier = np.zeros((P, W))
    earlier[W:] = mask[:W, :W].T
    d["L3_mask_w"] = np.tile(earlier[:, None, :], (1, HG, 1)).astype(bf)


def stage_mamba(c):
    nc, ins = c.nc, c.ins
    NS = 16
    RANK = P // 16
    ROWS = 3 * 2 * NS
    STEPS = 2 * NS
    TAPS = 4
    with ExitStack() as s:
        def sb(name, shape, dt=F32):
            return s.enter_context(nc.sbuf_tensor(f"ma_{name}", shape, dt))

        def psum(name):
            return s.enter_context(nc.psum_tensor(f"ma_{name}", [P, 2, TILE], F32))

        def sem(name):
            return s.enter_context(nc.semaphore(f"ma_{name}"))

        w_in, w_x = sb("w_in", [P, 4, P]), sb("w_x", [P, 2, ROWS + RANK])
        w_dt, w_out = sb("w_dt", [ROWS + RANK, 2, P]), sb("w_out", [P, 2, P])
        pick = sb("pick", [ROWS, 2 * NS, P], BF16)
        minus = sb("minus", [ROWS, 2])
        a, one = sb("a", [P, NS, 2]), sb("one", [P, 1])
        raw = sb("raw", [P, 2, TAPS - 1 + SEQ])
        conv, u, zs, low, dt, dtu, nab, yz = (sb(n, [P, 2, SEQ]) for n in
                                              ("conv", "u", "zs", "low", "dt", "dtu", "nab", "yz"))
        bc, rest = sb("bc", [ROWS + RANK, SEQ]), sb("rest", [ROWS, SEQ])
        part, bc3 = sb("part", [ROWS, SEQ], BF16), sb("bc3", [ROWS, SEQ], BF16)
        da, dbu = sb("da", [P, 3, SEQ]), sb("dbu", [P, 3, SEQ])
        bsb, state, hc = sb("bsb", [P, 2, SEQ]), sb("state", [P, 2, SEQ]), sb("hc", [P, 2, SEQ])
        in_ps, b_ps, c_ps, y_ps = (psum(n) for n in ("in_ps", "b_ps", "c_ps", "y_ps"))
        names = ("loaded", "set", "in_mm", "in_read", "conv_step", "u_ready", "xp_mm", "bc_ready", "split_step",
                 "dt_mm", "low_ready", "nab_ready", "exp_low", "ln_done", "dt_ready", "dtu_ready", "b_mm", "b_read",
                 "c_mm", "da_ready", "dbu_ready", "scan_done", "hc_ready", "sum_mm", "yd_ready", "yz_ready",
                 "o_mm", "x_ready")
        S = {n: sem(n) for n in names}
        with nc.Block() as block:
            @block.sync
            def _(sp):
                for dst, name in ((w_in, "w_in"), (w_x, "w_x"), (w_dt, "w_dt"), (w_out, "w_out"), (pick, "pick")):
                    sp.dma_start(dst[:, :, :], ins[f"ma_{name}"]).then_inc(S["loaded"], 16)
                sp.dma_start(minus[:, :], ins["ma_minus"]).then_inc(S["loaded"], 16)

            @block.tensor
            def _(pe):
                pe.wait_ge(S["loaded"], 16 * 6)
                pe.sem_inc(S["b_read"], 1)
                pe.sem_inc(S["hc_ready"], 2)
                pe.sem_inc(S["sum_mm"], 2)
                pe.sem_inc(S["scan_done"], 3)
                pe.sem_inc(S["dbu_ready"], 2)
                with pe.Fori(0, BATCH) as b:
                    for i in range(8):
                        if i >= 2:
                            pe.wait_ge(S["in_read"], b * 8 + (i - 1))
                        nc.tensor.matmul(in_ps[:, i % 2, :], w_in[:, i // 2, :], c.h_t[:, bass.ts(b * 2 + i % 2, TILE)],
                                         start=True, stop=True).then_inc(S["in_mm"], 1)
                    pe.wait_ge(S["u_ready"], b * 2 + 2)
                    for i in range(2):
                        pe.wait_ge(S["in_read"], b * 8 + (7 + i))
                        for h in range(2):
                            mm = nc.tensor.matmul(in_ps[0:ROWS + RANK, i, :], w_x[:, h, :],
                                                  u[:, h, i * TILE:(i + 1) * TILE], start=(h == 0), stop=(h == 1))
                        mm.then_inc(S["xp_mm"], 1)
                    for i in range(4):
                        h, t = divmod(i, 2)
                        if h == 0:
                            pe.wait_ge(S["bc_ready"], b * 2 + (t + 1))
                        else:
                            pe.wait_ge(S["low_ready"], b * 4 + (i - 1))
                        nc.tensor.matmul(in_ps[:, t, :], w_dt[:, h, :], bc[:, t * TILE:(t + 1) * TILE],
                                         start=True, stop=True).then_inc(S["dt_mm"], 1)

                    def spread(row, ps):
                        for t in range(2):
                            mm = nc.tensor.matmul(ps[:, t, :], pick[:, row, :], bc3[:, t * TILE:(t + 1) * TILE],
                                                  start=True, stop=True)
                        return mm

                    def spread_b(j):
                        pe.wait_ge(S["b_read"], b * STEPS + (j + 1))
                        spread(j % NS, b_ps).then_inc(S["b_mm"], 1)

                    def spread_c(j):
                        pe.wait_ge(S["hc_ready"], b * STEPS + (j + 2))
                        spread(NS + j % NS, c_ps).then_inc(S["c_mm"], 1)
                    pe.wait_ge(S["split_step"], b * 4 + 4)
                    spread_b(0)
                    spread_c(0)
                    spread_b(1)
                    for j in range(STEPS):
                        if j + 2 < STEPS:
                            spread_b(j + 2)
                        if j + 1 < STEPS:
                            spread_c(j + 1)
                        if j == NS:
                            pe.wait_ge(S["yd_ready"], b * 2 + 1)
                        pe.wait_ge(S["hc_ready"], b * STEPS + (j + 3))
                        for t in range(2):
                            mm = nc.tensor.matmul(y_ps[:, t, :], c.ident[:, :], hc[:, j % 2, t * TILE:(t + 1) * TILE],
                                                  start=(j % NS == 0), stop=(j % NS == NS - 1))
                        mm.then_inc(S["sum_mm"], 1)
                    pe.wait_ge(S["yz_ready"], b * 2 + 2)
                    for t in range(2):
                        for h in range(2):
                            mm = nc.tensor.matmul(y_ps[:, t, :], w_out[:, h, :], yz[:, h, t * TILE:(t + 1) * TILE],
                                                  start=(h == 0), stop=(h == 1))
                        mm.then_inc(S["o_mm"], 1)
                    pe.wait_ge(S["x_ready"], b * 2 + 2)

            @block.scalar
            def _(act):
                first = VECS.index("A_log00")
                nc.scalar.activation(a[:, :, :].rearrange("p s h -> p (s h)"), c.vecs[:, first:first + 2 * NS],
                                     ACT.Exp).then_inc(S["set"], 1)
                act.wait_ge(S["set"], 4)
                with act.Fori(0, BATCH) as b:
                    for i in range(4):
                        h, t = divmod(i, 2)
                        act.wait_ge(S["in_mm"], b * 8 + (i + 1))
                        at = TAPS - 1 + t * TILE
                        nc.scalar.copy(raw[:, h, at:at + TILE], in_ps[:, t, :]).then_inc(S["in_read"], 1)
                    for i in range(4):
                        h, t = divmod(i, 2)
                        act.wait_ge(S["in_mm"], b * 8 + (i + 5))
                        nc.scalar.activation(zs[:, h, t * TILE:(t + 1) * TILE], in_ps[:, t, :],
                                             ACT.Silu).then_inc(S["in_read"], 1)
                    for h in range(2):
                        act.wait_ge(S["conv_step"], b * 2 * TAPS + (h + 1) * TAPS)
                        nc.scalar.activation(u[:, h, :], conv[:, h, :], ACT.Silu,
                                             bias=vec(c, f"conv_b{h}")).then_inc(S["u_ready"], 1)
                    for t in range(2):
                        act.wait_ge(S["xp_mm"], b * 2 + (t + 1))
                        nc.scalar.copy(bc[:, t * TILE:(t + 1) * TILE], in_ps[0:ROWS + RANK, t, :]).then_inc(S["bc_ready"], 1)
                    for i in range(4):
                        h, t = divmod(i, 2)
                        act.wait_ge(S["dt_mm"], b * 4 + (i + 1))
                        nc.scalar.activation(low[:, h, t * TILE:(t + 1) * TILE], in_ps[:, t, :], ACT.Identity,
                                             bias=vec(c, f"dt_b{h}")).then_inc(S["low_ready"], 1)
                    for h in range(2):
                        act.wait_ge(S["nab_ready"], b * 2 + (h + 1))
                        nc.scalar.activation(nab[:, h, :], nab[:, h, :], ACT.Exp).then_inc(S["exp_low"], 1)
                        act.wait_ge(S["exp_low"], b * 2 + (h + 1))
                        nc.scalar.activation(nab[:, h, :], nab[:, h, :], ACT.Ln,
                                             bias=one[:, 0:1]).then_inc(S["ln_done"], 1)
                    for j in range(STEPS):
                        h, n = divmod(j, NS)
                        if n == 0:
                            act.wait_ge(S["dt_ready"], b * 2 + (h + 1))
                        act.wait_ge(S["b_mm"], b * STEPS + (j + 1))
                        act.wait_ge(S["dbu_ready"], b * STEPS + (j + 1))
                        nc.scalar.copy(bsb[:, j % 2, :], b_ps[:, :, :].rearrange("p t n -> p (t n)")).then_inc(S["b_read"], 1)
                        act.wait_ge(S["scan_done"], b * STEPS + (j + 1))
                        nc.scalar.activation(da[:, j % 3, :], dt[:, h, :], ACT.Exp,
                                             scale=a[:, n, h:h + 1]).then_inc(S["da_ready"], 1)

            @block.gpsimd
            def _(pool):
                with pool.Fori(0, BATCH) as b:
                    for h in range(2):
                        pool.wait_ge(S["dt_ready"], b * 2 + (h + 1))
                        nc.gpsimd.tensor_tensor(dtu[:, h, :], dt[:, h, :], u[:, h, :], ALU.mult).then_inc(S["dtu_ready"], 1)
                    pool.wait_ge(S["dtu_ready"], b * 2 + 2)
                    for j in range(STEPS):
                        pool.wait_ge(S["b_read"], b * STEPS + (j + 2))
                        pool.wait_ge(S["scan_done"], b * STEPS + (j + 1))
                        nc.gpsimd.tensor_tensor(dbu[:, j % 3, :], dtu[:, j // NS, :], bsb[:, j % 2, :],
                                                ALU.mult).then_inc(S["dbu_ready"], 1)

            @block.vector
            def _(dve):
                tt, ts, stt = nc.vector.tensor_tensor, nc.vector.tensor_scalar, nc.vector.scalar_tensor_tensor
                nc.vector.memset(one[:, :], 1.0).then_inc(S["set"], 1)
                nc.vector.memset(raw[:, :, 0:TAPS - 1], 0.0).then_inc(S["set"], 1)
                dve.wait_ge(S["set"], 3)
                ts(a[:, :, :], a[:, :, :], -1.0, None, ALU.mult).then_inc(S["set"], 1)
                dve.wait_ge(S["loaded"], 16 * 6)
                with dve.Fori(0, BATCH) as b:
                    for h in range(2):
                        dve.wait_ge(S["in_read"], b * 8 + (2 * h + 2))
                        for k in range(TAPS):
                            w = vec(c, f"conv_w{k}{h}")
                            if k == 0:
                                last = ts(conv[:, h, :], raw[:, h, 0:SEQ], w, None, ALU.mult)
                            else:
                                dve.wait_ge(S["conv_step"], b * 2 * TAPS + (h * TAPS + k))
                                last = stt(conv[:, h, :], raw[:, h, k:k + SEQ], w, conv[:, h, :], ALU.mult, ALU.add)
                            last.then_inc(S["conv_step"], 1)
                    for h in range(2):
                        dve.wait_ge(S["low_ready"], b * 4 + (2 * h + 2))
                        stt(nab[:, h, :], low[:, h, :], -1.0, low[:, h, :], ALU.mult, ALU.min).then_inc(S["nab_ready"], 1)
                    split = Chain(dve, S["split_step"], 4, b)
                    split(nc.vector.tensor_copy(part[:, :], bc[0:ROWS, :]))
                    split(stt(rest[:, :], part[:, :], minus[:, 0:1], bc[0:ROWS, :], ALU.mult, ALU.add))
                    split(nc.vector.tensor_copy(part[:, :], rest[:, :]))
                    split(stt(bc3[:, :], part[:, :], minus[:, 1:2], rest[:, :], ALU.mult, ALU.add))
                    for h in range(2):
                        dve.wait_ge(S["ln_done"], b * 2 + (h + 1))
                        stt(dt[:, h, :], low[:, h, :], 0.0, nab[:, h, :], ALU.max, ALU.add).then_inc(S["dt_ready"], 1)
                    for j in range(STEPS):
                        h, n = divmod(j, NS)
                        dve.wait_ge(S["da_ready"], b * STEPS + (j + 1))
                        dve.wait_ge(S["dbu_ready"], b * STEPS + (j + 3))
                        dve.wait_ge(S["hc_ready"], b * STEPS + (j + 1))
                        nc.vector.tensor_tensor_scan(state[:, j % 2, :], da[:, j % 3, :], dbu[:, j % 3, :], 0.0,
                                                     ALU.mult, ALU.add).then_inc(S["scan_done"], 1)
                        dve.wait_ge(S["scan_done"], b * STEPS + (j + 4))
                        dve.wait_ge(S["c_mm"], b * STEPS + (j + 1))
                        dve.wait_ge(S["sum_mm"], b * STEPS + (j + 1))
                        tt(hc[:, j % 2, :], state[:, j % 2, :], c_ps[:, :, :].rearrange("p t n -> p (t n)"),
                           ALU.mult).then_inc(S["hc_ready"], 1)
                        if n == NS - 1:
                            dve.wait_ge(S["sum_mm"], b * STEPS + (j + 3))
                            stt(yz[:, h, :], u[:, h, :], vec(c, f"D{h}"), y_ps[:, :, :].rearrange("p t n -> p (t n)"),
                                ALU.mult, ALU.add).then_inc(S["yd_ready"], 1)
                            dve.wait_ge(S["yd_ready"], b * 2 + (h + 1))
                            tt(yz[:, h, :], yz[:, h, :], zs[:, h, :], ALU.mult).then_inc(S["yz_ready"], 1)
                    for t in range(2):
                        dve.wait_ge(S["o_mm"], b * 2 + (t + 1))
                        tile = bass.ts(b * 2 + t, TILE)
                        stt(c.x_t[:, tile], y_ps[:, t, :], c.mod[:, 0, GA, bass.ds(b * 2 + t, 1)], c.x_t[:, tile],
                            ALU.mult, ALU.add).then_inc(S["x_ready"], 1)


def layout_mamba(a, d, bf):
    d["ma_w_in"] = a["L0_attn_in_proj_w"].reshape(P, 4, P)
    w = a["L0_attn_x_proj_w"].reshape(2, P, -1).transpose(1, 0, 2)
    rank = P // 16
    bc = w[:, :, rank:]
    d["ma_w_x"] = np.concatenate([bc, bc, bc, w[:, :, :rank]], 2)
    d["ma_w_dt"] = np.concatenate([np.zeros((96, 2, P), np.float32),
                                   a["L0_attn_dt_proj_w"].reshape(rank, 2, P)])
    d["ma_w_out"] = a["L0_attn_out_proj_w"].reshape(2, P, P).transpose(1, 0, 2)
    rows = np.arange(96)
    pick = (rows[:, None] % 32 == np.arange(32)[None]).astype(bf)
    d["ma_pick"] = np.repeat(pick[:, :, None], P, 2)
    d["ma_minus"] = -np.stack([rows >= 32, rows >= 64], 1).astype(np.float32)


def stage_slots(c):
    nc, ins = c.nc, c.ins
    G = 16
    SLOTS = P // 2
    GROUPS = TOK // G
    GPT = P // G
    PAIRS = SLOTS // 2
    F = P // 2
    with ExitStack() as s:
        def sb(name, shape, dt=F32):
            return s.enter_context(nc.sbuf_tensor(f"f0_{name}", shape, dt))

        def sem(name):
            return s.enter_context(nc.semaphore(f"f0_{name}"))

        ctrl, tie, parity = sb("ctrl", [P, P]), sb("tie", [P, G]), sb("parity", [P, 2])
        quarter = sb("quarter", [P, P // 32])
        f1, f2, bias = sb("f1", [P, SLOTS, F]), sb("f2", [P, PAIRS, P]), sb("bias", [P, PAIRS])
        perm_t, top = sb("perm_t", [P, TOK]), sb("top", [P, GROUPS])
        sel = sb("sel", [P, GROUPS, SLOTS])
        loaded, weights = sem("loaded"), sem("weights")
        names = ("lg_mm", "lg_read", "perm_step", "p_turned", "x_turned", "p_ready", "xk_ready", "sel_mm",
                 "sel_even", "sel_odd", "up_mm", "inner_ready", "down_mm", "out_ready", "o_turned", "turned_even",
                 "turned_odd", "o_mm", "x_ready")
        S = {n: sem(n) for n in names}

        with ExitStack() as s1, nc.Block() as block:
            lg_ps = s1.enter_context(nc.psum_tensor("f0_lg_ps", [P, 2, TILE], F32))

            @block.sync
            def _(sp):
                for dst, name in ((ctrl, "ctrl"), (tie, "tie"), (parity, "parity"), (quarter, "quarter"), (bias, "bias")):
                    sp.dma_start(dst[:, :], ins[f"f0_{name}"]).then_inc(loaded, 16)
                sp.dma_start(f1[:, :, :], ins["f0_f1"]).then_inc(weights, 16)
                sp.dma_start(f2[:, :, :], ins["f0_f2"]).then_inc(weights, 16)

            @block.tensor
            def _(pe):
                pe.wait_ge(loaded, 16 * 5)
                for t in range(NT):
                    if t >= 2:
                        pe.wait_ge(S["lg_read"], t - 1)
                    nc.tensor.matmul(lg_ps[:, t % 2, :], ctrl[:, :], c.h_t[:, t * TILE:(t + 1) * TILE],
                                     start=True, stop=True).then_inc(S["lg_mm"], 1)

            @block.vector
            def _(dve):
                tt = nc.vector.tensor_tensor
                dve.wait_ge(loaded, 16 * 5)
                per = TILE // G
                for t in range(NT):
                    dve.wait_ge(S["lg_mm"], t + 1)
                    at = slice(t * TILE, (t + 1) * TILE)
                    view = perm_t[:, at].rearrange("p (g k) -> p g k", k=G)
                    tt(view, lg_ps[:, t % 2, :].rearrange("p (g k) -> p g k", k=G),
                       tie[:, :].unsqueeze(1).to_broadcast([P, per, G]), ALU.add).then_inc(S["lg_read"], 1)
                step = Chain(dve, S["perm_step"])
                dve.wait_ge(S["lg_read"], NT)
                groups = perm_t[:, :].rearrange("p (g k) -> p g k", k=G)
                step(nc.vector.reduce_max(top[:, :], groups, AX.X))
                step(tt(groups, groups, top[:, :].unsqueeze(2).to_broadcast([P, GROUPS, G]), ALU.is_equal))
                pairs = perm_t[:, :].rearrange("p (m r k) -> p m r k", r=2, k=G)
                for r in range(2):
                    nc.vector.tensor_scalar(pairs[:, :, r, :], pairs[:, :, r, :], parity[:, r:r + 1], None,
                                            ALU.mult).then_inc(S["perm_step"], 1)
                dve.wait_ge(S["perm_step"], 4)

        with ExitStack() as s2, nc.Block() as block:
            pt_ps, xt_ps, sel_ps = (s2.enter_context(nc.psum_tensor(f"f0_{n}", [P, 2, TILE], F32))
                                    for n in ("pt_ps", "xt_ps", "sel_ps"))
            perm = s2.enter_context(nc.sbuf_tensor("f0_perm", [P, 2, P // 32, P], F32))
            xk = s2.enter_context(nc.sbuf_tensor("f0_xk", [P, 2, P], F32))

            def copied(eng, k):
                eng.wait_ge(S["sel_odd" if k % 2 else "sel_even"], k // 2 + 1)

            def take(copy, k):
                copy(sel[:, k * GPT:(k + 1) * GPT, :].rearrange("p g e -> p (g e)"), sel_ps[:, k % 2, :]).then_inc(S["sel_odd" if k % 2 else "sel_even"], 1)

            @block.tensor
            def _(pe):
                def turn(k):
                    at = slice(k * P, (k + 1) * P)
                    if k >= 2:
                        pe.wait_ge(S["p_ready"], k - 1)
                        pe.wait_ge(S["xk_ready"], k - 1)
                    nc.tensor.transpose(pt_ps[:, k % 2, 0:P], perm_t[:, at], c.ident[:, :]).then_inc(S["p_turned"], 1)
                    nc.tensor.transpose(xt_ps[:, k % 2, 0:P], c.h_t[:, at], c.ident[:, :]).then_inc(S["x_turned"], 1)
                turn(0)
                for k in range(KT):
                    if k + 1 < KT:
                        turn(k + 1)
                    pe.wait_ge(S["p_ready"], k + 1)
                    pe.wait_ge(S["xk_ready"], k + 1)
                    if k >= 2:
                        copied(pe, k - 2)
                    nc.tensor.matmul(sel_ps[:, k % 2, :], xk[:, k % 2, :], perm[:, k % 2, :, :], start=True,
                                     stop=True).then_inc(S["sel_mm"], 1)

            @block.scalar
            def _(act):
                for k in range(KT):
                    act.wait_ge(S["x_turned"], k + 1)
                    if k >= 2:
                        act.wait_ge(S["sel_mm"], k - 1)
                    nc.scalar.copy(xk[:, k % 2, :], xt_ps[:, k % 2, 0:P]).then_inc(S["xk_ready"], 1)
                    if k % 2 == 1:
                        act.wait_ge(S["sel_mm"], k)
                        take(nc.scalar.copy, k - 1)

            @block.vector
            def _(dve):
                shape = [P, P // 32, P]
                for k in range(KT):
                    dve.wait_ge(S["p_turned"], k + 1)
                    if k >= 2:
                        dve.wait_ge(S["sel_mm"], k - 1)
                    nc.vector.tensor_tensor(perm[:, k % 2, :, :], pt_ps[:, k % 2, 0:P].unsqueeze(1).to_broadcast(shape),
                                            quarter[:, :].unsqueeze(2).to_broadcast(shape),
                                            ALU.mult).then_inc(S["p_ready"], 1)
                    if k % 2 == 0 and k:
                        dve.wait_ge(S["sel_mm"], k)
                        take(nc.vector.tensor_copy, k - 1)
                dve.wait_ge(S["sel_mm"], KT)
                take(nc.vector.tensor_copy, KT - 1)

        with ExitStack() as s3, nc.Block() as block:
            up_ps = s3.enter_context(nc.psum_tensor("f0_up_ps", [P, 2, TILE], F32))
            down_ps = s3.enter_context(nc.psum_tensor("f0_down_ps", [P, 2, 2, TILE], F32))
            inner = s3.enter_context(nc.sbuf_tensor("f0_inner", [P, 2, GROUPS], F32))

            @block.tensor
            def _(pe):
                def up(i):
                    if i >= 2:
                        pe.wait_ge(S["inner_ready"], i - 1)
                    for r in range(2):
                        mm = nc.tensor.matmul(up_ps[r * F:(r + 1) * F, i % 2, 0:GROUPS], f1[:, 2 * i + r, :],
                                              sel[:, :, 2 * i + r], start=True, stop=True)
                    mm.then_inc(S["up_mm"], 1)
                pe.wait_ge(weights, 32)
                up(0)
                for i in range(PAIRS):
                    if i + 1 < PAIRS:
                        up(i + 1)
                    pe.wait_ge(S["inner_ready"], i + 1)
                    if i >= 2:
                        pe.wait_ge(S["out_ready"], i - 1)
                    for r in range(2):
                        mm = nc.tensor.matmul(down_ps[:, i % 2, r, 0:GROUPS], f2[r * F:(r + 1) * F, i, :],
                                              inner[r * F:(r + 1) * F, i % 2, :], start=True, stop=True)
                    mm.then_inc(S["down_mm"], 1)

            @block.scalar
            def _(act):
                for i in range(PAIRS):
                    act.wait_ge(S["up_mm"], i + 1)
                    if i >= 2:
                        act.wait_ge(S["down_mm"], i - 1)
                    nc.scalar.activation(inner[:, i % 2, :], up_ps[:, i % 2, 0:GROUPS], ACT.Relu,
                                         bias=bias[:, i:i + 1]).then_inc(S["inner_ready"], 1)

            @block.vector
            def _(dve):
                for i in range(PAIRS):
                    dve.wait_ge(S["down_mm"], i + 1)
                    nc.vector.tensor_copy(sel[:, :, 2 * i:2 * i + 2].rearrange("p g r -> p r g"), down_ps[:, i % 2, :, 0:GROUPS]).then_inc(S["out_ready"], 1)

        with ExitStack() as s4, nc.Block() as block:
            tr_ps, o_ps = (s4.enter_context(nc.psum_tensor(f"f0_{n}", [P, 2, TILE], F32)) for n in ("tr_ps", "o_ps"))
            out_rows = s4.enter_context(nc.sbuf_tensor("f0_out_rows", [P, 2, TILE], F32))
            parts = P // 32

            def turned(k):
                return S["turned_odd" if k % 2 else "turned_even"]

            def take_rows(eng, copy, k):
                eng.wait_ge(S["o_turned"], k + 1)
                if k >= 2:
                    eng.wait_ge(S["o_mm"], k - 1)
                copy(out_rows[:, k % 2, :], tr_ps[:, k % 2, :]).then_inc(turned(k), 1)

            @block.tensor
            def _(pe):
                def turn(k):
                    if k >= 2:
                        pe.wait_ge(turned(k), k // 2)
                    for j in range(parts):
                        g = k * GPT + 2 * j
                        mm = nc.tensor.transpose(tr_ps[:, k % 2, j * P:(j + 1) * P],
                                                 sel[:, g:g + 2, :].rearrange("p g e -> p (g e)"), c.ident[:, :])
                    mm.then_inc(S["o_turned"], 1)
                turn(0)
                for k in range(KT):
                    if k + 1 < KT:
                        turn(k + 1)
                    t, q = divmod(k, TILE // P)
                    pe.wait_ge(turned(k), k // 2 + 1)
                    if q == 0 and t >= 2:
                        pe.wait_ge(S["x_ready"], t - 1)
                    for j in range(parts):
                        at = k * P + j * 32
                        mm = nc.tensor.matmul(o_ps[:, t % 2, q * P + j * 32:q * P + (j + 1) * 32],
                                              out_rows[:, k % 2, j * P:(j + 1) * P], perm_t[:, at:at + 32],
                                              start=True, stop=True)
                    mm.then_inc(S["o_mm"], 1)

            @block.scalar
            def _(act):
                for k in range(0, KT, 2):
                    take_rows(act, nc.scalar.copy, k)

            @block.vector
            def _(dve):
                for k in range(1, KT, 2):
                    take_rows(dve, nc.vector.tensor_copy, k)
                    t = k * P // TILE
                    if (k + 1) * P % TILE == 0:
                        dve.wait_ge(S["o_mm"], k + 1)
                        at = slice(t * TILE, (t + 1) * TILE)
                        nc.vector.scalar_tensor_tensor(c.x_t[:, at], o_ps[:, t % 2, :], c.mod[:, 0, GB, t:t + 1],
                                                       c.x_t[:, at], ALU.mult, ALU.add).then_inc(S["x_ready"], 1)


def layout_slots(a, d, bf):
    ctrl = a["L0_ffn_controller"].reshape(P, 64)
    d["f0_ctrl"] = np.concatenate([ctrl, ctrl], 1)
    d["f0_tie"] = np.tile(np.linspace(0.0, 1e-6, 16, dtype=np.float32), (P, 1))
    rows = np.arange(P)
    d["f0_parity"] = (rows[:, None] // 64 == np.arange(2)[None]).astype(np.float32)
    d["f0_quarter"] = (rows[:, None] // 32 == np.arange(4)[None]).astype(np.float32)
    d["f0_f1"] = a["L0_ffn_f1"].reshape(P, 64, 64)
    d["f0_f2"] = a["L0_ffn_f2"].reshape(32, P, P).transpose(1, 0, 2)
    d["f0_bias"] = a["L0_ffn_bias"].reshape(32, P).T


def build(nc, ins, out):
    with ExitStack() as ctx:
        c = Core(nc, ctx, ins)
        stage_setup(c)
        adaln(c, 0, SA, CA)
        stage_mamba(c)
        adaln(c, 0, SB, CB)
        stage_slots(c)
        adaln(c, 1, SA, CA)
        stage_head_attention(c)
        adaln(c, 1, SB, CB)
        stage_moe1(c)
        recycle_semaphores(c)
        adaln(c, 2, SA, CA)
        stage_linear_attention(c)
        adaln(c, 2, SB, CB)
        stage_moe2(c)
        adaln(c, 3, SA, CA)
        stage_window_attention(c)
        adaln(c, 3, SB, CB)
        stage_moe3(c)
        stage_store(c, out)


def rope_swap(v):
    return v.reshape(v.shape[:-1] + (P // 8, 2, 4))[..., ::-1, :].reshape(v.shape)


def vectors(a):
    v = {}
    bgu = a["L1_ffn_bgu"]
    for e in range(16):
        v[f"bg{e}"], v[f"bu{e}"] = bgu[e, ::2], bgu[e, 1::2]
    for h in range(2):
        half = slice(h * P, (h + 1) * P)
        for k in range(4):
            v[f"conv_w{k}{h}"] = a["L0_attn_conv_w"][half, k]
        v[f"conv_b{h}"] = a["L0_attn_conv_b"][half]
        v[f"dt_b{h}"] = a["L0_attn_dt_proj_b"][half]
        v[f"D{h}"] = a["L0_attn_D_param"][half]
        for n in range(16):
            v[f"A_log{n}{h}"] = a["L0_attn_A_log"][half, n]
    bup = a["L1_attn_bup"].reshape(16, 2, 8)
    bk, bv = bup[:, 0].reshape(P), bup[:, 1].reshape(P)
    v["L1_bq"], v["L1_bq_rot"] = a["L1_attn_bq"], rope_swap(a["L1_attn_bq"])
    v["L1_bk"], v["L1_bk_rot"], v["L1_bv"] = bk, rope_swap(bk), bv
    v["L1_bout"], v["L1_bdown"] = a["L1_attn_bout"], a["L1_attn_bdown"]
    for n in "qkvuo":
        v[f"L2_b{n}"] = a[f"L2_attn_b{n}"]
    v["L2_scale"] = a["L2_attn_scale"]
    for n in "qkvo":
        v[f"L3_b{n}"] = a[f"L3_attn_b{n}"]
    for n in "qk":
        v[f"L3_b{n}"] = v[f"L3_b{n}"].reshape(4, HG, HD).transpose(0, 2, 1).reshape(P)
    v["ln_g"], v["ln_b"] = a["L3_ffn_ln_g"], a["L3_ffn_ln_b"]
    table = np.zeros((P, len(VECS)), np.float32)
    for k, name in enumerate(VECS):
        table[:len(v[name]), k] = v[name]
    return table


def layouts(inputs):
    a = {k: np.ascontiguousarray(np.asarray(v)) for k, v in inputs.items()}
    bf = mybir.dt.np(BF16)
    d = {}
    d["x_t"] = a["L0_attn_x"].reshape(TOK, P).T
    d["mean_w"] = np.full((P, P), 1.0 / P, np.float32)
    d["ident"] = np.eye(P, dtype=np.float32)
    d["ident_bf"] = np.eye(P).astype(bf)
    for l in range(LAYERS):
        d[f"L{l}_c_t"] = a[f"L{l}_c"].T
        d[f"L{l}_wmod"] = a[f"L{l}_wmod"]
    d["upper_bf"] = np.triu(np.ones((P, P))).astype(bf)
    d["ones_bf"] = np.ones((P, P)).astype(bf)
    d["vecs"] = vectors(a)
    layout_moe2(a, d, bf)
    layout_moe1(a, d, bf)
    layout_moe3(a, d, bf)
    layout_head_attention(a, d, bf)
    layout_linear_attention(a, d, bf)
    layout_window_attention(a, d, bf)
    layout_mamba(a, d, bf)
    layout_slots(a, d, bf)
    return {k: np.ascontiguousarray(v) for k, v in d.items()}


def kernel(**inputs):
    import concourse.bacc as bacc
    from concourse.bass_utils import run_bass_kernel_spmd
    nc = bacc.Bacc("TRN2", target_bir_lowering=False, num_devices=1)
    arrays = {f"in_{k}": v for k, v in layouts(inputs).items()}
    ins = {k[3:]: nc.dram_tensor(k, v.shape, mybir.dt.from_np(v.dtype), kind="ExternalInput").ap()
           for k, v in arrays.items()}
    out = nc.dram_tensor("out_t", (P, TOK), F32, kind="ExternalOutput").ap()
    build(nc, ins, out)
    r = run_bass_kernel_spmd(nc, [arrays], core_ids=[0])
    return np.ascontiguousarray(r.results[0]["out_t"].T).reshape(BATCH, SEQ, P)
```

```python
from contextlib import ExitStack

import concourse.bass as bass
from concourse import mybir
from concourse.alu_op_type import AluOpType as ALU
import numpy as np

F32 = mybir.dt.float32
BF16 = mybir.dt.bfloat16
U32 = mybir.dt.uint32
I32 = mybir.dt.int32
ACT = mybir.ActivationFunctionType
AX = mybir.AxisListType

P = 128
BATCH = 4
SEQ = 1024
TOK = BATCH * SEQ
TILE = 512
NT = TOK // TILE
TPB = SEQ // TILE
KT = TOK // P
LAYERS = 4
LN_EPS = 1e-5
LN_EXP_SET = "natural_log_exp_and_others"
SA, CA, GA, SB, CB, GB = range(6)


VECS = ([f"bg{e}" for e in range(16)] + [f"bu{e}" for e in range(16)]
        + [f"conv_w{k}{h}" for k in range(4) for h in range(2)]
        + [f"{n}{h}" for n in ("conv_b", "dt_b", "D") for h in range(2)]
        + [f"A_log{s}{h}" for s in range(16) for h in range(2)]
        + ["L1_bq", "L1_bq_rot", "L1_bk", "L1_bk_rot", "L1_bv", "L1_bout", "L1_bdown"]
        + ["L2_bq", "L2_bk", "L2_bv", "L2_bu", "L2_bo", "L2_scale"]
        + ["L3_bq", "L3_bk", "L3_bv", "L3_bo", "ln_g", "ln_b"])


class Core:

    def __init__(self, nc, ctx, ins):
        self.nc, self.ins = nc, ins
        self.ctx = ctx
        self.ln_calls = 0

        def sb(name, shape, dt=F32):
            return ctx.enter_context(nc.sbuf_tensor(name, shape, dt))

        self.x_t = sb("x_t", [P, TOK])
        self.h_t = sb("h_t", [P, TOK])
        self.mod = sb("mod", [P, LAYERS, 6, NT])
        self.mean_w = sb("mean_w", [P, P])
        self.ident = sb("ident", [P, P])
        self.ident_bf = sb("ident_bf", [P, P], BF16)
        self.vecs = sb("vecs", [P, len(VECS)])
        self.ln = {n: ctx.enter_context(nc.semaphore("ln_" + n))
                   for n in ("mean", "cent", "sq", "var", "logv", "rstd", "xn", "h")}


def vec(c, name):
    k = VECS.index(name)
    return c.vecs[:, k:k + 1]


def stage_setup(c):
    nc, ins = c.nc, c.ins
    with ExitStack() as s:
        wmod = s.enter_context(nc.sbuf_tensor("wmod", [P, LAYERS, 6 * P], F32))
        cond = s.enter_context(nc.sbuf_tensor("cond", [P, LAYERS, BATCH], F32))
        cond_silu = s.enter_context(nc.sbuf_tensor("cond_silu", [P, LAYERS, BATCH], F32))
        raw = s.enter_context(nc.sbuf_tensor("mod_raw", [P, LAYERS, 6, BATCH], F32))
        sign = s.enter_context(nc.sbuf_tensor("gate_sign", [P, LAYERS, 2, BATCH], F32))
        size = s.enter_context(nc.sbuf_tensor("gate_size", [P, LAYERS, 2, BATCH], F32))
        ps = s.enter_context(nc.psum_tensor("mod_ps", [P, LAYERS, 6, BATCH], F32))
        loaded = s.enter_context(nc.semaphore("setup_loaded"))
        silu_done = s.enter_context(nc.semaphore("setup_silu"))
        mod_done = s.enter_context(nc.semaphore("setup_mod"))
        step = s.enter_context(nc.semaphore("setup_step"))
        with nc.Block() as block:
            @block.sync
            def _(sp):
                sp.dma_start(c.x_t[:, :], ins["x_t"]).then_inc(loaded, 16)
                sp.dma_start(c.mean_w[:, :], ins["mean_w"]).then_inc(loaded, 16)
                sp.dma_start(c.ident[:, :], ins["ident"]).then_inc(loaded, 16)
                sp.dma_start(c.ident_bf[:, :], ins["ident_bf"]).then_inc(loaded, 16)
                sp.dma_start(c.vecs[:, :], ins["vecs"]).then_inc(loaded, 16)
                for l in range(LAYERS):
                    sp.dma_start(cond[:, l, :], ins[f"L{l}_c_t"]).then_inc(loaded, 16)
                    sp.dma_start(wmod[:, l, :], ins[f"L{l}_wmod"]).then_inc(loaded, 16)

            @block.scalar
            def _(act):
                act.wait_ge(loaded, 16 * (5 + 2 * LAYERS))
                nc.scalar.activation(cond_silu[:, :, :], cond[:, :, :], ACT.Silu).then_inc(silu_done, 1)

            @block.tensor
            def _(pe):
                pe.wait_ge(loaded, 16 * (5 + 2 * LAYERS))
                pe.wait_ge(silu_done, 1)
                for l in range(LAYERS):
                    for k in range(6):
                        mm = nc.tensor.matmul(ps[:, l, k, :], wmod[:, l, k * P:(k + 1) * P], cond_silu[:, l, :],
                                              start=True, stop=True)
                mm.then_inc(mod_done, 1)

            @block.vector
            def _(dve):
                dve.wait_ge(mod_done, 1)
                nc.vector.tensor_copy(raw[:, :, :, :], ps[:, :, :, :]).then_inc(step, 1)
                dve.wait_ge(step, 1)
                for n, k in enumerate((CA, CB)):
                    nc.vector.tensor_scalar(raw[:, :, k, :], raw[:, :, k, :], 1.0, None, ALU.add).then_inc(step, 1)
                for n, k in enumerate((GA, GB)):
                    nc.vector.tensor_scalar(sign[:, :, n, :], raw[:, :, k, :], 0.0, 2.0, ALU.is_ge,
                                            ALU.mult).then_inc(step, 1)
                dve.wait_ge(step, 5)
                for n, k in enumerate((GA, GB)):
                    nc.vector.scalar_tensor_tensor(size[:, :, n, :], sign[:, :, n, :], -1.0, raw[:, :, k, :],
                                                   ALU.add, ALU.mult).then_inc(step, 1)
                dve.wait_ge(step, 7)
                for n in range(2):
                    nc.vector.tensor_scalar(size[:, :, n, :], size[:, :, n, :], 0.25, None,
                                            ALU.max).then_inc(step, 1)
                dve.wait_ge(step, 9)
                for n, k in enumerate((GA, GB)):
                    nc.vector.scalar_tensor_tensor(raw[:, :, k, :], sign[:, :, n, :], -1.0, size[:, :, n, :],
                                                   ALU.add, ALU.mult).then_inc(step, 1)
                dve.wait_ge(step, 11)
                for l in range(LAYERS):
                    nc.vector.tensor_copy(
                        c.mod[:, l, :, :].rearrange("p k (b u) -> p k b u", u=TPB),
                        raw[:, l, :, :].unsqueeze(3).to_broadcast([P, 6, BATCH, TPB])).then_inc(step, 1)
                dve.wait_ge(step, 11 + LAYERS)


def stage_norm(c, src, dst, scale, shift):
    nc, base, call = c.nc, c.ln_calls * NT, c.ln_calls
    c.ln_calls += 1
    ln = c.ln
    with ExitStack() as s:
        xc = s.enter_context(nc.sbuf_tensor(f"ln_xc{call}", [P, 2, TILE], F32))
        sq = s.enter_context(nc.sbuf_tensor(f"ln_sq{call}", [P, 2, TILE], F32))
        lv = s.enter_context(nc.sbuf_tensor(f"ln_lv{call}", [P, 2, TILE], F32))
        eps = s.enter_context(nc.sbuf_tensor(f"ln_eps{call}", [P, 1], F32))
        mean_ps = s.enter_context(nc.psum_tensor(f"ln_mean_ps{call}", [P, 2, TILE], F32))
        var_ps = s.enter_context(nc.psum_tensor(f"ln_var_ps{call}", [P, 2, TILE], F32))
        eps_set = s.enter_context(nc.semaphore(f"ln_eps_set{call}"))
        with nc.Block() as block:
            @block.tensor
            def _(pe):
                with pe.Fori(0, NT // 2) as i:
                    for u in range(2):
                        nc.tensor.matmul(mean_ps[:, u, :], c.mean_w[:, :], src[:, bass.ts(i * 2 + u, TILE)],
                                         start=True, stop=True).then_inc(ln["mean"], 1)
                    for u in range(2):
                        pe.wait_ge(ln["sq"], i * 2 + (base + u + 1))
                        nc.tensor.matmul(var_ps[:, u, :], c.mean_w[:, :], sq[:, u, :],
                                         start=True, stop=True).then_inc(ln["var"], 1)

            @block.scalar
            def _(act):
                nc.scalar.preload_act_table_set(LN_EXP_SET)
                act.wait_ge(eps_set, 1)
                with act.Fori(0, NT // 2) as i:
                    for u in range(2):
                        act.wait_ge(ln["cent"], i * 2 + (base + u + 1))
                        nc.scalar.activation(sq[:, u, :], xc[:, u, :], ACT.Square).then_inc(ln["sq"], 1)
                    for u in range(2):
                        act.wait_ge(ln["var"], i * 2 + (base + u + 1))
                        nc.scalar.activation(lv[:, u, :], var_ps[:, u, :], ACT.Ln,
                                             bias=eps[:, 0:1]).then_inc(ln["logv"], 1)
                        act.wait_ge(ln["logv"], i * 2 + (base + u + 1))
                        nc.scalar.activation(lv[:, u, :], lv[:, u, :], ACT.Exp, scale=-0.5).then_inc(ln["rstd"], 1)

            @block.vector
            def _(dve):
                nc.vector.memset(eps[:, :], LN_EPS).then_inc(eps_set, 1)
                with dve.Fori(0, NT // 2) as i:
                    for u in range(2):
                        dve.wait_ge(ln["mean"], i * 2 + (base + u + 1))
                        nc.vector.tensor_tensor(xc[:, u, :], src[:, bass.ts(i * 2 + u, TILE)], mean_ps[:, u, :],
                                                ALU.subtract).then_inc(ln["cent"], 1)
                    for u in range(2):
                        dve.wait_ge(ln["rstd"], i * 2 + (base + u + 1))
                        nc.vector.tensor_tensor(xc[:, u, :], xc[:, u, :], lv[:, u, :],
                                                ALU.mult).then_inc(ln["xn"], 1)
                        dve.wait_ge(ln["xn"], i * 2 + (base + u + 1))
                        nc.vector.tensor_scalar(dst[:, bass.ts(i * 2 + u, TILE)], xc[:, u, :],
                                                scale(i * 2 + u), shift(i * 2 + u), ALU.mult,
                                                ALU.add).then_inc(ln["h"], 1)
                    dve.wait_ge(ln["h"], i * 2 + (base + 2))


def adaln(c, layer, k_shift, k_scale):
    stage_norm(c, c.x_t, c.h_t,
               lambda t: c.mod[:, layer, k_scale, bass.ds(t, 1)],
               lambda t: c.mod[:, layer, k_shift, bass.ds(t, 1)])


def recycle_semaphores(c):
    nc = c.nc
    given_back = sorted(nc.released_uncleared_semaphores)
    with nc.Block() as block:
        @block.gpsimd
        def _(pool):
            first = 0
            for k in range(1, len(given_back) + 1):
                if k == len(given_back) or given_back[k] != given_back[k - 1] + 1:
                    pool.sem_clear(range(given_back[first], given_back[k - 1] + 1))
                    first = k


def stage_store(c, out):
    nc = c.nc
    with ExitStack() as s:
        stored = s.enter_context(nc.semaphore("stored"))
        with nc.Block() as block:
            @block.sync
            def _(sp):
                sp.dma_start(out, c.x_t[:, :]).then_inc(stored, 16)
                sp.wait_ge(stored, 16)


LAG = 2
BUFS = LAG + 1


def stage_router(c, tag, experts, cw3, logits_bias=False, capacity=None, slots=None):
    nc, ins = c.nc, c.ins
    E = experts
    small = [P, KT]
    full = [P, KT, E]
    with ExitStack() as s:
        def sb(name, shape, dt=F32):
            return s.enter_context(nc.sbuf_tensor(f"{tag}_{name}", shape, dt))

        def sem(name):
            return s.enter_context(nc.semaphore(f"{tag}_{name}"))

        wr = sb("wr", [P, E])
        rank = sb("rank", full)
        lb = sb("lb", full)
        lg = sb("lg", full)
        eq = sb("eq", full)
        hot = [sb("hot0", full), sb("hot1", full)]
        tmp = sb("tmp", full)
        tmp2 = sb("tmp2", full)
        mx = [sb("mx0", small), sb("mx1", small)]
        mr = sb("mr", small)
        gate = [sb("gate0", small), sb("gate1", small)]
        ex = sb("ex", small)
        cw = sb("cw", full)
        parts = sb("parts", [P, KT, 3, E], BF16)
        lg_ps = s.enter_context(nc.psum_tensor(f"{tag}_lg_ps", full, F32))
        tr_ps = s.enter_context(nc.psum_tensor(f"{tag}_tr_ps", [3 * E, KT, P], BF16))
        loaded, logits, step, ex_ready, ex_done, parts_done, turned = (
            sem(n) for n in ("loaded", "logits", "step", "ex_ready", "ex_done", "parts_done", "turned"))
        if capacity:
            hots = sb("hots", [P, 2, KT, E], BF16)
            upper = sb("upper", [P, P], BF16)
            ones = sb("ones", [P, P], BF16)
            tot = sb("tot", [P, 2 * KT, E])
            cum = sb("cum", [P, E, 2 * KT])
            pos = sb("pos", [P, 2, KT, E])
            zero = sb("zero", [P, 2 * KT])
            pre_ps = s.enter_context(nc.psum_tensor(f"{tag}_pre_ps", [P, 2, KT, E], F32))
            tot_ps = s.enter_context(nc.psum_tensor(f"{tag}_tot_ps", [P, 2 * KT, E], F32))
            hots_done, counted = sem("hots_done"), sem("counted")
        loads = 2 + bool(logits_bias) + 2 * bool(capacity)
        with nc.Block() as block:
            @block.sync
            def _(sp):
                sp.dma_start(wr[:, :], ins[f"{tag}_wr"]).then_inc(loaded, 16)
                sp.dma_start(rank[:, :, :].rearrange("p k e -> p (k e)"), ins[f"{tag}_rank"]).then_inc(loaded, 16)
                if logits_bias:
                    sp.dma_start(lb[:, :, :].rearrange("p k e -> p (k e)"), ins[f"{tag}_lb"]).then_inc(loaded, 16)
                if capacity:
                    sp.dma_start(upper[:, :], ins["upper_bf"]).then_inc(loaded, 16)
                    sp.dma_start(ones[:, :], ins["ones_bf"]).then_inc(loaded, 16)

            @block.tensor
            def _(pe):
                pe.wait_ge(loaded, 16 * loads)
                for k in range(KT):
                    mm = nc.tensor.matmul(lg_ps[:, k, :], c.h_t[:, k * P:(k + 1) * P], wr[:, :],
                                          start=True, stop=True)
                mm.then_inc(logits, 1)
                if capacity:
                    pe.wait_ge(hots_done, 2)
                    flat = hots[:, :, :, :].rearrange("p s k e -> p (s k e)")
                    nc.tensor.matmul(pre_ps[:, :, :, :].rearrange("p s k e -> p (s k e)"), upper[:, :], flat,
                                     start=True, stop=True).then_inc(counted, 1)
                    nc.tensor.matmul(tot_ps[:, :, :].rearrange("p k e -> p (k e)"), ones[:, :], flat,
                                     start=True, stop=True).then_inc(counted, 1)
                    return
                pe.wait_ge(parts_done, 3)
                for k in range(KT):
                    mm = nc.tensor.transpose(tr_ps[:, k, :], parts[:, k, :, :].rearrange("p a e -> p (a e)"),
                                             c.ident_bf[:, :])
                mm.then_inc(turned, 1)

            @block.scalar
            def _(act):
                act.wait_ge(ex_ready, 1)
                nc.scalar.activation(ex[:, :], ex[:, :], ACT.Exp).then_inc(ex_done, 1)
                if capacity:
                    return
                act.wait_ge(turned, 1)
                half = KT // 2
                nc.scalar.copy(cw3[:, 0:half * P], tr_ps[:, 0:half, :].rearrange("p k t -> p (k t)"))

            @block.vector
            def _(dve):
                n = [0]

                def done(ins_):
                    n[0] += 1
                    ins_.then_inc(step, 1)
                    dve.wait_ge(step, n[0])

                def wide(a):
                    return a[:, :].unsqueeze(2).to_broadcast(full)

                tt, ts = nc.vector.tensor_tensor, nc.vector.tensor_scalar
                dve.wait_ge(loaded, 16 * loads)
                dve.wait_ge(logits, 1)
                if logits_bias:
                    done(tt(lg[:, :, :], lg_ps[:, :, :], lb[:, :, :], ALU.add))
                else:
                    done(nc.vector.tensor_copy(lg[:, :, :], lg_ps[:, :, :]))
                for k in range(2):
                    done(nc.vector.reduce_max(mx[k][:, :], lg[:, :, :], AX.X))
                    done(tt(eq[:, :, :], lg[:, :, :], wide(mx[k]), ALU.is_ge))
                    done(tt(eq[:, :, :], eq[:, :, :], rank[:, :, :], ALU.mult))
                    done(nc.vector.reduce_max(mr[:, :], eq[:, :, :], AX.X))
                    done(tt(hot[k][:, :, :], eq[:, :, :], wide(mr), ALU.is_equal))
                    if k == 0:
                        done(nc.vector.scalar_tensor_tensor(lg[:, :, :], hot[0][:, :, :], -3e38, lg[:, :, :],
                                                            ALU.mult, ALU.add))
                tt(ex[:, :], mx[1][:, :], mx[0][:, :], ALU.subtract).then_inc(ex_ready, 1)
                dve.wait_ge(ex_done, 1)
                done(ts(gate[1][:, :], ex[:, :], 1.0, None, ALU.add))
                done(nc.vector.reciprocal(gate[0][:, :], gate[1][:, :]))
                done(tt(gate[1][:, :], gate[0][:, :], ex[:, :], ALU.mult))
                if capacity:
                    for k in range(2):
                        nc.vector.tensor_copy(hots[:, k, :, :], hot[k][:, :, :]).then_inc(hots_done, 1)
                    done(nc.vector.memset(zero[:, :], 0.0))
                    dve.wait_ge(counted, 2)
                    done(nc.vector.tensor_copy(tot[:, :, :], tot_ps[:, :, :]))
                    for e in range(E):
                        done(nc.vector.tensor_tensor_scan(cum[:, e, :], tot[:, :, e], zero[:, :], 0.0,
                                                          ALU.add, ALU.add))
                    done(tt(tot[:, :, :], cum[:, :, :].rearrange("p e k -> p k e"), tot[:, :, :], ALU.subtract))
                    flat = pos[:, :, :, :].rearrange("p s k e -> p (s k) e")
                    done(tt(flat, pre_ps[:, :, :, :].rearrange("p s k e -> p (s k) e"), tot[:, :, :], ALU.add))
                    for k in range(2):
                        done(ts(tmp[:, :, :], pos[:, k, :, :], float(capacity), None, ALU.is_le))
                        done(tt(hot[k][:, :, :], hot[k][:, :, :], tmp[:, :, :], ALU.mult))
                    index, gates, per = slots
                    for k in range(2):
                        done(ts(tmp[:, :, :], rank[:, :, :], float(-per), -1.0, ALU.mult, ALU.add))
                        done(tt(tmp[:, :, :], tmp[:, :, :], pos[:, k, :, :], ALU.add))
                        done(tt(tmp[:, :, :], tmp[:, :, :], hot[k][:, :, :], ALU.mult))
                        done(nc.vector.reduce_sum(mr[:, :], tmp[:, :, :], AX.X))
                        done(ts(mr[:, :], mr[:, :], float(E * per), None, ALU.add))
                        done(nc.vector.tensor_copy(index[:, k, :], mr[:, :]))
                        done(nc.vector.tensor_copy(gates[:, k, :], gate[k][:, :]))
                    return
                done(tt(tmp[:, :, :], hot[0][:, :, :], wide(gate[0]), ALU.mult))
                done(tt(tmp2[:, :, :], hot[1][:, :, :], wide(gate[1]), ALU.mult))
                done(tt(cw[:, :, :], tmp[:, :, :], tmp2[:, :, :], ALU.add))
                rest = [cw, tmp, tmp2]
                for k in range(3):
                    nc.vector.tensor_copy(parts[:, :, k, :], rest[k][:, :, :]).then_inc(parts_done, 1)
                    if k < 2:
                        dve.wait_ge(parts_done, k + 1)
                        done(tt(rest[k + 1][:, :, :], rest[k][:, :, :], parts[:, :, k, :], ALU.subtract))
                dve.wait_ge(turned, 1)
                half = KT // 2
                nc.vector.tensor_copy(cw3[:, half * P:], tr_ps[:, half:, :].rearrange("p k t -> p (k t)"))


def stage_moe2(c):
    nc, ins, E, F = c.nc, c.ins, 8, 4
    S = E * F
    with ExitStack() as s:
        def sb(name, shape, dt=F32):
            return s.enter_context(nc.sbuf_tensor(f"m2_{name}", shape, dt))

        def sem(name):
            return s.enter_context(nc.semaphore(f"m2_{name}"))

        cw3 = sb("cw3", [3 * E, TOK], BF16)
        stage_router(c, "r2", E, cw3)
        w1 = sb("w1", [P, E, F, P])
        w2 = sb("w2", [P, E, F, P])
        pick = sb("pick", [3 * E, E, P], BF16)
        g = sb("g", [P, BUFS, TILE])
        gc = sb("gc", [P, BUFS, TILE])
        h_ps = s.enter_context(nc.psum_tensor("m2_h_ps", [P, BUFS, TILE], F32))
        cw_ps = s.enter_context(nc.psum_tensor("m2_cw_ps", [P, 2, TILE], F32))
        o_ps = s.enter_context(nc.psum_tensor("m2_o_ps", [P, 2, TILE], F32))
        loaded, h_ready, g_ready, gc_ready, cw_ready, o_ready, o_free = (
            sem(n) for n in ("loaded", "h_ready", "g_ready", "gc_ready", "cw_ready", "o_ready", "o_free"))
        with nc.Block() as block:
            @block.sync
            def _(sp):
                sp.dma_start(pick[:, :, :], ins["m2_pick"]).then_inc(loaded, 16)
                sp.dma_start(w1[:, :, :, :], ins["m2_w1"]).then_inc(loaded, 16)
                sp.dma_start(w2[:, :, :, :], ins["m2_w2"]).then_inc(loaded, 16)

            @block.tensor
            def _(pe):
                pe.wait_ge(loaded, 48)
                pe.sem_inc(o_free, 1)
                with pe.Fori(0, NT) as t:
                    tile = bass.ts(t, TILE)

                    def down(k):
                        pe.wait_ge(gc_ready, t * S + (k + 1))
                        return nc.tensor.matmul(o_ps[:, 0, :], w2[:, k // F, k % F, :], gc[:, k % BUFS, :],
                                                start=(k == 0), stop=(k == S - 1))
                    for k in range(S):
                        e, f = divmod(k, F)
                        if f == 0:
                            nc.tensor.matmul(cw_ps[:, e % 2, :], pick[:, e, :], cw3[:, tile], start=True,
                                             stop=True).then_inc(cw_ready, 1)
                        nc.tensor.matmul(h_ps[:, k % BUFS, :], w1[:, e, f, :], c.h_t[:, tile], start=True,
                                         stop=True).then_inc(h_ready, 1)
                        if k == LAG:
                            pe.wait_ge(o_free, t + 1)
                        if k >= LAG:
                            down(k - LAG)
                    for k in range(S - LAG, S):
                        mm = down(k)
                    mm.then_inc(o_ready, 1)

            @block.scalar
            def _(act):
                nc.scalar.preload_act_table(ACT.Gelu)
                with act.Fori(0, NT) as t:
                    for k in range(S):
                        act.wait_ge(h_ready, t * S + (k + 1))
                        nc.scalar.activation(g[:, k % BUFS, :], h_ps[:, k % BUFS, :], ACT.Gelu).then_inc(g_ready, 1)

            @block.vector
            def _(dve):
                with dve.Fori(0, NT) as t:
                    for k in range(S):
                        e, f = divmod(k, F)
                        if f == 0:
                            dve.wait_ge(cw_ready, t * E + (e + 1))
                        dve.wait_ge(g_ready, t * S + (k + 1))
                        m = nc.vector.tensor_tensor(gc[:, k % BUFS, :], g[:, k % BUFS, :], cw_ps[:, e % 2, :], ALU.mult)
                        m.then_inc(gc_ready, 1)
                    dve.wait_ge(o_ready, t + 1)
                    tile = bass.ts(t, TILE)
                    nc.vector.scalar_tensor_tensor(c.x_t[:, tile], o_ps[:, 0, :], c.mod[:, 2, GB, bass.ds(t, 1)],
                                                   c.x_t[:, tile], ALU.mult, ALU.add).then_inc(o_free, 1)


def layout_moe2(a, d, bf):
    d["r2_wr"] = a["L2_ffn_gate_w"]
    d["r2_rank"] = rank_const(8)
    d["m2_w1"] = a["L2_ffn_w1"].reshape(8, P, 4, P).transpose(1, 0, 2, 3)
    d["m2_w2"] = a["L2_ffn_w2"].reshape(8, 4, P, P).transpose(2, 0, 1, 3)
    d["m2_pick"] = pick_const(8, bf)


def rank_const(experts):
    return np.tile((experts - np.arange(experts, dtype=np.float32)), (P, KT)).astype(np.float32)


def pick_const(experts, bf):
    return np.tile(np.eye(experts)[:, :, None], (3, 1, P)).astype(bf)


LIMIT, ALPHA = 7.0, 1.702


def stage_moe1(c):
    nc, ins, S = c.nc, c.ins, 16
    with ExitStack() as s:
        def sb(name, shape, dt=F32):
            return s.enter_context(nc.sbuf_tensor(f"m1_{name}", shape, dt))

        def psum(name, bufs):
            return s.enter_context(nc.psum_tensor(f"m1_{name}", [P, bufs, TILE], F32))

        def sem(name):
            return s.enter_context(nc.semaphore(f"m1_{name}"))

        cw3 = sb("cw3", [3 * S, TOK], BF16)
        stage_router(c, "r1", S, cw3, logits_bias=True)
        wg, wu, wd = sb("wg", [P, S, P]), sb("wu", [P, S, P]), sb("wd", [P, S, P])
        bd3 = sb("bd3", [3 * S, P])
        cwf = sb("cwf", [3 * S, TILE])
        bu1 = sb("bu1", [P, S])
        pick = sb("pick", [3 * S, S, P], BF16)
        g, u, sg, gs, v, gc = (sb(n, [P, BUFS, TILE]) for n in ("g", "u", "sg", "gs", "v", "gc"))
        gate_ps, up_ps, cw_ps, o_ps = psum("gate_ps", 2), psum("up_ps", 2), psum("cw_ps", 2), psum("o_ps", 1)
        (loaded, bu1_set, gate_ready, up_ready, gu_free, cw_ready, g_ready, sg_ready, gs_ready, v_ready, gc_ready,
         cwf_ready, o_ready, o_free) = (
            sem(n) for n in ("loaded", "bu1_set", "gate_ready", "up_ready", "gu_free", "cw_ready", "g_ready",
                             "sg_ready", "gs_ready", "v_ready", "gc_ready", "cwf_ready", "o_ready", "o_free"))
        with nc.Block() as block:
            @block.sync
            def _(sp):
                for dst, name in ((wg, "m1_wg"), (wu, "m1_wu"), (wd, "m1_wd"), (pick, "m1_pick")):
                    sp.dma_start(dst[:, :, :], ins[name]).then_inc(loaded, 16)
                sp.dma_start(bd3[:, :], ins["m1_bd3"]).then_inc(loaded, 16)

            @block.tensor
            def _(pe):
                pe.wait_ge(loaded, 16 * 5)
                pe.sem_inc(gu_free, 2)
                pe.sem_inc(o_free, 1)
                with pe.Fori(0, NT) as t:
                    tile = bass.ts(t, TILE)

                    def down(k):
                        if k == 0:
                            pe.wait_ge(o_free, t + 1)
                            pe.wait_ge(cwf_ready, t + 1)
                            nc.tensor.matmul(o_ps[:, 0, :], bd3[:, :], cwf[:, :], start=True, stop=False)
                        pe.wait_ge(gc_ready, t * S + (k + 1))
                        return nc.tensor.matmul(o_ps[:, 0, :], wd[:, k, :], gc[:, k % BUFS, :], start=False,
                                                stop=(k == S - 1))
                    for k in range(S):
                        pe.wait_ge(gu_free, t * S + (k + 1))
                        nc.tensor.matmul(gate_ps[:, k % 2, :], wg[:, k, :], c.h_t[:, tile], start=True,
                                         stop=True).then_inc(gate_ready, 1)
                        nc.tensor.matmul(up_ps[:, k % 2, :], wu[:, k, :], c.h_t[:, tile], start=True,
                                         stop=True).then_inc(up_ready, 1)
                        if k >= LAG:
                            down(k - LAG)
                        nc.tensor.matmul(cw_ps[:, k % 2, :], pick[:, k, :], cw3[:, tile], start=True,
                                         stop=True).then_inc(cw_ready, 1)
                    for k in range(S - LAG, S):
                        mm = down(k)
                    mm.then_inc(o_ready, 1)

            @block.scalar
            def _(act):
                nc.scalar.preload_act_table(ACT.Sigmoid)
                with act.Fori(0, NT) as t:
                    for k in range(S):
                        act.wait_ge(g_ready, t * S + (k + 1))
                        nc.scalar.activation(sg[:, k % BUFS, :], g[:, k % BUFS, :], ACT.Sigmoid,
                                             scale=ALPHA).then_inc(sg_ready, 1)

            @block.gpsimd
            def _(pool):
                with pool.Fori(0, NT) as t:
                    nc.gpsimd.tensor_copy(cwf[:, :], cw3[:, bass.ts(t, TILE)]).then_inc(cwf_ready, 1)
                    for k in range(S):
                        b = k % BUFS
                        pool.wait_ge(sg_ready, t * S + (k + 1))
                        nc.gpsimd.tensor_tensor(gs[:, b, :], g[:, b, :], sg[:, b, :], ALU.mult).then_inc(gs_ready, 1)

            @block.vector
            def _(dve):
                first = VECS.index("bu0")
                nc.vector.tensor_scalar(bu1[:, :], c.vecs[:, first:first + S], 1.0, None, ALU.add).then_inc(bu1_set, 1)
                dve.wait_ge(bu1_set, 1)
                with dve.Fori(0, NT) as t:
                    tile = bass.ts(t, TILE)

                    def finish(k):
                        b = k % BUFS
                        dve.wait_ge(gs_ready, t * S + (k + 1))
                        dve.wait_ge(gu_free, t * S + (k + 3))
                        nc.vector.scalar_tensor_tensor(v[:, b, :], u[:, b, :], 1.0 - LIMIT, gs[:, b, :], ALU.max,
                                                       ALU.mult).then_inc(v_ready, 1)
                        dve.wait_ge(v_ready, t * S + (k + 1))
                        dve.wait_ge(cw_ready, t * S + (k + 1))
                        nc.vector.tensor_tensor(gc[:, b, :], v[:, b, :], cw_ps[:, k % 2, :],
                                                ALU.mult).then_inc(gc_ready, 1)
                    for k in range(S):
                        b = k % BUFS
                        dve.wait_ge(gate_ready, t * S + (k + 1))
                        nc.vector.tensor_scalar(g[:, b, :], gate_ps[:, k % 2, :], vec(c, f"bg{k}"), LIMIT, ALU.add,
                                                ALU.min).then_inc(g_ready, 1)
                        dve.wait_ge(up_ready, t * S + (k + 1))
                        nc.vector.tensor_scalar(u[:, b, :], up_ps[:, k % 2, :], bu1[:, k:k + 1], LIMIT + 1.0,
                                                ALU.add, ALU.min).then_inc(gu_free, 1)
                        if k >= 1:
                            finish(k - 1)
                    finish(S - 1)
                    dve.wait_ge(gc_ready, t * S + S)
                    dve.wait_ge(o_ready, t + 1)
                    nc.vector.scalar_tensor_tensor(c.x_t[:, tile], o_ps[:, 0, :], c.mod[:, 1, GB, bass.ds(t, 1)],
                                                   c.x_t[:, tile], ALU.mult, ALU.add).then_inc(o_free, 1)


def layout_moe1(a, d, bf):
    d["r1_wr"] = a["L1_ffn_Wg"].T
    d["r1_rank"] = rank_const(16)
    d["r1_lb"] = np.tile(a["L1_ffn_bg"], (P, KT))
    wgu = a["L1_ffn_Wgu"].transpose(1, 0, 2)
    d["m1_wg"], d["m1_wu"] = wgu[:, :, ::2], wgu[:, :, 1::2]
    d["m1_wd"] = a["L1_ffn_Wd"].transpose(1, 0, 2)
    d["m1_bd3"] = np.tile(a["L1_ffn_bd"], (3, 1))
    d["m1_pick"] = pick_const(16, bf)


def stage_moe3(c):
    nc, ins, E, F = c.nc, c.ins, 7, 4
    capacity = -(-5 * 1024 * 2 // (4 * E))
    BLOCKS = -(-capacity // P)
    PER = BLOCKS * P
    ALL = E * BLOCKS
    stage_norm(c, c.h_t, c.h_t, lambda t: vec(c, "ln_g"), lambda t: vec(c, "ln_b"))
    with ExitStack() as s:
        def sb(name, shape, dt=F32):
            return s.enter_context(nc.sbuf_tensor(f"m3_{name}", shape, dt))

        def sem(name):
            return s.enter_context(nc.semaphore(f"m3_{name}"))

        index = sb("index", [P, 2, KT], U32)
        gates = sb("gates", [P, 2, KT])
        stage_router(c, "r3", E, None, capacity=capacity, slots=(index, gates, PER))
        w1, w3, w2 = (sb(n, [P, E + 1, F, P]) for n in ("w1", "w3", "w2"))
        sa, v = sb("sa", [P, BUFS, TILE]), sb("v", [P, BUFS, TILE])
        sent = nc.dram_tensor("m3_sent", (ALL * P, P), F32, kind="Internal").ap()
        back = nc.dram_tensor("m3_back", ((ALL + 1) * P, P), F32, kind="Internal").ap()
        names = ("loaded", "zeros_set", "zeroed", "turned", "rows_even", "rows_odd", "scattered", "a_ready", "b_ready",
                 "sa_ready", "v_ready", "o_ready", "o_free", "slots_in", "xs_turned", "xs_even", "xs_odd", "ra_ready",
                 "rb_ready", "rsa_ready", "rv_ready", "ro_ready", "ro_read", "oo_turned", "rows_ready", "returned",
                 "first_ready", "sum_ready", "sum_turned", "x_ready")
        S = {n: sem(n) for n in names}

        gathered = [sem(f"gathered{t}") for t in range(NT)]

        with ExitStack() as s1, nc.Block() as block:
            tr_ps, a_ps, b_ps = (s1.enter_context(nc.psum_tensor(f"m3_{n}", [P, 2, TILE], F32))
                                 for n in ("tr_ps", "a_ps", "b_ps"))
            o_ps = s1.enter_context(nc.psum_tensor("m3_o_ps", [P, TILE], F32))
            rows = s1.enter_context(nc.sbuf_tensor("m3_rows", [P, KT, P], F32))
            zeros = s1.enter_context(nc.sbuf_tensor("m3_zeros", [P, ALL * P], F32))

            @block.sync
            def _(sp):
                for dst, name in ((w1, "m3_w1"), (w3, "m3_w3"), (w2, "m3_w2")):
                    sp.dma_start(dst[:, :, :, :], ins[name]).then_inc(S["loaded"], 16)
                sp.wait_ge(S["zeros_set"], 1)
                sp.dma_start(sent.rearrange("(p r) d -> p (r d)", p=P), zeros[:, :]).then_inc(S["zeroed"], 16)
                sp.dma_start(back[ALL * P:(ALL + 1) * P, :], zeros[:, 0:P]).then_inc(S["zeroed"], 16)
                sp.wait_ge(S["zeroed"], 32)

            @block.gpsimd
            def _(pool):
                nc.gpsimd.memset(zeros[:, :], 0.0).then_inc(S["zeros_set"], 1)
                pool.wait_ge(S["zeroed"], 32)
                for k in range(KT):
                    q = k // 4
                    pool.wait_ge(S["rows_odd" if q % 2 else "rows_even"], q // 2 + 1)
                    for choice in range(2):
                        nc.gpsimd.indirect_dma_start(
                            sent, bass.IndirectOffsetOnAxis(index[:, choice, k:k + 1], 0), rows[:, k, :], None,
                            bounds_check=ALL * P - 1, oob_is_err=False).then_inc(S["scattered"], 16)
                pool.wait_ge(S["scattered"], 16 * 2 * KT)

            @block.tensor
            def _(pe):
                for q in range(KT // 4):
                    if q >= 2:
                        pe.wait_ge(S["rows_odd" if q % 2 else "rows_even"], q // 2)
                    for j in range(4):
                        at = (4 * q + j) * P
                        mm = nc.tensor.transpose(tr_ps[:, q % 2, j * P:(j + 1) * P], c.h_t[:, at:at + P], c.ident[:, :])
                    mm.then_inc(S["turned"], 1)
                pe.wait_ge(S["loaded"], 48)
                pe.sem_inc(S["v_ready"], 2)
                pe.sem_inc(S["o_free"], 1)
                with pe.Fori(0, NT) as t:
                    tile = bass.ts(t, TILE)

                    def down(f):
                        pe.wait_ge(S["v_ready"], t * F + (f + 3))
                        if f == 0:
                            pe.wait_ge(S["o_free"], t + 1)
                        return nc.tensor.matmul(o_ps[:, :], w2[:, E, f, :], v[:, f % 2, :], start=(f == 0),
                                                stop=(f == F - 1))
                    for f in range(F):
                        pe.wait_ge(S["v_ready"], t * F + (f + 1))
                        nc.tensor.matmul(a_ps[:, f % 2, :], w1[:, E, f, :], c.h_t[:, tile], start=True,
                                         stop=True).then_inc(S["a_ready"], 1)
                        nc.tensor.matmul(b_ps[:, f % 2, :], w3[:, E, f, :], c.h_t[:, tile], start=True,
                                         stop=True).then_inc(S["b_ready"], 1)
                        if f:
                            down(f - 1)
                    down(F - 1).then_inc(S["o_ready"], 1)

            @block.scalar
            def _(act):
                for q in range(0, KT // 4, 2):
                    act.wait_ge(S["turned"], q + 1)
                    nc.scalar.copy(rows[:, 4 * q:4 * q + 4, :].rearrange("p k d -> p (k d)"),
                                   tr_ps[:, 0, :]).then_inc(S["rows_even"], 1)
                nc.scalar.preload_act_table(ACT.Silu)
                with act.Fori(0, NT) as t:
                    for f in range(F):
                        act.wait_ge(S["a_ready"], t * F + (f + 1))
                        nc.scalar.activation(sa[:, f % 2, :], a_ps[:, f % 2, :], ACT.Silu).then_inc(S["sa_ready"], 1)

            @block.vector
            def _(dve):
                for q in range(1, KT // 4, 2):
                    dve.wait_ge(S["turned"], q + 1)
                    nc.vector.tensor_copy(rows[:, 4 * q:4 * q + 4, :].rearrange("p k d -> p (k d)"),
                                          tr_ps[:, 1, :]).then_inc(S["rows_odd"], 1)
                with dve.Fori(0, NT) as t:
                    tile = bass.ts(t, TILE)
                    for f in range(F):
                        dve.wait_ge(S["sa_ready"], t * F + (f + 1))
                        dve.wait_ge(S["b_ready"], t * F + (f + 1))
                        nc.vector.tensor_tensor(v[:, f % 2, :], sa[:, f % 2, :], b_ps[:, f % 2, :],
                                                ALU.mult).then_inc(S["v_ready"], 1)
                    dve.wait_ge(S["o_ready"], t + 1)
                    nc.vector.scalar_tensor_tensor(c.x_t[:, tile], o_ps[:, :], c.mod[:, 3, GB, bass.ds(t, 1)],
                                                   c.x_t[:, tile], ALU.mult, ALU.add).then_inc(S["o_free"], 1)

        with ExitStack() as s2, nc.Block() as block:
            tr_ps, a_ps, b_ps, o_ps = (s2.enter_context(nc.psum_tensor(f"m3_r_{n}", [P, 2, TILE], F32))
                                       for n in ("tr_ps", "a_ps", "b_ps", "o_ps"))
            xs = s2.enter_context(nc.sbuf_tensor("m3_xs", [P, ALL, P], F32))
            xs_t = s2.enter_context(nc.sbuf_tensor("m3_xs_t", [P, ALL, P], F32))
            out_t = s2.enter_context(nc.sbuf_tensor("m3_out_t", [P, 2, PER], F32))
            out_rows = s2.enter_context(nc.sbuf_tensor("m3_out_rows", [P, 2, PER], F32))

            @block.sync
            def _(sp):
                half = ALL // 2
                for part in (slice(0, half), slice(half, ALL)):
                    sp.dma_start(xs[:, part, :], sent.rearrange("(k p) d -> p k d", p=P)[:, part, :]
                                 ).then_inc(S["slots_in"], 16)
                for e in range(E):
                    sp.wait_ge(S["rows_ready"], e + 1)
                    at = e * PER
                    sp.dma_start(back[at:at + PER, :].rearrange("(k p) d -> p k d", p=P),
                                 out_rows[:, e % 2, :].rearrange("p (k d) -> p k d", d=P)).then_inc(S["returned"], 16)
                    sp.wait_ge(S["returned"], 16 * (e + 1))

            @block.tensor
            def _(pe):
                def up(n):
                    e, f = divmod(n, F)
                    if n >= 2:
                        pe.wait_ge(S["rv_ready"], n - 1)
                    if f == 0:
                        pe.wait_ge(S["xs_odd" if e % 2 else "xs_even"], e // 2 + 1)
                    x = xs_t[:, e * BLOCKS:(e + 1) * BLOCKS, :].rearrange("p k s -> p (k s)")
                    nc.tensor.matmul(a_ps[:, n % 2, 0:PER], w1[:, e, f, :], x, start=True,
                                     stop=True).then_inc(S["ra_ready"], 1)
                    nc.tensor.matmul(b_ps[:, n % 2, 0:PER], w3[:, e, f, :], x, start=True,
                                     stop=True).then_inc(S["rb_ready"], 1)

                def down(n):
                    e, f = divmod(n, F)
                    if f == 0 and e >= 2:
                        pe.wait_ge(S["ro_read"], e - 1)
                    pe.wait_ge(S["rv_ready"], n + 1)
                    mm = nc.tensor.matmul(o_ps[:, e % 2, 0:PER], w2[:, e, f, :], v[:, n % BUFS, 0:PER],
                                          start=(f == 0), stop=(f == F - 1))
                    if f == F - 1:
                        mm.then_inc(S["ro_ready"], 1)

                def turn_out(e):
                    pe.wait_ge(S["ro_read"], e + 1)
                    if e >= 2:
                        pe.wait_ge(S["rows_ready"], e - 1)
                    for j in range(BLOCKS):
                        mm = nc.tensor.transpose(tr_ps[:, e % 2, j * P:(j + 1) * P], out_t[:, e % 2, j * P:(j + 1) * P],
                                                 c.ident[:, :])
                    mm.then_inc(S["oo_turned"], 1)
                pe.wait_ge(S["slots_in"], 32)
                for e in range(E):
                    if e >= 2:
                        pe.wait_ge(S["xs_odd" if e % 2 else "xs_even"], e // 2)
                    for j in range(BLOCKS):
                        mm = nc.tensor.transpose(tr_ps[:, e % 2, j * P:(j + 1) * P], xs[:, e * BLOCKS + j, :],
                                                 c.ident[:, :])
                    mm.then_inc(S["xs_turned"], 1)
                pe.wait_ge(S["xs_odd"], E // 2)
                pe.wait_ge(S["xs_even"], (E + 1) // 2)
                for n in range(E * F):
                    up(n)
                    if n:
                        down(n - 1)
                    if n > F and n % F == 1:
                        turn_out(n // F - 1)
                down(E * F - 1)
                turn_out(E - 1)

            @block.scalar
            def _(act):
                def xs_copy(e):
                    act.wait_ge(S["xs_turned"], e + 1)
                    nc.scalar.copy(xs_t[:, e * BLOCKS:(e + 1) * BLOCKS, :].rearrange("p k s -> p (k s)"),
                                   tr_ps[:, e % 2, 0:PER]).then_inc(S["xs_odd" if e % 2 else "xs_even"], 1)
                for e in range(0, E, 2):
                    xs_copy(e)
                for n in range(E * F):
                    act.wait_ge(S["ra_ready"], n + 1)
                    if n >= BUFS:
                        act.wait_ge(S["rv_ready"], n - BUFS + 1)
                    nc.scalar.activation(sa[:, n % BUFS, 0:PER], a_ps[:, n % 2, 0:PER], ACT.Silu).then_inc(S["rsa_ready"], 1)
                    if n % F == 0 and n:
                        e = n // F - 1
                        act.wait_ge(S["ro_ready"], e + 1)
                        if e >= 2:
                            act.wait_ge(S["oo_turned"], e - 1)
                        nc.scalar.copy(out_t[:, e % 2, :], o_ps[:, e % 2, 0:PER]).then_inc(S["ro_read"], 1)
                act.wait_ge(S["ro_ready"], E)
                act.wait_ge(S["oo_turned"], E - 2)
                nc.scalar.copy(out_t[:, (E - 1) % 2, :], o_ps[:, (E - 1) % 2, 0:PER]).then_inc(S["ro_read"], 1)

            @block.vector
            def _(dve):
                def rows_copy(e):
                    dve.wait_ge(S["oo_turned"], e + 1)
                    if e >= 2:
                        dve.wait_ge(S["returned"], 16 * (e - 1))
                    nc.vector.tensor_copy(out_rows[:, e % 2, :], tr_ps[:, e % 2, 0:PER]).then_inc(S["rows_ready"], 1)
                for e in range(1, E, 2):
                    dve.wait_ge(S["xs_turned"], e + 1)
                    nc.vector.tensor_copy(xs_t[:, e * BLOCKS:(e + 1) * BLOCKS, :].rearrange("p k s -> p (k s)"),
                                          tr_ps[:, e % 2, 0:PER]).then_inc(S["xs_odd"], 1)
                for n in range(E * F):
                    dve.wait_ge(S["rsa_ready"], n + 1)
                    dve.wait_ge(S["rb_ready"], n + 1)
                    nc.vector.tensor_tensor(v[:, n % BUFS, 0:PER], sa[:, n % BUFS, 0:PER], b_ps[:, n % 2, 0:PER],
                                            ALU.mult).then_inc(S["rv_ready"], 1)
                    if n > F and n % F == 2:
                        rows_copy(n // F - 1)
                rows_copy(E - 1)

        with ExitStack() as s3, nc.Block() as block:
            tr_ps = s3.enter_context(nc.psum_tensor("m3_g_tr_ps", [P, 2, TILE], F32))
            got = s3.enter_context(nc.sbuf_tensor("m3_got", [P, 2, KT, P], F32))
            z = s3.enter_context(nc.sbuf_tensor("m3_z", [P, 4, P], F32))
            both = s3.enter_context(nc.sbuf_tensor("m3_both", [P, KT, P], F32))

            @block.gpsimd
            def _(pool):
                for k in range(KT):
                    for choice in range(2):
                        nc.gpsimd.indirect_dma_start(
                            got[:, choice, k, :], None, back,
                            bass.IndirectOffsetOnAxis(index[:, choice, k:k + 1], 0)).then_inc(gathered[k // 4], 16)

            @block.vector
            def _(dve):
                tt, ts, stt = nc.vector.tensor_tensor, nc.vector.tensor_scalar, nc.vector.scalar_tensor_tensor

                def add_to_x(t):
                    dve.wait_ge(S["sum_turned"], t + 1)
                    at = slice(t * TILE, (t + 1) * TILE)
                    stt(c.x_t[:, at], tr_ps[:, t % 2, :], c.mod[:, 3, GB, t:t + 1], c.x_t[:, at], ALU.mult,
                        ALU.add).then_inc(S["x_ready"], 1)
                for t in range(NT):
                    dve.wait_ge(gathered[t], 16 * 8)
                    for j in range(4):
                        k = 4 * t + j
                        if t:
                            dve.wait_ge(S["sum_ready"], 4 * (t - 1) + j + 1)
                        ts(z[:, j, :], got[:, 0, k, :], gates[:, 0, k:k + 1], None, ALU.mult).then_inc(S["first_ready"], 1)
                    for j in range(4):
                        k = 4 * t + j
                        dve.wait_ge(S["first_ready"], k + 1)
                        stt(both[:, k, :], got[:, 1, k, :], gates[:, 1, k:k + 1], z[:, j, :], ALU.mult,
                            ALU.add).then_inc(S["sum_ready"], 1)
                    if t:
                        add_to_x(t - 1)
                add_to_x(NT - 1)

            @block.tensor
            def _(pe):
                for t in range(NT):
                    pe.wait_ge(S["sum_ready"], 4 * t + 4)
                    if t >= 2:
                        pe.wait_ge(S["x_ready"], t - 1)
                    for j in range(4):
                        mm = nc.tensor.transpose(tr_ps[:, t % 2, j * P:(j + 1) * P], both[:, 4 * t + j, :], c.ident[:, :])
                    mm.then_inc(S["sum_turned"], 1)


def layout_moe3(a, d, bf):
    d["r3_wr"] = a["L3_ffn_Wr"]
    d["r3_rank"] = rank_const(7)
    for n in ("w1", "w3"):
        w = np.concatenate([a[f"L3_ffn_{n.upper()}"], a[f"L3_ffn_{n.upper()}s"][None]])
        d[f"m3_{n}"] = w.reshape(8, P, 4, P).transpose(1, 0, 2, 3)
    w = np.concatenate([a["L3_ffn_W2"], a["L3_ffn_W2s"][None]])
    d["m3_w2"] = w.reshape(8, 4, P, P).transpose(2, 0, 1, 3)


HEADS, HD = 16, 8
SOFTMAX_SCALE = HD ** -0.5


class Chain:

    def __init__(self, eng, sem, per_turn=0, turn=0):
        self.eng, self.sem, self.base, self.n = eng, sem, turn * per_turn, 0
        self.per_turn = per_turn

    def __call__(self, ins):
        self.n += 1
        ins.then_inc(self.sem, 1)
        self.eng.wait_ge(self.sem, self.base + self.n)


def stage_head_attention(c):
    nc, ins = c.nc, c.ins
    SUB = SEQ // P
    POOL1, POOL2 = 13, 12
    with ExitStack() as s:
        def sb(name, shape, dt=F32):
            return s.enter_context(nc.sbuf_tensor(f"h1_{name}", shape, dt))

        def psum(name, shape):
            return s.enter_context(nc.psum_tensor(f"h1_{name}", shape, F32))

        def sem(name):
            return s.enter_context(nc.semaphore(f"h1_{name}"))

        wq = sb("wq", [P, 2, P])
        wkv = sb("wkv", [33, 3, P])
        bq = sb("bq", [1, 2, P])
        one = sb("one", [1, P])
        wdown, wo = sb("wdown", [P, 32]), sb("wo", [P, P])
        turn = sb("turn", [P, SUB, 2, HD])
        hb = sb("hb", [P, SEQ])
        lat = sb("lat", [33, SEQ])
        rc, rs = sb("rc", [P, 2, 2, P]), sb("rs", [P, 2, 2, P])
        qk, v = sb("qk", [P, 2, 2, P]), sb("v", [P, 2, P])
        pr1, pr2 = sb("pr1", [P, 2, HEADS, HEADS, HD]), sb("pr2", [P, 2, HEADS, HD, HEADS])
        sc, pe_ = sb("sc", [P, 2, HEADS, HEADS]), sb("e", [P, 2, HEADS, HEADS])
        mx, den, rden = sb("mx", [P, HEADS]), sb("den", [P, HEADS]), sb("rden", [P, HEADS])
        o, on = sb("o", [P, 2, P]), sb("on", [P, 2, P])
        y, z = sb("y", [P, 2, TILE]), sb("z", [P, 2, TILE])
        qk_ps = psum("qk_ps", [P, 2, 2, 2, P])
        v_ps = psum("v_ps", [P, 2, 4, P])
        lat_ps = psum("lat_ps", [32, TILE])
        y_ps, o_ps = psum("y_ps", [P, 2, TILE]), psum("o_ps", [P, TILE])
        names = ("loaded", "set", "h_copied", "lat_mm", "lat_ready", "qk_mm", "v_ready", "chain", "rope_ready", "p1",
                 "p1d", "s_ready", "e_ready", "p2", "p2d", "on_ready", "turned", "y_ready", "o_mm", "v_mm")
        (loaded, set_, h_copied, lat_mm, lat_ready, qk_mm, v_ready, chain, rope_ready, p1, p1d, s_ready, e_ready, p2,
         p2d, on_ready, turned, y_ready, o_mm, v_mm) = (sem(n) for n in names)
        CHAIN = 9 * SUB + 2 * TPB
        with nc.Block() as block:
            @block.sync
            def _(sp):
                for dst, name in ((wq[:, :, :], "h1_wq"), (wkv[:, :, :], "h1_wkv"), (bq[:, :, :], "h1_bq"),
                                  (wdown[:, :], "h1_wdown"), (wo[:, :], "h1_wo"), (turn[:, :, :, :], "h1_rope")):
                    sp.dma_start(dst, ins[name]).then_inc(loaded, 16)

            @block.tensor
            def _(pe):
                pe.wait_ge(loaded, 16 * 6)
                pe.wait_ge(set_, 2)
                with pe.Fori(0, BATCH) as b:
                    pe.wait_ge(h_copied, b + 1)
                    for u in range(TPB):
                        if u:
                            pe.wait_ge(lat_ready, b * 2 + u)
                        nc.tensor.matmul(lat_ps[:, :], wdown[:, :], hb[:, u * TILE:(u + 1) * TILE], start=True,
                                         stop=True).then_inc(lat_mm, 1)

                    def project(n):
                        if n >= 2:
                            pe.wait_ge(rope_ready, b * SUB + (n - 1))
                            pe.wait_ge(v_ready, b * SUB + (n - 1))
                        tok = slice(n * P, (n + 1) * P)
                        ps = qk_ps[:, n % 2, :, :, :]
                        nc.tensor.matmul(ps[:, :, 0, :], hb[:, tok], wq[:, :, :], start=True, stop=False,
                                         skip_group_check=True)
                        nc.tensor.matmul(ps[:, :, 0, :], one[:, :], bq[:, :, :], start=False, stop=True,
                                         skip_group_check=True)
                        nc.tensor.matmul(ps[:, :, 1, :], lat[:, tok], wkv[:, 0:2, :], start=False, stop=True,
                                         skip_group_check=True).then_inc(qk_mm, 1)
                        nc.tensor.matmul(v_ps[:, n % 2, 0, :], lat[:, tok], wkv[:, 2, :], start=True,
                                         stop=True).then_inc(v_mm, 1)

                    def turn_back(n):
                        pe.wait_ge(on_ready, b * SUB + (n + 1))
                        u, j = divmod(n, 4)
                        nc.tensor.transpose(y_ps[:, u, j * P:(j + 1) * P], on[:, n % 2, :],
                                            c.ident[:, :]).then_inc(turned, 1)

                    def out(u):
                        pe.wait_ge(y_ready, b * 2 + (u + 1))
                        nc.tensor.matmul(o_ps[:, :], wo[:, :], y[:, u, :], start=True, stop=True).then_inc(o_mm, 1)
                    pe.wait_ge(lat_ready, b * 2 + 2)
                    for n in range(SUB):
                        project(n)
                        if n >= 3:
                            turn_back(n - 3)
                    for n in range(SUB - 3, SUB):
                        turn_back(n)
                        if n == 5:
                            out(0)
                    out(1)

            @block.scalar
            def _(act):
                nc.scalar.preload_act_table(ACT.Exp)
                with act.Fori(0, BATCH) as b:
                    for u in range(TPB):
                        act.wait_ge(lat_mm, b * 2 + (u + 1))
                        nc.scalar.activation(lat[0:32, u * TILE:(u + 1) * TILE], lat_ps[:, :], ACT.Identity,
                                             bias=vec(c, "L1_bdown")[0:32, :]).then_inc(lat_ready, 1)
                    for n in range(SUB):
                        act.wait_ge(v_mm, b * SUB + (n + 1))
                        if n >= 2:
                            act.wait_ge(on_ready, b * SUB + (n - 1))
                        nc.scalar.copy(v[:, n % 2, :], v_ps[:, n % 2, 0, :]).then_inc(v_ready, 1)
                        if n >= 1:
                            act.wait_ge(s_ready, b * SUB + n)
                            nc.scalar.activation(pe_[:, (n - 1) % 2, :, :], sc[:, (n - 1) % 2, :, :], ACT.Exp,
                                                 scale=SOFTMAX_SCALE).then_inc(e_ready, 1)
                    act.wait_ge(s_ready, b * SUB + SUB)
                    nc.scalar.activation(pe_[:, (SUB - 1) % 2, :, :], sc[:, (SUB - 1) % 2, :, :], ACT.Exp,
                                         scale=SOFTMAX_SCALE).then_inc(e_ready, 1)

            def product1(eng, n, h0, h1):
                q = qk[:, n % 2, 0, h0 * HD:h1 * HD].rearrange("p (h d) -> p h d", d=HD)
                k = qk[:, n % 2, 1, :].rearrange("p (g d) -> p g d", d=HD)
                shape = [P, h1 - h0, HEADS, HD]
                return eng.tensor_tensor(pr1[:, n % 2, h0:h1, :, :], q.unsqueeze(2).to_broadcast(shape),
                                         k.unsqueeze(1).to_broadcast(shape), ALU.mult)

            def product2(eng, n, h0, h1):
                e = pe_[:, n % 2, h0:h1, :]
                w = v[:, n % 2, :].rearrange("p (g d) -> p d g", d=HD)
                shape = [P, h1 - h0, HD, HEADS]
                return eng.tensor_tensor(pr2[:, n % 2, h0:h1, :, :], e.unsqueeze(2).to_broadcast(shape),
                                         w.unsqueeze(1).to_broadcast(shape), ALU.mult)

            @block.gpsimd
            def _(pool):
                with pool.Fori(0, BATCH) as b:
                    def first(n):
                        pool.wait_ge(rope_ready, b * SUB + (n + 1))
                        if n >= 2:
                            pool.wait_ge(s_ready, b * SUB + (n - 1))
                        product1(nc.gpsimd, n, 0, POOL1).then_inc(p1, 1)

                    def second(n):
                        pool.wait_ge(e_ready, b * SUB + (n + 1))
                        pool.wait_ge(v_ready, b * SUB + (n + 1))
                        if n >= 2:
                            pool.wait_ge(on_ready, b * SUB + (n - 1))
                        product2(nc.gpsimd, n, 0, POOL2).then_inc(p2, 1)
                    first(0)
                    for n in range(SUB):
                        if n + 1 < SUB:
                            first(n + 1)
                        second(n)

            @block.vector
            def _(dve):
                nc.vector.memset(one[:, :], 1.0).then_inc(set_, 1)
                nc.vector.memset(lat[32:33, :], 1.0).then_inc(set_, 1)
                dve.wait_ge(loaded, 16 * 6)
                with dve.Fori(0, BATCH) as b:
                    done = Chain(dve, chain, CHAIN, b)
                    tt = nc.vector.tensor_tensor
                    nc.vector.tensor_copy(hb[:, :], c.h_t[:, bass.ts(b, SEQ)]).then_inc(h_copied, 1)

                    def rope(n):
                        dve.wait_ge(qk_mm, b * SUB + (n + 1))
                        if n >= 2:
                            dve.wait_ge(p1, b * SUB + (n - 1))
                        ps = qk_ps[:, n % 2, :, :, :]
                        for r, dst in ((0, rc), (1, rs)):
                            cs = turn[:, n, r, :].unsqueeze(1).to_broadcast([P, 2 * HEADS, HD])
                            done(tt(dst[:, n % 2, :, :].rearrange("p x (h d) -> p (x h) d", d=HD),
                                    ps[:, r, :, :].rearrange("p x (h d) -> p (x h) d", d=HD), cs, ALU.mult))
                        tt(qk[:, n % 2, :, :], rc[:, n % 2, :, :], rs[:, n % 2, :, :], ALU.add).then_inc(rope_ready, 1)

                    def scores(n):
                        dve.wait_ge(rope_ready, b * SUB + (n + 1))
                        done(product1(nc.vector, n, POOL1, HEADS))
                        dve.wait_ge(p1, b * SUB + (n + 1))
                        x = n % 2
                        done(nc.vector.reduce_sum(sc[:, x, :, :], pr1[:, x, :, :, :], AX.X))
                        done(nc.vector.reduce_max(mx[:, :], sc[:, x, :, :], AX.X))
                        tt(sc[:, x, :, :], sc[:, x, :, :], mx[:, :].unsqueeze(2).to_broadcast([P, HEADS, HEADS]),
                           ALU.subtract).then_inc(s_ready, 1)
                        dve.wait_ge(s_ready, b * SUB + (n + 1))

                    def weigh(n):
                        x = n % 2
                        dve.wait_ge(e_ready, b * SUB + (n + 1))
                        dve.wait_ge(v_ready, b * SUB + (n + 1))
                        done(product2(nc.vector, n, POOL2, HEADS))
                        done(nc.vector.reduce_sum(den[:, :], pe_[:, x, :, :], AX.X))
                        done(nc.vector.reciprocal(rden[:, :], den[:, :]))
                        dve.wait_ge(p2, b * SUB + (n + 1))
                        if n >= 2:
                            dve.wait_ge(turned, b * SUB + (n - 1))
                        done(nc.vector.reduce_sum(o[:, x, :].rearrange("p (h d) -> p h d", d=HD), pr2[:, x, :, :, :],
                                                  AX.X))
                        tt(on[:, x, :].rearrange("p (h d) -> p h d", d=HD),
                           o[:, x, :].rearrange("p (h d) -> p h d", d=HD),
                           rden[:, :].unsqueeze(2).to_broadcast([P, HEADS, HD]), ALU.mult).then_inc(on_ready, 1)
                        dve.wait_ge(on_ready, b * SUB + (n + 1))

                    def gather(u):
                        dve.wait_ge(turned, b * SUB + 4 * (u + 1))
                        nc.vector.tensor_copy(y[:, u, :], y_ps[:, u, :]).then_inc(y_ready, 1)

                    def add(u):
                        dve.wait_ge(o_mm, b * 2 + (u + 1))
                        t = b * 2 + u
                        done(nc.vector.tensor_scalar(z[:, u, :], o_ps[:, :], vec(c, "L1_bout"),
                                                     c.mod[:, 1, GA, bass.ds(t, 1)], ALU.add, ALU.mult))
                        done(tt(c.x_t[:, bass.ts(t, TILE)], c.x_t[:, bass.ts(t, TILE)], z[:, u, :], ALU.add))
                    rope(0)
                    rope(1)
                    for n in range(SUB):
                        scores(n)
                        if n + 2 < SUB:
                            rope(n + 2)
                        if n >= 1:
                            weigh(n - 1)
                    weigh(SUB - 1)
                    gather(0)
                    add(0)
                    gather(1)
                    add(1)
                    assert done.n == CHAIN


def layout_head_attention(a, d, bf):
    up = a["L1_attn_Wup"].reshape(32, HEADS, 2, HD)
    bup = a["L1_attn_bup"].reshape(HEADS, 2, HD)
    wk, wv = up[:, :, 0].reshape(32, P), up[:, :, 1].reshape(32, P)
    bk, bv = bup[:, 0].reshape(1, P), bup[:, 1].reshape(1, P)
    d["h1_wq"] = np.stack([a["L1_attn_Wq"], rope_swap(a["L1_attn_Wq"])], 1)
    d["h1_wkv"] = np.concatenate([np.stack([wk, rope_swap(wk), wv], 1), np.stack([bk, rope_swap(bk), bv], 1)])
    bq = a["L1_attn_bq"][None]
    d["h1_bq"] = np.stack([bq, rope_swap(bq)], 1)
    d["h1_wdown"], d["h1_wo"] = a["L1_attn_Wdown"], a["L1_attn_Wout"]
    inv = 1.0 / 10000.0 ** (np.arange(0, HD, 2, dtype=np.float32) / np.float32(HD))
    freqs = np.arange(SEQ, dtype=np.float32)[:, None] * inv[None, :].astype(np.float32)
    cos, sin = np.cos(freqs), np.sin(freqs)
    table = np.stack([np.concatenate([cos, cos], 1), np.concatenate([-sin, sin], 1)], 1)
    d["h1_rope"] = table.reshape(SEQ // P, P, 2, HD).transpose(1, 0, 2, 3).astype(np.float32)


def stage_linear_attention(c):
    nc, ins = c.nc, c.ins
    H = 8
    D = P // H
    CH = SEQ // P
    with ExitStack() as s:
        def sb(name, shape, dt=F32):
            return s.enter_context(nc.sbuf_tensor(f"a2_{name}", shape, dt))

        def psum(name, shape):
            return s.enter_context(nc.psum_tensor(f"a2_{name}", shape, F32))

        def sem(name):
            return s.enter_context(nc.semaphore(f"a2_{name}"))

        w = sb("w", [P, 4, P])
        wo = sb("wo", [P, P])
        tri = sb("tri", [P, P])
        hmask = sb("hmask", [P, H])
        bmask = sb("bmask", [P, P])
        vt, ut = sb("vt", [P, SEQ]), sb("ut", [P, SEQ])
        xb, neg, pos = (sb(n, [P, 2, TILE]) for n in ("xb", "neg", "pos"))
        qt, kt = sb("qt", [P, SEQ]), sb("kt", [P, SEQ])
        vn, kn = sb("vn", [P, CH, P]), sb("kn", [P, CH, P])
        qx = sb("qx", [P, 2, H, P])
        en = sb("en", [P, 2, H, P])
        kvm, kvs = sb("kvm", [P, P]), sb("kvs", [P, 2, P])
        o, on, sq = sb("o", [P, CH, P]), sb("on", [P, CH, P]), sb("sq", [P, P])
        ss, rr, tiny = sb("ss", [P, CH]), sb("rr", [P, CH]), sb("tiny", [P, 1])
        y, z = sb("y", [P, 2, TILE]), sb("z", [P, 2, TILE])
        ps = psum("ps", [P, 2, TILE])
        en_ps = psum("en_ps", [P, 2, TILE])
        tr_ps, out_ps, kv_ps, oo_ps = (psum(n, [P, TILE]) for n in ("tr_ps", "out_ps", "kv_ps", "oo_ps"))
        names = ("loaded", "set", "proj_mm", "proj_read", "silu_done", "exp_done", "neg_ready", "pos_ready",
                 "elu_ready", "turned", "tok_ready", "qx_ready", "en_mm", "en_ready", "kv_mm", "kvm_ready",
                 "kvs_ready", "out_mm", "out_read", "ss_ready", "ln_done", "rms_ready", "rms_chain", "on_ready",
                 "back", "y_ready", "o_mm", "z_ready", "x_ready")
        S = {n: sem(n) for n in names}
        with nc.Block() as block:
            @block.sync
            def _(sp):
                for dst, name in ((w[:, :, :], "a2_w"), (wo[:, :], "a2_wo"), (tri[:, :], "a2_tri"),
                                  (hmask[:, :], "a2_hmask"), (bmask[:, :], "a2_bmask")):
                    sp.dma_start(dst, ins[name]).then_inc(S["loaded"], 16)

            def energies(n):
                return en_ps if n % 2 == 0 else ps

            @block.tensor
            def _(pe):
                pe.wait_ge(S["loaded"], 16 * 5)
                with pe.Fori(0, BATCH) as b:
                    for i in range(8):
                        if i >= 2:
                            pe.wait_ge(S["proj_read"], b * 8 + (i - 1))
                        nc.tensor.matmul(ps[:, i % 2, :], w[:, i // 2, :], c.h_t[:, bass.ts(b * 2 + i % 2, TILE)],
                                         start=True, stop=True).then_inc(S["proj_mm"], 1)

                    def to_tokens(i, src, ready, value):
                        pe.wait_ge(S[ready], value)
                        if i:
                            pe.wait_ge(S["tok_ready"], b * 4 + i)
                        for j in range(4):
                            at = (i % 2) * 4 + j
                            mm = nc.tensor.transpose(tr_ps[:, j * P:(j + 1) * P], src[:, at * P:(at + 1) * P],
                                                     c.ident[:, :])
                        mm.then_inc(S["turned"], 1)
                    for i in range(2):
                        to_tokens(i, vt, "silu_done", b * 4 + (i + 1))
                    for i in range(2):
                        to_tokens(2 + i, kt, "elu_ready", b * 4 + (3 + i))

                    def energy(n):
                        pe.wait_ge(S["qx_ready"], b * CH + (n + 1))
                        if n >= 2:
                            pe.wait_ge(S["en_ready"], b * CH + (n - 1))
                        for j in range(2):
                            mm = nc.tensor.matmul(energies(n)[:, j, :], kt[:, n * P:(n + 1) * P],
                                                  qx[:, n % 2, 4 * j:4 * j + 4, :], start=True, stop=True)
                        mm.then_inc(S["en_mm"], 1)

                    def output(n):
                        pe.wait_ge(S["en_ready"], b * CH + (n + 1))
                        if n == 0:
                            pe.wait_ge(S["tok_ready"], b * 4 + 4)
                        else:
                            pe.wait_ge(S["kvs_ready"], b * CH + n)
                            pe.wait_ge(S["out_read"], b * CH + n)
                        if n:
                            nc.tensor.matmul(out_ps[:, 0:P], qt[:, n * P:(n + 1) * P], kvs[:, (n - 1) % 2, :],
                                             start=True, stop=False, skip_group_check=True)
                        for h in range(H):
                            mm = nc.tensor.matmul(out_ps[:, h * D:(h + 1) * D], en[:, n % 2, h, :],
                                                  vn[:, n, h * D:(h + 1) * D], start=(n == 0 and h == 0), stop=(h == H - 1),
                                                  skip_group_check=True)
                        mm.then_inc(S["out_mm"], 1)
                        if n:
                            pe.wait_ge(S["kvm_ready"], b * CH + n)
                        nc.tensor.matmul(kv_ps[:, 0:P], kn[:, n, :], vn[:, n, :], start=True,
                                         stop=True).then_inc(S["kv_mm"], 1)
                    energy(0)
                    for n in range(CH):
                        if n + 1 < CH:
                            energy(n + 1)
                        output(n)

                    def project(u):
                        pe.wait_ge(S["y_ready"], b * 2 + (u + 1))
                        if u:
                            pe.wait_ge(S["z_ready"], b * 2 + u)
                        nc.tensor.matmul(oo_ps[:, :], wo[:, :], y[:, u, :], start=True, stop=True).then_inc(S["o_mm"], 1)
                    pe.wait_ge(S["on_ready"], b + 1)
                    for u in range(2):
                        if u:
                            pe.wait_ge(S["y_ready"], b * 2 + u)
                        for j in range(4):
                            mm = nc.tensor.transpose(tr_ps[:, j * P:(j + 1) * P], on[:, u * 4 + j, :], c.ident[:, :])
                        mm.then_inc(S["back"], 1)
                        project(u)
                    pe.wait_ge(S["x_ready"], b * 2 + 2)

            @block.scalar
            def _(act):
                act.wait_ge(S["set"], 1)
                with act.Fori(0, BATCH) as b:
                    for i in range(4):
                        n, u = divmod(i, 2)
                        act.wait_ge(S["proj_mm"], b * 8 + (i + 1))
                        nc.scalar.activation((vt, ut)[n][:, u * TILE:(u + 1) * TILE], ps[:, u, :], ACT.Silu,
                                             bias=vec(c, ("L2_bv", "L2_bu")[n])).then_inc(S["silu_done"], 1)
                        act.wait_ge(S["silu_done"], b * 4 + (i + 1))
                        act.sem_inc(S["proj_read"], 1)
                    for i in range(4):
                        n, u = divmod(i, 2)
                        act.wait_ge(S["proj_mm"], b * 8 + (i + 5))
                        if i >= 2:
                            act.wait_ge(S["elu_ready"], b * 4 + (i - 1))
                        nc.scalar.activation(xb[:, u, :], ps[:, u, :], ACT.Identity,
                                             bias=vec(c, ("L2_bq", "L2_bk")[n])).then_inc(S["proj_read"], 1)
                        act.wait_ge(S["neg_ready"], b * 4 + (i + 1))
                        nc.scalar.activation(neg[:, u, :], neg[:, u, :], ACT.Exp).then_inc(S["exp_done"], 1)
                    for n in range(CH):
                        act.wait_ge(S["out_mm"], b * CH + (n + 1))
                        nc.scalar.copy(o[:, n, :], out_ps[:, 0:P]).then_inc(S["out_read"], 1)
                        act.wait_ge(S["out_read"], b * CH + (n + 1))
                        nc.scalar.activation(sq[:, :], o[:, n, :], ACT.Square, accum_out=ss[:, n:n + 1]).then_inc(S["ss_ready"], 1)
                        act.wait_ge(S["ss_ready"], b * CH + (n + 1))
                    nc.scalar.activation(rr[:, :], ss[:, :], ACT.Ln, bias=tiny[:, 0:1], scale=1.0 / P).then_inc(S["ln_done"], 1)
                    act.wait_ge(S["ln_done"], b + 1)
                    nc.scalar.activation(rr[:, :], rr[:, :], ACT.Exp, scale=0.5).then_inc(S["rms_ready"], 1)

            @block.gpsimd
            def _(pool):
                pool.wait_ge(S["loaded"], 16 * 5)
                with pool.Fori(0, BATCH) as b:
                    for n in range(CH):
                        pool.wait_ge(S["elu_ready"], b * 4 + (n // 4 + 1))
                        if n >= 2:
                            pool.wait_ge(S["en_mm"], b * CH + (n - 1))
                        shape = [P, H, P]
                        nc.gpsimd.tensor_tensor(qx[:, n % 2, :, :],
                                                qt[:, n * P:(n + 1) * P].unsqueeze(1).to_broadcast(shape),
                                                hmask[:, :].unsqueeze(2).to_broadcast(shape),
                                                ALU.mult).then_inc(S["qx_ready"], 1)

            @block.vector
            def _(dve):
                tt, ts = nc.vector.tensor_tensor, nc.vector.tensor_scalar
                nc.vector.memset(tiny[:, :], 1e-30).then_inc(S["set"], 1)
                dve.wait_ge(S["loaded"], 16 * 5)
                with dve.Fori(0, BATCH) as b:
                    def tokens(i):
                        dve.wait_ge(S["turned"], b * 4 + (i + 1))
                        dst = (vn, kn)[i // 2][:, (i % 2) * 4:(i % 2) * 4 + 4, :]
                        nc.vector.tensor_copy(dst, tr_ps[:, :].rearrange("p (j t) -> p j t", j=4)).then_inc(S["tok_ready"], 1)
                    for i in range(4):
                        n, u = divmod(i, 2)
                        dve.wait_ge(S["proj_read"], b * 8 + (i + 5))
                        ts(neg[:, u, :], xb[:, u, :], 0.0, None, ALU.min).then_inc(S["neg_ready"], 1)
                        ts(pos[:, u, :], xb[:, u, :], 0.0, None, ALU.max).then_inc(S["pos_ready"], 1)
                        dve.wait_ge(S["pos_ready"], b * 4 + (i + 1))
                        dve.wait_ge(S["exp_done"], b * 4 + (i + 1))
                        nc.vector.scalar_tensor_tensor((qt, kt)[n][:, u * TILE:(u + 1) * TILE], neg[:, u, :], -1.0,
                                                       pos[:, u, :], ALU.add, ALU.add).then_inc(S["elu_ready"], 1)
                    dve.wait_ge(S["elu_ready"], b * 4 + 4)
                    for i in range(4):
                        tokens(i)
                    for n in range(CH):
                        dve.wait_ge(S["en_mm"], b * CH + (n + 1))
                        if n >= 2:
                            dve.wait_ge(S["out_mm"], b * CH + (n - 1))
                        shape = [P, H, P]
                        tt(en[:, n % 2, :, :], energies(n)[:, :, :].rearrange("p j (h q) -> p (j h) q", q=P),
                           tri[:, :].unsqueeze(1).to_broadcast(shape), ALU.mult).then_inc(S["en_ready"], 1)
                        dve.wait_ge(S["kv_mm"], b * CH + (n + 1))
                        tt(kvm[:, :], kv_ps[:, 0:P], bmask[:, :], ALU.mult).then_inc(S["kvm_ready"], 1)
                        dve.wait_ge(S["kvm_ready"], b * CH + (n + 1))
                        if n == 0:
                            last = nc.vector.tensor_copy(kvs[:, 0, :], kvm[:, :])
                        else:
                            last = tt(kvs[:, n % 2, :], kvs[:, (n - 1) % 2, :], kvm[:, :], ALU.add)
                        last.then_inc(S["kvs_ready"], 1)
                        dve.wait_ge(S["kvs_ready"], b * CH + (n + 1))
                    dve.wait_ge(S["rms_ready"], b + 1)
                    chain = Chain(dve, S["rms_chain"], 2, b)
                    chain(ts(rr[:, :], rr[:, :], 1e-8, None, ALU.add))
                    chain(nc.vector.reciprocal(rr[:, :], rr[:, :]))
                    tt(on[:, :, :], o[:, :, :], rr[:, :].unsqueeze(2).to_broadcast([P, CH, P]),
                       ALU.mult).then_inc(S["on_ready"], 1)
                    for u in range(2):
                        t = b * 2 + u
                        dve.wait_ge(S["back"], b * 2 + (u + 1))
                        nc.vector.scalar_tensor_tensor(y[:, u, :], tr_ps[:, :], vec(c, "L2_scale"),
                                                       ut[:, u * TILE:(u + 1) * TILE], ALU.mult,
                                                       ALU.mult).then_inc(S["y_ready"], 1)
                        dve.wait_ge(S["o_mm"], b * 2 + (u + 1))
                        ts(z[:, u, :], oo_ps[:, :], vec(c, "L2_bo"), c.mod[:, 2, GA, bass.ds(t, 1)], ALU.add,
                           ALU.mult).then_inc(S["z_ready"], 1)
                        dve.wait_ge(S["z_ready"], b * 2 + (u + 1))
                        tt(c.x_t[:, bass.ts(t, TILE)], c.x_t[:, bass.ts(t, TILE)], z[:, u, :],
                           ALU.add).then_inc(S["x_ready"], 1)
                    dve.wait_ge(S["x_ready"], b * 2 + 2)


def layout_linear_attention(a, d, bf):
    d["a2_w"] = np.stack([a[f"L2_attn_W{n}"].T for n in "vuqk"], 1)
    d["a2_wo"] = a["L2_attn_Wo"].T
    d["a2_tri"] = np.triu(np.ones((P, P), np.float32))
    head = np.arange(P) // 16
    d["a2_hmask"] = (head[:, None] == np.arange(8)[None]).astype(np.float32)
    d["a2_bmask"] = (head[:, None] == head[None]).astype(np.float32)


HG = 4
GROUPS = BATCH * HEADS // HG
GCH = HG * HD
KP = 9 * HD
SOFTMAX_SCALE = HD ** -0.5


class Heads:

    def __init__(self, c, tag, stack):
        nc = c.nc
        self.parts = nc.dram_tensor(f"{tag}_parts", (2, 3, BATCH * P, SEQ), BF16, kind="Internal").ap()
        self.neg = nc.dram_tensor(f"{tag}_neg", (GROUPS * 2 * 3, HG * SEQ // 2), BF16, kind="Internal").ap()
        self.out = nc.dram_tensor(f"{tag}_out", (GROUPS * P, SEQ), F32, kind="Internal").ap()
        self.v_all = stack.enter_context(nc.sbuf_tensor(f"{tag}_v_all", [P, GROUPS, SEQ // P, GCH], F32))


def stage_project(c, tag, hd):
    nc, ins = c.nc, c.ins
    with ExitStack() as s:
        def sb(name, shape, dt=F32):
            return s.enter_context(nc.sbuf_tensor(f"{tag}p_{name}", shape, dt))

        def psum(name, shape):
            return s.enter_context(nc.psum_tensor(f"{tag}p_{name}", shape, F32))

        def sem(name):
            return s.enter_context(nc.semaphore(f"{tag}p_{name}"))

        wq, wk, wv = sb("wq", [P, P]), sb("wk", [P, P]), sb("wv", [P, P])
        hs = sb("hs", [P, 2, TILE])
        f = [sb(f"f{x}", [P, TILE]) for x in range(2)]
        r1 = [sb(f"r1{x}", [P, TILE]) for x in range(2)]
        r2 = [sb(f"r2{x}", [P, TILE]) for x in range(2)]
        pt = [sb(f"pt{x}", [P, 2, 3, TILE], BF16) for x in range(2)]
        qk_ps = [psum(f"qk_ps{x}", [P, TILE]) for x in range(2)]
        v_ps = psum("v_ps", [P, TILE // P, P])
        loaded, hs_ready, v_mm, v_free = (sem(n) for n in ("loaded", "hs_ready", "v_mm", "v_free"))
        mm, ps_free, f_ready, hi, r1_ready, mid, r2_ready, lo = (
            [sem(f"{n}{x}") for x in range(2)] for n in ("mm", "ps_free", "f_ready", "hi", "r1_ready", "mid",
                                                         "r2_ready", "lo"))
        stored = [[sem(f"stored{x}{u}") for u in range(2)] for x in range(2)]
        bias = [vec(c, f"{tag}_b{n}") for n in "qk"]
        with nc.Block() as block:
            @block.sync
            def _(sp):
                sp.dma_start(wq[:, :], ins[f"{tag}_wq"]).then_inc(loaded, 16)
                sp.dma_start(wk[:, :], ins[f"{tag}_wk"]).then_inc(loaded, 16)
                sp.dma_start(wv[:, :], ins[f"{tag}_wv"]).then_inc(loaded, 16)
                with sp.Fori(0, BATCH) as b:
                    for u in range(TPB):
                        for x in range(2):
                            sp.wait_ge(lo[x], b * 2 + (u + 2))
                            dst = hd.parts[x, :, bass.ts(b, P), u * TILE:(u + 1) * TILE]
                            sp.dma_start(dst.rearrange("r p t -> p r t"), pt[x][:, u, :, :]).then_inc(stored[x][u], 16)
                for x in range(2):
                    for u in range(2):
                        sp.wait_ge(stored[x][u], 16 * (BATCH + 1))

            @block.tensor
            def _(pe):
                pe.wait_ge(loaded, 16 * 3)
                for x in range(2):
                    pe.sem_inc(ps_free[x], 1)
                pe.sem_inc(v_free, 1)
                with pe.Fori(0, BATCH) as b:
                    for u in range(TPB):
                        n = b * 2 + (u + 1)
                        tile = bass.ts(b * 2 + u, TILE)
                        for x, w in enumerate((wq, wk)):
                            pe.wait_ge(ps_free[x], n)
                            nc.tensor.matmul(qk_ps[x][:, :], w[:, :], c.h_t[:, tile], start=True,
                                             stop=True).then_inc(mm[x], 1)
                        pe.wait_ge(hs_ready, n)
                        pe.wait_ge(v_free, n)
                        for j in range(TILE // P):
                            v = nc.tensor.matmul(v_ps[:, j, :], hs[:, u, j * P:(j + 1) * P], wv[:, :], start=True,
                                                 stop=True)
                        v.then_inc(v_mm, 1)

            @block.scalar
            def _(act):
                for x in range(2):
                    for u in range(2):
                        act.sem_inc(stored[x][u], 16)
                    act.sem_inc(lo[x], 1)
                with act.Fori(0, BATCH) as b:
                    for u in range(TPB):
                        n = b * 2 + (u + 1)
                        for x in range(2):
                            act.wait_ge(f_ready[x], n)
                            act.wait_ge(stored[x][u], b * 16 + 16)
                            nc.scalar.copy(pt[x][:, u, 0, :], f[x][:, :]).then_inc(hi[x], 1)
                        for x in range(2):
                            act.wait_ge(r1_ready[x], n)
                            nc.scalar.copy(pt[x][:, u, 1, :], r1[x][:, :]).then_inc(mid[x], 1)
                        for x in range(2):
                            act.wait_ge(r2_ready[x], n)
                            nc.scalar.copy(pt[x][:, u, 2, :], r2[x][:, :]).then_inc(lo[x], 1)

            @block.gpsimd
            def _(pool):
                with pool.Fori(0, BATCH) as b:
                    for u in range(TPB):
                        n = b * 2 + (u + 1)
                        for x in range(2):
                            pool.wait_ge(hi[x], n)
                            nc.gpsimd.tensor_tensor(r1[x][:, :], f[x][:, :], pt[x][:, u, 0, :],
                                                    ALU.subtract).then_inc(r1_ready[x], 1)
                        for x in range(2):
                            pool.wait_ge(mid[x], n)
                            nc.gpsimd.tensor_tensor(r2[x][:, :], r1[x][:, :], pt[x][:, u, 1, :],
                                                    ALU.subtract).then_inc(r2_ready[x], 1)

            @block.vector
            def _(dve):
                dve.wait_ge(loaded, 16 * 3)
                with dve.Fori(0, BATCH) as b:
                    for u in range(TPB):
                        n = b * 2 + (u + 1)
                        nc.vector.tensor_copy(hs[:, u, :], c.h_t[:, bass.ts(b * 2 + u, TILE)]).then_inc(hs_ready, 1)
                        for x in range(2):
                            dve.wait_ge(mm[x], n)
                            dve.wait_ge(lo[x], n)
                            nc.vector.tensor_scalar(f[x][:, :], qk_ps[x][:, :], bias[x], None,
                                                    ALU.add).then_inc(f_ready[x], 1)
                            dve.wait_ge(f_ready[x], n)
                            nc.vector.sem_inc(ps_free[x], 1)
                        dve.wait_ge(v_mm, n)
                        dst = hd.v_all[:, bass.ts(b, HG), u * 4:(u + 1) * 4, :]
                        nc.vector.tensor_copy(dst, v_ps[:, :, :].rearrange("p k (g c) -> p g k c", g=HG)).then_inc(v_free, 1)


def load_group(sp, hd, g, q9, k9, done):
    rows = [[hd.parts[x, part, bass.ts(g, GCH), :].rearrange("(d h) t -> d (h t)", h=HG) for part in range(3)]
            for x in range(2)]
    for a in range(3):
        at = slice(a * 3 * HD, (a + 1) * 3 * HD)
        sp.dma_start(q9[at, :, :].rearrange("p h t -> p (h t)"),
                     rows[0][a].unsqueeze(0).to_broadcast([3, HD, HG * SEQ])).then_inc(done, 16)
        sp.dma_start(k9[at, :, :].rearrange("p h t -> p (h t)"),
                     hd.parts[1, :, bass.ts(g, GCH), :].rearrange("r (d h) t -> r d (h t)", h=HG)).then_inc(done, 16)


LOADS = 6 * 16


def stage_window_attention(c):
    tag = "L3"
    nc, ins = c.nc, c.ins
    W = 64
    QT = SEQ // P
    with ExitStack() as s0:
        hd = Heads(c, tag, s0)
        stage_project(c, tag, hd)
        with ExitStack() as s:
            def sb(name, shape, dt=F32):
                return s.enter_context(nc.sbuf_tensor(f"{tag}a_{name}", shape, dt))

            def psum(name, shape):
                return s.enter_context(nc.psum_tensor(f"{tag}a_{name}", shape, F32))

            def sem(name):
                return s.enter_context(nc.semaphore(f"{tag}a_{name}"))

            q9 = [sb(f"q9_{i}", [KP + 3, HG, SEQ], BF16) for i in range(3)]
            k9 = [sb(f"k9_{i}", [KP + 3, HG, SEQ], BF16) for i in range(3)]
            va = [sb(f"va_{i}", [P, QT, HG, 32]) for i in range(3)]
            mask_q = sb("mask_q", [P, 2, W + P], BF16)
            mask_k = sb("mask_k", [P, HG, P], BF16)
            mask_w = sb("mask_w", [P, HG, W], BF16)
            p = sb("p", [P, 2, HG, P])
            pw = sb("pw", [P, 2, HG, W])
            neg = sb("neg", [P, 2, HG, 4])
            np_ = sb("neg_parts", [16, 2, 3, P], BF16)
            nr = sb("neg_rest", [16, 2, 2, P])
            o_sb = sb("o_sb", [P, 2, TILE])
            mx_ps, st_ps, sw_ps = psum("mx_ps", [P, 2, TILE]), psum("st_ps", [P, 2, HG, P]), psum("sw_ps", [P, 2, TILE])
            acc, tr_ps = psum("acc", [P, 4, P]), psum("tr_ps", [P, TILE])
            names = ("set", "masks", "va_ready", "mx_mm", "mx_done", "neg_turned", "neg_chain", "neg_parts",
                     "neg_out", "st_ready", "exp_done", "pv_done", "acc_out")
            (set_, masks, va_ready, mx_mm, mx_done, neg_turned, neg_chain, neg_parts, neg_out, st_ready,
             exp_done, pv_done, acc_out) = (sem(n) for n in names)
            loaded = [sem(f"loaded{i}") for i in range(3)]
            neg_in = [sem(f"neg_in{i}") for i in range(2)]
            stored = [sem(f"stored{i}") for i in range(2)]
            SLOTS = 2 * QT

            with nc.Block() as block:
                @block.sync
                def _(sp):
                    for dst, name in ((mask_q, "L3_mask_q"), (mask_k, "L3_mask_k"), (mask_w, "L3_mask_w")):
                        sp.dma_start(dst[:, :, :], ins[name]).then_inc(masks, 16)
                    sp.wait_ge(set_, 9)
                    for g in range(3):
                        load_group(sp, hd, g, q9[g], k9[g], loaded[g])

                    def maxima(g, u, half):
                        rows = hd.neg[bass.ds(g * 6 + half * 3, 3), :]
                        sp.wait_ge(neg_parts, g * 2 + (half + 1))
                        sp.dma_start(rows.rearrange("r (q t) -> q r t", t=P), np_[:, half, :, :]).then_inc(neg_out, 16)
                        sp.wait_ge(neg_out, g * 32 + 16 * (half + 1))
                        sp.dma_start(q9[u][KP:KP + 3, :, half * TILE:(half + 1) * TILE],
                                     rows.rearrange("r (h t) -> r h t", h=HG)).then_inc(neg_in[half], 16)

                    def store(g, half):
                        sp.wait_ge(acc_out, g * 2 + (half + 2))
                        sp.dma_start(hd.out[bass.ts(g, P), half * TILE:(half + 1) * TILE],
                                     o_sb[:, half, :]).then_inc(stored[half], 16)

                    def group(g, u, last=False, load=True):
                        for half in range(2):
                            if not last:
                                maxima(g + 1, (u + 1) % 3, half)
                            store(g, half)
                        if load:
                            load_group(sp, hd, g + 3, q9[u], k9[u], loaded[u])
                    for half in range(2):
                        sp.sem_inc(stored[half], 16)
                        maxima(0, 0, half)
                    loop = (GROUPS - 3) // 3
                    with sp.Fori(0, loop) as i:
                        for u in range(3):
                            group(i * 3 + u, u)
                    for g in range(3 * loop, GROUPS):
                        group(g, g % 3, last=(g == GROUPS - 1), load=(g + 3 < GROUPS))
                    for half in range(2):
                        sp.wait_ge(stored[half], (GROUPS + 1) * 16)

                @block.gpsimd
                def _(pool):
                    for i in range(3):
                        nc.gpsimd.memset(k9[i][64:, :, :], 1.0).then_inc(set_, 1)
                        pool.wait_ge(set_, 3 * i + 1)
                        nc.gpsimd.memset(va[i][:, :, :, HD:2 * HD], 1.0).then_inc(set_, 1)
                        pool.wait_ge(set_, 3 * i + 2)
                        nc.gpsimd.memset(va[i][:, :, :, 2 * HD:], 0.0).then_inc(set_, 1)
                        pool.wait_ge(set_, 3 * i + 3)

                    def values(g, u):
                        nc.gpsimd.tensor_copy(va[u][:, :, :, 0:HD],
                                              hd.v_all[:, bass.ds(g, 1), :, :].rearrange(
                                                  "p g k (h d) -> p (g k) h d", h=HG)).then_inc(va_ready, 1)
                    for g in range(3):
                        values(g, g)

                    def next_values(g, u):
                        pool.wait_ge(pv_done, g * QT - (2 * QT - 2))
                        values(g, u)
                    with pool.Fori(1, GROUPS // 3) as i:
                        for u in range(3):
                            next_values(i * 3 + u, u)
                    next_values(GROUPS - 1, 0)

                @block.tensor
                def _(pe):
                    pe.sem_inc(exp_done, 2)
                    pe.sem_inc(pv_done, 2)
                    pe.sem_inc(acc_out, 1)

                    def scores(g, u, n):
                        q, x = divmod(n, 2)
                        back = W if q else 0
                        free = g * SLOTS + (n - 1)
                        if not (isinstance(g, int) and free <= 0):
                            pe.wait_ge(mx_done, free)
                        out = mx_ps[:, x, 0:2 * (W + P)].rearrange("p (h k) -> p h k", h=2)[:, :, W - back:]
                        nc.tensor.matmul(out, c.ident_bf[:, :], mask_q[:, :, W - back:], start=True, stop=False,
                                         skip_group_check=True)
                        for h in range(2):
                            mm = nc.tensor.matmul(out[:, h, :], q9[u][0:KP, 2 * x + h, q * P:(q + 1) * P],
                                                  k9[u][0:KP, 2 * x + h, q * P - back:(q + 1) * P], start=False,
                                                  stop=True, skip_group_check=True)
                        mm.then_inc(mx_mm, 1)

                    def turn(g, half):
                        pe.wait_ge(mx_done, g * SLOTS + 8 * (half + 1))
                        if not (isinstance(g, int) and g + half == 0):
                            pe.wait_ge(neg_parts, g * 2 + half)
                        nc.tensor.transpose(tr_ps[0:16, 0:P], neg[:, half, :, :].rearrange("p h q -> p (h q)"),
                                            c.ident[:, :]).then_inc(neg_turned, 1)

                    def score(g, u, m):
                        pe.wait_ge(exp_done, g * QT + (m + 1))
                        q = slice(m * P, (m + 1) * P)
                        if m:
                            nc.tensor.matmul(sw_ps[W:, m % 2, 0:HG * W], c.ident_bf[:, W:], mask_w[:, :, :], start=True,
                                             stop=False, skip_group_check=True)
                            for h in range(HG):
                                nc.tensor.matmul(sw_ps[W:, m % 2, h * W:(h + 1) * W], k9[u][:, h, m * P - W:m * P],
                                                 q9[u][:, h, m * P:m * P + W], start=False, stop=True,
                                                 skip_group_check=True)
                        nc.tensor.matmul(st_ps[:, m % 2, :, :], c.ident_bf[:, :], mask_k[:, :, :], start=True, stop=False,
                                         skip_group_check=True)
                        for h in range(HG):
                            mm = nc.tensor.matmul(st_ps[:, m % 2, h, :], k9[u][:, h, q], q9[u][:, h, q], start=False,
                                                  stop=True, skip_group_check=True)
                        mm.then_inc(st_ready, 1)

                    def weigh(g, u, m):
                        half, j = divmod(m, 4)
                        if j == 0:
                            pe.wait_ge(acc_out, g * 2 + (half + 1))
                        pe.wait_ge(exp_done, g * QT + (m + 3))
                        for h in range(HG):
                            mm = nc.tensor.matmul(acc[32 * h:32 * h + 32, j, :], va[u][:, m, h, :], p[:, m % 2, h, :],
                                                  start=True, stop=(m == 0), skip_group_check=True)
                        if m:
                            for h in range(HG):
                                mm = nc.tensor.matmul(acc[32 * h:32 * h + 32, j, 0:W], va[u][W:, m - 1, h, :],
                                                      pw[W:, m % 2, h, :], start=False, stop=True, skip_group_check=True)
                        mm.then_inc(pv_done, 1)

                    def group(g, u, turn_, ahead):
                        pe.wait_ge(va_ready, g + 1)
                        if ahead:
                            pe.wait_ge(loaded[(u + 1) % 3], (turn_ + (u + 1) // 3) * LOADS + LOADS)
                        for n in range(SLOTS):
                            if ahead:
                                scores(g + 1, (u + 1) % 3, n)
                                if n == 9:
                                    turn(g + 1, 0)
                            m = n // 2
                            if n % 8 == 0:
                                pe.wait_ge(neg_in[n // 8], g * 16 + 16)
                            if n % 2 == 0:
                                score(g, u, m)
                            elif m:
                                weigh(g, u, m - 1)
                        if ahead:
                            turn(g + 1, 1)
                        weigh(g, u, QT - 1)
                    pe.wait_ge(masks, 48)
                    pe.wait_ge(loaded[0], LOADS)
                    for n in range(SLOTS):
                        scores(0, 0, n)
                        if n == 9:
                            turn(0, 0)
                    turn(0, 1)
                    with pe.Fori(0, GROUPS // 3) as i:
                        for u in range(3):
                            group(i * 3 + u, u, i, True)
                    group(GROUPS - 1, 0, GROUPS // 3, False)

                @block.scalar
                def _(act):
                    nc.scalar.preload_act_table(ACT.Exp)
                    with act.Fori(0, GROUPS) as g:
                        for m in range(QT):
                            act.wait_ge(st_ready, g * QT + (m + 1))
                            act.wait_ge(pv_done, g * QT + (m + 1))
                            if m:
                                nc.scalar.activation(pw[W:, m % 2, :, :],
                                                     sw_ps[W:, m % 2, 0:HG * W].rearrange("p (h q) -> p h q", h=HG),
                                                     ACT.Exp, scale=SOFTMAX_SCALE)
                            nc.scalar.activation(p[:, m % 2, :, :], st_ps[:, m % 2, :, :], ACT.Exp,
                                                 scale=SOFTMAX_SCALE).then_inc(exp_done, 1)

                @block.vector
                def _(dve):
                    def maximum(g, n):
                        q, x = divmod(n, 2)
                        dve.wait_ge(mx_mm, g * SLOTS + (n + 1))
                        keys = mx_ps[:, x, 0:2 * (W + P)].rearrange("p (h k) -> p h k", h=2)[:, :, 0 if q else W:]
                        nc.vector.tensor_reduce(neg[:, q // 4, 2 * x:2 * x + 2, q % 4:q % 4 + 1], keys, AX.X, ALU.max,
                                                negate=True).then_inc(mx_done, 1)

                    def split(g, half):
                        dve.wait_ge(neg_turned, g * 2 + (half + 1))
                        if not isinstance(g, int):
                            dve.wait_ge(neg_out, g * 32 + 16 * (half - 1))
                        src, k = tr_ps[0:16, 0:P], g * 8 + half * 4
                        for r in range(3):
                            out = np_[:, half, r, :]
                            if r == 2:
                                nc.vector.tensor_copy(out, src).then_inc(neg_parts, 1)
                                break
                            nc.vector.tensor_copy(out, src).then_inc(neg_chain, 1)
                            dve.wait_ge(neg_chain, k + (2 * r + 1))
                            nc.vector.tensor_tensor(nr[:, half, r, :], src, out, ALU.subtract).then_inc(neg_chain, 1)
                            dve.wait_ge(neg_chain, k + (2 * r + 2))
                            src = nr[:, half, r, :]

                    def evacuate(g, half):
                        dve.wait_ge(pv_done, g * QT + (4 * half + 6))
                        dve.wait_ge(stored[half], g * 16 + 16)
                        nc.vector.tensor_copy(o_sb[:, half, :], acc[:, :, :].rearrange("p j t -> p (j t)")).then_inc(acc_out, 1)

                    def maxima(g, own):
                        for n in range(SLOTS):
                            maximum(g, n)
                            if n == 10:
                                split(g, 0)
                            if n == 11 and own is not None:
                                evacuate(own, 0)
                        split(g, 1)
                    maxima(0, None)
                    with dve.Fori(0, GROUPS - 1) as g:
                        maxima(g + 1, g)
                        evacuate(g, 1)
                    evacuate(GROUPS - 1, 0)
                    evacuate(GROUPS - 1, 1)
        stage_attention_out(c, tag, 3, hd)


def stage_attention_out(c, tag, layer, hd):
    nc, ins = c.nc, c.ins
    with ExitStack() as s:
        def sb(name, shape, dt=F32):
            return s.enter_context(nc.sbuf_tensor(f"{tag}o_{name}", shape, dt))

        def sem(name):
            return s.enter_context(nc.semaphore(f"{tag}o_{name}"))

        wo = sb("wo", [P, P])
        od, r, y, z = (sb(n, [P, 2] + ([2] if n == "od" else []) + [TILE]) for n in ("od", "r", "y", "z"))
        o_ps = s.enter_context(nc.psum_tensor(f"{tag}o_ps", [P, 2, TILE], F32))
        loaded = [sem(f"loaded{u}") for u in range(2)]
        w_loaded, rec, scaled, ready, mm, gated, added = (
            sem(n) for n in ("w_loaded", "rec", "scaled", "ready", "mm", "gated", "added"))
        with nc.Block() as block:
            @block.sync
            def _(sp):
                sp.dma_start(wo[:, :], ins[f"{tag}_wo"]).then_inc(w_loaded, 16)
                sp.sem_inc(ready, 2)
                with sp.Fori(0, BATCH) as b:
                    for u in range(TPB):
                        sp.wait_ge(ready, b * 2 + (u + 1))
                        rows = hd.out[bass.ts(b, HG * P), u * TILE:(u + 1) * TILE].rearrange("(h r) t -> h r t", r=32)
                        for k in range(2):
                            sp.dma_start(od[:, u, k, :], rows[:, k * HD:(k + 1) * HD, :]).then_inc(loaded[u], 16)

            @block.tensor
            def _(pe):
                pe.wait_ge(w_loaded, 16)
                with pe.Fori(0, BATCH) as b:
                    for u in range(TPB):
                        pe.wait_ge(ready, b * 2 + (u + 3))
                        nc.tensor.matmul(o_ps[:, u, :], wo[:, :], y[:, u, :], start=True, stop=True).then_inc(mm, 1)

            @block.vector
            def _(dve):
                with dve.Fori(0, BATCH) as b:
                    for u in range(TPB):
                        n = b * 2 + (u + 1)
                        dve.wait_ge(loaded[u], b * 32 + 32)
                        nc.vector.reciprocal(r[:, u, :], od[:, u, 1, :]).then_inc(rec, 1)
                        dve.wait_ge(rec, n)
                        nc.vector.tensor_tensor(r[:, u, :], od[:, u, 0, :], r[:, u, :], ALU.mult).then_inc(scaled, 1)
                        dve.wait_ge(scaled, n)
                        nc.vector.tensor_scalar(y[:, u, :], r[:, u, :], vec(c, f"{tag}_bv"), None,
                                                ALU.add).then_inc(ready, 1)
                    for u in range(TPB):
                        n = b * 2 + (u + 1)
                        tile = bass.ts(b * 2 + u, TILE)
                        dve.wait_ge(mm, n)
                        nc.vector.tensor_scalar(z[:, u, :], o_ps[:, u, :], vec(c, f"{tag}_bo"),
                                                c.mod[:, layer, GA, bass.ds(b * 2 + u, 1)], ALU.add,
                                                ALU.mult).then_inc(gated, 1)
                        dve.wait_ge(gated, n)
                        nc.vector.tensor_tensor(c.x_t[:, tile], c.x_t[:, tile], z[:, u, :], ALU.add).then_inc(added, 1)
                    dve.wait_ge(added, b * 2 + 2)


def layout_window_attention(a, d, bf):
    order = np.arange(P).reshape(4, HG, HD).transpose(0, 2, 1).reshape(P)
    d["L3_wq"], d["L3_wk"] = a["L3_attn_Wq"].T[:, order], a["L3_attn_Wk"].T[:, order]
    d["L3_wv"], d["L3_wo"] = a["L3_attn_Wv"].T, a["L3_attn_Wo"].T
    W, never = 64, -1e9
    q = np.arange(P)[:, None]
    k = np.arange(-W, P)[None]
    mask = np.where((k <= q) & (k > q - W), 0.0, never)
    d["L3_mask_q"] = np.tile(mask[:, None, :], (1, 2, 1)).astype(bf)
    d["L3_mask_k"] = np.tile(mask[:, W:].T[:, None, :], (1, HG, 1)).astype(bf)
    earlier = np.zeros((P, W))
    earlier[W:] = mask[:W, :W].T
    d["L3_mask_w"] = np.tile(earlier[:, None, :], (1, HG, 1)).astype(bf)


def stage_mamba(c):
    nc, ins = c.nc, c.ins
    NS = 16
    RANK = P // 16
    ROWS = 3 * 2 * NS
    STEPS = 2 * NS
    TAPS = 4
    with ExitStack() as s:
        def sb(name, shape, dt=F32):
            return s.enter_context(nc.sbuf_tensor(f"ma_{name}", shape, dt))

        def psum(name):
            return s.enter_context(nc.psum_tensor(f"ma_{name}", [P, 2, TILE], F32))

        def sem(name):
            return s.enter_context(nc.semaphore(f"ma_{name}"))

        w_in, w_x = sb("w_in", [P, 4, P]), sb("w_x", [P, 2, ROWS + RANK])
        w_dt, w_out = sb("w_dt", [ROWS + RANK, 2, P]), sb("w_out", [P, 2, P])
        pick = sb("pick", [ROWS, 2 * NS, P], BF16)
        minus = sb("minus", [ROWS, 2])
        a, one = sb("a", [P, NS, 2]), sb("one", [P, 1])
        raw = sb("raw", [P, 2, TAPS - 1 + SEQ])
        conv, zs, dtu, yz = (sb(n, [P, 2, SEQ]) for n in ("conv", "zs", "dtu", "yz"))
        nab = conv
        u, dt = sb("u", [P, 2 * 2 * SEQ]), sb("dt", [P, 2 * 2 * SEQ])
        bc, rest = sb("bc", [ROWS + RANK, SEQ]), sb("rest", [ROWS, SEQ])
        part, bc3 = sb("part", [ROWS, SEQ], BF16), sb("bc3", [ROWS, 2 * SEQ], BF16)
        da, dbu = sb("da", [P, 4, SEQ]), sb("dbu", [P, 2, SEQ])
        bsb, state, hc = sb("bsb", [P, 4, SEQ]), sb("state", [P, 2, SEQ]), sb("hc", [P, 2, SEQ])
        in_ps, b_ps, c_ps, y_ps = (psum(n) for n in ("in_ps", "b_ps", "c_ps", "y_ps"))
        names = ("loaded", "set", "in_mm", "in_read", "z_mm", "z_read", "zs_ready", "conv_step", "u_ready", "xp_mm", "bc_ready", "split_step",
                 "dt_mm", "low_ready", "nab_ready", "exp_low", "ln_done", "dt_ready", "dtu_ready", "b_mm", "b_read",
                 "c_mm", "da_ready", "dbu_ready", "scan_done", "hc_ready", "sum_mm", "yd_ready", "yz_ready",
                 "o_mm", "x_ready", "act_go")
        S = {n: sem(n) for n in names}
        with nc.Block() as block:
            @block.sync
            def _(sp):
                for dst, name in ((w_in, "w_in"), (w_x, "w_x"), (w_dt, "w_dt"), (w_out, "w_out"), (pick, "pick")):
                    sp.dma_start(dst[:, :, :], ins[f"ma_{name}"]).then_inc(S["loaded"], 16)
                sp.dma_start(minus[:, :], ins["ma_minus"]).then_inc(S["loaded"], 16)

            def both(b, h, t=0, n=SEQ):
                return bass.ds((b % 2) * (2 * SEQ) + h * SEQ + t * TILE, n)

            def parts_of(b, t=0, n=SEQ):
                return bass.ds((b % 2) * SEQ + t * TILE, n)

            def rows(scans, eng):
                with eng.Fori(0, BATCH - 1) as b:
                    scans(b, True)
                scans(BATCH - 1, False)

            @block.tensor
            def _(pe):
                def tokens(b, t):
                    return c.h_t[:, bass.ds(b * SEQ + t * TILE, TILE)]

                def conv_in(b, i, first):
                    h, t = divmod(i, 2)
                    if i >= 2:
                        pe.wait_ge(S["in_read"], b * 4 + (i - 1))
                    elif not first:
                        pe.wait_ge(S["low_ready"], b * 4 + (i - 1))
                    nc.tensor.matmul(in_ps[:, t, :], w_in[:, h, :], tokens(b, t), start=True,
                                     stop=True).then_inc(S["in_mm"], 1)

                def gate_in(b, i, last):
                    h, t = divmod(i, 2)
                    if i >= 2:
                        pe.wait_ge(S["z_read"], b * 4 + (i - 1))
                    elif last:
                        pe.wait_ge(S["low_ready"], b * 4 + (3 + i))
                    else:
                        pe.wait_ge(S["in_read"], b * 4 + (7 + i))
                    nc.tensor.matmul(in_ps[:, t, :], w_in[:, 2 + h, :], tokens(b, t), start=True,
                                     stop=True).then_inc(S["z_mm"], 1)

                def x_proj(b, first):
                    pe.wait_ge(S["u_ready"], b * 2 + 2)
                    for t in range(2):
                        if first:
                            pe.wait_ge(S["in_read"], 3 + t)
                        else:
                            pe.wait_ge(S["z_read"], b * 4 + (t - 1))
                        for h in range(2):
                            mm = nc.tensor.matmul(in_ps[0:ROWS + RANK, t, :], w_x[:, h, :], u[:, both(b, h, t, TILE)],
                                                  start=(h == 0), stop=(h == 1))
                        mm.then_inc(S["xp_mm"], 1)

                def dt_proj(b, h):
                    for t in range(2):
                        if h == 0:
                            pe.wait_ge(S["bc_ready"], b * 2 + (t + 1))
                        else:
                            pe.wait_ge(S["low_ready"], b * 4 + (t + 1))
                        nc.tensor.matmul(in_ps[:, t, :], w_dt[:, h, :], bc[:, t * TILE:(t + 1) * TILE],
                                         start=True, stop=True).then_inc(S["dt_mm"], 1)

                prepare = {}
                for i in range(4):
                    prepare[(0, 1, 4, 5)[i]] = lambda b, first, i=i: conv_in(b, i, first)
                prepare[15] = x_proj
                prepare[18] = lambda b, first: dt_proj(b, 0)
                prepare[21] = lambda b, first: dt_proj(b, 1)

                def spread(row, b, ps):
                    for t in range(2):
                        mm = nc.tensor.matmul(ps[:, t, :], pick[:, row, :], bc3[:, parts_of(b, t, TILE)],
                                              start=True, stop=True)
                    return mm

                def spread_b(b, j):
                    pe.wait_ge(S["b_read"], b * STEPS + (j + 1))
                    spread(j % NS, b, b_ps).then_inc(S["b_mm"], 1)

                def spread_c(b, j):
                    pe.wait_ge(S["hc_ready"], b * STEPS + (j + 2))
                    spread(NS + j % NS, b, c_ps).then_inc(S["c_mm"], 1)

                def scans(b, more):
                    for j in range(STEPS):
                        if j + 3 < STEPS:
                            spread_b(b, j + 3)
                        elif more:
                            pe.wait_ge(S["split_step"], b * 4 + 8)
                            spread_b(b + 1, j + 3 - STEPS)
                        if j + 1 < STEPS:
                            spread_c(b, j + 1)
                        elif more:
                            spread_c(b + 1, 0)
                        if j == NS:
                            pe.wait_ge(S["yd_ready"], b * 2 + 1)
                        pe.wait_ge(S["hc_ready"], b * STEPS + (j + 3))
                        for t in range(2):
                            mm = nc.tensor.matmul(y_ps[:, t, :], c.ident[:, :], hc[:, j % 2, t * TILE:(t + 1) * TILE],
                                                  start=(j % NS == 0), stop=(j % NS == NS - 1))
                        mm.then_inc(S["sum_mm"], 1)
                        if more and j in prepare:
                            prepare[j](b + 1, False)
                        if j in (7, 8, 10, 11):
                            gate_in(b, (7, 8, 10, 11).index(j), not more)
                    pe.wait_ge(S["yz_ready"], b * 2 + 4)
                    for t in range(2):
                        for h in range(2):
                            mm = nc.tensor.matmul(y_ps[:, t, :], w_out[:, h, :], yz[:, h, t * TILE:(t + 1) * TILE],
                                                  start=(h == 0), stop=(h == 1))
                        mm.then_inc(S["o_mm"], 1)
                    pe.wait_ge(S["x_ready"], b * 2 + 2)

                pe.wait_ge(S["loaded"], 16 * 6)
                pe.sem_inc(S["b_read"], 1)
                pe.sem_inc(S["hc_ready"], 2)
                pe.sem_inc(S["sum_mm"], 2)
                pe.sem_inc(S["scan_done"], 4)
                pe.sem_inc(S["dbu_ready"], 4)
                pe.sem_inc(S["yz_ready"], 2)
                for piece in sorted(prepare):
                    prepare[piece](0, True)
                pe.wait_ge(S["split_step"], 4)
                spread_b(0, 0)
                spread_c(0, 0)
                spread_b(0, 1)
                spread_b(0, 2)
                rows(scans, pe)

            @block.scalar
            def _(act):
                def go():
                    act.sem_inc(S["act_go"], 1)

                def conv_copy(b, i, first):
                    h, t = divmod(i, 2)
                    if i == 0 and not first:
                        act.wait_ge(S["conv_step"], b * 2 * TAPS)
                    act.wait_ge(S["in_mm"], b * 4 + (i + 1))
                    at = TAPS - 1 + t * TILE
                    nc.scalar.copy(raw[:, h, at:at + TILE], in_ps[:, t, :]).then_inc(S["in_read"], 1)

                def gate(b, i):
                    h, t = divmod(i, 2)
                    act.wait_ge(S["z_mm"], b * 4 + (i + 1))
                    nc.scalar.copy(zs[:, h, t * TILE:(t + 1) * TILE], in_ps[:, t, :]).then_inc(S["z_read"], 1)

                def gate_silu(b):
                    for h in range(2):
                        act.wait_ge(S["z_read"], b * 4 + (2 * h + 2))
                        nc.scalar.activation(zs[:, h, :], zs[:, h, :], ACT.Silu).then_inc(S["zs_ready"], 1)

                def conv_out(b, first):
                    for h in range(2):
                        act.wait_ge(S["conv_step"], b * 2 * TAPS + (h + 1) * TAPS)
                        go()
                        nc.scalar.activation(u[:, both(b, h)], conv[:, h, :], ACT.Silu,
                                             bias=vec(c, f"conv_b{h}")).then_inc(S["u_ready"], 1)

                def bc_copy(b, first):
                    for t in range(2):
                        act.wait_ge(S["xp_mm"], b * 2 + (t + 1))
                        nc.scalar.copy(bc[:, t * TILE:(t + 1) * TILE], in_ps[0:ROWS + RANK, t, :]).then_inc(S["bc_ready"], 1)

                def dt_low(b, h):
                    for t in range(2):
                        act.wait_ge(S["dt_mm"], b * 4 + (2 * h + t + 1))
                        go()
                        nc.scalar.activation(dt[:, both(b, h, t, TILE)], in_ps[:, t, :], ACT.Identity,
                                             bias=vec(c, f"dt_b{h}")).then_inc(S["low_ready"], 1)

                def dt_log(b, first):
                    for h in range(2):
                        act.wait_ge(S["nab_ready"], b * 2 + (h + 1))
                        nc.scalar.activation(nab[:, h, :], nab[:, h, :], ACT.Exp).then_inc(S["exp_low"], 1)
                        act.wait_ge(S["exp_low"], b * 2 + (h + 1))
                        nc.scalar.activation(nab[:, h, :], nab[:, h, :], ACT.Ln,
                                             bias=one[:, 0:1]).then_inc(S["ln_done"], 1)

                prepare = {}
                for i in range(4):
                    prepare[(3, 4, 7, 8)[i]] = lambda b, first, i=i: conv_copy(b, i, first)
                prepare[14] = conv_out
                prepare[18] = bc_copy
                prepare[21] = lambda b, first: dt_low(b, 0)
                prepare[24] = lambda b, first: dt_low(b, 1)
                prepare[27] = dt_log

                def spread_copy(b, j):
                    act.wait_ge(S["b_mm"], b * STEPS + (j + 1))
                    act.wait_ge(S["dbu_ready"], b * STEPS + (j + 1))
                    nc.scalar.copy(bsb[:, j % 4, :], b_ps[:, :, :].rearrange("p t n -> p (t n)")).then_inc(S["b_read"], 1)

                def scans(b, more):
                    for j in range(STEPS):
                        h, n = divmod(j, NS)
                        if n == 0:
                            act.wait_ge(S["dt_ready"], b * 2 + (h + 1))
                        spread_copy(b, j)
                        act.wait_ge(S["scan_done"], b * STEPS + (j + 1))
                        go()
                        nc.scalar.activation(da[:, j % 4, :], dt[:, both(b, h)], ACT.Exp,
                                             scale=a[:, n, h:h + 1]).then_inc(S["da_ready"], 1)
                        if j in (10, 11, 13, 14):
                            if j == 10:
                                act.wait_ge(S["yz_ready"], b * 2 + 2)
                            gate(b, (10, 11, 13, 14).index(j))
                        if more and j in prepare:
                            prepare[j](b + 1, False)
                        if j == 14:
                            gate_silu(b)
                            nc.scalar.preload_act_table_set(LN_EXP_SET)

                first = VECS.index("A_log00")
                nc.scalar.activation(a[:, :, :].rearrange("p s h -> p (s h)"), c.vecs[:, first:first + 2 * NS],
                                     ACT.Exp).then_inc(S["set"], 1)
                act.wait_ge(S["set"], 4)
                for piece in sorted(prepare):
                    prepare[piece](0, True)
                    if piece == 14:
                        nc.scalar.preload_act_table_set(LN_EXP_SET)
                rows(scans, act)

            @block.gpsimd
            def _(pool):
                def step_in(b, h):
                    pool.wait_ge(S["dt_ready"], b * 2 + (h + 1))
                    nc.gpsimd.tensor_tensor(dtu[:, h, :], dt[:, both(b, h)], u[:, both(b, h)],
                                            ALU.mult).then_inc(S["dtu_ready"], 1)

                def scans(b, more):
                    for j in range(STEPS):
                        if j % NS == 0:
                            pool.wait_ge(S["dtu_ready"], b * 2 + (j // NS + 1))
                        pool.wait_ge(S["b_read"], b * STEPS + (j + 2))
                        pool.wait_ge(S["scan_done"], b * STEPS + (j + 3))
                        nc.gpsimd.tensor_tensor(dbu[:, j % 2, :], dtu[:, j // NS, :], bsb[:, j % 4, :],
                                                ALU.mult).then_inc(S["dbu_ready"], 1)
                        if j == 7:
                            pool.wait_ge(S["dbu_ready"], b * STEPS + 4)
                            step_in(b, 1)
                        if j == 29 and more:
                            pool.wait_ge(S["dbu_ready"], b * STEPS + (NS + 4))
                            step_in(b + 1, 0)

                step_in(0, 0)
                rows(scans, pool)

            @block.vector
            def _(dve):
                tt, ts, stt = nc.vector.tensor_tensor, nc.vector.tensor_scalar, nc.vector.scalar_tensor_tensor

                def conv_tap(b, h, k, first):
                    w = vec(c, f"conv_w{k}{h}")
                    if k == 0:
                        if not first:
                            dve.wait_ge(S["dt_ready"], b * 2)
                        dve.wait_ge(S["in_read"], b * 4 + (2 * h + 2))
                        last = ts(conv[:, h, :], raw[:, h, 0:SEQ], w, None, ALU.mult)
                    else:
                        dve.wait_ge(S["conv_step"], b * 2 * TAPS + (h * TAPS + k))
                        last = stt(conv[:, h, :], raw[:, h, k:k + SEQ], w, conv[:, h, :], ALU.mult, ALU.add)
                    last.then_inc(S["conv_step"], 1)

                def split(b, k):
                    if k:
                        dve.wait_ge(S["split_step"], b * 4 + k)
                    else:
                        dve.wait_ge(S["bc_ready"], b * 2 + 2)
                    (lambda: nc.vector.tensor_copy(part[:, :], bc[0:ROWS, :]),
                     lambda: stt(rest[:, :], part[:, :], minus[:, 0:1], bc[0:ROWS, :], ALU.mult, ALU.add),
                     lambda: nc.vector.tensor_copy(part[:, :], rest[:, :]),
                     lambda: stt(bc3[:, parts_of(b)], part[:, :], minus[:, 1:2], rest[:, :], ALU.mult,
                                 ALU.add))[k]().then_inc(S["split_step"], 1)

                def softplus_in(b, h):
                    dve.wait_ge(S["low_ready"], b * 4 + (2 * h + 2))
                    x = dt[:, both(b, h)]
                    stt(nab[:, h, :], x, -1.0, x, ALU.mult, ALU.min).then_inc(S["nab_ready"], 1)

                def softplus_out(b, h):
                    dve.wait_ge(S["ln_done"], b * 2 + (h + 1))
                    x = dt[:, both(b, h)]
                    stt(x, x, 0.0, nab[:, h, :], ALU.max, ALU.add).then_inc(S["dt_ready"], 1)

                prepare = {}
                for i in range(2 * TAPS):
                    prepare[3 + i] = lambda b, first, i=i: conv_tap(b, i // TAPS, i % TAPS, first)
                for k in range(4):
                    prepare[17 + k] = lambda b, first, k=k: split(b, k)
                for h in range(2):
                    prepare[21 + 3 * h] = lambda b, first, h=h: softplus_in(b, h)
                    prepare[27 + h] = lambda b, first, h=h: softplus_out(b, h)

                def scans(b, more):
                    for j in range(STEPS):
                        h, n = divmod(j, NS)
                        dve.wait_ge(S["da_ready"], b * STEPS + (j + 1))
                        dve.wait_ge(S["dbu_ready"], b * STEPS + (j + 5))
                        dve.wait_ge(S["hc_ready"], b * STEPS + (j + 1))
                        nc.vector.tensor_tensor_scan(state[:, j % 2, :], da[:, j % 4, :], dbu[:, j % 2, :], 0.0,
                                                     ALU.mult, ALU.add).then_inc(S["scan_done"], 1)
                        if more and j in prepare:
                            prepare[j](b + 1, False)
                        dve.wait_ge(S["scan_done"], b * STEPS + (j + 5))
                        dve.wait_ge(S["c_mm"], b * STEPS + (j + 1))
                        dve.wait_ge(S["sum_mm"], b * STEPS + (j + 1))
                        tt(hc[:, j % 2, :], state[:, j % 2, :], c_ps[:, :, :].rearrange("p t n -> p (t n)"),
                           ALU.mult).then_inc(S["hc_ready"], 1)
                        if n == NS - 1:
                            dve.wait_ge(S["sum_mm"], b * STEPS + (j + 3))
                            stt(yz[:, h, :], u[:, both(b, h)], vec(c, f"D{h}"),
                                y_ps[:, :, :].rearrange("p t n -> p (t n)"), ALU.mult, ALU.add).then_inc(S["yd_ready"], 1)
                            dve.wait_ge(S["yd_ready"], b * 2 + (h + 1))
                            dve.wait_ge(S["zs_ready"], b * 2 + (h + 1))
                            tt(yz[:, h, :], yz[:, h, :], zs[:, h, :], ALU.mult).then_inc(S["yz_ready"], 1)
                    for t in range(2):
                        dve.wait_ge(S["o_mm"], b * 2 + (t + 1))
                        tile = bass.ds(b * SEQ + t * TILE, TILE)
                        stt(c.x_t[:, tile], y_ps[:, t, :], c.mod[:, 0, GA, bass.ds(b * 2 + t, 1)], c.x_t[:, tile],
                            ALU.mult, ALU.add).then_inc(S["x_ready"], 1)

                nc.vector.memset(one[:, :], 1.0).then_inc(S["set"], 1)
                nc.vector.memset(raw[:, :, 0:TAPS - 1], 0.0).then_inc(S["set"], 1)
                dve.wait_ge(S["set"], 3)
                ts(a[:, :, :], a[:, :, :], -1.0, None, ALU.mult).then_inc(S["set"], 1)
                dve.wait_ge(S["loaded"], 16 * 6)
                for piece in sorted(prepare):
                    prepare[piece](0, True)
                rows(scans, dve)


def layout_mamba(a, d, bf):
    d["ma_w_in"] = a["L0_attn_in_proj_w"].reshape(P, 4, P)
    w = a["L0_attn_x_proj_w"].reshape(2, P, -1).transpose(1, 0, 2)
    rank = P // 16
    bc = w[:, :, rank:]
    d["ma_w_x"] = np.concatenate([bc, bc, bc, w[:, :, :rank]], 2)
    d["ma_w_dt"] = np.concatenate([np.zeros((96, 2, P), np.float32),
                                   a["L0_attn_dt_proj_w"].reshape(rank, 2, P)])
    d["ma_w_out"] = a["L0_attn_out_proj_w"].reshape(2, P, P).transpose(1, 0, 2)
    rows = np.arange(96)
    pick = (rows[:, None] % 32 == np.arange(32)[None]).astype(bf)
    d["ma_pick"] = np.repeat(pick[:, :, None], P, 2)
    d["ma_minus"] = -np.stack([rows >= 32, rows >= 64], 1).astype(np.float32)


def stage_slots(c):
    nc, ins = c.nc, c.ins
    G = 16
    SLOTS = P // 2
    GROUPS = TOK // G
    GPT = P // G
    PAIRS = SLOTS // 2
    F = P // 2
    with ExitStack() as s:
        def sb(name, shape, dt=F32):
            return s.enter_context(nc.sbuf_tensor(f"f0_{name}", shape, dt))

        def sem(name):
            return s.enter_context(nc.semaphore(f"f0_{name}"))

        ctrl, tie, parity = sb("ctrl", [P, P]), sb("tie", [P, G]), sb("parity", [P, 2])
        quarter = sb("quarter", [P, P // 32])
        f1, f2, bias = sb("f1", [P, SLOTS, F]), sb("f2", [P, PAIRS, P]), sb("bias", [P, PAIRS])
        perm_t, top = sb("perm_t", [P, TOK]), sb("top", [P, GROUPS])
        sel = sb("sel", [P, GROUPS, SLOTS])
        loaded, weights = sem("loaded"), sem("weights")
        names = ("lg_mm", "lg_read", "perm_step", "p_turned", "x_turned", "p_ready", "xk_ready", "sel_mm",
                 "sel_even", "sel_odd", "up_mm", "inner_ready", "down_mm", "out_ready", "o_turned", "turned_even",
                 "turned_odd", "o_mm", "x_ready")
        S = {n: sem(n) for n in names}

        with ExitStack() as s1, nc.Block() as block:
            lg_ps = s1.enter_context(nc.psum_tensor("f0_lg_ps", [P, 2, TILE], F32))

            @block.sync
            def _(sp):
                for dst, name in ((ctrl, "ctrl"), (tie, "tie"), (parity, "parity"), (quarter, "quarter"), (bias, "bias")):
                    sp.dma_start(dst[:, :], ins[f"f0_{name}"]).then_inc(loaded, 16)
                sp.dma_start(f1[:, :, :], ins["f0_f1"]).then_inc(weights, 16)
                sp.dma_start(f2[:, :, :], ins["f0_f2"]).then_inc(weights, 16)

            @block.tensor
            def _(pe):
                pe.wait_ge(loaded, 16 * 5)
                for t in range(NT):
                    if t >= 2:
                        pe.wait_ge(S["lg_read"], t - 1)
                    nc.tensor.matmul(lg_ps[:, t % 2, :], ctrl[:, :], c.h_t[:, t * TILE:(t + 1) * TILE],
                                     start=True, stop=True).then_inc(S["lg_mm"], 1)

            @block.vector
            def _(dve):
                tt = nc.vector.tensor_tensor
                dve.wait_ge(loaded, 16 * 5)
                per = TILE // G
                for t in range(NT):
                    dve.wait_ge(S["lg_mm"], t + 1)
                    at = slice(t * TILE, (t + 1) * TILE)
                    view = perm_t[:, at].rearrange("p (g k) -> p g k", k=G)
                    tt(view, lg_ps[:, t % 2, :].rearrange("p (g k) -> p g k", k=G),
                       tie[:, :].unsqueeze(1).to_broadcast([P, per, G]), ALU.add).then_inc(S["lg_read"], 1)
                step = Chain(dve, S["perm_step"])
                dve.wait_ge(S["lg_read"], NT)
                groups = perm_t[:, :].rearrange("p (g k) -> p g k", k=G)
                step(nc.vector.reduce_max(top[:, :], groups, AX.X))
                step(tt(groups, groups, top[:, :].unsqueeze(2).to_broadcast([P, GROUPS, G]), ALU.is_equal))
                pairs = perm_t[:, :].rearrange("p (m r k) -> p m r k", r=2, k=G)
                for r in range(2):
                    nc.vector.tensor_scalar(pairs[:, :, r, :], pairs[:, :, r, :], parity[:, r:r + 1], None,
                                            ALU.mult).then_inc(S["perm_step"], 1)
                dve.wait_ge(S["perm_step"], 4)

        with ExitStack() as s2, nc.Block() as block:
            pt_ps, xt_ps, sel_ps = (s2.enter_context(nc.psum_tensor(f"f0_{n}", [P, 2, TILE], F32))
                                    for n in ("pt_ps", "xt_ps", "sel_ps"))
            perm = s2.enter_context(nc.sbuf_tensor("f0_perm", [P, 2, P // 32, P], F32))
            xk = s2.enter_context(nc.sbuf_tensor("f0_xk", [P, 2, P], F32))

            def copied(eng, k):
                eng.wait_ge(S["sel_odd" if k % 2 else "sel_even"], k // 2 + 1)

            def take(copy, k):
                copy(sel[:, k * GPT:(k + 1) * GPT, :].rearrange("p g e -> p (g e)"), sel_ps[:, k % 2, :]).then_inc(S["sel_odd" if k % 2 else "sel_even"], 1)

            @block.tensor
            def _(pe):
                def turn(k):
                    at = slice(k * P, (k + 1) * P)
                    if k >= 2:
                        pe.wait_ge(S["p_ready"], k - 1)
                        pe.wait_ge(S["xk_ready"], k - 1)
                    nc.tensor.transpose(pt_ps[:, k % 2, 0:P], perm_t[:, at], c.ident[:, :]).then_inc(S["p_turned"], 1)
                    nc.tensor.transpose(xt_ps[:, k % 2, 0:P], c.h_t[:, at], c.ident[:, :]).then_inc(S["x_turned"], 1)
                turn(0)
                for k in range(KT):
                    if k + 1 < KT:
                        turn(k + 1)
                    pe.wait_ge(S["p_ready"], k + 1)
                    pe.wait_ge(S["xk_ready"], k + 1)
                    if k >= 2:
                        copied(pe, k - 2)
                    nc.tensor.matmul(sel_ps[:, k % 2, :], xk[:, k % 2, :], perm[:, k % 2, :, :], start=True,
                                     stop=True).then_inc(S["sel_mm"], 1)

            @block.scalar
            def _(act):
                for k in range(KT):
                    act.wait_ge(S["x_turned"], k + 1)
                    if k >= 2:
                        act.wait_ge(S["sel_mm"], k - 1)
                    nc.scalar.copy(xk[:, k % 2, :], xt_ps[:, k % 2, 0:P]).then_inc(S["xk_ready"], 1)
                    if k % 2 == 1:
                        act.wait_ge(S["sel_mm"], k)
                        take(nc.scalar.copy, k - 1)

            @block.vector
            def _(dve):
                shape = [P, P // 32, P]
                for k in range(KT):
                    dve.wait_ge(S["p_turned"], k + 1)
                    if k >= 2:
                        dve.wait_ge(S["sel_mm"], k - 1)
                    nc.vector.tensor_tensor(perm[:, k % 2, :, :], pt_ps[:, k % 2, 0:P].unsqueeze(1).to_broadcast(shape),
                                            quarter[:, :].unsqueeze(2).to_broadcast(shape),
                                            ALU.mult).then_inc(S["p_ready"], 1)
                    if k % 2 == 0 and k:
                        dve.wait_ge(S["sel_mm"], k)
                        take(nc.vector.tensor_copy, k - 1)
                dve.wait_ge(S["sel_mm"], KT)
                take(nc.vector.tensor_copy, KT - 1)

        with ExitStack() as s3, nc.Block() as block:
            up_ps = s3.enter_context(nc.psum_tensor("f0_up_ps", [P, 2, TILE], F32))
            down_ps = s3.enter_context(nc.psum_tensor("f0_down_ps", [P, 2, 2, TILE], F32))
            inner = s3.enter_context(nc.sbuf_tensor("f0_inner", [P, 2, GROUPS], F32))

            @block.tensor
            def _(pe):
                def up(i):
                    if i >= 2:
                        pe.wait_ge(S["inner_ready"], i - 1)
                    for r in range(2):
                        mm = nc.tensor.matmul(up_ps[r * F:(r + 1) * F, i % 2, 0:GROUPS], f1[:, 2 * i + r, :],
                                              sel[:, :, 2 * i + r], start=True, stop=True)
                    mm.then_inc(S["up_mm"], 1)
                pe.wait_ge(weights, 32)
                up(0)
                for i in range(PAIRS):
                    if i + 1 < PAIRS:
                        up(i + 1)
                    pe.wait_ge(S["inner_ready"], i + 1)
                    if i >= 2:
                        pe.wait_ge(S["out_ready"], i - 1)
                    for r in range(2):
                        mm = nc.tensor.matmul(down_ps[:, i % 2, r, 0:GROUPS], f2[r * F:(r + 1) * F, i, :],
                                              inner[r * F:(r + 1) * F, i % 2, :], start=True, stop=True)
                    mm.then_inc(S["down_mm"], 1)

            @block.scalar
            def _(act):
                for i in range(PAIRS):
                    act.wait_ge(S["up_mm"], i + 1)
                    if i >= 2:
                        act.wait_ge(S["down_mm"], i - 1)
                    nc.scalar.activation(inner[:, i % 2, :], up_ps[:, i % 2, 0:GROUPS], ACT.Relu,
                                         bias=bias[:, i:i + 1]).then_inc(S["inner_ready"], 1)

            @block.vector
            def _(dve):
                for i in range(PAIRS):
                    dve.wait_ge(S["down_mm"], i + 1)
                    nc.vector.tensor_copy(sel[:, :, 2 * i:2 * i + 2].rearrange("p g r -> p r g"), down_ps[:, i % 2, :, 0:GROUPS]).then_inc(S["out_ready"], 1)

        with ExitStack() as s4, nc.Block() as block:
            tr_ps, o_ps = (s4.enter_context(nc.psum_tensor(f"f0_{n}", [P, 2, TILE], F32)) for n in ("tr_ps", "o_ps"))
            out_rows = s4.enter_context(nc.sbuf_tensor("f0_out_rows", [P, 2, TILE], F32))
            parts = P // 32

            def turned(k):
                return S["turned_odd" if k % 2 else "turned_even"]

            def take_rows(eng, copy, k):
                eng.wait_ge(S["o_turned"], k + 1)
                if k >= 2:
                    eng.wait_ge(S["o_mm"], k - 1)
                copy(out_rows[:, k % 2, :], tr_ps[:, k % 2, :]).then_inc(turned(k), 1)

            @block.tensor
            def _(pe):
                def turn(k):
                    if k >= 2:
                        pe.wait_ge(turned(k), k // 2)
                    for j in range(parts):
                        g = k * GPT + 2 * j
                        mm = nc.tensor.transpose(tr_ps[:, k % 2, j * P:(j + 1) * P],
                                                 sel[:, g:g + 2, :].rearrange("p g e -> p (g e)"), c.ident[:, :])
                    mm.then_inc(S["o_turned"], 1)
                turn(0)
                for k in range(KT):
                    if k + 1 < KT:
                        turn(k + 1)
                    t, q = divmod(k, TILE // P)
                    pe.wait_ge(turned(k), k // 2 + 1)
                    if q == 0 and t >= 2:
                        pe.wait_ge(S["x_ready"], t - 1)
                    for j in range(parts):
                        at = k * P + j * 32
                        mm = nc.tensor.matmul(o_ps[:, t % 2, q * P + j * 32:q * P + (j + 1) * 32],
                                              out_rows[:, k % 2, j * P:(j + 1) * P], perm_t[:, at:at + 32],
                                              start=True, stop=True)
                    mm.then_inc(S["o_mm"], 1)

            @block.scalar
            def _(act):
                for k in range(0, KT, 2):
                    take_rows(act, nc.scalar.copy, k)

            @block.vector
            def _(dve):
                for k in range(1, KT, 2):
                    take_rows(dve, nc.vector.tensor_copy, k)
                    t = k * P // TILE
                    if (k + 1) * P % TILE == 0:
                        dve.wait_ge(S["o_mm"], k + 1)
                        at = slice(t * TILE, (t + 1) * TILE)
                        nc.vector.scalar_tensor_tensor(c.x_t[:, at], o_ps[:, t % 2, :], c.mod[:, 0, GB, t:t + 1],
                                                       c.x_t[:, at], ALU.mult, ALU.add).then_inc(S["x_ready"], 1)


def layout_slots(a, d, bf):
    ctrl = a["L0_ffn_controller"].reshape(P, 64)
    d["f0_ctrl"] = np.concatenate([ctrl, ctrl], 1)
    d["f0_tie"] = np.tile(np.linspace(0.0, 1e-6, 16, dtype=np.float32), (P, 1))
    rows = np.arange(P)
    d["f0_parity"] = (rows[:, None] // 64 == np.arange(2)[None]).astype(np.float32)
    d["f0_quarter"] = (rows[:, None] // 32 == np.arange(4)[None]).astype(np.float32)
    d["f0_f1"] = a["L0_ffn_f1"].reshape(P, 64, 64)
    d["f0_f2"] = a["L0_ffn_f2"].reshape(32, P, P).transpose(1, 0, 2)
    d["f0_bias"] = a["L0_ffn_bias"].reshape(32, P).T


def build(nc, ins, out):
    with ExitStack() as ctx:
        c = Core(nc, ctx, ins)
        stage_setup(c)
        adaln(c, 0, SA, CA)
        stage_mamba(c)
        adaln(c, 0, SB, CB)
        stage_slots(c)
        adaln(c, 1, SA, CA)
        stage_head_attention(c)
        adaln(c, 1, SB, CB)
        stage_moe1(c)
        recycle_semaphores(c)
        adaln(c, 2, SA, CA)
        stage_linear_attention(c)
        adaln(c, 2, SB, CB)
        stage_moe2(c)
        recycle_semaphores(c)
        adaln(c, 3, SA, CA)
        stage_window_attention(c)
        adaln(c, 3, SB, CB)
        stage_moe3(c)
        stage_store(c, out)


def rope_swap(v):
    return v.reshape(v.shape[:-1] + (P // 8, 2, 4))[..., ::-1, :].reshape(v.shape)


def vectors(a):
    v = {}
    bgu = a["L1_ffn_bgu"]
    for e in range(16):
        v[f"bg{e}"], v[f"bu{e}"] = bgu[e, ::2], bgu[e, 1::2]
    for h in range(2):
        half = slice(h * P, (h + 1) * P)
        for k in range(4):
            v[f"conv_w{k}{h}"] = a["L0_attn_conv_w"][half, k]
        v[f"conv_b{h}"] = a["L0_attn_conv_b"][half]
        v[f"dt_b{h}"] = a["L0_attn_dt_proj_b"][half]
        v[f"D{h}"] = a["L0_attn_D_param"][half]
        for n in range(16):
            v[f"A_log{n}{h}"] = a["L0_attn_A_log"][half, n]
    bup = a["L1_attn_bup"].reshape(16, 2, 8)
    bk, bv = bup[:, 0].reshape(P), bup[:, 1].reshape(P)
    v["L1_bq"], v["L1_bq_rot"] = a["L1_attn_bq"], rope_swap(a["L1_attn_bq"])
    v["L1_bk"], v["L1_bk_rot"], v["L1_bv"] = bk, rope_swap(bk), bv
    v["L1_bout"], v["L1_bdown"] = a["L1_attn_bout"], a["L1_attn_bdown"]
    for n in "qkvuo":
        v[f"L2_b{n}"] = a[f"L2_attn_b{n}"]
    v["L2_scale"] = a["L2_attn_scale"]
    for n in "qkvo":
        v[f"L3_b{n}"] = a[f"L3_attn_b{n}"]
    for n in "qk":
        v[f"L3_b{n}"] = v[f"L3_b{n}"].reshape(4, HG, HD).transpose(0, 2, 1).reshape(P)
    v["ln_g"], v["ln_b"] = a["L3_ffn_ln_g"], a["L3_ffn_ln_b"]
    table = np.zeros((P, len(VECS)), np.float32)
    for k, name in enumerate(VECS):
        table[:len(v[name]), k] = v[name]
    return table


def layouts(inputs):
    a = {k: np.ascontiguousarray(np.asarray(v)) for k, v in inputs.items()}
    bf = mybir.dt.np(BF16)
    d = {}
    d["x_t"] = a["L0_attn_x"].reshape(TOK, P).T
    d["mean_w"] = np.full((P, P), 1.0 / P, np.float32)
    d["ident"] = np.eye(P, dtype=np.float32)
    d["ident_bf"] = np.eye(P).astype(bf)
    for l in range(LAYERS):
        d[f"L{l}_c_t"] = a[f"L{l}_c"].T
        d[f"L{l}_wmod"] = a[f"L{l}_wmod"]
    d["upper_bf"] = np.triu(np.ones((P, P))).astype(bf)
    d["ones_bf"] = np.ones((P, P)).astype(bf)
    d["vecs"] = vectors(a)
    layout_moe2(a, d, bf)
    layout_moe1(a, d, bf)
    layout_moe3(a, d, bf)
    layout_head_attention(a, d, bf)
    layout_linear_attention(a, d, bf)
    layout_window_attention(a, d, bf)
    layout_mamba(a, d, bf)
    layout_slots(a, d, bf)
    return {k: np.ascontiguousarray(v) for k, v in d.items()}


def kernel(**inputs):
    import concourse.bacc as bacc
    from concourse.bass_utils import run_bass_kernel_spmd
    nc = bacc.Bacc("TRN2", target_bir_lowering=False, num_devices=1)
    arrays = {f"in_{k}": v for k, v in layouts(inputs).items()}
    ins = {k[3:]: nc.dram_tensor(k, v.shape, mybir.dt.from_np(v.dtype), kind="ExternalInput").ap()
           for k, v in arrays.items()}
    out = nc.dram_tensor("out_t", (P, TOK), F32, kind="ExternalOutput").ap()
    build(nc, ins, out)
    r = run_bass_kernel_spmd(nc, [arrays], core_ids=[0])
    return np.ascontiguousarray(r.results[0]["out_t"].T).reshape(BATCH, SEQ, P)
```

```python
from contextlib import ExitStack

import concourse.bass as bass
from concourse import mybir
from concourse.alu_op_type import AluOpType as ALU
import numpy as np

F32 = mybir.dt.float32
BF16 = mybir.dt.bfloat16
U32 = mybir.dt.uint32
I32 = mybir.dt.int32
ACT = mybir.ActivationFunctionType
AX = mybir.AxisListType

P = 128
BATCH = 4
SEQ = 1024
TOK = BATCH * SEQ
TILE = 512
NT = TOK // TILE
TPB = SEQ // TILE
KT = TOK // P
LAYERS = 4
LN_EPS = 1e-5
LN_EXP_SET = "natural_log_exp_and_others"
SA, CA, GA, SB, CB, GB = range(6)


VECS = ([f"bg{e}" for e in range(16)] + [f"bu{e}" for e in range(16)]
        + [f"conv_w{k}{h}" for k in range(4) for h in range(2)]
        + [f"{n}{h}" for n in ("conv_b", "dt_b", "D") for h in range(2)]
        + [f"A_log{s}{h}" for s in range(16) for h in range(2)]
        + ["L1_bq", "L1_bq_rot", "L1_bk", "L1_bk_rot", "L1_bv", "L1_bout", "L1_bdown"]
        + ["L2_bq", "L2_bk", "L2_bv", "L2_bu", "L2_bo", "L2_scale"]
        + ["L3_bq", "L3_bk", "L3_bv", "L3_bo", "ln_g", "ln_b"])


class Chain:

    def __init__(self, eng, sem, per_turn=0, turn=0):
        self.eng, self.sem, self.base, self.n = eng, sem, turn * per_turn, 0
        self.per_turn = per_turn

    def __call__(self, ins):
        self.wait(self.add(ins))

    def add(self, ins):
        self.n += 1
        ins.then_inc(self.sem, 1)
        return self.n

    def wait(self, n):
        self.eng.wait_ge(self.sem, self.base + n)


class Core:

    def __init__(self, nc, ctx, ins):
        self.nc, self.ins = nc, ins
        self.ctx = ctx
        self.ln_calls = 0

        def sb(name, shape, dt=F32):
            return ctx.enter_context(nc.sbuf_tensor(name, shape, dt))

        self.x_t = sb("x_t", [P, TOK])
        self.h_t = sb("h_t", [P, TOK])
        self.mod = sb("mod", [P, LAYERS, 6, NT])
        self.mean_w = sb("mean_w", [P, P])
        self.ident = sb("ident", [P, P])
        self.ident_bf = sb("ident_bf", [P, P], BF16)
        slots = (2 * KT + 16) * P
        self.sent = nc.dram_tensor("slots_sent", (slots, P), F32, kind="Internal").ap()
        self.back = nc.dram_tensor("slots_back", (slots, P), F32, kind="Internal").ap()
        self.mixtures = 0
        self.scattered = ctx.enter_context(nc.semaphore("scattered"))
        self.gathered = [ctx.enter_context(nc.semaphore(f"gathered{t}")) for t in range(NT)]
        self.vecs = sb("vecs", [P, len(VECS)])
        self.ln = {n: ctx.enter_context(nc.semaphore("ln_" + n))
                   for n in ("mean", "cent", "sq", "var", "logv", "rstd", "xn", "h")}


def vec(c, name):
    k = VECS.index(name)
    return c.vecs[:, k:k + 1]


def stage_setup(c):
    nc, ins = c.nc, c.ins
    with ExitStack() as s:
        wmod = s.enter_context(nc.sbuf_tensor("wmod", [P, LAYERS, 6 * P], F32))
        cond = s.enter_context(nc.sbuf_tensor("cond", [P, LAYERS, BATCH], F32))
        cond_silu = s.enter_context(nc.sbuf_tensor("cond_silu", [P, LAYERS, BATCH], F32))
        raw = s.enter_context(nc.sbuf_tensor("mod_raw", [P, LAYERS, 6, BATCH], F32))
        sign = s.enter_context(nc.sbuf_tensor("gate_sign", [P, LAYERS, 2, BATCH], F32))
        size = s.enter_context(nc.sbuf_tensor("gate_size", [P, LAYERS, 2, BATCH], F32))
        ps = s.enter_context(nc.psum_tensor("mod_ps", [P, LAYERS, 6, BATCH], F32))
        zeros = s.enter_context(nc.sbuf_tensor("zeros", [P, (KT // 2 + 4) * P], F32))
        zeros_set = s.enter_context(nc.semaphore("setup_zeros_set"))
        zeroed = s.enter_context(nc.semaphore("setup_zeroed"))
        loaded = s.enter_context(nc.semaphore("setup_loaded"))
        silu_done = s.enter_context(nc.semaphore("setup_silu"))
        mod_done = s.enter_context(nc.semaphore("setup_mod"))
        step = s.enter_context(nc.semaphore("setup_step"))
        with nc.Block() as block:
            @block.sync
            def _(sp):
                sp.dma_start(c.x_t[:, :], ins["x_t"]).then_inc(loaded, 16)
                sp.dma_start(c.mean_w[:, :], ins["mean_w"]).then_inc(loaded, 16)
                sp.dma_start(c.ident[:, :], ins["ident"]).then_inc(loaded, 16)
                sp.dma_start(c.ident_bf[:, :], ins["ident_bf"]).then_inc(loaded, 16)
                sp.dma_start(c.vecs[:, :], ins["vecs"]).then_inc(loaded, 16)
                for l in range(LAYERS):
                    sp.dma_start(cond[:, l, :], ins[f"L{l}_c_t"]).then_inc(loaded, 16)
                    sp.dma_start(wmod[:, l, :], ins[f"L{l}_wmod"]).then_inc(loaded, 16)
                sp.wait_ge(zeros_set, 1)
                n = c.sent.shape[0] // 4
                for q in range(4):
                    sp.dma_start(c.sent[q * n:(q + 1) * n, :].rearrange("(p r) d -> p (r d)", p=P),
                                 zeros[:, :]).then_inc(zeroed, 16)
                sp.wait_ge(zeroed, 64)

            @block.gpsimd
            def _(pool):
                nc.gpsimd.memset(zeros[:, :], 0.0).then_inc(zeros_set, 1)

            @block.scalar
            def _(act):
                act.wait_ge(loaded, 16 * (5 + 2 * LAYERS))
                nc.scalar.activation(cond_silu[:, :, :], cond[:, :, :], ACT.Silu).then_inc(silu_done, 1)

            @block.tensor
            def _(pe):
                pe.wait_ge(loaded, 16 * (5 + 2 * LAYERS))
                pe.wait_ge(silu_done, 1)
                for l in range(LAYERS):
                    for k in range(6):
                        mm = nc.tensor.matmul(ps[:, l, k, :], wmod[:, l, k * P:(k + 1) * P], cond_silu[:, l, :],
                                              start=True, stop=True)
                mm.then_inc(mod_done, 1)

            @block.vector
            def _(dve):
                dve.wait_ge(mod_done, 1)
                nc.vector.tensor_copy(raw[:, :, :, :], ps[:, :, :, :]).then_inc(step, 1)
                dve.wait_ge(step, 1)
                for n, k in enumerate((CA, CB)):
                    nc.vector.tensor_scalar(raw[:, :, k, :], raw[:, :, k, :], 1.0, None, ALU.add).then_inc(step, 1)
                for n, k in enumerate((GA, GB)):
                    nc.vector.tensor_scalar(sign[:, :, n, :], raw[:, :, k, :], 0.0, 2.0, ALU.is_ge,
                                            ALU.mult).then_inc(step, 1)
                dve.wait_ge(step, 5)
                for n, k in enumerate((GA, GB)):
                    nc.vector.scalar_tensor_tensor(size[:, :, n, :], sign[:, :, n, :], -1.0, raw[:, :, k, :],
                                                   ALU.add, ALU.mult).then_inc(step, 1)
                dve.wait_ge(step, 7)
                for n in range(2):
                    nc.vector.tensor_scalar(size[:, :, n, :], size[:, :, n, :], 0.25, None,
                                            ALU.max).then_inc(step, 1)
                dve.wait_ge(step, 9)
                for n, k in enumerate((GA, GB)):
                    nc.vector.scalar_tensor_tensor(raw[:, :, k, :], sign[:, :, n, :], -1.0, size[:, :, n, :],
                                                   ALU.add, ALU.mult).then_inc(step, 1)
                dve.wait_ge(step, 11)
                for l in range(LAYERS):
                    nc.vector.tensor_copy(
                        c.mod[:, l, :, :].rearrange("p k (b u) -> p k b u", u=TPB),
                        raw[:, l, :, :].unsqueeze(3).to_broadcast([P, 6, BATCH, TPB])).then_inc(step, 1)
                dve.wait_ge(step, 11 + LAYERS)


def stage_norm(c, src, dst, scale, shift):
    U = 4
    nc, base, call = c.nc, c.ln_calls * NT, c.ln_calls
    c.ln_calls += 1
    ln = c.ln
    with ExitStack() as s:
        xc = s.enter_context(nc.sbuf_tensor(f"ln_xc{call}", [P, U, TILE], F32))
        sq = s.enter_context(nc.sbuf_tensor(f"ln_sq{call}", [P, U, TILE], F32))
        lv = s.enter_context(nc.sbuf_tensor(f"ln_lv{call}", [P, U, TILE], F32))
        eps = s.enter_context(nc.sbuf_tensor(f"ln_eps{call}", [P, 1], F32))
        mean_ps = s.enter_context(nc.psum_tensor(f"ln_mean_ps{call}", [P, U, TILE], F32))
        var_ps = s.enter_context(nc.psum_tensor(f"ln_var_ps{call}", [P, U, TILE], F32))
        eps_set = s.enter_context(nc.semaphore(f"ln_eps_set{call}"))
        with nc.Block() as block:
            @block.tensor
            def _(pe):
                with pe.Fori(0, NT // U) as i:
                    for u in range(U):
                        nc.tensor.matmul(mean_ps[:, u, :], c.mean_w[:, :], src[:, bass.ts(i * U + u, TILE)],
                                         start=True, stop=True).then_inc(ln["mean"], 1)
                    for u in range(U):
                        pe.wait_ge(ln["sq"], i * U + (base + u + 1))
                        nc.tensor.matmul(var_ps[:, u, :], c.mean_w[:, :], sq[:, u, :],
                                         start=True, stop=True).then_inc(ln["var"], 1)

            @block.scalar
            def _(act):
                nc.scalar.preload_act_table_set(LN_EXP_SET)
                act.wait_ge(eps_set, 1)
                with act.Fori(0, NT // U) as i:
                    for u in range(U):
                        act.wait_ge(ln["cent"], i * U + (base + u + 1))
                        nc.scalar.activation(sq[:, u, :], xc[:, u, :], ACT.Square).then_inc(ln["sq"], 1)
                    for u in range(U):
                        act.wait_ge(ln["var"], i * U + (base + u + 1))
                        nc.scalar.activation(lv[:, u, :], var_ps[:, u, :], ACT.Ln,
                                             bias=eps[:, 0:1]).then_inc(ln["logv"], 1)
                        act.wait_ge(ln["logv"], i * U + (base + u + 1))
                        nc.scalar.activation(lv[:, u, :], lv[:, u, :], ACT.Exp, scale=-0.5).then_inc(ln["rstd"], 1)

            @block.vector
            def _(dve):
                nc.vector.memset(eps[:, :], LN_EPS).then_inc(eps_set, 1)
                with dve.Fori(0, NT // U) as i:
                    for u in range(U):
                        dve.wait_ge(ln["mean"], i * U + (base + u + 1))
                        nc.vector.tensor_tensor(xc[:, u, :], src[:, bass.ts(i * U + u, TILE)], mean_ps[:, u, :],
                                                ALU.subtract).then_inc(ln["cent"], 1)
                    for u in range(U):
                        dve.wait_ge(ln["rstd"], i * U + (base + u + 1))
                        nc.vector.tensor_tensor(xc[:, u, :], xc[:, u, :], lv[:, u, :],
                                                ALU.mult).then_inc(ln["xn"], 1)
                        dve.wait_ge(ln["xn"], i * U + (base + u + 1))
                        nc.vector.tensor_scalar(dst[:, bass.ts(i * U + u, TILE)], xc[:, u, :],
                                                scale(i * U + u), shift(i * U + u), ALU.mult,
                                                ALU.add).then_inc(ln["h"], 1)
                    dve.wait_ge(ln["h"], i * U + (base + U))


def adaln(c, layer, k_shift, k_scale):
    stage_norm(c, c.x_t, c.h_t,
               lambda t: c.mod[:, layer, k_scale, bass.ds(t, 1)],
               lambda t: c.mod[:, layer, k_shift, bass.ds(t, 1)])


def recycle_semaphores(c):
    nc = c.nc
    given_back = sorted(nc.released_uncleared_semaphores)
    with nc.Block() as block:
        @block.gpsimd
        def _(pool):
            first = 0
            for k in range(1, len(given_back) + 1):
                if k == len(given_back) or given_back[k] != given_back[k - 1] + 1:
                    pool.sem_clear(range(given_back[first], given_back[k - 1] + 1))
                    first = k


def stage_store(c, out):
    nc = c.nc
    with ExitStack() as s:
        stored = s.enter_context(nc.semaphore("stored"))
        with nc.Block() as block:
            @block.sync
            def _(sp):
                sp.dma_start(out, c.x_t[:, :]).then_inc(stored, 16)
                sp.wait_ge(stored, 16)


BUFS = 3
LIMIT, ALPHA = 7.0, 1.702


def stage_router(c, tag, experts, index, gates, logits_bias=False, capacity=None, per=None, of_block=None):
    nc, ins = c.nc, c.ins
    E = experts
    small = [P, KT]
    full = [P, KT, E]
    with ExitStack() as s:
        def sb(name, shape, dt=F32):
            return s.enter_context(nc.sbuf_tensor(f"{tag}_{name}", shape, dt))

        def sem(name):
            return s.enter_context(nc.semaphore(f"{tag}_{name}"))

        wr = sb("wr", [P, E])
        rank = sb("rank", full)
        lb = sb("lb", full)
        lg = sb("lg", full)
        eq = sb("eq", full)
        hot = [sb("hot0", full), sb("hot1", full)]
        tmp = sb("tmp", full)
        tmp2 = sb("tmp2", full)
        mx = [sb("mx0", small), sb("mx1", small)]
        mr = sb("mr", small)
        gate = [sb("gate0", small), sb("gate1", small)]
        ex = sb("ex", small)
        lg_ps = s.enter_context(nc.psum_tensor(f"{tag}_lg_ps", full, F32))
        loaded, logits, step, ex_ready, ex_done, hots_done, counted = (
            sem(n) for n in ("loaded", "logits", "step", "ex_ready", "ex_done", "hots_done", "counted"))
        hots = sb("hots", [P, 2, KT, E], BF16)
        upper = sb("upper", [P, P], BF16)
        ones = sb("ones", [P, P], BF16)
        tot = sb("tot", [P, 2 * KT, E])
        cum = sb("cum", [P, E, 2 * KT])
        pos = sb("pos", [P, 2, KT, E])
        zero = sb("zero", [P, 2 * KT])
        pre_ps = s.enter_context(nc.psum_tensor(f"{tag}_pre_ps", [P, 2, TILE], F32))
        tot_ps = s.enter_context(nc.psum_tensor(f"{tag}_tot_ps", [P, 2, TILE], F32))
        loads = 4 + bool(logits_bias)
        if not capacity:
            NB = 2 * KT + E
            loads += 1
            ramp = sb("ramp", [P, NB])
            fits = sb("fits", [P, E, KT])
            size, end, start = sb("size", [P, E]), sb("end", [P, E]), sb("start", [P, E])
            past = sb("past", [P, NB, E])
            owner = sb("owner", [P, NB])
        with nc.Block() as block:
            @block.sync
            def _(sp):
                sp.dma_start(wr[:, :], ins[f"{tag}_wr"]).then_inc(loaded, 16)
                sp.dma_start(rank[:, :, :].rearrange("p k e -> p (k e)"), ins[f"{tag}_rank"]).then_inc(loaded, 16)
                if logits_bias:
                    sp.dma_start(lb[:, :, :].rearrange("p k e -> p (k e)"), ins[f"{tag}_lb"]).then_inc(loaded, 16)
                sp.dma_start(upper[:, :], ins["upper_bf"]).then_inc(loaded, 16)
                sp.dma_start(ones[:, :], ins["ones_bf"]).then_inc(loaded, 16)
                if not capacity:
                    sp.dma_start(ramp[:, :], ins[f"{tag}_ramp"]).then_inc(loaded, 16)

            @block.tensor
            def _(pe):
                pe.wait_ge(loaded, 16 * loads)
                for k in range(KT):
                    mm = nc.tensor.matmul(lg_ps[:, k, :], c.h_t[:, k * P:(k + 1) * P], wr[:, :],
                                          start=True, stop=True)
                mm.then_inc(logits, 1)
                pe.wait_ge(hots_done, 2)
                for k in range(2):
                    flat = hots[:, k, :, :].rearrange("p k e -> p (k e)")
                    nc.tensor.matmul(pre_ps[:, k, 0:KT * E], upper[:, :], flat, start=True, stop=True)
                    nc.tensor.matmul(tot_ps[:, k, 0:KT * E], ones[:, :], flat, start=True,
                                     stop=True).then_inc(counted, 1)

            @block.scalar
            def _(act):
                act.wait_ge(ex_ready, 1)
                nc.scalar.activation(ex[:, :], ex[:, :], ACT.Exp).then_inc(ex_done, 1)

            @block.vector
            def _(dve):
                n = [0]

                def done(ins_):
                    n[0] += 1
                    ins_.then_inc(step, 1)
                    dve.wait_ge(step, n[0])

                def wide(a):
                    return a[:, :].unsqueeze(2).to_broadcast(full)

                tt, ts = nc.vector.tensor_tensor, nc.vector.tensor_scalar
                dve.wait_ge(loaded, 16 * loads)
                dve.wait_ge(logits, 1)
                if logits_bias:
                    done(tt(lg[:, :, :], lg_ps[:, :, :], lb[:, :, :], ALU.add))
                else:
                    done(nc.vector.tensor_copy(lg[:, :, :], lg_ps[:, :, :]))
                for k in range(2):
                    done(nc.vector.reduce_max(mx[k][:, :], lg[:, :, :], AX.X))
                    done(tt(eq[:, :, :], lg[:, :, :], wide(mx[k]), ALU.is_ge))
                    done(tt(eq[:, :, :], eq[:, :, :], rank[:, :, :], ALU.mult))
                    done(nc.vector.reduce_max(mr[:, :], eq[:, :, :], AX.X))
                    done(tt(hot[k][:, :, :], eq[:, :, :], wide(mr), ALU.is_equal))
                    if k == 0:
                        done(nc.vector.scalar_tensor_tensor(lg[:, :, :], hot[0][:, :, :], -3e38, lg[:, :, :],
                                                            ALU.mult, ALU.add))
                tt(ex[:, :], mx[1][:, :], mx[0][:, :], ALU.subtract).then_inc(ex_ready, 1)
                dve.wait_ge(ex_done, 1)
                done(ts(gate[1][:, :], ex[:, :], 1.0, None, ALU.add))
                done(nc.vector.reciprocal(gate[0][:, :], gate[1][:, :]))
                done(tt(gate[1][:, :], gate[0][:, :], ex[:, :], ALU.mult))
                for k in range(2):
                    nc.vector.tensor_copy(hots[:, k, :, :], hot[k][:, :, :]).then_inc(hots_done, 1)
                done(nc.vector.memset(zero[:, :], 0.0))
                dve.wait_ge(counted, 2)
                per_choice = tot[:, :, :].rearrange("p (s k) e -> p s (k e)", s=2)
                done(nc.vector.tensor_copy(per_choice, tot_ps[:, :, 0:KT * E]))
                for e in range(E):
                    done(nc.vector.tensor_tensor_scan(cum[:, e, :], tot[:, :, e], zero[:, :], 0.0,
                                                      ALU.add, ALU.add))
                done(tt(tot[:, :, :], cum[:, :, :].rearrange("p e k -> p k e"), tot[:, :, :], ALU.subtract))
                done(tt(pos[:, :, :, :].rearrange("p s k e -> p s (k e)"), pre_ps[:, :, 0:KT * E], per_choice, ALU.add))
                if capacity:
                    for k in range(2):
                        done(ts(tmp[:, :, :], pos[:, k, :, :], float(capacity), None, ALU.is_le))
                        done(tt(hot[k][:, :, :], hot[k][:, :, :], tmp[:, :, :], ALU.mult))
                    done(ts(tmp2[:, :, :], rank[:, :, :], float(-per), -1.0, ALU.mult, ALU.add))
                    offset = float(E * per)
                else:
                    done(ts(owner[:, 0:KT], ramp[:, 0:KT], float(P), None, ALU.mult))
                    done(tt(fits[:, :, :], cum[:, :, 2 * KT - 1].unsqueeze(2).to_broadcast([P, E, KT]),
                            owner[:, 0:KT].unsqueeze(1).to_broadcast([P, E, KT]), ALU.is_gt))
                    done(nc.vector.reduce_sum(size[:, :], fits[:, :, :], AX.X))
                    done(nc.vector.tensor_tensor_scan(end[:, :], size[:, :], zero[:, 0:E], 0.0, ALU.add, ALU.add))
                    done(tt(start[:, :], end[:, :], size[:, :], ALU.subtract))
                    done(tt(past[:, :, :], ramp[:, :].unsqueeze(2).to_broadcast([P, NB, E]),
                            end[:, :].unsqueeze(1).to_broadcast([P, NB, E]), ALU.is_ge))
                    done(nc.vector.reduce_sum(owner[:, :], past[:, :, :], AX.X))
                    done(ts(owner[:, :], owner[:, :], float(E - 1), None, ALU.min))
                    done(nc.vector.tensor_copy(of_block[:, :], owner[:, :]))
                    done(ts(start[:, :], start[:, :], float(P), -1.0, ALU.mult, ALU.add))
                    done(nc.vector.tensor_copy(tmp2[:, :, :], start[:, :].unsqueeze(1).to_broadcast(full)))
                    offset = 0.0
                for k in range(2):
                    done(tt(tmp[:, :, :], tmp2[:, :, :], pos[:, k, :, :], ALU.add))
                    done(tt(tmp[:, :, :], tmp[:, :, :], hot[k][:, :, :], ALU.mult))
                    done(nc.vector.reduce_sum(mr[:, :], tmp[:, :, :], AX.X))
                    done(ts(mr[:, :], mr[:, :], offset, None, ALU.add))
                    done(nc.vector.tensor_copy(index[:, k, :], mr[:, :]))
                    done(nc.vector.tensor_copy(gates[:, k, :], gate[k][:, :]))


def stage_combine(c, tag, layer, index, gates, back):
    nc = c.nc
    with ExitStack() as s:
        tr_ps = s.enter_context(nc.psum_tensor(f"{tag}_c_tr_ps", [P, 2, TILE], F32))
        got = s.enter_context(nc.sbuf_tensor(f"{tag}_got", [P, 2, KT, P], F32))
        first = s.enter_context(nc.sbuf_tensor(f"{tag}_first", [P, 4, P], F32))
        both = s.enter_context(nc.sbuf_tensor(f"{tag}_both", [P, KT, P], F32))
        first_ready, sum_ready, sum_turned, x_ready = (
            s.enter_context(nc.semaphore(f"{tag}_{n}")) for n in ("first_ready", "sum_ready", "sum_turned", "x_ready"))
        before = 16 * 8 * c.mixtures
        c.mixtures += 1
        with nc.Block() as block:
            @block.gpsimd
            def _(pool):
                for k in range(KT):
                    for choice in range(2):
                        nc.gpsimd.indirect_dma_start(
                            got[:, choice, k, :], None, back,
                            bass.IndirectOffsetOnAxis(index[:, choice, k:k + 1], 0)).then_inc(c.gathered[k // 4], 16)

            @block.vector
            def _(dve):
                tt, ts, stt = nc.vector.tensor_tensor, nc.vector.tensor_scalar, nc.vector.scalar_tensor_tensor

                def add_to_x(t):
                    dve.wait_ge(sum_turned, t + 1)
                    at = slice(t * TILE, (t + 1) * TILE)
                    stt(c.x_t[:, at], tr_ps[:, t % 2, :], c.mod[:, layer, GB, t:t + 1], c.x_t[:, at], ALU.mult,
                        ALU.add).then_inc(x_ready, 1)
                for t in range(NT):
                    dve.wait_ge(c.gathered[t], before + 16 * 8)
                    for j in range(4):
                        k = 4 * t + j
                        if t:
                            dve.wait_ge(sum_ready, 4 * (t - 1) + j + 1)
                        ts(first[:, j, :], got[:, 0, k, :], gates[:, 0, k:k + 1], None,
                           ALU.mult).then_inc(first_ready, 1)
                    for j in range(4):
                        k = 4 * t + j
                        dve.wait_ge(first_ready, k + 1)
                        stt(both[:, k, :], got[:, 1, k, :], gates[:, 1, k:k + 1], first[:, j, :], ALU.mult,
                            ALU.add).then_inc(sum_ready, 1)
                    if t:
                        add_to_x(t - 1)
                add_to_x(NT - 1)

            @block.tensor
            def _(pe):
                for t in range(NT):
                    pe.wait_ge(sum_ready, 4 * t + 4)
                    if t >= 2:
                        pe.wait_ge(x_ready, t - 1)
                    for j in range(4):
                        mm = nc.tensor.transpose(tr_ps[:, t % 2, j * P:(j + 1) * P], both[:, 4 * t + j, :],
                                                 c.ident[:, :])
                    mm.then_inc(sum_turned, 1)


def stage_experts(c, tag, E, F, index, of_block, back, clamped):
    nc, ins = c.nc, c.ins
    NB = 2 * KT + E
    U = 4
    TURNS = NB // U
    WIDE = 2 * P if clamped else F * P
    with ExitStack() as s:
        def sb(name, shape, dt=F32):
            return s.enter_context(nc.sbuf_tensor(f"{tag}_{name}", shape, dt))

        def sem(name):
            return s.enter_context(nc.semaphore(f"{tag}_{name}"))

        w1, w2 = sb("w1", [P, E * WIDE]), sb("w2", [P, E * F * P])
        names = ("loaded", "turned", "rows_even", "rows_odd", "x_turned", "xt_ready", "h_ready", "gate_ready",
                 "sig_ready", "up_ready", "glu_ready", "g_ready", "g_turned", "gt_ready", "o_ready", "out_ready", "bias_in", "bias_step")
        S = {n: sem(n) for n in names}
        fetched = [sem(f"fetched{u}") for u in range(U)]
        stored = [sem(f"stored{u}") for u in range(U)]
        if clamped:
            BIAS = E * (WIDE + P)
            bias, rest, part = sb("bias", [3, BIAS]), sb("rest", [3, BIAS]), sb("part", [3, BIAS], BF16)
            bias3, ones3, minus = sb("bias3", [3, BIAS], BF16), sb("ones3", [3, P], BF16), sb("minus", [3, 2])
        with ExitStack() as s1, nc.Block() as block:
            tr_ps = s1.enter_context(nc.psum_tensor(f"{tag}_tr_ps", [P, 2, TILE], F32))
            rows = s1.enter_context(nc.sbuf_tensor(f"{tag}_rows", [P, KT, P], F32))

            @block.sync
            def _(sp):
                sp.dma_start(w1[:, :], ins[f"{tag}_w1"]).then_inc(S["loaded"], 16)
                sp.dma_start(w2[:, :], ins[f"{tag}_w2"]).then_inc(S["loaded"], 16)
                if clamped:
                    sp.dma_start(bias[:, :], ins[f"{tag}_bias"]).then_inc(S["bias_in"], 16)
                    sp.dma_start(minus[:, :], ins[f"{tag}_minus"]).then_inc(S["bias_in"], 16)
                    sp.dma_start(ones3[:, :], ins["ones_bf"][0:3, :]).then_inc(S["loaded"], 16)

            @block.gpsimd
            def _(pool):
                for k in range(KT):
                    q = k // 4
                    pool.wait_ge(S["rows_odd" if q % 2 else "rows_even"], q // 2 + 1)
                    for choice in range(2):
                        nc.gpsimd.indirect_dma_start(
                            c.sent, bass.IndirectOffsetOnAxis(index[:, choice, k:k + 1], 0), rows[:, k, :],
                            None).then_inc(c.scattered, 16)
                pool.wait_ge(c.scattered, 16 * 2 * KT * (c.mixtures + 1))

            @block.tensor
            def _(pe):
                for q in range(KT // 4):
                    if q >= 2:
                        pe.wait_ge(S["rows_odd" if q % 2 else "rows_even"], q // 2)
                    for j in range(4):
                        at = (4 * q + j) * P
                        mm = nc.tensor.transpose(tr_ps[:, q % 2, j * P:(j + 1) * P], c.h_t[:, at:at + P], c.ident[:, :])
                    mm.then_inc(S["turned"], 1)

            @block.scalar
            def _(act):
                for q in range(0, KT // 4, 2):
                    act.wait_ge(S["turned"], q + 1)
                    nc.scalar.copy(rows[:, 4 * q:4 * q + 4, :].rearrange("p k d -> p (k d)"),
                                   tr_ps[:, 0, :]).then_inc(S["rows_even"], 1)

            @block.vector
            def _(dve):
                for q in range(1, KT // 4, 2):
                    dve.wait_ge(S["turned"], q + 1)
                    nc.vector.tensor_copy(rows[:, 4 * q:4 * q + 4, :].rearrange("p k d -> p (k d)"),
                                          tr_ps[:, 1, :]).then_inc(S["rows_odd"], 1)
                if clamped:
                    stt = nc.vector.scalar_tensor_tensor
                    split = Chain(dve, S["bias_step"])
                    dve.wait_ge(S["bias_in"], 32)
                    split(nc.vector.tensor_copy(part[:, :], bias[:, :]))
                    split(stt(rest[:, :], part[:, :], minus[:, 0:1], bias[:, :], ALU.mult, ALU.add))
                    split(nc.vector.tensor_copy(part[:, :], rest[:, :]))
                    split(stt(bias3[:, :], part[:, :], minus[:, 1:2], rest[:, :], ALU.mult, ALU.add))

        with ExitStack() as s2, nc.Block() as block:
            def psum(name):
                return s2.enter_context(nc.psum_tensor(f"{tag}_{name}", [P, 2, TILE], F32))

            def sb2(name, shape):
                return s2.enter_context(nc.sbuf_tensor(f"{tag}_{name}", shape, F32))

            xt_ps, h_ps, gt_ps, o_ps = (psum(n) for n in ("xt_ps", "h_ps", "gt_ps", "o_ps"))
            xs, xt, out = (sb2(n, [P, U, P]) for n in ("xs", "xt", "out"))
            g, gt = sb2("g", [P, 2, F * P]), sb2("gt", [P, 2, F * P])
            gate, sig, up, glu = (sb2(n, [P, 2, P]) for n in ("gate", "sig", "up", "glu"))

            def turns(eng, turn):
                turn(0, True, False)
                with eng.Fori(0, TURNS - 2) as i:
                    turn(i + 1, False, False)
                turn(TURNS - 1, False, True)

            @block.sync
            def _(sp):
                def fetch(i, u):
                    sp.dma_start(xs[:, u, :], c.sent[bass.ds(i * (U * P) + u * P, P), :]).then_inc(fetched[u], 16)

                def store(i, u):
                    sp.wait_ge(S["out_ready"], i * U + (u + 1))
                    sp.dma_start(back[bass.ds(i * (U * P) + u * P, P), :], out[:, u, :]).then_inc(stored[u], 16)

                def turn(i, first, last):
                    for u in range(U):
                        if not last:
                            sp.wait_ge(S["x_turned"], i * U + (u + 1))
                            fetch(i + 1, u)
                        if not first:
                            store(i - 1, u)
                for u in range(U):
                    fetch(0, u)
                turns(sp, turn)
                for u in range(U):
                    store(TURNS - 1, u)
                for u in range(U):
                    sp.wait_ge(stored[u], 16 * TURNS)

            @block.tensor
            def _(pe):
                def turn_x(i, u):
                    n = i * U + u
                    pe.wait_ge(fetched[u % U], i * 16 + (u // U + 1) * 16)
                    if not (isinstance(n, int) and n < 2):
                        pe.wait_ge(S["xt_ready"], n - 1)
                    nc.tensor.transpose(xt_ps[:, u % 2, 0:P], xs[:, u % U, :], c.ident[:, :]).then_inc(S["x_turned"], 1)

                def first_product(i, u):
                    n = i * U + u
                    e = pe.value_load(of_block[0:1, bass.ds(n, 1)], min_val=0, max_val=E - 1)
                    pe.wait_ge(S["xt_ready"], n + 1)
                    if not (isinstance(n, int) and n < 2):
                        pe.wait_ge(S["g_ready"], n - 1)
                    mm = nc.tensor.matmul(h_ps[:, u % 2, 0:WIDE], xt[:, u % U, :], w1[:, bass.ds(e * WIDE, WIDE)],
                                          start=True, stop=not clamped)
                    if clamped:
                        mm = nc.tensor.matmul(h_ps[:, u % 2, 0:WIDE], ones3[:, :], bias3[:, bass.ds(e * WIDE, WIDE)],
                                              start=False, stop=True)
                    mm.then_inc(S["h_ready"], 1)

                def turn_g(i, u):
                    n = i * U + u
                    pe.wait_ge(S["g_ready"], n + 1)
                    if not (isinstance(n, int) and n < 2):
                        pe.wait_ge(S["gt_ready"], n - 1)
                    for f in range(F):
                        mm = nc.tensor.transpose(gt_ps[:, u % 2, f * P:(f + 1) * P], g[:, u % 2, f * P:(f + 1) * P],
                                                 c.ident[:, :])
                    mm.then_inc(S["g_turned"], 1)

                def second_product(i, u):
                    n = i * U + u
                    e = pe.value_load(of_block[0:1, bass.ds(n, 1)], min_val=0, max_val=E - 1)
                    pe.wait_ge(S["gt_ready"], n + 1)
                    if not (isinstance(n, int) and n < 2):
                        pe.wait_ge(S["out_ready"], n - 1)
                    if clamped:
                        nc.tensor.matmul(o_ps[:, u % 2, 0:P], ones3[:, :], bias3[:, bass.ds(e * P + E * WIDE, P)], start=True, stop=False)
                    for f in range(F):
                        mm = nc.tensor.matmul(o_ps[:, u % 2, 0:P], gt[:, u % 2, f * P:(f + 1) * P],
                                              w2[:, bass.ds(e * (F * P) + f * P, P)], start=(f == 0 and not clamped),
                                              stop=(f == F - 1))
                    mm.then_inc(S["o_ready"], 1)

                def turn(i, first, last):
                    for u in range(U):
                        if not (last and u + 2 >= U):
                            turn_x(i, u + 2)
                        if not (last and u + 1 >= U):
                            first_product(i, u + 1)
                        turn_g(i, u)
                        if u:
                            second_product(i, u - 1)
                        elif not first:
                            second_product(i - 1, U - 1)
                pe.wait_ge(S["loaded"], 16 * (3 if clamped else 2))
                turn_x(0, 0)
                turn_x(0, 1)
                first_product(0, 0)
                turns(pe, turn)
                second_product(TURNS - 1, U - 1)

            @block.scalar
            def _(act):
                def copy_x(i, u):
                    n = i * U + u
                    act.wait_ge(S["x_turned"], n + 1)
                    nc.scalar.copy(xt[:, u % U, :], xt_ps[:, u % 2, 0:P]).then_inc(S["xt_ready"], 1)

                def turn(i, first, last):
                    for u in range(U):
                        if not (last and u + 1 >= U):
                            copy_x(i, u + 1)
                        n = i * U + u
                        if clamped:
                            act.wait_ge(S["gate_ready"], n + 1)
                            nc.scalar.activation(sig[:, u % 2, :], gate[:, u % 2, :], ACT.Sigmoid,
                                                 scale=ALPHA).then_inc(S["sig_ready"], 1)
                        else:
                            act.wait_ge(S["h_ready"], n + 1)
                            if not (isinstance(n, int) and n < 2):
                                act.wait_ge(S["g_turned"], n - 1)
                            nc.scalar.activation(g[:, u % 2, :], h_ps[:, u % 2, 0:WIDE], ACT.Gelu).then_inc(S["g_ready"], 1)
                nc.scalar.preload_act_table(ACT.Sigmoid if clamped else ACT.Gelu)
                copy_x(0, 0)
                turns(act, turn)

            @block.vector
            def _(dve):
                def glu_of(i, u):
                    n = i * U + u
                    dve.wait_ge(S["h_ready"], n + 1)
                    nc.vector.tensor_scalar(gate[:, u % 2, :], h_ps[:, u % 2, 0:P], LIMIT, None,
                                            ALU.min).then_inc(S["gate_ready"], 1)
                    nc.vector.tensor_scalar(up[:, u % 2, :], h_ps[:, u % 2, P:2 * P], LIMIT, -LIMIT, ALU.min,
                                            ALU.max).then_inc(S["up_ready"], 1)
                    dve.wait_ge(S["sig_ready"], n + 1)
                    nc.vector.tensor_tensor(glu[:, u % 2, :], gate[:, u % 2, :], sig[:, u % 2, :],
                                            ALU.mult).then_inc(S["glu_ready"], 1)
                    dve.wait_ge(S["glu_ready"], n + 1)
                    if not (isinstance(n, int) and n < 2):
                        dve.wait_ge(S["g_turned"], n - 1)
                    nc.vector.scalar_tensor_tensor(g[:, u % 2, :], up[:, u % 2, :], 1.0, glu[:, u % 2, :], ALU.add,
                                                   ALU.mult).then_inc(S["g_ready"], 1)

                def copy_g(i, u):
                    n = i * U + u
                    dve.wait_ge(S["g_turned"], n + 1)
                    if not (isinstance(n, int) and n < 2):
                        dve.wait_ge(S["o_ready"], n - 1)
                    nc.vector.tensor_copy(gt[:, u % 2, :], gt_ps[:, u % 2, 0:F * P]).then_inc(S["gt_ready"], 1)

                def copy_out(i, u, first):
                    n = i * U + u
                    dve.wait_ge(S["o_ready"], n + 1)
                    if not first:
                        dve.wait_ge(stored[u], i * 16)
                    nc.vector.tensor_copy(out[:, u, :], o_ps[:, u % 2, 0:P]).then_inc(S["out_ready"], 1)

                def turn(i, first, last):
                    for u in range(U):
                        if clamped and not (last and u + 1 >= U):
                            glu_of(i, u + 1)
                        copy_g(i, u)
                        if u:
                            copy_out(i, u - 1, first)
                        elif not first:
                            copy_out(i - 1, U - 1, isinstance(i, int) and i == 1)
                if clamped:
                    glu_of(0, 0)
                turns(dve, turn)
                copy_out(TURNS - 1, U - 1, False)


def stage_moe2(c):
    nc, E = c.nc, 8
    with ExitStack() as s:
        index = s.enter_context(nc.sbuf_tensor("m2_index", [P, 2, KT], U32))
        gates = s.enter_context(nc.sbuf_tensor("m2_gates", [P, 2, KT], F32))
        of_block = s.enter_context(nc.sbuf_tensor("m2_of_block", [P, 2 * KT + E], I32))
        stage_router(c, "r2", E, index, gates, of_block=of_block)
        stage_experts(c, "m2", E, 4, index, of_block, c.back, clamped=False)
        stage_combine(c, "m2", 2, index, gates, c.back[0:(2 * KT + E) * P, :])


def layout_moe2(a, d, bf):
    d["r2_wr"] = a["L2_ffn_gate_w"]
    d["r2_rank"] = rank_const(8)
    d["r2_ramp"] = ramp_const(8)
    d["m2_w1"] = a["L2_ffn_w1"].transpose(1, 0, 2).reshape(P, -1)
    d["m2_w2"] = a["L2_ffn_w2"].reshape(32, P, P).transpose(1, 0, 2).reshape(P, -1)


def rank_const(experts):
    return np.tile((experts - np.arange(experts, dtype=np.float32)), (P, KT)).astype(np.float32)


def ramp_const(experts):
    return np.tile(np.arange(2 * KT + experts, dtype=np.float32), (P, 1))


def stage_moe1(c):
    nc, E = c.nc, 16
    with ExitStack() as s:
        index = s.enter_context(nc.sbuf_tensor("m1_index", [P, 2, KT], U32))
        gates = s.enter_context(nc.sbuf_tensor("m1_gates", [P, 2, KT], F32))
        of_block = s.enter_context(nc.sbuf_tensor("m1_of_block", [P, 2 * KT + E], I32))
        stage_router(c, "r1", E, index, gates, logits_bias=True, of_block=of_block)
        stage_experts(c, "m1", E, 1, index, of_block, c.back, clamped=True)
        stage_combine(c, "m1", 1, index, gates, c.back[0:(2 * KT + E) * P, :])


def layout_moe1(a, d, bf):
    d["r1_wr"] = a["L1_ffn_Wg"].T
    d["r1_rank"] = rank_const(16)
    d["r1_ramp"] = ramp_const(16)
    d["r1_lb"] = np.tile(a["L1_ffn_bg"], (P, KT))
    wgu = a["L1_ffn_Wgu"].transpose(1, 0, 2)
    d["m1_w1"] = np.concatenate([wgu[:, :, ::2], wgu[:, :, 1::2]], 2).reshape(P, -1)
    d["m1_w2"] = a["L1_ffn_Wd"].transpose(1, 0, 2).reshape(P, -1)
    b1 = np.concatenate([a["L1_ffn_bgu"][:, ::2], a["L1_ffn_bgu"][:, 1::2]], 1).reshape(1, -1)
    d["m1_bias"] = np.tile(np.concatenate([b1, a["L1_ffn_bd"].reshape(1, -1)], 1), (3, 1))
    d["m1_minus"] = -np.array([[0, 0], [1, 0], [1, 1]], np.float32)


def stage_moe3(c):
    nc, ins, E, F = c.nc, c.ins, 7, 4
    capacity = -(-5 * 1024 * 2 // (4 * E))
    BLOCKS = -(-capacity // P)
    PER = BLOCKS * P
    ALL = E * BLOCKS
    stage_norm(c, c.h_t, c.h_t, lambda t: vec(c, "ln_g"), lambda t: vec(c, "ln_b"))
    with ExitStack() as s:
        def sb(name, shape, dt=F32):
            return s.enter_context(nc.sbuf_tensor(f"m3_{name}", shape, dt))

        def sem(name):
            return s.enter_context(nc.semaphore(f"m3_{name}"))

        index = sb("index", [P, 2, KT], U32)
        gates = sb("gates", [P, 2, KT])
        stage_router(c, "r3", E, index, gates, capacity=capacity, per=PER)
        w1, w3, w2 = (sb(n, [P, E + 1, F, P]) for n in ("w1", "w3", "w2"))
        sa, v = sb("sa", [P, BUFS, TILE]), sb("v", [P, BUFS, TILE])
        sent, back = c.sent[0:ALL * P, :], c.back[0:(ALL + 1) * P, :]
        names = ("loaded", "zeros_set", "zeroed", "turned", "rows_even", "rows_odd", "a_ready", "b_ready",
                 "sa_ready", "v_ready", "o_ready", "o_free", "slots_in", "xs_turned", "xs_even", "xs_odd", "ra_ready",
                 "rb_ready", "rsa_ready", "rv_ready", "ro_ready", "ro_read", "oo_turned", "rows_ready", "returned")
        S = {n: sem(n) for n in names}


        with ExitStack() as s1, nc.Block() as block:
            tr_ps, a_ps, b_ps = (s1.enter_context(nc.psum_tensor(f"m3_{n}", [P, 2, TILE], F32))
                                 for n in ("tr_ps", "a_ps", "b_ps"))
            o_ps = s1.enter_context(nc.psum_tensor("m3_o_ps", [P, TILE], F32))
            rows = s1.enter_context(nc.sbuf_tensor("m3_rows", [P, KT, P], F32))
            zeros = s1.enter_context(nc.sbuf_tensor("m3_zeros", [P, P], F32))

            @block.sync
            def _(sp):
                for dst, name in ((w1, "m3_w1"), (w3, "m3_w3"), (w2, "m3_w2")):
                    sp.dma_start(dst[:, :, :, :], ins[name]).then_inc(S["loaded"], 16)
                sp.wait_ge(S["zeros_set"], 1)
                sp.dma_start(back[ALL * P:(ALL + 1) * P, :], zeros[:, :]).then_inc(S["zeroed"], 16)
                sp.wait_ge(S["zeroed"], 16)

            @block.gpsimd
            def _(pool):
                nc.gpsimd.memset(zeros[:, :], 0.0).then_inc(S["zeros_set"], 1)
                for k in range(KT):
                    q = k // 4
                    pool.wait_ge(S["rows_odd" if q % 2 else "rows_even"], q // 2 + 1)
                    for choice in range(2):
                        nc.gpsimd.indirect_dma_start(
                            sent, bass.IndirectOffsetOnAxis(index[:, choice, k:k + 1], 0), rows[:, k, :], None,
                            bounds_check=ALL * P - 1, oob_is_err=False).then_inc(c.scattered, 16)
                pool.wait_ge(c.scattered, 16 * 2 * KT * (c.mixtures + 1))

            @block.tensor
            def _(pe):
                for q in range(KT // 4):
                    if q >= 2:
                        pe.wait_ge(S["rows_odd" if q % 2 else "rows_even"], q // 2)
                    for j in range(4):
                        at = (4 * q + j) * P
                        mm = nc.tensor.transpose(tr_ps[:, q % 2, j * P:(j + 1) * P], c.h_t[:, at:at + P], c.ident[:, :])
                    mm.then_inc(S["turned"], 1)
                pe.wait_ge(S["loaded"], 48)
                pe.sem_inc(S["v_ready"], 2)
                pe.sem_inc(S["o_free"], 1)
                with pe.Fori(0, NT) as t:
                    tile = bass.ts(t, TILE)

                    def down(f):
                        pe.wait_ge(S["v_ready"], t * F + (f + 3))
                        if f == 0:
                            pe.wait_ge(S["o_free"], t + 1)
                        return nc.tensor.matmul(o_ps[:, :], w2[:, E, f, :], v[:, f % 2, :], start=(f == 0),
                                                stop=(f == F - 1))
                    for f in range(F):
                        pe.wait_ge(S["v_ready"], t * F + (f + 1))
                        nc.tensor.matmul(a_ps[:, f % 2, :], w1[:, E, f, :], c.h_t[:, tile], start=True,
                                         stop=True).then_inc(S["a_ready"], 1)
                        nc.tensor.matmul(b_ps[:, f % 2, :], w3[:, E, f, :], c.h_t[:, tile], start=True,
                                         stop=True).then_inc(S["b_ready"], 1)
                        if f:
                            down(f - 1)
                    down(F - 1).then_inc(S["o_ready"], 1)

            @block.scalar
            def _(act):
                for q in range(0, KT // 4, 2):
                    act.wait_ge(S["turned"], q + 1)
                    nc.scalar.copy(rows[:, 4 * q:4 * q + 4, :].rearrange("p k d -> p (k d)"),
                                   tr_ps[:, 0, :]).then_inc(S["rows_even"], 1)
                nc.scalar.preload_act_table(ACT.Silu)
                with act.Fori(0, NT) as t:
                    for f in range(F):
                        act.wait_ge(S["a_ready"], t * F + (f + 1))
                        nc.scalar.activation(sa[:, f % 2, :], a_ps[:, f % 2, :], ACT.Silu).then_inc(S["sa_ready"], 1)

            @block.vector
            def _(dve):
                for q in range(1, KT // 4, 2):
                    dve.wait_ge(S["turned"], q + 1)
                    nc.vector.tensor_copy(rows[:, 4 * q:4 * q + 4, :].rearrange("p k d -> p (k d)"),
                                          tr_ps[:, 1, :]).then_inc(S["rows_odd"], 1)
                with dve.Fori(0, NT) as t:
                    tile = bass.ts(t, TILE)
                    for f in range(F):
                        dve.wait_ge(S["sa_ready"], t * F + (f + 1))
                        dve.wait_ge(S["b_ready"], t * F + (f + 1))
                        nc.vector.tensor_tensor(v[:, f % 2, :], sa[:, f % 2, :], b_ps[:, f % 2, :],
                                                ALU.mult).then_inc(S["v_ready"], 1)
                    dve.wait_ge(S["o_ready"], t + 1)
                    nc.vector.scalar_tensor_tensor(c.x_t[:, tile], o_ps[:, :], c.mod[:, 3, GB, bass.ds(t, 1)],
                                                   c.x_t[:, tile], ALU.mult, ALU.add).then_inc(S["o_free"], 1)

        with ExitStack() as s2, nc.Block() as block:
            tr_ps, a_ps, b_ps, o_ps = (s2.enter_context(nc.psum_tensor(f"m3_r_{n}", [P, 2, TILE], F32))
                                       for n in ("tr_ps", "a_ps", "b_ps", "o_ps"))
            xs = s2.enter_context(nc.sbuf_tensor("m3_xs", [P, ALL, P], F32))
            xs_t = s2.enter_context(nc.sbuf_tensor("m3_xs_t", [P, ALL, P], F32))
            out_t = s2.enter_context(nc.sbuf_tensor("m3_out_t", [P, 2, PER], F32))
            out_rows = s2.enter_context(nc.sbuf_tensor("m3_out_rows", [P, 2, PER], F32))

            @block.sync
            def _(sp):
                half = ALL // 2
                for part in (slice(0, half), slice(half, ALL)):
                    sp.dma_start(xs[:, part, :], sent.rearrange("(k p) d -> p k d", p=P)[:, part, :]
                                 ).then_inc(S["slots_in"], 16)
                for e in range(E):
                    sp.wait_ge(S["rows_ready"], e + 1)
                    at = e * PER
                    sp.dma_start(back[at:at + PER, :].rearrange("(k p) d -> p k d", p=P),
                                 out_rows[:, e % 2, :].rearrange("p (k d) -> p k d", d=P)).then_inc(S["returned"], 16)
                    sp.wait_ge(S["returned"], 16 * (e + 1))

            @block.tensor
            def _(pe):
                def up(n):
                    e, f = divmod(n, F)
                    if n >= 2:
                        pe.wait_ge(S["rv_ready"], n - 1)
                    if f == 0:
                        pe.wait_ge(S["xs_odd" if e % 2 else "xs_even"], e // 2 + 1)
                    x = xs_t[:, e * BLOCKS:(e + 1) * BLOCKS, :].rearrange("p k s -> p (k s)")
                    nc.tensor.matmul(a_ps[:, n % 2, 0:PER], w1[:, e, f, :], x, start=True,
                                     stop=True).then_inc(S["ra_ready"], 1)
                    nc.tensor.matmul(b_ps[:, n % 2, 0:PER], w3[:, e, f, :], x, start=True,
                                     stop=True).then_inc(S["rb_ready"], 1)

                def down(n):
                    e, f = divmod(n, F)
                    if f == 0 and e >= 2:
                        pe.wait_ge(S["ro_read"], e - 1)
                    pe.wait_ge(S["rv_ready"], n + 1)
                    mm = nc.tensor.matmul(o_ps[:, e % 2, 0:PER], w2[:, e, f, :], v[:, n % BUFS, 0:PER],
                                          start=(f == 0), stop=(f == F - 1))
                    if f == F - 1:
                        mm.then_inc(S["ro_ready"], 1)

                def turn_out(e):
                    pe.wait_ge(S["ro_read"], e + 1)
                    if e >= 2:
                        pe.wait_ge(S["rows_ready"], e - 1)
                    for j in range(BLOCKS):
                        mm = nc.tensor.transpose(tr_ps[:, e % 2, j * P:(j + 1) * P], out_t[:, e % 2, j * P:(j + 1) * P],
                                                 c.ident[:, :])
                    mm.then_inc(S["oo_turned"], 1)
                pe.wait_ge(S["slots_in"], 32)
                for e in range(E):
                    if e >= 2:
                        pe.wait_ge(S["xs_odd" if e % 2 else "xs_even"], e // 2)
                    for j in range(BLOCKS):
                        mm = nc.tensor.transpose(tr_ps[:, e % 2, j * P:(j + 1) * P], xs[:, e * BLOCKS + j, :],
                                                 c.ident[:, :])
                    mm.then_inc(S["xs_turned"], 1)
                pe.wait_ge(S["xs_odd"], E // 2)
                pe.wait_ge(S["xs_even"], (E + 1) // 2)
                for n in range(E * F):
                    up(n)
                    if n:
                        down(n - 1)
                    if n > F and n % F == 1:
                        turn_out(n // F - 1)
                down(E * F - 1)
                turn_out(E - 1)

            @block.scalar
            def _(act):
                def xs_copy(e):
                    act.wait_ge(S["xs_turned"], e + 1)
                    nc.scalar.copy(xs_t[:, e * BLOCKS:(e + 1) * BLOCKS, :].rearrange("p k s -> p (k s)"),
                                   tr_ps[:, e % 2, 0:PER]).then_inc(S["xs_odd" if e % 2 else "xs_even"], 1)
                for e in range(0, E, 2):
                    xs_copy(e)
                for n in range(E * F):
                    act.wait_ge(S["ra_ready"], n + 1)
                    if n >= BUFS:
                        act.wait_ge(S["rv_ready"], n - BUFS + 1)
                    nc.scalar.activation(sa[:, n % BUFS, 0:PER], a_ps[:, n % 2, 0:PER], ACT.Silu).then_inc(S["rsa_ready"], 1)
                    if n % F == 0 and n:
                        e = n // F - 1
                        act.wait_ge(S["ro_ready"], e + 1)
                        if e >= 2:
                            act.wait_ge(S["oo_turned"], e - 1)
                        nc.scalar.copy(out_t[:, e % 2, :], o_ps[:, e % 2, 0:PER]).then_inc(S["ro_read"], 1)
                act.wait_ge(S["ro_ready"], E)
                act.wait_ge(S["oo_turned"], E - 2)
                nc.scalar.copy(out_t[:, (E - 1) % 2, :], o_ps[:, (E - 1) % 2, 0:PER]).then_inc(S["ro_read"], 1)

            @block.vector
            def _(dve):
                def rows_copy(e):
                    dve.wait_ge(S["oo_turned"], e + 1)
                    if e >= 2:
                        dve.wait_ge(S["returned"], 16 * (e - 1))
                    nc.vector.tensor_copy(out_rows[:, e % 2, :], tr_ps[:, e % 2, 0:PER]).then_inc(S["rows_ready"], 1)
                for e in range(1, E, 2):
                    dve.wait_ge(S["xs_turned"], e + 1)
                    nc.vector.tensor_copy(xs_t[:, e * BLOCKS:(e + 1) * BLOCKS, :].rearrange("p k s -> p (k s)"),
                                          tr_ps[:, e % 2, 0:PER]).then_inc(S["xs_odd"], 1)
                for n in range(E * F):
                    dve.wait_ge(S["rsa_ready"], n + 1)
                    dve.wait_ge(S["rb_ready"], n + 1)
                    nc.vector.tensor_tensor(v[:, n % BUFS, 0:PER], sa[:, n % BUFS, 0:PER], b_ps[:, n % 2, 0:PER],
                                            ALU.mult).then_inc(S["rv_ready"], 1)
                    if n > F and n % F == 2:
                        rows_copy(n // F - 1)
                rows_copy(E - 1)

        stage_combine(c, "m3", 3, index, gates, back)


def layout_moe3(a, d, bf):
    d["r3_wr"] = a["L3_ffn_Wr"]
    d["r3_rank"] = rank_const(7)
    for n in ("w1", "w3"):
        w = np.concatenate([a[f"L3_ffn_{n.upper()}"], a[f"L3_ffn_{n.upper()}s"][None]])
        d[f"m3_{n}"] = w.reshape(8, P, 4, P).transpose(1, 0, 2, 3)
    w = np.concatenate([a["L3_ffn_W2"], a["L3_ffn_W2s"][None]])
    d["m3_w2"] = w.reshape(8, 4, P, P).transpose(2, 0, 1, 3)


HEADS, HD = 16, 8
SOFTMAX_SCALE = HD ** -0.5


def stage_head_attention(c):
    nc, ins = c.nc, c.ins
    SUB = SEQ // P
    POOL1, POOL2 = 13, 13
    with ExitStack() as s:
        def sb(name, shape, dt=F32):
            return s.enter_context(nc.sbuf_tensor(f"h1_{name}", shape, dt))

        def psum(name, shape):
            return s.enter_context(nc.psum_tensor(f"h1_{name}", shape, F32))

        def sem(name):
            return s.enter_context(nc.semaphore(f"h1_{name}"))

        wq = sb("wq", [P, 2, P])
        wkv = sb("wkv", [33, 3, P])
        bq = sb("bq", [1, 2, P])
        one = sb("one", [1, P])
        wdown, wo = sb("wdown", [P, 32]), sb("wo", [P, P])
        turn = sb("turn", [P, SUB, 2, HD])
        hb = sb("hb", [P, SEQ])
        lat = sb("lat", [33, SEQ])
        rc, rs = sb("rc", [P, 2, 2, P]), sb("rs", [P, 2, 2, P])
        qk, v = sb("qk", [P, 2, 2, P]), sb("v", [P, 2, P])
        pr1, pr2 = sb("pr1", [P, 2, HEADS, HEADS, HD]), sb("pr2", [P, 2, HEADS, HD, HEADS])
        sc, pe_ = sb("sc", [P, 2, HEADS, HEADS]), sb("e", [P, 2, HEADS, HEADS])
        mx, den, rden = sb("mx", [P, HEADS]), sb("den", [P, HEADS]), sb("rden", [P, HEADS])
        o, on = sb("o", [P, 2, P]), sb("on", [P, 2, P])
        y, z = sb("y", [P, 2, TILE]), sb("z", [P, 2, TILE])
        qk_ps = psum("qk_ps", [P, 2, 2, 2, P])
        v_ps = psum("v_ps", [P, 2, 4, P])
        lat_ps = psum("lat_ps", [32, TILE])
        y_ps, o_ps = psum("y_ps", [P, 2, TILE]), psum("o_ps", [P, TILE])
        names = ("loaded", "set", "h_copied", "lat_mm", "lat_ready", "qk_mm", "v_ready", "chain", "rope_ready", "p1",
                 "p1d", "s_ready", "e_ready", "p2", "p2d", "on_ready", "turned", "y_ready", "o_mm", "v_mm")
        (loaded, set_, h_copied, lat_mm, lat_ready, qk_mm, v_ready, chain, rope_ready, p1, p1d, s_ready, e_ready, p2,
         p2d, on_ready, turned, y_ready, o_mm, v_mm) = (sem(n) for n in names)
        CHAIN = 9 * SUB + 2 * TPB
        with nc.Block() as block:
            @block.sync
            def _(sp):
                for dst, name in ((wq[:, :, :], "h1_wq"), (wkv[:, :, :], "h1_wkv"), (bq[:, :, :], "h1_bq"),
                                  (wdown[:, :], "h1_wdown"), (wo[:, :], "h1_wo"), (turn[:, :, :, :], "h1_rope")):
                    sp.dma_start(dst, ins[name]).then_inc(loaded, 16)

            @block.tensor
            def _(pe):
                pe.wait_ge(loaded, 16 * 6)
                pe.wait_ge(set_, 2)
                with pe.Fori(0, BATCH) as b:
                    pe.wait_ge(h_copied, b + 1)
                    for u in range(TPB):
                        if u:
                            pe.wait_ge(lat_ready, b * 2 + u)
                        nc.tensor.matmul(lat_ps[:, :], wdown[:, :], hb[:, u * TILE:(u + 1) * TILE], start=True,
                                         stop=True).then_inc(lat_mm, 1)

                    def project(n):
                        if n >= 2:
                            pe.wait_ge(rope_ready, b * SUB + (n - 1))
                        tok = slice(n * P, (n + 1) * P)
                        ps = qk_ps[:, n % 2, :, :, :]
                        nc.tensor.matmul(ps[:, :, 0, :], hb[:, tok], wq[:, :, :], start=True, stop=False,
                                         skip_group_check=True)
                        nc.tensor.matmul(ps[:, :, 0, :], one[:, :], bq[:, :, :], start=False, stop=True,
                                         skip_group_check=True)
                        nc.tensor.matmul(ps[:, :, 1, :], lat[:, tok], wkv[:, 0:2, :], start=False, stop=True,
                                         skip_group_check=True).then_inc(qk_mm, 1)
                        if n >= 2:
                            pe.wait_ge(v_ready, b * SUB + (n - 1))
                        nc.tensor.matmul(v_ps[:, n % 2, 0, :], lat[:, tok], wkv[:, 2, :], start=True,
                                         stop=True).then_inc(v_mm, 1)

                    def turn_back(n):
                        pe.wait_ge(on_ready, b * SUB + (n + 1))
                        u, j = divmod(n, 4)
                        nc.tensor.transpose(y_ps[:, u, j * P:(j + 1) * P], on[:, n % 2, :],
                                            c.ident[:, :]).then_inc(turned, 1)

                    def out(u):
                        pe.wait_ge(y_ready, b * 2 + (u + 1))
                        nc.tensor.matmul(o_ps[:, :], wo[:, :], y[:, u, :], start=True, stop=True).then_inc(o_mm, 1)
                    pe.wait_ge(lat_ready, b * 2 + 2)
                    for n in range(SUB):
                        project(n)
                        if n >= 3:
                            turn_back(n - 3)
                    for n in range(SUB - 3, SUB):
                        turn_back(n)
                        if n == 5:
                            out(0)
                    out(1)

            @block.scalar
            def _(act):
                nc.scalar.preload_act_table(ACT.Exp)
                with act.Fori(0, BATCH) as b:
                    for u in range(TPB):
                        act.wait_ge(lat_mm, b * 2 + (u + 1))
                        nc.scalar.activation(lat[0:32, u * TILE:(u + 1) * TILE], lat_ps[:, :], ACT.Identity,
                                             bias=vec(c, "L1_bdown")[0:32, :]).then_inc(lat_ready, 1)
                    for n in range(SUB):
                        if n >= 1:
                            act.wait_ge(s_ready, b * SUB + n)
                            nc.scalar.activation(pe_[:, (n - 1) % 2, :, :], sc[:, (n - 1) % 2, :, :], ACT.Exp,
                                                 scale=SOFTMAX_SCALE).then_inc(e_ready, 1)
                        act.wait_ge(v_mm, b * SUB + (n + 1))
                        if n >= 2:
                            act.wait_ge(on_ready, b * SUB + (n - 1))
                        nc.scalar.copy(v[:, n % 2, :], v_ps[:, n % 2, 0, :]).then_inc(v_ready, 1)
                    act.wait_ge(s_ready, b * SUB + SUB)
                    nc.scalar.activation(pe_[:, (SUB - 1) % 2, :, :], sc[:, (SUB - 1) % 2, :, :], ACT.Exp,
                                         scale=SOFTMAX_SCALE).then_inc(e_ready, 1)

            def product1(eng, n, h0, h1):
                q = qk[:, n % 2, 0, h0 * HD:h1 * HD].rearrange("p (h d) -> p h d", d=HD)
                k = qk[:, n % 2, 1, :].rearrange("p (g d) -> p g d", d=HD)
                shape = [P, h1 - h0, HEADS, HD]
                return eng.tensor_tensor(pr1[:, n % 2, h0:h1, :, :], q.unsqueeze(2).to_broadcast(shape),
                                         k.unsqueeze(1).to_broadcast(shape), ALU.mult)

            def product2(eng, n, h0, h1):
                e = pe_[:, n % 2, h0:h1, :]
                w = v[:, n % 2, :].rearrange("p (g d) -> p d g", d=HD)
                shape = [P, h1 - h0, HD, HEADS]
                return eng.tensor_tensor(pr2[:, n % 2, h0:h1, :, :], e.unsqueeze(2).to_broadcast(shape),
                                         w.unsqueeze(1).to_broadcast(shape), ALU.mult)

            @block.gpsimd
            def _(pool):
                with pool.Fori(0, BATCH) as b:
                    def first(n):
                        pool.wait_ge(rope_ready, b * SUB + (n + 1))
                        if n >= 2:
                            pool.wait_ge(s_ready, b * SUB + (n - 1))
                        product1(nc.gpsimd, n, 0, POOL1).then_inc(p1, 1)

                    def second(n):
                        pool.wait_ge(e_ready, b * SUB + (n + 1))
                        pool.wait_ge(v_ready, b * SUB + (n + 1))
                        if n >= 2:
                            pool.wait_ge(on_ready, b * SUB + (n - 1))
                        product2(nc.gpsimd, n, 0, POOL2).then_inc(p2, 1)
                    first(0)
                    for n in range(SUB):
                        if n + 1 < SUB:
                            first(n + 1)
                        second(n)

            @block.vector
            def _(dve):
                nc.vector.memset(one[:, :], 1.0).then_inc(set_, 1)
                nc.vector.memset(lat[32:33, :], 1.0).then_inc(set_, 1)
                dve.wait_ge(loaded, 16 * 6)
                with dve.Fori(0, BATCH) as b:
                    done = Chain(dve, chain, CHAIN, b)
                    tt = nc.vector.tensor_tensor
                    nc.vector.tensor_copy(hb[:, :], c.h_t[:, bass.ts(b, SEQ)]).then_inc(h_copied, 1)

                    def rope_part(n, r):
                        if r == 0:
                            dve.wait_ge(qk_mm, b * SUB + (n + 1))
                        dst = (rc, rs)[r]
                        cs = turn[:, n, r, :].unsqueeze(1).to_broadcast([P, 2 * HEADS, HD])
                        return done.add(tt(dst[:, n % 2, :, :].rearrange("p x (h d) -> p (x h) d", d=HD),
                                           qk_ps[:, n % 2, r, :, :].rearrange("p x (h d) -> p (x h) d", d=HD), cs,
                                           ALU.mult))

                    def rope_sum(n, part):
                        if n >= 2:
                            dve.wait_ge(p1, b * SUB + (n - 1))
                        done.wait(part)
                        tt(qk[:, n % 2, :, :], rc[:, n % 2, :, :], rs[:, n % 2, :, :], ALU.add).then_inc(rope_ready, 1)

                    def scores(n):
                        ahead = n + 2 < SUB
                        dve.wait_ge(rope_ready, b * SUB + (n + 1))
                        product = done.add(product1(nc.vector, n, POOL1, HEADS))
                        dve.wait_ge(p1, b * SUB + (n + 1))
                        done.wait(product)
                        x = n % 2
                        total = done.add(nc.vector.reduce_sum(sc[:, x, :, :], pr1[:, x, :, :, :], AX.X))
                        if ahead:
                            rope_part(n + 2, 0)
                        done.wait(total)
                        most = done.add(nc.vector.reduce_max(mx[:, :], sc[:, x, :, :], AX.X))
                        if ahead:
                            part = rope_part(n + 2, 1)
                        done.wait(most)
                        tt(sc[:, x, :, :], sc[:, x, :, :], mx[:, :].unsqueeze(2).to_broadcast([P, HEADS, HEADS]),
                           ALU.subtract).then_inc(s_ready, 1)
                        if ahead:
                            rope_sum(n + 2, part)

                    def weigh(n):
                        x = n % 2
                        dve.wait_ge(s_ready, b * SUB + min(n + 2, SUB))
                        if n:
                            dve.wait_ge(on_ready, b * SUB + n)
                        dve.wait_ge(e_ready, b * SUB + (n + 1))
                        sums = done.add(nc.vector.reduce_sum(den[:, :], pe_[:, x, :, :], AX.X))
                        dve.wait_ge(v_ready, b * SUB + (n + 1))
                        product = done.add(product2(nc.vector, n, POOL2, HEADS))
                        done.wait(sums)
                        done.add(nc.vector.reciprocal(rden[:, :], den[:, :]))
                        dve.wait_ge(p2, b * SUB + (n + 1))
                        if n >= 2:
                            dve.wait_ge(turned, b * SUB + (n - 1))
                        done.wait(product)
                        done(nc.vector.reduce_sum(o[:, x, :].rearrange("p (h d) -> p h d", d=HD), pr2[:, x, :, :, :],
                                                  AX.X))
                        tt(on[:, x, :].rearrange("p (h d) -> p h d", d=HD),
                           o[:, x, :].rearrange("p (h d) -> p h d", d=HD),
                           rden[:, :].unsqueeze(2).to_broadcast([P, HEADS, HD]), ALU.mult).then_inc(on_ready, 1)

                    def gather(u):
                        dve.wait_ge(turned, b * SUB + 4 * (u + 1))
                        nc.vector.tensor_copy(y[:, u, :], y_ps[:, u, :]).then_inc(y_ready, 1)

                    def add(u):
                        dve.wait_ge(o_mm, b * 2 + (u + 1))
                        t = b * 2 + u
                        done(nc.vector.tensor_scalar(z[:, u, :], o_ps[:, :], vec(c, "L1_bout"),
                                                     c.mod[:, 1, GA, bass.ds(t, 1)], ALU.add, ALU.mult))
                        done(tt(c.x_t[:, bass.ts(t, TILE)], c.x_t[:, bass.ts(t, TILE)], z[:, u, :], ALU.add))
                    for n in range(2):
                        rope_part(n, 0)
                        rope_sum(n, rope_part(n, 1))
                    for n in range(SUB):
                        scores(n)
                        if n >= 1:
                            weigh(n - 1)
                    weigh(SUB - 1)
                    dve.wait_ge(on_ready, b * SUB + SUB)
                    gather(0)
                    add(0)
                    gather(1)
                    add(1)
                    assert done.n == CHAIN


def layout_head_attention(a, d, bf):
    up = a["L1_attn_Wup"].reshape(32, HEADS, 2, HD)
    bup = a["L1_attn_bup"].reshape(HEADS, 2, HD)
    wk, wv = up[:, :, 0].reshape(32, P), up[:, :, 1].reshape(32, P)
    bk, bv = bup[:, 0].reshape(1, P), bup[:, 1].reshape(1, P)
    d["h1_wq"] = np.stack([a["L1_attn_Wq"], rope_swap(a["L1_attn_Wq"])], 1)
    d["h1_wkv"] = np.concatenate([np.stack([wk, rope_swap(wk), wv], 1), np.stack([bk, rope_swap(bk), bv], 1)])
    bq = a["L1_attn_bq"][None]
    d["h1_bq"] = np.stack([bq, rope_swap(bq)], 1)
    d["h1_wdown"], d["h1_wo"] = a["L1_attn_Wdown"], a["L1_attn_Wout"]
    inv = 1.0 / 10000.0 ** (np.arange(0, HD, 2, dtype=np.float32) / np.float32(HD))
    freqs = np.arange(SEQ, dtype=np.float32)[:, None] * inv[None, :].astype(np.float32)
    cos, sin = np.cos(freqs), np.sin(freqs)
    table = np.stack([np.concatenate([cos, cos], 1), np.concatenate([-sin, sin], 1)], 1)
    d["h1_rope"] = table.reshape(SEQ // P, P, 2, HD).transpose(1, 0, 2, 3).astype(np.float32)


def stage_linear_attention(c):
    nc, ins = c.nc, c.ins
    H = 8
    D = P // H
    CH = SEQ // P
    with ExitStack() as s:
        def sb(name, shape, dt=F32):
            return s.enter_context(nc.sbuf_tensor(f"a2_{name}", shape, dt))

        def psum(name, shape):
            return s.enter_context(nc.psum_tensor(f"a2_{name}", shape, F32))

        def sem(name):
            return s.enter_context(nc.semaphore(f"a2_{name}"))

        w = sb("w", [P, 4, P])
        wo = sb("wo", [P, P])
        tri = sb("tri", [P, P])
        hmask = sb("hmask", [P, H])
        bmask = sb("bmask", [P, P])
        vt, ut = sb("vt", [P, SEQ]), sb("ut", [P, SEQ])
        xb, neg, pos = (sb(n, [P, 2, TILE]) for n in ("xb", "neg", "pos"))
        qt, kt = sb("qt", [P, SEQ]), sb("kt", [P, SEQ])
        vn, kn = sb("vn", [P, CH, P]), sb("kn", [P, CH, P])
        qx = sb("qx", [P, 2, H, P])
        en = sb("en", [P, 2, H, P])
        kvm, kvs = sb("kvm", [P, P]), sb("kvs", [P, 2, P])
        o, on, sq = sb("o", [P, CH, P]), sb("on", [P, CH, P]), sb("sq", [P, P])
        ss, rr, tiny = sb("ss", [P, CH]), sb("rr", [P, CH]), sb("tiny", [P, 1])
        y, z = sb("y", [P, 2, TILE]), sb("z", [P, 2, TILE])
        ps = psum("ps", [P, 2, TILE])
        en_ps = psum("en_ps", [P, 2, TILE])
        tr_ps, out_ps, kv_ps, oo_ps = (psum(n, [P, TILE]) for n in ("tr_ps", "out_ps", "kv_ps", "oo_ps"))
        names = ("loaded", "set", "proj_mm", "proj_read", "silu_done", "exp_done", "neg_ready", "pos_ready",
                 "elu_ready", "turned", "tok_ready", "qx_ready", "en_mm", "en_ready", "kv_mm", "kvm_ready",
                 "kvs_ready", "out_mm", "out_read", "ss_ready", "ln_done", "rms_ready", "rms_chain", "on_ready",
                 "back", "y_ready", "o_mm", "z_ready", "x_ready")
        S = {n: sem(n) for n in names}
        with nc.Block() as block:
            @block.sync
            def _(sp):
                for dst, name in ((w[:, :, :], "a2_w"), (wo[:, :], "a2_wo"), (tri[:, :], "a2_tri"),
                                  (hmask[:, :], "a2_hmask"), (bmask[:, :], "a2_bmask")):
                    sp.dma_start(dst, ins[name]).then_inc(S["loaded"], 16)

            def energies(n):
                return en_ps if n % 2 == 0 else ps

            @block.tensor
            def _(pe):
                pe.wait_ge(S["loaded"], 16 * 5)
                with pe.Fori(0, BATCH) as b:
                    for i in range(8):
                        if i >= 2:
                            pe.wait_ge(S["proj_read"], b * 8 + (i - 1))
                        nc.tensor.matmul(ps[:, i % 2, :], w[:, i // 2, :], c.h_t[:, bass.ts(b * 2 + i % 2, TILE)],
                                         start=True, stop=True).then_inc(S["proj_mm"], 1)

                    def to_tokens(i, src, ready, value):
                        pe.wait_ge(S[ready], value)
                        if i:
                            pe.wait_ge(S["tok_ready"], b * 4 + i)
                        for j in range(4):
                            at = (i % 2) * 4 + j
                            mm = nc.tensor.transpose(tr_ps[:, j * P:(j + 1) * P], src[:, at * P:(at + 1) * P],
                                                     c.ident[:, :])
                        mm.then_inc(S["turned"], 1)
                    for i in range(2):
                        to_tokens(i, vt, "silu_done", b * 4 + (i + 1))
                    for i in range(2):
                        to_tokens(2 + i, kt, "elu_ready", b * 4 + (3 + i))

                    def energy(n):
                        pe.wait_ge(S["qx_ready"], b * CH + (n + 1))
                        if n >= 2:
                            pe.wait_ge(S["en_ready"], b * CH + (n - 1))
                        for j in range(2):
                            mm = nc.tensor.matmul(energies(n)[:, j, :], kt[:, n * P:(n + 1) * P],
                                                  qx[:, n % 2, 4 * j:4 * j + 4, :], start=True, stop=True)
                        mm.then_inc(S["en_mm"], 1)

                    def keys_values(n):
                        if n == 0:
                            pe.wait_ge(S["tok_ready"], b * 4 + 4)
                        else:
                            pe.wait_ge(S["kvm_ready"], b * CH + n)
                        nc.tensor.matmul(kv_ps[:, 0:P], kn[:, n, :], vn[:, n, :], start=True,
                                         stop=True).then_inc(S["kv_mm"], 1)

                    def output(n):
                        pe.wait_ge(S["en_ready"], b * CH + (n + 1))
                        if n:
                            pe.wait_ge(S["kvs_ready"], b * CH + n)
                            pe.wait_ge(S["out_read"], b * CH + n)
                        if n:
                            nc.tensor.matmul(out_ps[:, 0:P], qt[:, n * P:(n + 1) * P], kvs[:, (n - 1) % 2, :],
                                             start=True, stop=False, skip_group_check=True)
                        for h in range(H):
                            mm = nc.tensor.matmul(out_ps[:, h * D:(h + 1) * D], en[:, n % 2, h, :],
                                                  vn[:, n, h * D:(h + 1) * D], start=(n == 0 and h == 0), stop=(h == H - 1),
                                                  skip_group_check=True)
                        mm.then_inc(S["out_mm"], 1)
                    energy(0)
                    for n in range(CH):
                        if n + 1 < CH:
                            energy(n + 1)
                        keys_values(n)
                        output(n)

                    def project(u):
                        pe.wait_ge(S["y_ready"], b * 2 + (u + 1))
                        if u:
                            pe.wait_ge(S["z_ready"], b * 2 + u)
                        nc.tensor.matmul(oo_ps[:, :], wo[:, :], y[:, u, :], start=True, stop=True).then_inc(S["o_mm"], 1)
                    pe.wait_ge(S["on_ready"], b + 1)
                    for u in range(2):
                        if u:
                            pe.wait_ge(S["y_ready"], b * 2 + u)
                        for j in range(4):
                            mm = nc.tensor.transpose(tr_ps[:, j * P:(j + 1) * P], on[:, u * 4 + j, :], c.ident[:, :])
                        mm.then_inc(S["back"], 1)
                        project(u)
                    pe.wait_ge(S["x_ready"], b * 2 + 2)

            @block.scalar
            def _(act):
                act.wait_ge(S["set"], 1)
                with act.Fori(0, BATCH) as b:
                    for i in range(4):
                        n, u = divmod(i, 2)
                        act.wait_ge(S["proj_mm"], b * 8 + (i + 1))
                        nc.scalar.activation((vt, ut)[n][:, u * TILE:(u + 1) * TILE], ps[:, u, :], ACT.Silu,
                                             bias=vec(c, ("L2_bv", "L2_bu")[n])).then_inc(S["silu_done"], 1)
                        act.wait_ge(S["silu_done"], b * 4 + (i + 1))
                        act.sem_inc(S["proj_read"], 1)
                    for i in range(4):
                        n, u = divmod(i, 2)
                        act.wait_ge(S["proj_mm"], b * 8 + (i + 5))
                        if i >= 2:
                            act.wait_ge(S["elu_ready"], b * 4 + (i - 1))
                        nc.scalar.activation(xb[:, u, :], ps[:, u, :], ACT.Identity,
                                             bias=vec(c, ("L2_bq", "L2_bk")[n])).then_inc(S["proj_read"], 1)
                        act.wait_ge(S["neg_ready"], b * 4 + (i + 1))
                        nc.scalar.activation(neg[:, u, :], neg[:, u, :], ACT.Exp).then_inc(S["exp_done"], 1)
                    for n in range(CH):
                        act.wait_ge(S["out_mm"], b * CH + (n + 1))
                        nc.scalar.copy(o[:, n, :], out_ps[:, 0:P]).then_inc(S["out_read"], 1)
                        act.wait_ge(S["out_read"], b * CH + (n + 1))
                        nc.scalar.activation(sq[:, :], o[:, n, :], ACT.Square, accum_out=ss[:, n:n + 1]).then_inc(S["ss_ready"], 1)
                        act.wait_ge(S["ss_ready"], b * CH + (n + 1))
                    nc.scalar.activation(rr[:, :], ss[:, :], ACT.Ln, bias=tiny[:, 0:1], scale=1.0 / P).then_inc(S["ln_done"], 1)
                    act.wait_ge(S["ln_done"], b + 1)
                    nc.scalar.activation(rr[:, :], rr[:, :], ACT.Exp, scale=0.5).then_inc(S["rms_ready"], 1)

            @block.gpsimd
            def _(pool):
                pool.wait_ge(S["loaded"], 16 * 5)
                with pool.Fori(0, BATCH) as b:
                    for n in range(CH):
                        pool.wait_ge(S["elu_ready"], b * 4 + (n // 4 + 1))
                        if n >= 2:
                            pool.wait_ge(S["en_mm"], b * CH + (n - 1))
                        shape = [P, H, P]
                        nc.gpsimd.tensor_tensor(qx[:, n % 2, :, :],
                                                qt[:, n * P:(n + 1) * P].unsqueeze(1).to_broadcast(shape),
                                                hmask[:, :].unsqueeze(2).to_broadcast(shape),
                                                ALU.mult).then_inc(S["qx_ready"], 1)

            @block.vector
            def _(dve):
                tt, ts = nc.vector.tensor_tensor, nc.vector.tensor_scalar
                nc.vector.memset(tiny[:, :], 1e-30).then_inc(S["set"], 1)
                dve.wait_ge(S["loaded"], 16 * 5)
                with dve.Fori(0, BATCH) as b:
                    def tokens(i):
                        dve.wait_ge(S["turned"], b * 4 + (i + 1))
                        dst = (vn, kn)[i // 2][:, (i % 2) * 4:(i % 2) * 4 + 4, :]
                        nc.vector.tensor_copy(dst, tr_ps[:, :].rearrange("p (j t) -> p j t", j=4)).then_inc(S["tok_ready"], 1)
                    for i in range(4):
                        n, u = divmod(i, 2)
                        dve.wait_ge(S["proj_read"], b * 8 + (i + 5))
                        ts(neg[:, u, :], xb[:, u, :], 0.0, None, ALU.min).then_inc(S["neg_ready"], 1)
                        ts(pos[:, u, :], xb[:, u, :], 0.0, None, ALU.max).then_inc(S["pos_ready"], 1)
                        dve.wait_ge(S["pos_ready"], b * 4 + (i + 1))
                        dve.wait_ge(S["exp_done"], b * 4 + (i + 1))
                        nc.vector.scalar_tensor_tensor((qt, kt)[n][:, u * TILE:(u + 1) * TILE], neg[:, u, :], -1.0,
                                                       pos[:, u, :], ALU.add, ALU.add).then_inc(S["elu_ready"], 1)
                    dve.wait_ge(S["elu_ready"], b * 4 + 4)
                    for i in range(4):
                        tokens(i)

                    def mask(n):
                        dve.wait_ge(S["en_mm"], b * CH + (n + 1))
                        if n >= 2:
                            dve.wait_ge(S["out_mm"], b * CH + (n - 1))
                        shape = [P, H, P]
                        tt(en[:, n % 2, :, :], energies(n)[:, :, :].rearrange("p j (h q) -> p (j h) q", q=P),
                           tri[:, :].unsqueeze(1).to_broadcast(shape), ALU.mult).then_inc(S["en_ready"], 1)
                    mask(0)
                    for n in range(CH):
                        if n + 1 < CH:
                            mask(n + 1)
                        dve.wait_ge(S["kv_mm"], b * CH + (n + 1))
                        tt(kvm[:, :], kv_ps[:, 0:P], bmask[:, :], ALU.mult).then_inc(S["kvm_ready"], 1)
                        dve.wait_ge(S["kvm_ready"], b * CH + (n + 1))
                        if n >= 2:
                            dve.wait_ge(S["out_mm"], b * CH + n)
                        if n == 0:
                            last = nc.vector.tensor_copy(kvs[:, 0, :], kvm[:, :])
                        else:
                            last = tt(kvs[:, n % 2, :], kvs[:, (n - 1) % 2, :], kvm[:, :], ALU.add)
                        last.then_inc(S["kvs_ready"], 1)
                        dve.wait_ge(S["kvs_ready"], b * CH + (n + 1))
                    dve.wait_ge(S["rms_ready"], b + 1)
                    chain = Chain(dve, S["rms_chain"], 2, b)
                    chain(ts(rr[:, :], rr[:, :], 1e-8, None, ALU.add))
                    chain(nc.vector.reciprocal(rr[:, :], rr[:, :]))
                    tt(on[:, :, :], o[:, :, :], rr[:, :].unsqueeze(2).to_broadcast([P, CH, P]),
                       ALU.mult).then_inc(S["on_ready"], 1)
                    for u in range(2):
                        t = b * 2 + u
                        dve.wait_ge(S["back"], b * 2 + (u + 1))
                        nc.vector.scalar_tensor_tensor(y[:, u, :], tr_ps[:, :], vec(c, "L2_scale"),
                                                       ut[:, u * TILE:(u + 1) * TILE], ALU.mult,
                                                       ALU.mult).then_inc(S["y_ready"], 1)
                        dve.wait_ge(S["o_mm"], b * 2 + (u + 1))
                        ts(z[:, u, :], oo_ps[:, :], vec(c, "L2_bo"), c.mod[:, 2, GA, bass.ds(t, 1)], ALU.add,
                           ALU.mult).then_inc(S["z_ready"], 1)
                        dve.wait_ge(S["z_ready"], b * 2 + (u + 1))
                        tt(c.x_t[:, bass.ts(t, TILE)], c.x_t[:, bass.ts(t, TILE)], z[:, u, :],
                           ALU.add).then_inc(S["x_ready"], 1)
                    dve.wait_ge(S["x_ready"], b * 2 + 2)


def layout_linear_attention(a, d, bf):
    d["a2_w"] = np.stack([a[f"L2_attn_W{n}"].T for n in "vuqk"], 1)
    d["a2_wo"] = a["L2_attn_Wo"].T
    d["a2_tri"] = np.triu(np.ones((P, P), np.float32))
    head = np.arange(P) // 16
    d["a2_hmask"] = (head[:, None] == np.arange(8)[None]).astype(np.float32)
    d["a2_bmask"] = (head[:, None] == head[None]).astype(np.float32)


HG = 4
GROUPS = BATCH * HEADS // HG
GCH = HG * HD
KP = 9 * HD
SOFTMAX_SCALE = HD ** -0.5


class Heads:

    def __init__(self, c, tag, stack):
        nc = c.nc
        self.parts = nc.dram_tensor(f"{tag}_parts", (2, 3, BATCH * P, SEQ), BF16, kind="Internal").ap()
        self.neg = nc.dram_tensor(f"{tag}_neg", (GROUPS * 2 * 3, HG * SEQ // 2), BF16, kind="Internal").ap()
        self.out = nc.dram_tensor(f"{tag}_out", (GROUPS * P, SEQ), F32, kind="Internal").ap()
        self.v_all = stack.enter_context(nc.sbuf_tensor(f"{tag}_v_all", [P, GROUPS, SEQ // P, GCH], F32))


def stage_project(c, tag, hd):
    nc, ins = c.nc, c.ins
    with ExitStack() as s:
        def sb(name, shape, dt=F32):
            return s.enter_context(nc.sbuf_tensor(f"{tag}p_{name}", shape, dt))

        def psum(name, shape):
            return s.enter_context(nc.psum_tensor(f"{tag}p_{name}", shape, F32))

        def sem(name):
            return s.enter_context(nc.semaphore(f"{tag}p_{name}"))

        wq, wk, wv = sb("wq", [P, P]), sb("wk", [P, P]), sb("wv", [P, P])
        hs = sb("hs", [P, 2, TILE])
        f = [sb(f"f{x}", [P, TILE]) for x in range(2)]
        r1 = [sb(f"r1{x}", [P, TILE]) for x in range(2)]
        r2 = [sb(f"r2{x}", [P, TILE]) for x in range(2)]
        pt = [sb(f"pt{x}", [P, 2, 3, TILE], BF16) for x in range(2)]
        qk_ps = [psum(f"qk_ps{x}", [P, TILE]) for x in range(2)]
        v_ps = psum("v_ps", [P, TILE // P, P])
        loaded, hs_ready, v_mm, v_free = (sem(n) for n in ("loaded", "hs_ready", "v_mm", "v_free"))
        mm, ps_free, f_ready, hi, r1_ready, mid, r2_ready, lo = (
            [sem(f"{n}{x}") for x in range(2)] for n in ("mm", "ps_free", "f_ready", "hi", "r1_ready", "mid",
                                                         "r2_ready", "lo"))
        stored = [[sem(f"stored{x}{u}") for u in range(2)] for x in range(2)]
        bias = [vec(c, f"{tag}_b{n}") for n in "qk"]
        with nc.Block() as block:
            @block.sync
            def _(sp):
                sp.dma_start(wq[:, :], ins[f"{tag}_wq"]).then_inc(loaded, 16)
                sp.dma_start(wk[:, :], ins[f"{tag}_wk"]).then_inc(loaded, 16)
                sp.dma_start(wv[:, :], ins[f"{tag}_wv"]).then_inc(loaded, 16)
                with sp.Fori(0, BATCH) as b:
                    for u in range(TPB):
                        for x in range(2):
                            sp.wait_ge(lo[x], b * 2 + (u + 2))
                            dst = hd.parts[x, :, bass.ts(b, P), u * TILE:(u + 1) * TILE]
                            sp.dma_start(dst.rearrange("r p t -> p r t"), pt[x][:, u, :, :]).then_inc(stored[x][u], 16)
                for x in range(2):
                    for u in range(2):
                        sp.wait_ge(stored[x][u], 16 * (BATCH + 1))

            @block.tensor
            def _(pe):
                pe.wait_ge(loaded, 16 * 3)
                for x in range(2):
                    pe.sem_inc(ps_free[x], 1)
                pe.sem_inc(v_free, 1)
                with pe.Fori(0, BATCH) as b:
                    for u in range(TPB):
                        n = b * 2 + (u + 1)
                        tile = bass.ts(b * 2 + u, TILE)
                        for x, w in enumerate((wq, wk)):
                            pe.wait_ge(ps_free[x], n)
                            nc.tensor.matmul(qk_ps[x][:, :], w[:, :], c.h_t[:, tile], start=True,
                                             stop=True).then_inc(mm[x], 1)
                        pe.wait_ge(hs_ready, n)
                        pe.wait_ge(v_free, n)
                        for j in range(TILE // P):
                            v = nc.tensor.matmul(v_ps[:, j, :], hs[:, u, j * P:(j + 1) * P], wv[:, :], start=True,
                                                 stop=True)
                        v.then_inc(v_mm, 1)

            @block.scalar
            def _(act):
                for x in range(2):
                    for u in range(2):
                        act.sem_inc(stored[x][u], 16)
                    act.sem_inc(lo[x], 1)
                with act.Fori(0, BATCH) as b:
                    for u in range(TPB):
                        n = b * 2 + (u + 1)
                        for x in range(2):
                            act.wait_ge(f_ready[x], n)
                            act.wait_ge(stored[x][u], b * 16 + 16)
                            nc.scalar.copy(pt[x][:, u, 0, :], f[x][:, :]).then_inc(hi[x], 1)
                        for x in range(2):
                            act.wait_ge(r1_ready[x], n)
                            nc.scalar.copy(pt[x][:, u, 1, :], r1[x][:, :]).then_inc(mid[x], 1)
                        for x in range(2):
                            act.wait_ge(r2_ready[x], n)
                            nc.scalar.copy(pt[x][:, u, 2, :], r2[x][:, :]).then_inc(lo[x], 1)

            @block.gpsimd
            def _(pool):
                with pool.Fori(0, BATCH) as b:
                    for u in range(TPB):
                        n = b * 2 + (u + 1)
                        for x in range(2):
                            pool.wait_ge(hi[x], n)
                            nc.gpsimd.tensor_tensor(r1[x][:, :], f[x][:, :], pt[x][:, u, 0, :],
                                                    ALU.subtract).then_inc(r1_ready[x], 1)
                        for x in range(2):
                            pool.wait_ge(mid[x], n)
                            nc.gpsimd.tensor_tensor(r2[x][:, :], r1[x][:, :], pt[x][:, u, 1, :],
                                                    ALU.subtract).then_inc(r2_ready[x], 1)

            @block.vector
            def _(dve):
                dve.wait_ge(loaded, 16 * 3)
                with dve.Fori(0, BATCH) as b:
                    for u in range(TPB):
                        n = b * 2 + (u + 1)
                        nc.vector.tensor_copy(hs[:, u, :], c.h_t[:, bass.ts(b * 2 + u, TILE)]).then_inc(hs_ready, 1)
                        for x in range(2):
                            dve.wait_ge(mm[x], n)
                            dve.wait_ge(lo[x], n)
                            nc.vector.tensor_scalar(f[x][:, :], qk_ps[x][:, :], bias[x], None,
                                                    ALU.add).then_inc(f_ready[x], 1)
                            dve.wait_ge(f_ready[x], n)
                            nc.vector.sem_inc(ps_free[x], 1)
                        dve.wait_ge(v_mm, n)
                        dst = hd.v_all[:, bass.ts(b, HG), u * 4:(u + 1) * 4, :]
                        nc.vector.tensor_copy(dst, v_ps[:, :, :].rearrange("p k (g c) -> p g k c", g=HG)).then_inc(v_free, 1)


def load_group(sp, hd, g, q9, k9, done):
    rows = [[hd.parts[x, part, bass.ts(g, GCH), :].rearrange("(d h) t -> d (h t)", h=HG) for part in range(3)]
            for x in range(2)]
    for a in range(3):
        at = slice(a * 3 * HD, (a + 1) * 3 * HD)
        sp.dma_start(q9[at, :, :].rearrange("p h t -> p (h t)"),
                     rows[0][a].unsqueeze(0).to_broadcast([3, HD, HG * SEQ])).then_inc(done, 16)
        sp.dma_start(k9[at, :, :].rearrange("p h t -> p (h t)"),
                     hd.parts[1, :, bass.ts(g, GCH), :].rearrange("r (d h) t -> r d (h t)", h=HG)).then_inc(done, 16)


LOADS = 6 * 16


def stage_window_attention(c):
    tag = "L3"
    nc, ins = c.nc, c.ins
    W = 64
    QT = SEQ // P
    with ExitStack() as s0:
        hd = Heads(c, tag, s0)
        stage_project(c, tag, hd)
        with ExitStack() as s:
            def sb(name, shape, dt=F32):
                return s.enter_context(nc.sbuf_tensor(f"{tag}a_{name}", shape, dt))

            def psum(name, shape):
                return s.enter_context(nc.psum_tensor(f"{tag}a_{name}", shape, F32))

            def sem(name):
                return s.enter_context(nc.semaphore(f"{tag}a_{name}"))

            q9 = [sb(f"q9_{i}", [KP + 3, HG, SEQ], BF16) for i in range(3)]
            k9 = [sb(f"k9_{i}", [KP + 3, HG, SEQ], BF16) for i in range(3)]
            va = [sb(f"va_{i}", [P, QT, HG, 32]) for i in range(3)]
            mask_q = sb("mask_q", [P, 2, W + P], BF16)
            mask_k = sb("mask_k", [P, HG, P], BF16)
            mask_w = sb("mask_w", [P, HG, W], BF16)
            p = sb("p", [P, 2, HG, P])
            pw = sb("pw", [P, 2, HG, W])
            neg = sb("neg", [P, 2, HG, 4])
            np_ = sb("neg_parts", [16, 2, 3, P], BF16)
            nr = sb("neg_rest", [16, 2, 2, P])
            o_sb = sb("o_sb", [P, 2, TILE])
            mx_ps, st_ps, sw_ps = psum("mx_ps", [P, 2, TILE]), psum("st_ps", [P, 2, HG, P]), psum("sw_ps", [P, 2, TILE])
            acc, tr_ps = psum("acc", [P, 4, P]), psum("tr_ps", [P, TILE])
            names = ("set", "masks", "va_ready", "mx_mm", "mx_done", "neg_turned", "neg_chain", "neg_parts",
                     "neg_out", "st_ready", "exp_done", "pv_done", "acc_out")
            (set_, masks, va_ready, mx_mm, mx_done, neg_turned, neg_chain, neg_parts, neg_out, st_ready,
             exp_done, pv_done, acc_out) = (sem(n) for n in names)
            loaded = [sem(f"loaded{i}") for i in range(3)]
            neg_in = [sem(f"neg_in{i}") for i in range(2)]
            stored = [sem(f"stored{i}") for i in range(2)]
            SLOTS = 2 * QT

            with nc.Block() as block:
                @block.sync
                def _(sp):
                    for dst, name in ((mask_q, "L3_mask_q"), (mask_k, "L3_mask_k"), (mask_w, "L3_mask_w")):
                        sp.dma_start(dst[:, :, :], ins[name]).then_inc(masks, 16)
                    sp.wait_ge(set_, 9)
                    for g in range(3):
                        load_group(sp, hd, g, q9[g], k9[g], loaded[g])

                    def maxima(g, u, half):
                        rows = hd.neg[bass.ds(g * 6 + half * 3, 3), :]
                        sp.wait_ge(neg_parts, g * 2 + (half + 1))
                        sp.dma_start(rows.rearrange("r (q t) -> q r t", t=P), np_[:, half, :, :]).then_inc(neg_out, 16)
                        sp.wait_ge(neg_out, g * 32 + 16 * (half + 1))
                        sp.dma_start(q9[u][KP:KP + 3, :, half * TILE:(half + 1) * TILE],
                                     rows.rearrange("r (h t) -> r h t", h=HG)).then_inc(neg_in[half], 16)

                    def store(g, half):
                        sp.wait_ge(acc_out, g * 2 + (half + 2))
                        sp.dma_start(hd.out[bass.ts(g, P), half * TILE:(half + 1) * TILE],
                                     o_sb[:, half, :]).then_inc(stored[half], 16)

                    def group(g, u, last=False, load=True):
                        for half in range(2):
                            if not last:
                                maxima(g + 1, (u + 1) % 3, half)
                            store(g, half)
                        if load:
                            load_group(sp, hd, g + 3, q9[u], k9[u], loaded[u])
                    for half in range(2):
                        sp.sem_inc(stored[half], 16)
                        maxima(0, 0, half)
                    loop = (GROUPS - 3) // 3
                    with sp.Fori(0, loop) as i:
                        for u in range(3):
                            group(i * 3 + u, u)
                    for g in range(3 * loop, GROUPS):
                        group(g, g % 3, last=(g == GROUPS - 1), load=(g + 3 < GROUPS))
                    for half in range(2):
                        sp.wait_ge(stored[half], (GROUPS + 1) * 16)

                @block.gpsimd
                def _(pool):
                    for i in range(3):
                        nc.gpsimd.memset(k9[i][64:, :, :], 1.0).then_inc(set_, 1)
                        pool.wait_ge(set_, 3 * i + 1)
                        nc.gpsimd.memset(va[i][:, :, :, HD:2 * HD], 1.0).then_inc(set_, 1)
                        pool.wait_ge(set_, 3 * i + 2)
                        nc.gpsimd.memset(va[i][:, :, :, 2 * HD:], 0.0).then_inc(set_, 1)
                        pool.wait_ge(set_, 3 * i + 3)

                    def values(g, u):
                        nc.gpsimd.tensor_copy(va[u][:, :, :, 0:HD],
                                              hd.v_all[:, bass.ds(g, 1), :, :].rearrange(
                                                  "p g k (h d) -> p (g k) h d", h=HG)).then_inc(va_ready, 1)
                    for g in range(3):
                        values(g, g)

                    def next_values(g, u):
                        pool.wait_ge(pv_done, g * QT - (2 * QT - 2))
                        values(g, u)
                    with pool.Fori(1, GROUPS // 3) as i:
                        for u in range(3):
                            next_values(i * 3 + u, u)
                    next_values(GROUPS - 1, 0)

                @block.tensor
                def _(pe):
                    pe.sem_inc(exp_done, 2)
                    pe.sem_inc(pv_done, 2)
                    pe.sem_inc(acc_out, 1)

                    def scores(g, u, n):
                        q, x = divmod(n, 2)
                        back = W if q else 0
                        free = g * SLOTS + (n - 1)
                        if not (isinstance(g, int) and free <= 0):
                            pe.wait_ge(mx_done, free)
                        out = mx_ps[:, x, 0:2 * (W + P)].rearrange("p (h k) -> p h k", h=2)[:, :, W - back:]
                        nc.tensor.matmul(out, c.ident_bf[:, :], mask_q[:, :, W - back:], start=True, stop=False,
                                         skip_group_check=True)
                        for h in range(2):
                            mm = nc.tensor.matmul(out[:, h, :], q9[u][0:KP, 2 * x + h, q * P:(q + 1) * P],
                                                  k9[u][0:KP, 2 * x + h, q * P - back:(q + 1) * P], start=False,
                                                  stop=True, skip_group_check=True)
                        mm.then_inc(mx_mm, 1)

                    def turn(g, half):
                        pe.wait_ge(mx_done, g * SLOTS + 8 * (half + 1))
                        if not (isinstance(g, int) and g + half == 0):
                            pe.wait_ge(neg_parts, g * 2 + half)
                        nc.tensor.transpose(tr_ps[0:16, 0:P], neg[:, half, :, :].rearrange("p h q -> p (h q)"),
                                            c.ident[:, :]).then_inc(neg_turned, 1)

                    def score(g, u, m):
                        pe.wait_ge(exp_done, g * QT + (m + 1))
                        q = slice(m * P, (m + 1) * P)
                        if m:
                            nc.tensor.matmul(sw_ps[W:, m % 2, 0:HG * W], c.ident_bf[:, W:], mask_w[:, :, :], start=True,
                                             stop=False, skip_group_check=True)
                            for h in range(HG):
                                nc.tensor.matmul(sw_ps[W:, m % 2, h * W:(h + 1) * W], k9[u][:, h, m * P - W:m * P],
                                                 q9[u][:, h, m * P:m * P + W], start=False, stop=True,
                                                 skip_group_check=True)
                        nc.tensor.matmul(st_ps[:, m % 2, :, :], c.ident_bf[:, :], mask_k[:, :, :], start=True, stop=False,
                                         skip_group_check=True)
                        for h in range(HG):
                            mm = nc.tensor.matmul(st_ps[:, m % 2, h, :], k9[u][:, h, q], q9[u][:, h, q], start=False,
                                                  stop=True, skip_group_check=True)
                        mm.then_inc(st_ready, 1)

                    def weigh(g, u, m):
                        half, j = divmod(m, 4)
                        if j == 0:
                            pe.wait_ge(acc_out, g * 2 + (half + 1))
                        pe.wait_ge(exp_done, g * QT + (m + 3))
                        for h in range(HG):
                            mm = nc.tensor.matmul(acc[32 * h:32 * h + 32, j, :], va[u][:, m, h, :], p[:, m % 2, h, :],
                                                  start=True, stop=(m == 0), skip_group_check=True)
                        if m:
                            for h in range(HG):
                                mm = nc.tensor.matmul(acc[32 * h:32 * h + 32, j, 0:W], va[u][W:, m - 1, h, :],
                                                      pw[W:, m % 2, h, :], start=False, stop=True, skip_group_check=True)
                        mm.then_inc(pv_done, 1)

                    def group(g, u, turn_, ahead):
                        pe.wait_ge(va_ready, g + 1)
                        if ahead:
                            pe.wait_ge(loaded[(u + 1) % 3], (turn_ + (u + 1) // 3) * LOADS + LOADS)
                        for n in range(SLOTS):
                            if ahead:
                                scores(g + 1, (u + 1) % 3, n)
                                if n == 9:
                                    turn(g + 1, 0)
                            m = n // 2
                            if n % 8 == 0:
                                pe.wait_ge(neg_in[n // 8], g * 16 + 16)
                            if n % 2 == 0:
                                score(g, u, m)
                            elif m:
                                weigh(g, u, m - 1)
                        if ahead:
                            turn(g + 1, 1)
                        weigh(g, u, QT - 1)
                    pe.wait_ge(masks, 48)
                    pe.wait_ge(loaded[0], LOADS)
                    for n in range(SLOTS):
                        scores(0, 0, n)
                        if n == 9:
                            turn(0, 0)
                    turn(0, 1)
                    with pe.Fori(0, GROUPS // 3) as i:
                        for u in range(3):
                            group(i * 3 + u, u, i, True)
                    group(GROUPS - 1, 0, GROUPS // 3, False)

                @block.scalar
                def _(act):
                    nc.scalar.preload_act_table(ACT.Exp)
                    with act.Fori(0, GROUPS) as g:
                        for m in range(QT):
                            act.wait_ge(st_ready, g * QT + (m + 1))
                            act.wait_ge(pv_done, g * QT + (m + 1))
                            if m:
                                nc.scalar.activation(pw[W:, m % 2, :, :],
                                                     sw_ps[W:, m % 2, 0:HG * W].rearrange("p (h q) -> p h q", h=HG),
                                                     ACT.Exp, scale=SOFTMAX_SCALE)
                            nc.scalar.activation(p[:, m % 2, :, :], st_ps[:, m % 2, :, :], ACT.Exp,
                                                 scale=SOFTMAX_SCALE).then_inc(exp_done, 1)

                @block.vector
                def _(dve):
                    def maximum(g, n):
                        q, x = divmod(n, 2)
                        dve.wait_ge(mx_mm, g * SLOTS + (n + 1))
                        keys = mx_ps[:, x, 0:2 * (W + P)].rearrange("p (h k) -> p h k", h=2)[:, :, 0 if q else W:]
                        nc.vector.tensor_reduce(neg[:, q // 4, 2 * x:2 * x + 2, q % 4:q % 4 + 1], keys, AX.X, ALU.max,
                                                negate=True).then_inc(mx_done, 1)

                    def split(g, half):
                        dve.wait_ge(neg_turned, g * 2 + (half + 1))
                        if not isinstance(g, int):
                            dve.wait_ge(neg_out, g * 32 + 16 * (half - 1))
                        src, k = tr_ps[0:16, 0:P], g * 8 + half * 4
                        for r in range(3):
                            out = np_[:, half, r, :]
                            if r == 2:
                                nc.vector.tensor_copy(out, src).then_inc(neg_parts, 1)
                                break
                            nc.vector.tensor_copy(out, src).then_inc(neg_chain, 1)
                            dve.wait_ge(neg_chain, k + (2 * r + 1))
                            nc.vector.tensor_tensor(nr[:, half, r, :], src, out, ALU.subtract).then_inc(neg_chain, 1)
                            dve.wait_ge(neg_chain, k + (2 * r + 2))
                            src = nr[:, half, r, :]

                    def evacuate(g, half):
                        dve.wait_ge(pv_done, g * QT + (4 * half + 6))
                        dve.wait_ge(stored[half], g * 16 + 16)
                        nc.vector.tensor_copy(o_sb[:, half, :], acc[:, :, :].rearrange("p j t -> p (j t)")).then_inc(acc_out, 1)

                    def maxima(g, own):
                        for n in range(SLOTS):
                            maximum(g, n)
                            if n == 10:
                                split(g, 0)
                            if n == 11 and own is not None:
                                evacuate(own, 0)
                        split(g, 1)
                    maxima(0, None)
                    with dve.Fori(0, GROUPS - 1) as g:
                        maxima(g + 1, g)
                        evacuate(g, 1)
                    evacuate(GROUPS - 1, 0)
                    evacuate(GROUPS - 1, 1)
        stage_attention_out(c, tag, 3, hd)


def stage_attention_out(c, tag, layer, hd):
    nc, ins = c.nc, c.ins
    with ExitStack() as s:
        def sb(name, shape, dt=F32):
            return s.enter_context(nc.sbuf_tensor(f"{tag}o_{name}", shape, dt))

        def sem(name):
            return s.enter_context(nc.semaphore(f"{tag}o_{name}"))

        wo = sb("wo", [P, P])
        od, r, y, z = (sb(n, [P, 2] + ([2] if n == "od" else []) + [TILE]) for n in ("od", "r", "y", "z"))
        o_ps = s.enter_context(nc.psum_tensor(f"{tag}o_ps", [P, 2, TILE], F32))
        loaded = [sem(f"loaded{u}") for u in range(2)]
        w_loaded, rec, scaled, ready, mm, gated, added = (
            sem(n) for n in ("w_loaded", "rec", "scaled", "ready", "mm", "gated", "added"))
        with nc.Block() as block:
            @block.sync
            def _(sp):
                sp.dma_start(wo[:, :], ins[f"{tag}_wo"]).then_inc(w_loaded, 16)
                sp.sem_inc(ready, 2)
                with sp.Fori(0, BATCH) as b:
                    for u in range(TPB):
                        sp.wait_ge(ready, b * 2 + (u + 1))
                        rows = hd.out[bass.ts(b, HG * P), u * TILE:(u + 1) * TILE].rearrange("(h r) t -> h r t", r=32)
                        for k in range(2):
                            sp.dma_start(od[:, u, k, :], rows[:, k * HD:(k + 1) * HD, :]).then_inc(loaded[u], 16)

            @block.tensor
            def _(pe):
                pe.wait_ge(w_loaded, 16)
                with pe.Fori(0, BATCH) as b:
                    for u in range(TPB):
                        pe.wait_ge(ready, b * 2 + (u + 3))
                        nc.tensor.matmul(o_ps[:, u, :], wo[:, :], y[:, u, :], start=True, stop=True).then_inc(mm, 1)

            @block.vector
            def _(dve):
                with dve.Fori(0, BATCH) as b:
                    for u in range(TPB):
                        n = b * 2 + (u + 1)
                        dve.wait_ge(loaded[u], b * 32 + 32)
                        nc.vector.reciprocal(r[:, u, :], od[:, u, 1, :]).then_inc(rec, 1)
                        dve.wait_ge(rec, n)
                        nc.vector.tensor_tensor(r[:, u, :], od[:, u, 0, :], r[:, u, :], ALU.mult).then_inc(scaled, 1)
                        dve.wait_ge(scaled, n)
                        nc.vector.tensor_scalar(y[:, u, :], r[:, u, :], vec(c, f"{tag}_bv"), None,
                                                ALU.add).then_inc(ready, 1)
                    for u in range(TPB):
                        n = b * 2 + (u + 1)
                        tile = bass.ts(b * 2 + u, TILE)
                        dve.wait_ge(mm, n)
                        nc.vector.tensor_scalar(z[:, u, :], o_ps[:, u, :], vec(c, f"{tag}_bo"),
                                                c.mod[:, layer, GA, bass.ds(b * 2 + u, 1)], ALU.add,
                                                ALU.mult).then_inc(gated, 1)
                        dve.wait_ge(gated, n)
                        nc.vector.tensor_tensor(c.x_t[:, tile], c.x_t[:, tile], z[:, u, :], ALU.add).then_inc(added, 1)
                    dve.wait_ge(added, b * 2 + 2)


def layout_window_attention(a, d, bf):
    order = np.arange(P).reshape(4, HG, HD).transpose(0, 2, 1).reshape(P)
    d["L3_wq"], d["L3_wk"] = a["L3_attn_Wq"].T[:, order], a["L3_attn_Wk"].T[:, order]
    d["L3_wv"], d["L3_wo"] = a["L3_attn_Wv"].T, a["L3_attn_Wo"].T
    W, never = 64, -1e9
    q = np.arange(P)[:, None]
    k = np.arange(-W, P)[None]
    mask = np.where((k <= q) & (k > q - W), 0.0, never)
    d["L3_mask_q"] = np.tile(mask[:, None, :], (1, 2, 1)).astype(bf)
    d["L3_mask_k"] = np.tile(mask[:, W:].T[:, None, :], (1, HG, 1)).astype(bf)
    earlier = np.zeros((P, W))
    earlier[W:] = mask[:W, :W].T
    d["L3_mask_w"] = np.tile(earlier[:, None, :], (1, HG, 1)).astype(bf)


def stage_mamba(c):
    nc, ins = c.nc, c.ins
    NS = 16
    RANK = P // 16
    ROWS = 3 * 2 * NS
    STEPS = 2 * NS
    TAPS = 4
    with ExitStack() as s:
        def sb(name, shape, dt=F32):
            return s.enter_context(nc.sbuf_tensor(f"ma_{name}", shape, dt))

        def psum(name):
            return s.enter_context(nc.psum_tensor(f"ma_{name}", [P, 2, TILE], F32))

        def sem(name):
            return s.enter_context(nc.semaphore(f"ma_{name}"))

        w_in, w_x = sb("w_in", [P, 4, P]), sb("w_x", [P, 2, ROWS + RANK])
        w_dt, w_out = sb("w_dt", [ROWS + RANK, 2, P]), sb("w_out", [P, 2, P])
        pick = sb("pick", [ROWS, 2 * NS, P], BF16)
        minus = sb("minus", [ROWS, 2])
        a, one = sb("a", [P, NS, 2]), sb("one", [P, 1])
        raw = sb("raw", [P, 2, TAPS - 1 + SEQ])
        conv, zs, dtu, yz = (sb(n, [P, 2, SEQ]) for n in ("conv", "zs", "dtu", "yz"))
        nab = conv
        u, dt = sb("u", [P, 2 * 2 * SEQ]), sb("dt", [P, 2 * 2 * SEQ])
        bc, rest = sb("bc", [ROWS + RANK, SEQ]), sb("rest", [ROWS, SEQ])
        part, bc3 = sb("part", [ROWS, SEQ], BF16), sb("bc3", [ROWS, 2 * SEQ], BF16)
        da, dbu = sb("da", [P, 4, SEQ]), sb("dbu", [P, 2, SEQ])
        bsb, state, hc = sb("bsb", [P, 4, SEQ]), sb("state", [P, 2, SEQ]), sb("hc", [P, 2, SEQ])
        in_ps, b_ps, c_ps, y_ps = (psum(n) for n in ("in_ps", "b_ps", "c_ps", "y_ps"))
        names = ("loaded", "set", "in_mm", "in_read", "z_mm", "z_read", "zs_ready", "conv_step", "u_ready", "xp_mm", "bc_ready", "split_step",
                 "dt_mm", "low_ready", "nab_ready", "exp_low", "ln_done", "dt_ready", "dtu_ready", "b_mm", "b_read",
                 "c_mm", "da_ready", "dbu_ready", "scan_done", "hc_ready", "sum_mm", "yd_ready", "yz_ready",
                 "o_mm", "x_ready", "act_go")
        S = {n: sem(n) for n in names}
        with nc.Block() as block:
            @block.sync
            def _(sp):
                for dst, name in ((w_in, "w_in"), (w_x, "w_x"), (w_dt, "w_dt"), (w_out, "w_out"), (pick, "pick")):
                    sp.dma_start(dst[:, :, :], ins[f"ma_{name}"]).then_inc(S["loaded"], 16)
                sp.dma_start(minus[:, :], ins["ma_minus"]).then_inc(S["loaded"], 16)

            def both(b, h, t=0, n=SEQ):
                return bass.ds((b % 2) * (2 * SEQ) + h * SEQ + t * TILE, n)

            def parts_of(b, t=0, n=SEQ):
                return bass.ds((b % 2) * SEQ + t * TILE, n)

            def rows(scans, eng):
                with eng.Fori(0, BATCH - 1) as b:
                    scans(b, True)
                scans(BATCH - 1, False)

            @block.tensor
            def _(pe):
                def tokens(b, t):
                    return c.h_t[:, bass.ds(b * SEQ + t * TILE, TILE)]

                def conv_in(b, i, first):
                    h, t = divmod(i, 2)
                    if i >= 2:
                        pe.wait_ge(S["in_read"], b * 4 + (i - 1))
                    elif not first:
                        pe.wait_ge(S["low_ready"], b * 4 + (i - 1))
                    nc.tensor.matmul(in_ps[:, t, :], w_in[:, h, :], tokens(b, t), start=True,
                                     stop=True).then_inc(S["in_mm"], 1)

                def gate_in(b, i, last):
                    h, t = divmod(i, 2)
                    if i >= 2:
                        pe.wait_ge(S["z_read"], b * 4 + (i - 1))
                    elif last:
                        pe.wait_ge(S["low_ready"], b * 4 + (3 + i))
                    else:
                        pe.wait_ge(S["in_read"], b * 4 + (7 + i))
                    nc.tensor.matmul(in_ps[:, t, :], w_in[:, 2 + h, :], tokens(b, t), start=True,
                                     stop=True).then_inc(S["z_mm"], 1)

                def x_proj(b, first):
                    pe.wait_ge(S["u_ready"], b * 2 + 2)
                    for t in range(2):
                        if first:
                            pe.wait_ge(S["in_read"], 3 + t)
                        else:
                            pe.wait_ge(S["z_read"], b * 4 + (t - 1))
                        for h in range(2):
                            mm = nc.tensor.matmul(in_ps[0:ROWS + RANK, t, :], w_x[:, h, :], u[:, both(b, h, t, TILE)],
                                                  start=(h == 0), stop=(h == 1))
                        mm.then_inc(S["xp_mm"], 1)

                def dt_proj(b, h):
                    for t in range(2):
                        if h == 0:
                            pe.wait_ge(S["bc_ready"], b * 2 + (t + 1))
                        else:
                            pe.wait_ge(S["low_ready"], b * 4 + (t + 1))
                        nc.tensor.matmul(in_ps[:, t, :], w_dt[:, h, :], bc[:, t * TILE:(t + 1) * TILE],
                                         start=True, stop=True).then_inc(S["dt_mm"], 1)

                prepare = {}
                for i in range(4):
                    prepare[(0, 1, 4, 5)[i]] = lambda b, first, i=i: conv_in(b, i, first)
                prepare[15] = x_proj
                prepare[18] = lambda b, first: dt_proj(b, 0)
                prepare[21] = lambda b, first: dt_proj(b, 1)

                def spread(row, b, ps):
                    for t in range(2):
                        mm = nc.tensor.matmul(ps[:, t, :], pick[:, row, :], bc3[:, parts_of(b, t, TILE)],
                                              start=True, stop=True)
                    return mm

                def spread_b(b, j):
                    pe.wait_ge(S["b_read"], b * STEPS + (j + 1))
                    spread(j % NS, b, b_ps).then_inc(S["b_mm"], 1)

                def spread_c(b, j):
                    pe.wait_ge(S["hc_ready"], b * STEPS + (j + 2))
                    spread(NS + j % NS, b, c_ps).then_inc(S["c_mm"], 1)

                def scans(b, more):
                    for j in range(STEPS):
                        if j + 1 < STEPS:
                            spread_c(b, j + 1)
                        elif more:
                            spread_c(b + 1, 0)
                        if j + 3 < STEPS:
                            spread_b(b, j + 3)
                        elif more:
                            pe.wait_ge(S["split_step"], b * 4 + 8)
                            spread_b(b + 1, j + 3 - STEPS)
                        if j == NS:
                            pe.wait_ge(S["yd_ready"], b * 2 + 1)
                        pe.wait_ge(S["hc_ready"], b * STEPS + (j + 3))
                        for t in range(2):
                            mm = nc.tensor.matmul(y_ps[:, t, :], c.ident[:, :], hc[:, j % 2, t * TILE:(t + 1) * TILE],
                                                  start=(j % NS == 0), stop=(j % NS == NS - 1))
                        mm.then_inc(S["sum_mm"], 1)
                        if more and j in prepare:
                            prepare[j](b + 1, False)
                        if j in (7, 8, 10, 11):
                            gate_in(b, (7, 8, 10, 11).index(j), not more)
                    pe.wait_ge(S["yz_ready"], b * 2 + 4)
                    for t in range(2):
                        for h in range(2):
                            mm = nc.tensor.matmul(y_ps[:, t, :], w_out[:, h, :], yz[:, h, t * TILE:(t + 1) * TILE],
                                                  start=(h == 0), stop=(h == 1))
                        mm.then_inc(S["o_mm"], 1)
                    pe.wait_ge(S["x_ready"], b * 2 + 2)

                pe.wait_ge(S["loaded"], 16 * 6)
                pe.sem_inc(S["b_read"], 1)
                pe.sem_inc(S["hc_ready"], 2)
                pe.sem_inc(S["sum_mm"], 2)
                pe.sem_inc(S["scan_done"], 4)
                pe.sem_inc(S["dbu_ready"], 4)
                pe.sem_inc(S["yz_ready"], 2)
                for piece in sorted(prepare):
                    prepare[piece](0, True)
                pe.wait_ge(S["split_step"], 4)
                spread_b(0, 0)
                spread_c(0, 0)
                spread_b(0, 1)
                spread_b(0, 2)
                rows(scans, pe)

            @block.scalar
            def _(act):
                def go():
                    act.sem_inc(S["act_go"], 1)

                def conv_copy(b, i, first):
                    h, t = divmod(i, 2)
                    if i == 0 and not first:
                        act.wait_ge(S["conv_step"], b * 2 * TAPS)
                    act.wait_ge(S["in_mm"], b * 4 + (i + 1))
                    at = TAPS - 1 + t * TILE
                    nc.scalar.copy(raw[:, h, at:at + TILE], in_ps[:, t, :]).then_inc(S["in_read"], 1)

                def gate(b, i):
                    h, t = divmod(i, 2)
                    act.wait_ge(S["z_mm"], b * 4 + (i + 1))
                    nc.scalar.copy(zs[:, h, t * TILE:(t + 1) * TILE], in_ps[:, t, :]).then_inc(S["z_read"], 1)

                def gate_silu(b):
                    for h in range(2):
                        act.wait_ge(S["z_read"], b * 4 + (2 * h + 2))
                        nc.scalar.activation(zs[:, h, :], zs[:, h, :], ACT.Silu).then_inc(S["zs_ready"], 1)

                def conv_out(b, first):
                    for h in range(2):
                        act.wait_ge(S["conv_step"], b * 2 * TAPS + (h + 1) * TAPS)
                        go()
                        nc.scalar.activation(u[:, both(b, h)], conv[:, h, :], ACT.Silu,
                                             bias=vec(c, f"conv_b{h}")).then_inc(S["u_ready"], 1)

                def bc_copy(b, first):
                    for t in range(2):
                        act.wait_ge(S["xp_mm"], b * 2 + (t + 1))
                        nc.scalar.copy(bc[:, t * TILE:(t + 1) * TILE], in_ps[0:ROWS + RANK, t, :]).then_inc(S["bc_ready"], 1)

                def dt_low(b, h):
                    for t in range(2):
                        act.wait_ge(S["dt_mm"], b * 4 + (2 * h + t + 1))
                        go()
                        nc.scalar.activation(dt[:, both(b, h, t, TILE)], in_ps[:, t, :], ACT.Identity,
                                             bias=vec(c, f"dt_b{h}")).then_inc(S["low_ready"], 1)

                def dt_log(b, first):
                    for h in range(2):
                        act.wait_ge(S["nab_ready"], b * 2 + (h + 1))
                        nc.scalar.activation(nab[:, h, :], nab[:, h, :], ACT.Exp).then_inc(S["exp_low"], 1)
                        act.wait_ge(S["exp_low"], b * 2 + (h + 1))
                        nc.scalar.activation(nab[:, h, :], nab[:, h, :], ACT.Ln,
                                             bias=one[:, 0:1]).then_inc(S["ln_done"], 1)

                prepare = {}
                for i in range(4):
                    prepare[(3, 4, 7, 8)[i]] = lambda b, first, i=i: conv_copy(b, i, first)
                prepare[14] = conv_out
                prepare[18] = bc_copy
                prepare[21] = lambda b, first: dt_low(b, 0)
                prepare[24] = lambda b, first: dt_low(b, 1)
                prepare[27] = dt_log

                def spread_copy(b, j):
                    act.wait_ge(S["b_mm"], b * STEPS + (j + 1))
                    act.wait_ge(S["dbu_ready"], b * STEPS + (j + 1))
                    nc.scalar.copy(bsb[:, j % 4, :], b_ps[:, :, :].rearrange("p t n -> p (t n)")).then_inc(S["b_read"], 1)

                def scans(b, more):
                    for j in range(STEPS):
                        h, n = divmod(j, NS)
                        if n == 0:
                            act.wait_ge(S["dt_ready"], b * 2 + (h + 1))
                        spread_copy(b, j)
                        act.wait_ge(S["scan_done"], b * STEPS + (j + 1))
                        go()
                        nc.scalar.activation(da[:, j % 4, :], dt[:, both(b, h)], ACT.Exp,
                                             scale=a[:, n, h:h + 1]).then_inc(S["da_ready"], 1)
                        if j in (10, 11, 13, 14):
                            if j == 10:
                                act.wait_ge(S["yz_ready"], b * 2 + 2)
                            gate(b, (10, 11, 13, 14).index(j))
                        if more and j in prepare:
                            prepare[j](b + 1, False)
                        if j == 14:
                            gate_silu(b)
                            nc.scalar.preload_act_table_set(LN_EXP_SET)

                first = VECS.index("A_log00")
                nc.scalar.activation(a[:, :, :].rearrange("p s h -> p (s h)"), c.vecs[:, first:first + 2 * NS],
                                     ACT.Exp).then_inc(S["set"], 1)
                act.wait_ge(S["set"], 4)
                for piece in sorted(prepare):
                    prepare[piece](0, True)
                    if piece == 14:
                        nc.scalar.preload_act_table_set(LN_EXP_SET)
                rows(scans, act)

            @block.gpsimd
            def _(pool):
                def step_in(b, h):
                    pool.wait_ge(S["dt_ready"], b * 2 + (h + 1))
                    nc.gpsimd.tensor_tensor(dtu[:, h, :], dt[:, both(b, h)], u[:, both(b, h)],
                                            ALU.mult).then_inc(S["dtu_ready"], 1)

                def scans(b, more):
                    for j in range(STEPS):
                        if j % NS == 0:
                            pool.wait_ge(S["dtu_ready"], b * 2 + (j // NS + 1))
                        pool.wait_ge(S["b_read"], b * STEPS + (j + 2))
                        pool.wait_ge(S["scan_done"], b * STEPS + (j + 3))
                        nc.gpsimd.tensor_tensor(dbu[:, j % 2, :], dtu[:, j // NS, :], bsb[:, j % 4, :],
                                                ALU.mult).then_inc(S["dbu_ready"], 1)
                        if j == 7:
                            pool.wait_ge(S["dbu_ready"], b * STEPS + 4)
                            step_in(b, 1)
                        if j == 29 and more:
                            pool.wait_ge(S["dbu_ready"], b * STEPS + (NS + 4))
                            step_in(b + 1, 0)

                step_in(0, 0)
                rows(scans, pool)

            @block.vector
            def _(dve):
                tt, ts, stt = nc.vector.tensor_tensor, nc.vector.tensor_scalar, nc.vector.scalar_tensor_tensor

                def conv_tap(b, h, k, first):
                    w = vec(c, f"conv_w{k}{h}")
                    if k == 0:
                        if not first:
                            dve.wait_ge(S["dt_ready"], b * 2)
                        dve.wait_ge(S["in_read"], b * 4 + (2 * h + 2))
                        last = ts(conv[:, h, :], raw[:, h, 0:SEQ], w, None, ALU.mult)
                    else:
                        dve.wait_ge(S["conv_step"], b * 2 * TAPS + (h * TAPS + k))
                        last = stt(conv[:, h, :], raw[:, h, k:k + SEQ], w, conv[:, h, :], ALU.mult, ALU.add)
                    last.then_inc(S["conv_step"], 1)

                def split(b, k):
                    if k:
                        dve.wait_ge(S["split_step"], b * 4 + k)
                    else:
                        dve.wait_ge(S["bc_ready"], b * 2 + 2)
                    (lambda: nc.vector.tensor_copy(part[:, :], bc[0:ROWS, :]),
                     lambda: stt(rest[:, :], part[:, :], minus[:, 0:1], bc[0:ROWS, :], ALU.mult, ALU.add),
                     lambda: nc.vector.tensor_copy(part[:, :], rest[:, :]),
                     lambda: stt(bc3[:, parts_of(b)], part[:, :], minus[:, 1:2], rest[:, :], ALU.mult,
                                 ALU.add))[k]().then_inc(S["split_step"], 1)

                def softplus_in(b, h):
                    dve.wait_ge(S["low_ready"], b * 4 + (2 * h + 2))
                    x = dt[:, both(b, h)]
                    stt(nab[:, h, :], x, -1.0, x, ALU.mult, ALU.min).then_inc(S["nab_ready"], 1)

                def softplus_out(b, h):
                    dve.wait_ge(S["ln_done"], b * 2 + (h + 1))
                    x = dt[:, both(b, h)]
                    stt(x, x, 0.0, nab[:, h, :], ALU.max, ALU.add).then_inc(S["dt_ready"], 1)

                def finish_sum(b, h):
                    dve.wait_ge(S["sum_mm"], b * STEPS + (h * NS + NS + 2))
                    stt(yz[:, h, :], u[:, both(b, h)], vec(c, f"D{h}"), y_ps[:, :, :].rearrange("p t n -> p (t n)"),
                        ALU.mult, ALU.add).then_inc(S["yd_ready"], 1)

                def finish_gate(b, h):
                    dve.wait_ge(S["yd_ready"], b * 2 + (h + 1))
                    dve.wait_ge(S["zs_ready"], b * 2 + (h + 1))
                    tt(yz[:, h, :], yz[:, h, :], zs[:, h, :], ALU.mult).then_inc(S["yz_ready"], 1)

                prepare = {}
                for i in range(2 * TAPS):
                    prepare[3 + i] = lambda b, first, i=i: conv_tap(b, i // TAPS, i % TAPS, first)
                for k in range(4):
                    prepare[17 + k] = lambda b, first, k=k: split(b, k)
                for h in range(2):
                    prepare[21 + 3 * h] = lambda b, first, h=h: softplus_in(b, h)
                    prepare[27 + h] = lambda b, first, h=h: softplus_out(b, h)

                def scans(b, more):
                    for j in range(STEPS):
                        h, n = divmod(j, NS)
                        dve.wait_ge(S["da_ready"], b * STEPS + (j + 1))
                        dve.wait_ge(S["dbu_ready"], b * STEPS + (j + 5))
                        dve.wait_ge(S["hc_ready"], b * STEPS + (j + 1))
                        nc.vector.tensor_tensor_scan(state[:, j % 2, :], da[:, j % 4, :], dbu[:, j % 2, :], 0.0,
                                                     ALU.mult, ALU.add).then_inc(S["scan_done"], 1)
                        if more and j in prepare:
                            prepare[j](b + 1, False)
                        if j == NS:
                            finish_sum(b, 0)
                        dve.wait_ge(S["scan_done"], b * STEPS + (j + 5))
                        dve.wait_ge(S["c_mm"], b * STEPS + (j + 1))
                        dve.wait_ge(S["sum_mm"], b * STEPS + (j + 1))
                        tt(hc[:, j % 2, :], state[:, j % 2, :], c_ps[:, :, :].rearrange("p t n -> p (t n)"),
                           ALU.mult).then_inc(S["hc_ready"], 1)
                        if j == NS:
                            finish_gate(b, 0)
                    finish_sum(b, 1)
                    finish_gate(b, 1)
                    for t in range(2):
                        dve.wait_ge(S["o_mm"], b * 2 + (t + 1))
                        tile = bass.ds(b * SEQ + t * TILE, TILE)
                        stt(c.x_t[:, tile], y_ps[:, t, :], c.mod[:, 0, GA, bass.ds(b * 2 + t, 1)], c.x_t[:, tile],
                            ALU.mult, ALU.add).then_inc(S["x_ready"], 1)

                nc.vector.memset(one[:, :], 1.0).then_inc(S["set"], 1)
                nc.vector.memset(raw[:, :, 0:TAPS - 1], 0.0).then_inc(S["set"], 1)
                dve.wait_ge(S["set"], 3)
                ts(a[:, :, :], a[:, :, :], -1.0, None, ALU.mult).then_inc(S["set"], 1)
                dve.wait_ge(S["loaded"], 16 * 6)
                for piece in sorted(prepare):
                    prepare[piece](0, True)
                rows(scans, dve)


def layout_mamba(a, d, bf):
    d["ma_w_in"] = a["L0_attn_in_proj_w"].reshape(P, 4, P)
    w = a["L0_attn_x_proj_w"].reshape(2, P, -1).transpose(1, 0, 2)
    rank = P // 16
    bc = w[:, :, rank:]
    d["ma_w_x"] = np.concatenate([bc, bc, bc, w[:, :, :rank]], 2)
    d["ma_w_dt"] = np.concatenate([np.zeros((96, 2, P), np.float32),
                                   a["L0_attn_dt_proj_w"].reshape(rank, 2, P)])
    d["ma_w_out"] = a["L0_attn_out_proj_w"].reshape(2, P, P).transpose(1, 0, 2)
    rows = np.arange(96)
    pick = (rows[:, None] % 32 == np.arange(32)[None]).astype(bf)
    d["ma_pick"] = np.repeat(pick[:, :, None], P, 2)
    d["ma_minus"] = -np.stack([rows >= 32, rows >= 64], 1).astype(np.float32)


def stage_slots(c):
    nc, ins = c.nc, c.ins
    G = 16
    SLOTS = P // 2
    GROUPS = TOK // G
    GPT = P // G
    PAIRS = SLOTS // 2
    F = P // 2
    with ExitStack() as s:
        def sb(name, shape, dt=F32):
            return s.enter_context(nc.sbuf_tensor(f"f0_{name}", shape, dt))

        def sem(name):
            return s.enter_context(nc.semaphore(f"f0_{name}"))

        ctrl, tie, parity = sb("ctrl", [P, P]), sb("tie", [P, G]), sb("parity", [P, 2])
        quarter = sb("quarter", [P, P // 32])
        f1, f2, bias = sb("f1", [P, SLOTS, F]), sb("f2", [P, PAIRS, P]), sb("bias", [P, PAIRS])
        perm_t, top = sb("perm_t", [P, TOK]), sb("top", [P, GROUPS])
        sel = sb("sel", [P, GROUPS, SLOTS])
        loaded, weights = sem("loaded"), sem("weights")
        names = ("lg_mm", "lg_read", "perm_step", "p_turned", "x_turned", "p_ready", "xk_ready", "sel_mm",
                 "sel_even", "sel_odd", "up_mm", "inner_ready", "down_mm", "out_ready", "o_turned", "turned_even",
                 "turned_odd", "o_mm", "x_ready")
        S = {n: sem(n) for n in names}

        with ExitStack() as s1, nc.Block() as block:
            lg_ps = s1.enter_context(nc.psum_tensor("f0_lg_ps", [P, 2, TILE], F32))

            @block.sync
            def _(sp):
                for dst, name in ((ctrl, "ctrl"), (tie, "tie"), (parity, "parity"), (quarter, "quarter"), (bias, "bias")):
                    sp.dma_start(dst[:, :], ins[f"f0_{name}"]).then_inc(loaded, 16)
                sp.dma_start(f1[:, :, :], ins["f0_f1"]).then_inc(weights, 16)
                sp.dma_start(f2[:, :, :], ins["f0_f2"]).then_inc(weights, 16)

            @block.tensor
            def _(pe):
                pe.wait_ge(loaded, 16 * 5)
                for t in range(NT):
                    if t >= 2:
                        pe.wait_ge(S["lg_read"], t - 1)
                    nc.tensor.matmul(lg_ps[:, t % 2, :], ctrl[:, :], c.h_t[:, t * TILE:(t + 1) * TILE],
                                     start=True, stop=True).then_inc(S["lg_mm"], 1)

            @block.vector
            def _(dve):
                tt = nc.vector.tensor_tensor
                dve.wait_ge(loaded, 16 * 5)
                per = TILE // G
                for t in range(NT):
                    dve.wait_ge(S["lg_mm"], t + 1)
                    at = slice(t * TILE, (t + 1) * TILE)
                    view = perm_t[:, at].rearrange("p (g k) -> p g k", k=G)
                    tt(view, lg_ps[:, t % 2, :].rearrange("p (g k) -> p g k", k=G),
                       tie[:, :].unsqueeze(1).to_broadcast([P, per, G]), ALU.add).then_inc(S["lg_read"], 1)
                step = Chain(dve, S["perm_step"])
                dve.wait_ge(S["lg_read"], NT)
                groups = perm_t[:, :].rearrange("p (g k) -> p g k", k=G)
                step(nc.vector.reduce_max(top[:, :], groups, AX.X))
                step(tt(groups, groups, top[:, :].unsqueeze(2).to_broadcast([P, GROUPS, G]), ALU.is_equal))
                pairs = perm_t[:, :].rearrange("p (m r k) -> p m r k", r=2, k=G)
                for r in range(2):
                    nc.vector.tensor_scalar(pairs[:, :, r, :], pairs[:, :, r, :], parity[:, r:r + 1], None,
                                            ALU.mult).then_inc(S["perm_step"], 1)
                dve.wait_ge(S["perm_step"], 4)

        with ExitStack() as s2, nc.Block() as block:
            pt_ps, xt_ps, sel_ps = (s2.enter_context(nc.psum_tensor(f"f0_{n}", [P, 2, TILE], F32))
                                    for n in ("pt_ps", "xt_ps", "sel_ps"))
            perm = s2.enter_context(nc.sbuf_tensor("f0_perm", [P, 2, P // 32, P], F32))
            xk = s2.enter_context(nc.sbuf_tensor("f0_xk", [P, 2, P], F32))

            def copied(eng, k):
                eng.wait_ge(S["sel_odd" if k % 2 else "sel_even"], k // 2 + 1)

            def take(copy, k):
                copy(sel[:, k * GPT:(k + 1) * GPT, :].rearrange("p g e -> p (g e)"), sel_ps[:, k % 2, :]).then_inc(S["sel_odd" if k % 2 else "sel_even"], 1)

            @block.tensor
            def _(pe):
                def turn(k):
                    at = slice(k * P, (k + 1) * P)
                    if k >= 2:
                        pe.wait_ge(S["p_ready"], k - 1)
                        pe.wait_ge(S["xk_ready"], k - 1)
                    nc.tensor.transpose(pt_ps[:, k % 2, 0:P], perm_t[:, at], c.ident[:, :]).then_inc(S["p_turned"], 1)
                    nc.tensor.transpose(xt_ps[:, k % 2, 0:P], c.h_t[:, at], c.ident[:, :]).then_inc(S["x_turned"], 1)
                turn(0)
                for k in range(KT):
                    if k + 1 < KT:
                        turn(k + 1)
                    pe.wait_ge(S["p_ready"], k + 1)
                    pe.wait_ge(S["xk_ready"], k + 1)
                    if k >= 2:
                        copied(pe, k - 2)
                    nc.tensor.matmul(sel_ps[:, k % 2, :], xk[:, k % 2, :], perm[:, k % 2, :, :], start=True,
                                     stop=True).then_inc(S["sel_mm"], 1)

            @block.scalar
            def _(act):
                for k in range(KT):
                    act.wait_ge(S["x_turned"], k + 1)
                    if k >= 2:
                        act.wait_ge(S["sel_mm"], k - 1)
                    nc.scalar.copy(xk[:, k % 2, :], xt_ps[:, k % 2, 0:P]).then_inc(S["xk_ready"], 1)
                    if k % 2 == 1:
                        act.wait_ge(S["sel_mm"], k)
                        take(nc.scalar.copy, k - 1)

            @block.vector
            def _(dve):
                shape = [P, P // 32, P]
                for k in range(KT):
                    dve.wait_ge(S["p_turned"], k + 1)
                    if k >= 2:
                        dve.wait_ge(S["sel_mm"], k - 1)
                    nc.vector.tensor_tensor(perm[:, k % 2, :, :], pt_ps[:, k % 2, 0:P].unsqueeze(1).to_broadcast(shape),
                                            quarter[:, :].unsqueeze(2).to_broadcast(shape),
                                            ALU.mult).then_inc(S["p_ready"], 1)
                    if k % 2 == 0 and k:
                        dve.wait_ge(S["sel_mm"], k)
                        take(nc.vector.tensor_copy, k - 1)
                dve.wait_ge(S["sel_mm"], KT)
                take(nc.vector.tensor_copy, KT - 1)

        with ExitStack() as s3, nc.Block() as block:
            up_ps = s3.enter_context(nc.psum_tensor("f0_up_ps", [P, 2, TILE], F32))
            down_ps = s3.enter_context(nc.psum_tensor("f0_down_ps", [P, 2, 2, TILE], F32))
            inner = s3.enter_context(nc.sbuf_tensor("f0_inner", [P, 2, GROUPS], F32))

            @block.tensor
            def _(pe):
                def up(i):
                    if i >= 2:
                        pe.wait_ge(S["inner_ready"], i - 1)
                    for r in range(2):
                        mm = nc.tensor.matmul(up_ps[r * F:(r + 1) * F, i % 2, 0:GROUPS], f1[:, 2 * i + r, :],
                                              sel[:, :, 2 * i + r], start=True, stop=True)
                    mm.then_inc(S["up_mm"], 1)
                pe.wait_ge(weights, 32)
                up(0)
                for i in range(PAIRS):
                    if i + 1 < PAIRS:
                        up(i + 1)
                    pe.wait_ge(S["inner_ready"], i + 1)
                    if i >= 2:
                        pe.wait_ge(S["out_ready"], i - 1)
                    for r in range(2):
                        mm = nc.tensor.matmul(down_ps[:, i % 2, r, 0:GROUPS], f2[r * F:(r + 1) * F, i, :],
                                              inner[r * F:(r + 1) * F, i % 2, :], start=True, stop=True)
                    mm.then_inc(S["down_mm"], 1)

            @block.scalar
            def _(act):
                for i in range(PAIRS):
                    act.wait_ge(S["up_mm"], i + 1)
                    if i >= 2:
                        act.wait_ge(S["down_mm"], i - 1)
                    nc.scalar.activation(inner[:, i % 2, :], up_ps[:, i % 2, 0:GROUPS], ACT.Relu,
                                         bias=bias[:, i:i + 1]).then_inc(S["inner_ready"], 1)

            @block.vector
            def _(dve):
                for i in range(PAIRS):
                    dve.wait_ge(S["down_mm"], i + 1)
                    nc.vector.tensor_copy(sel[:, :, 2 * i:2 * i + 2].rearrange("p g r -> p r g"), down_ps[:, i % 2, :, 0:GROUPS]).then_inc(S["out_ready"], 1)

        with ExitStack() as s4, nc.Block() as block:
            tr_ps, o_ps = (s4.enter_context(nc.psum_tensor(f"f0_{n}", [P, 2, TILE], F32)) for n in ("tr_ps", "o_ps"))
            out_rows = s4.enter_context(nc.sbuf_tensor("f0_out_rows", [P, 2, TILE], F32))
            parts = P // 32

            def turned(k):
                return S["turned_odd" if k % 2 else "turned_even"]

            def take_rows(eng, copy, k):
                eng.wait_ge(S["o_turned"], k + 1)
                if k >= 2:
                    eng.wait_ge(S["o_mm"], k - 1)
                copy(out_rows[:, k % 2, :], tr_ps[:, k % 2, :]).then_inc(turned(k), 1)

            @block.tensor
            def _(pe):
                def turn(k):
                    if k >= 2:
                        pe.wait_ge(turned(k), k // 2)
                    for j in range(parts):
                        g = k * GPT + 2 * j
                        mm = nc.tensor.transpose(tr_ps[:, k % 2, j * P:(j + 1) * P],
                                                 sel[:, g:g + 2, :].rearrange("p g e -> p (g e)"), c.ident[:, :])
                    mm.then_inc(S["o_turned"], 1)
                turn(0)
                for k in range(KT):
                    if k + 1 < KT:
                        turn(k + 1)
                    t, q = divmod(k, TILE // P)
                    pe.wait_ge(turned(k), k // 2 + 1)
                    if q == 0 and t >= 2:
                        pe.wait_ge(S["x_ready"], t - 1)
                    for j in range(parts):
                        at = k * P + j * 32
                        mm = nc.tensor.matmul(o_ps[:, t % 2, q * P + j * 32:q * P + (j + 1) * 32],
                                              out_rows[:, k % 2, j * P:(j + 1) * P], perm_t[:, at:at + 32],
                                              start=True, stop=True)
                    mm.then_inc(S["o_mm"], 1)

            @block.scalar
            def _(act):
                for k in range(0, KT, 2):
                    take_rows(act, nc.scalar.copy, k)

            @block.vector
            def _(dve):
                for k in range(1, KT, 2):
                    take_rows(dve, nc.vector.tensor_copy, k)
                    t = k * P // TILE
                    if (k + 1) * P % TILE == 0:
                        dve.wait_ge(S["o_mm"], k + 1)
                        at = slice(t * TILE, (t + 1) * TILE)
                        nc.vector.scalar_tensor_tensor(c.x_t[:, at], o_ps[:, t % 2, :], c.mod[:, 0, GB, t:t + 1],
                                                       c.x_t[:, at], ALU.mult, ALU.add).then_inc(S["x_ready"], 1)


def layout_slots(a, d, bf):
    ctrl = a["L0_ffn_controller"].reshape(P, 64)
    d["f0_ctrl"] = np.concatenate([ctrl, ctrl], 1)
    d["f0_tie"] = np.tile(np.linspace(0.0, 1e-6, 16, dtype=np.float32), (P, 1))
    rows = np.arange(P)
    d["f0_parity"] = (rows[:, None] // 64 == np.arange(2)[None]).astype(np.float32)
    d["f0_quarter"] = (rows[:, None] // 32 == np.arange(4)[None]).astype(np.float32)
    d["f0_f1"] = a["L0_ffn_f1"].reshape(P, 64, 64)
    d["f0_f2"] = a["L0_ffn_f2"].reshape(32, P, P).transpose(1, 0, 2)
    d["f0_bias"] = a["L0_ffn_bias"].reshape(32, P).T


def build(nc, ins, out):
    with ExitStack() as ctx:
        c = Core(nc, ctx, ins)
        stage_setup(c)
        adaln(c, 0, SA, CA)
        stage_mamba(c)
        adaln(c, 0, SB, CB)
        stage_slots(c)
        adaln(c, 1, SA, CA)
        stage_head_attention(c)
        adaln(c, 1, SB, CB)
        stage_moe1(c)
        recycle_semaphores(c)
        adaln(c, 2, SA, CA)
        stage_linear_attention(c)
        adaln(c, 2, SB, CB)
        stage_moe2(c)
        recycle_semaphores(c)
        adaln(c, 3, SA, CA)
        stage_window_attention(c)
        adaln(c, 3, SB, CB)
        stage_moe3(c)
        stage_store(c, out)


def rope_swap(v):
    return v.reshape(v.shape[:-1] + (P // 8, 2, 4))[..., ::-1, :].reshape(v.shape)


def vectors(a):
    v = {}
    bgu = a["L1_ffn_bgu"]
    for e in range(16):
        v[f"bg{e}"], v[f"bu{e}"] = bgu[e, ::2], bgu[e, 1::2]
    for h in range(2):
        half = slice(h * P, (h + 1) * P)
        for k in range(4):
            v[f"conv_w{k}{h}"] = a["L0_attn_conv_w"][half, k]
        v[f"conv_b{h}"] = a["L0_attn_conv_b"][half]
        v[f"dt_b{h}"] = a["L0_attn_dt_proj_b"][half]
        v[f"D{h}"] = a["L0_attn_D_param"][half]
        for n in range(16):
            v[f"A_log{n}{h}"] = a["L0_attn_A_log"][half, n]
    bup = a["L1_attn_bup"].reshape(16, 2, 8)
    bk, bv = bup[:, 0].reshape(P), bup[:, 1].reshape(P)
    v["L1_bq"], v["L1_bq_rot"] = a["L1_attn_bq"], rope_swap(a["L1_attn_bq"])
    v["L1_bk"], v["L1_bk_rot"], v["L1_bv"] = bk, rope_swap(bk), bv
    v["L1_bout"], v["L1_bdown"] = a["L1_attn_bout"], a["L1_attn_bdown"]
    for n in "qkvuo":
        v[f"L2_b{n}"] = a[f"L2_attn_b{n}"]
    v["L2_scale"] = a["L2_attn_scale"]
    for n in "qkvo":
        v[f"L3_b{n}"] = a[f"L3_attn_b{n}"]
    for n in "qk":
        v[f"L3_b{n}"] = v[f"L3_b{n}"].reshape(4, HG, HD).transpose(0, 2, 1).reshape(P)
    v["ln_g"], v["ln_b"] = a["L3_ffn_ln_g"], a["L3_ffn_ln_b"]
    table = np.zeros((P, len(VECS)), np.float32)
    for k, name in enumerate(VECS):
        table[:len(v[name]), k] = v[name]
    return table


def layouts(inputs):
    a = {k: np.ascontiguousarray(np.asarray(v)) for k, v in inputs.items()}
    bf = mybir.dt.np(BF16)
    d = {}
    d["x_t"] = a["L0_attn_x"].reshape(TOK, P).T
    d["mean_w"] = np.full((P, P), 1.0 / P, np.float32)
    d["ident"] = np.eye(P, dtype=np.float32)
    d["ident_bf"] = np.eye(P).astype(bf)
    for l in range(LAYERS):
        d[f"L{l}_c_t"] = a[f"L{l}_c"].T
        d[f"L{l}_wmod"] = a[f"L{l}_wmod"]
    d["upper_bf"] = np.triu(np.ones((P, P))).astype(bf)
    d["ones_bf"] = np.ones((P, P)).astype(bf)
    d["vecs"] = vectors(a)
    layout_moe2(a, d, bf)
    layout_moe1(a, d, bf)
    layout_moe3(a, d, bf)
    layout_head_attention(a, d, bf)
    layout_linear_attention(a, d, bf)
    layout_window_attention(a, d, bf)
    layout_mamba(a, d, bf)
    layout_slots(a, d, bf)
    return {k: np.ascontiguousarray(v) for k, v in d.items()}


def kernel(**inputs):
    import concourse.bacc as bacc
    from concourse.bass_utils import run_bass_kernel_spmd
    nc = bacc.Bacc("TRN2", target_bir_lowering=False, num_devices=1)
    arrays = {f"in_{k}": v for k, v in layouts(inputs).items()}
    ins = {k[3:]: nc.dram_tensor(k, v.shape, mybir.dt.from_np(v.dtype), kind="ExternalInput").ap()
           for k, v in arrays.items()}
    out = nc.dram_tensor("out_t", (P, TOK), F32, kind="ExternalOutput").ap()
    build(nc, ins, out)
    r = run_bass_kernel_spmd(nc, [arrays], core_ids=[0])
    return np.ascontiguousarray(r.results[0]["out_t"].T).reshape(BATCH, SEQ, P)
```
